# Optimizing a Trainium2 kernel written in Bass

```python
import numpy as np
import jax
import jax.numpy as jnp

def _softmax(x, axis=-1):
    return jax.nn.softmax(x, axis=axis)

def _gelu(x):
    return jax.nn.gelu(x, approximate=True)

def _silu(x):
    return jax.nn.silu(x)

def _sigmoid(x):
    return jax.nn.sigmoid(x)

def _layernorm(x, axis=-1, eps=1e-05):
    m = jnp.mean(x, axis=axis, keepdims=True)
    v = jnp.var(x, axis=axis, keepdims=True)
    return (x - m) / jnp.sqrt(v + eps)

def _scatter_add(tgt, idx, src, axis=0):
    return tgt.at[idx].add(src)

def _segment_sum(src, seg, n):
    return jax.ops.segment_sum(src, seg, n)
kernel_name = 'mk_decoder_postln_d4_seqx_r8_1f97e3'

def setup_inputs(seed: int=0):
    np.random.seed(seed)
    _w = jnp.asarray

    def _rec_inputs():
        import jax
        import jax.numpy as jnp
        _rk = jax.random.key(seed)
        x = -1.394e-06 + 0.9999 * jax.random.normal(jax.random.fold_in(_rk, 1), (2, 512, 128), jnp.float32)
        _lenS = 512 - jax.random.randint(jax.random.fold_in(_rk, 7), (2,), 0, max(1, 512 // 4) + 1, jnp.int32)
        _lenS2 = 154 - jax.random.randint(jax.random.fold_in(_rk, 8), (2,), 0, max(1, 154 // 4) + 1, jnp.int32)
        _ctx_1024P = jax.random.normal(jax.random.fold_in(_rk, 11), (2, 16, 128), jnp.float32)
        _ctx_1024c = jax.random.dirichlet(jax.random.fold_in(_rk, 511), 0.3 * jnp.ones((16,), jnp.float32), (2, 154))
        _ctx_1024t = jnp.einsum('bsk,bkd->bsd', _ctx_1024c, _ctx_1024P)
        _ctx_1024t = _ctx_1024t * jax.lax.rsqrt(jnp.mean(jnp.square(_ctx_1024t)) + 1e-12) * 0.953939
        ctx_1024 = -0.000392918 + 0.999932 * (_ctx_1024t + 0.3 * jax.random.normal(jax.random.fold_in(_rk, 611), (2, 154, 128), jnp.float32))
        itok_BxS2_0_2047 = jax.random.randint(jax.random.fold_in(_rk, 13), (2, 154), 0, 256, jnp.int32)
        itok_BxS_0_511 = jax.random.randint(jax.random.fold_in(_rk, 14), (2, 512), 0, 64, jnp.int32)
        _validS = jnp.arange(512)[None, :] < _lenS[:, None]
        _validS2 = jnp.arange(154)[None, :] < _lenS2[:, None]
        _causal = jnp.tril(jnp.ones((512, 512), dtype=bool))
        mask_BxS2_bk0 = jnp.logical_not(jnp.broadcast_to(_validS2[:, :], (2, 154)))
        return (x, ctx_1024, itok_BxS2_0_2047, itok_BxS_0_511, mask_BxS2_bk0)
    x, ctx_1024, itok_BxS2_0_2047, itok_BxS_0_511, mask_BxS2_bk0 = _rec_inputs()

    def _L0_attn_setup():
        import jax, jax.numpy as jnp
        import numpy as np
        B, T, C = (4, 128, 128)
        HS = 64
        H = C // HS
        D_W, D_A, D_V, D_G = (64, 64, 32, 128)
        EPS = 0.00064

        def _wkv(r, w, k, v, a, b):
            Bv, Tv, Cv = r.shape
            rs = lambda t: t.reshape(Bv, Tv, H, HS)
            r, k, v, a, b = (rs(r), rs(k), rs(v), rs(a), rs(b))
            wd = jnp.exp(-jnp.exp(rs(w)))

            def step(S, xs):
                r_, w_, k_, v_, a_, b_ = xs
                sa = jnp.einsum('bhij,bhj->bhi', S, a_)
                S = S * w_[:, :, None, :] + sa[..., None] * b_[:, :, None, :] + v_[..., None] * k_[:, :, None, :]
                y = jnp.einsum('bhij,bhj->bhi', S, r_)
                return (S, y)
            xs = tuple((jnp.swapaxes(t, 0, 1) for t in (r, wd, k, v, a, b)))
            S0 = jnp.zeros((Bv, H, HS, HS), r.dtype)
            _, ys = jax.lax.scan(step, S0, xs)
            return jnp.swapaxes(ys, 0, 1).reshape(Bv, Tv, Cv)

        def _forward(x, x_r, x_w, x_k, x_v, x_a, x_g, w0, w1, w2, a0, a1, a2, v0, v1, v2, g1, g2, k_k, k_a, r_k, Wr, Wk, Wv, Wo, ln_w, ln_b):
            Bv, Tv, Cv = x.shape
            xx = jnp.concatenate([jnp.zeros_like(x[:, :1]), x[:, :-1]], axis=1) - x
            xr = x + xx * x_r
            xw = x + xx * x_w
            xk = x + xx * x_k
            xv = x + xx * x_v
            xa = x + xx * x_a
            xg = x + xx * x_g
            r = xr @ Wr
            w = -jax.nn.softplus(-(w0 + jnp.tanh(xw @ w1) @ w2)) - 0.5
            k = xk @ Wk
            v = xv @ Wv
            v_first = jax.lax.stop_gradient(v)
            v = v + (v_first - v) * jax.nn.sigmoid(v0 + xv @ v1 @ v2)
            a = jax.nn.sigmoid(a0 + xa @ a1 @ a2)
            g = jax.nn.sigmoid(xg @ g1) @ g2
            kk = k * k_k
            kkh = kk.reshape(Bv, Tv, H, HS)
            kkh = kkh / jnp.maximum(jnp.linalg.norm(kkh, axis=-1, keepdims=True), 1e-12)
            kk = kkh.reshape(Bv, Tv, Cv)
            k = k * (1 + (a - 1) * k_a)
            y = _wkv(r, w, k, v, -kk, kk * a)
            yh = y.reshape(Bv, Tv, H, HS)
            mu = jnp.mean(yh, axis=-1, keepdims=True)
            var = jnp.var(yh, axis=-1, keepdims=True)
            y = ((yh - mu) / jnp.sqrt(var + EPS)).reshape(Bv, Tv, Cv) * ln_w + ln_b
            rt = (r.reshape(Bv, Tv, H, HS) * k.reshape(Bv, Tv, H, HS) * r_k).sum(-1, keepdims=True) * v.reshape(Bv, Tv, H, HS)
            y = y + rt.reshape(Bv, Tv, Cv)
            return y * g @ Wo
        key = jax.random.key(seed)
        ks = jax.random.split(key, 28)
        it = iter(range(28))
        n = lambda shape, std: jax.random.normal(ks[next(it)], shape, jnp.float32) * std
        s = C ** (-0.5)
        return {'x': n((B, T, C), 1.0), 'x_r': n((1, 1, C), 0.01), 'x_w': n((1, 1, C), 0.01), 'x_k': n((1, 1, C), 0.01), 'x_v': n((1, 1, C), 0.01), 'x_a': n((1, 1, C), 0.01), 'x_g': n((1, 1, C), 0.01), 'w0': n((1, 1, C), 0.02), 'w1': n((C, D_W), 0.04), 'w2': n((D_W, C), 0.04), 'a0': n((1, 1, C), 0.02), 'a1': n((C, D_A), 0.04), 'a2': n((D_A, C), 0.04), 'v0': n((1, 1, C), 0.02), 'v1': n((C, D_V), 0.04), 'v2': n((D_V, C), 0.04), 'g1': n((C, D_G), 0.04), 'g2': n((D_G, C), 0.04), 'k_k': n((1, 1, C), 0.02), 'k_a': n((1, 1, C), 0.02), 'r_k': n((H, HS), 0.1) + 0.1 * jnp.arange(H, dtype=jnp.float32)[:, None], 'Wr': n((C, C), s), 'Wk': n((C, C), s), 'Wv': n((C, C), s), 'Wo': n((C, C), s), 'ln_w': jnp.ones((C,), jnp.float32), 'ln_b': jnp.zeros((C,), jnp.float32)}
    _L0_attn_all = _L0_attn_setup()
    _L0_attn_in = {k: v for k, v in _L0_attn_all.items() if k in ('x_r', 'x_w', 'x_k', 'x_v', 'x_a', 'x_g', 'w0', 'w1', 'w2', 'a0', 'a1', 'a2', 'v0', 'v1', 'v2', 'g1', 'g2', 'k_k', 'k_a', 'r_k', 'Wr', 'Wk', 'Wv', 'Wo', 'ln_w', 'ln_b')}
    del _L0_attn_all

    def _L0_xattn_setup():
        import jax, jax.numpy as jnp
        import numpy as np
        DIM = 128
        DIM_LATENT = 128
        DIM_HEAD = 64
        INNER = max(DIM, DIM_LATENT)
        HEADS = INNER // DIM_HEAD
        SCALE = DIM_HEAD ** (-0.5)
        LN_EPS = 1e-05
        RMS_EPS = 1e-08

        def layernorm(x, g, b):
            mu = jnp.mean(x, axis=-1, keepdims=True)
            var = jnp.mean(jnp.square(x - mu), axis=-1, keepdims=True)
            return (x - mu) * jax.lax.rsqrt(var + LN_EPS) * g + b

        def rmsnorm(x, gamma):
            n = jnp.linalg.norm(x, axis=-1, keepdims=True) * x.shape[-1] ** (-0.5)
            return x / jnp.maximum(n, RMS_EPS) * gamma
        key = jax.random.key(seed)
        ks = jax.random.split(key, 8)
        b, n, nl = (8, 256, 64)
        x = jax.random.normal(ks[0], (b, n, DIM), dtype=jnp.float32)
        latents = jax.random.normal(ks[1], (b, nl, DIM_LATENT), dtype=jnp.float32)
        mask = jax.random.randint(ks[2], (b, n), 0, 2).astype(bool)
        init = lambda k, shape, fan_in: jax.random.normal(k, shape, jnp.float32) * fan_in ** (-0.5)
        return {'x': x, 'latents': latents, 'mask': mask, 'ln_x_g': jnp.ones((DIM,), jnp.float32), 'ln_x_b': jnp.zeros((DIM,), jnp.float32), 'ln_l_g': jnp.ones((DIM_LATENT,), jnp.float32), 'ln_l_b': jnp.zeros((DIM_LATENT,), jnp.float32), 'q_gamma': jnp.ones((DIM_HEAD,), jnp.float32), 'k_gamma': jnp.ones((DIM_HEAD,), jnp.float32), 'W_q': init(ks[3], (DIM_LATENT, INNER), DIM_LATENT), 'W_kv': init(ks[4], (DIM, 2 * INNER), DIM), 'W_out': init(ks[5], (INNER, DIM_LATENT), INNER), 'b_out': jnp.zeros((DIM_LATENT,), jnp.float32)}
    _L0_xattn_all = _L0_xattn_setup()
    _L0_xattn_in = {k: v for k, v in _L0_xattn_all.items() if k in ('ln_x_g', 'ln_x_b', 'ln_l_g', 'ln_l_b', 'q_gamma', 'k_gamma', 'W_q', 'W_kv', 'W_out', 'b_out')}
    del _L0_xattn_all

    def _L0_ffn_setup():
        import jax, jax.numpy as jnp
        import numpy as np
        TOPK = 4
        key = jax.random.key(seed)
        ks = jax.random.split(key, 9)
        B, T, D = (4, 256, 128)
        E, H = (32, 128)
        HS = H * TOPK
        s = lambda k, shape, fan: jax.random.normal(k, shape, dtype=jnp.float32) / np.sqrt(fan)
        return {'x': jax.random.normal(ks[0], (B, T, D), dtype=jnp.float32), 'router_w': s(ks[1], (E, D), D), 'router_bias': jnp.zeros((E,), dtype=jnp.float32), 'gate_w': s(ks[2], (E, H, D), D), 'up_w': s(ks[3], (E, H, D), D), 'down_w': s(ks[4], (E, D, H), H), 'sgate_w': s(ks[5], (HS, D), D), 'sup_w': s(ks[6], (HS, D), D), 'sdown_w': s(ks[7], (D, HS), HS)}
    _L0_ffn_all = _L0_ffn_setup()
    _L0_ffn_in = {k: v for k, v in _L0_ffn_all.items() if k in ('router_w', 'router_bias', 'gate_w', 'up_w', 'down_w', 'sgate_w', 'sup_w', 'sdown_w')}
    del _L0_ffn_all

    def _L1_attn_setup():
        import jax, jax.numpy as jnp
        import numpy as np
        B, T, E, H = (2, 256, 128, 16)
        HD = E // H

        def _xavier(key, shape):
            limit = float(np.sqrt(6.0 / (shape[0] + shape[1])))
            return jax.random.uniform(key, shape, dtype=jnp.float32, minval=-limit, maxval=limit)
        key = jax.random.key(seed)
        kx, kq, kk, kv = jax.random.split(key, 4)
        return {'x': jax.random.normal(kx, (B, T, E), dtype=jnp.float32), 'w_Q': _xavier(kq, (E, E)), 'w_K': _xavier(kk, (E, E)), 'w_V': _xavier(kv, (E, E))}
    _L1_attn_all = _L1_attn_setup()
    _L1_attn_in = {k: v for k, v in _L1_attn_all.items() if k in ('w_Q', 'w_K', 'w_V')}
    del _L1_attn_all

    def _L1_xattn_setup():
        import jax, jax.numpy as jnp
        import numpy as np
        D_MODEL = 128
        N_HEADS = 16
        D_HEAD = D_MODEL // N_HEADS
        key = jax.random.key(seed)
        ks = jax.random.split(key, 11)
        B, L = (2, 256)
        s = 1.0 / np.sqrt(D_MODEL)
        return {'query': jax.random.normal(ks[0], (B, L, D_MODEL), jnp.float32), 'key': jax.random.normal(ks[1], (B, L, D_MODEL), jnp.float32), 'value': jax.random.normal(ks[2], (B, L, D_MODEL), jnp.float32), 'Wq': jax.random.normal(ks[3], (D_MODEL, D_MODEL), jnp.float32) * s, 'bq': jnp.zeros((D_MODEL,), jnp.float32), 'Wk': jax.random.normal(ks[4], (D_MODEL, D_MODEL), jnp.float32) * s, 'bk': jnp.zeros((D_MODEL,), jnp.float32), 'Wv': jax.random.normal(ks[5], (D_MODEL, D_MODEL), jnp.float32) * s, 'bv': jnp.zeros((D_MODEL,), jnp.float32), 'Wo': jax.random.normal(ks[6], (D_MODEL, D_MODEL), jnp.float32) * s, 'bo': jnp.zeros((D_MODEL,), jnp.float32)}
    _L1_xattn_all = _L1_xattn_setup()
    _L1_xattn_in = {k: v for k, v in _L1_xattn_all.items() if k in ('Wq', 'bq', 'Wk', 'bk', 'Wv', 'bv', 'Wo', 'bo')}
    del _L1_xattn_all

    def _L1_ffn_setup():
        import jax, jax.numpy as jnp
        import numpy as np
        DIM = 128
        DEPTH = 6
        HEADS = 16
        DIM_HEAD = 64
        WINDOW = 32
        INNER = HEADS * DIM_HEAD
        DIM_INNER = int(DIM * 4 * 2 / 3)
        QK_SCALE = 8.0

        def shift_tokens(t):
            a, s = jnp.split(t, 2, -1)
            s = jnp.pad(s, ((0, 0), (1, 0), (0, 0)))[:, :-1]
            return jnp.concatenate([a, s], -1)

        def l2norm(t):
            return t / jnp.maximum(jnp.linalg.norm(t, axis=-1, keepdims=True), 1e-12)

        def rotate_half(x):
            x1, x2 = jnp.split(x, 2, -1)
            return jnp.concatenate([-x2, x1], -1)

        def rotary_tables(n):
            half = jnp.arange(0, DIM_HEAD, 2, dtype=jnp.float32)
            inv_freq = 1.0 / 10000.0 ** (half / DIM_HEAD)
            t = jnp.arange(n, dtype=jnp.float32)
            freqs = t[:, None] * inv_freq[None, :]
            freqs = jnp.concatenate([freqs, freqs], -1)
            base_scale = (half + 0.4 * DIM_HEAD) / (1.4 * DIM_HEAD)
            power = (t - n // 2) / (WINDOW // 2)
            scale = base_scale[None, :] ** power[:, None]
            scale = jnp.concatenate([scale, scale], -1)
            return (freqs, scale)

        def local_attention(q, k, v):
            b, h, n, d = q.shape
            w = WINDOW
            nw = n // w
            bq = q.reshape(b, h, nw, w, d)
            bk = k.reshape(b, h, nw, w, d)
            bv = v.reshape(b, h, nw, w, d)

            def look(t):
                p = jnp.pad(t, ((0, 0), (0, 0), (1, 0), (0, 0), (0, 0)))
                return jnp.concatenate([p[:, :, :nw], p[:, :, 1:]], axis=3)
            bk2, bv2 = (look(bk), look(bv))
            seq = jnp.arange(n).reshape(nw, w)
            seq_p = jnp.pad(seq, ((1, 0), (0, 0)), constant_values=-1)
            jt = jnp.concatenate([seq_p[:nw], seq_p[1:]], axis=1)
            it = seq[:, :, None]
            jb = jt[:, None, :]
            mask = (it < jb) | (it > jb + w) | (jb == -1)
            sim = jnp.einsum('bhwie,bhwje->bhwij', bq, bk2) * QK_SCALE
            sim = jnp.where(mask, -jnp.finfo(sim.dtype).max, sim)
            attn = jax.nn.softmax(sim, -1)
            out = jnp.einsum('bhwij,bhwje->bhwie', attn, bv2)
            return out.reshape(b, h, n, d)

        def attn_layer(x, Wqkv, qs, ksc, Wo):
            b, n, _ = x.shape
            qkv = x @ Wqkv
            q, k, v = jnp.split(qkv, 3, -1)
            sh = lambda t: t.reshape(b, n, HEADS, DIM_HEAD).transpose(0, 2, 1, 3)
            q, k, v = (sh(q), sh(k), sh(v))
            q = l2norm(q) * qs
            k = l2norm(k) * ksc
            freqs, scale = rotary_tables(n)
            cos, sin = (jnp.cos(freqs), jnp.sin(freqs))
            q = q * cos * scale + rotate_half(q) * sin * scale
            inv = 1.0 / scale
            k = k * cos * inv + rotate_half(k) * sin * inv
            out = local_attention(q, k, v)
            out = out.transpose(0, 2, 1, 3).reshape(b, n, INNER)
            return out @ Wo

        def ffn_layer(x, g, bln, W1, b1, W2, b2):
            mu = x.mean(-1, keepdims=True)
            var = ((x - mu) ** 2).mean(-1, keepdims=True)
            xn = (x - mu) / jnp.sqrt(var + 1e-05) * g + bln
            hg = xn @ W1 + b1
            a, gate = jnp.split(hg, 2, -1)
            return a * jax.nn.gelu(gate, approximate=False) @ W2 + b2
        key = jax.random.key(seed)
        ks = jax.random.split(key, 8)
        B, N = (2, 256)
        init = lambda k, shape: jax.random.normal(k, shape, jnp.float32) * 0.02
        return {'x': jax.random.normal(ks[0], (B, N, DIM), jnp.float32), 'Wqkv': init(ks[1], (DEPTH, DIM, 3 * INNER)), 'q_scale': jnp.ones((DEPTH, DIM_HEAD), jnp.float32), 'k_scale': jnp.ones((DEPTH, DIM_HEAD), jnp.float32), 'Wo': init(ks[2], (DEPTH, INNER, DIM)), 'ln_g': jnp.ones((DEPTH, DIM), jnp.float32), 'ln_b': jnp.zeros((DEPTH, DIM), jnp.float32), 'W1': init(ks[3], (DEPTH, DIM, 2 * DIM_INNER)), 'b1': jnp.zeros((DEPTH, 2 * DIM_INNER), jnp.float32), 'W2': init(ks[4], (DEPTH, DIM_INNER, DIM)), 'b2': jnp.zeros((DEPTH, DIM), jnp.float32)}
    _L1_ffn_all = _L1_ffn_setup()
    _L1_ffn_in = {k: v for k, v in _L1_ffn_all.items() if k in ('Wqkv', 'q_scale', 'k_scale', 'Wo', 'ln_g', 'ln_b', 'W1', 'b1', 'W2', 'b2')}
    del _L1_ffn_all

    def _L2_attn_setup():
        import jax, jax.numpy as jnp
        import numpy as np
        import math
        B, L, E, H, K = (4, 128, 128, 16, 64)
        D = E // H

        def _attend(q, in_proj_weight, in_proj_bias, out_w, out_b, rel_pe):
            b, l, e = q.shape
            h, d = (H, D)
            qkv = q @ in_proj_weight.T + in_proj_bias
            qh, kh, vh = jnp.split(qkv, 3, axis=-1)
            qh = qh.reshape(b, l, h, d).transpose(0, 2, 1, 3)
            kh = kh.reshape(b, l, h, d).transpose(0, 2, 1, 3)
            vh = vh.reshape(b, l, h, d).transpose(0, 2, 1, 3)
            qh = qh / math.sqrt(d)
            scores = jnp.einsum('bhid,bhjd->bhij', qh, kh)
            pos = jnp.arange(l)
            rel = jnp.clip(pos[None, :] - pos[:, None], -K, K) + K
            bias_r = jnp.einsum('bhid,rd->bhir', qh, rel_pe)
            bias = jnp.take_along_axis(bias_r, jnp.broadcast_to(rel[None, None], (b, h, l, l)), axis=-1)
            attn = jax.nn.softmax(scores + bias, axis=-1)
            out = jnp.einsum('bhij,bhjd->bhid', attn, vh)
            out = out.transpose(0, 2, 1, 3).reshape(b, l, e)
            return out @ out_w.T + out_b
        key = jax.random.key(seed)
        ks = jax.random.split(key, 4)
        s = 1.0 / math.sqrt(E)
        return {'q': jax.random.normal(ks[0], (B, L, E), dtype=jnp.float32), 'in_proj_weight': jax.random.normal(ks[1], (3 * E, E), dtype=jnp.float32) * s, 'in_proj_bias': jnp.zeros((3 * E,), dtype=jnp.float32), 'out_w': jax.random.normal(ks[2], (E, E), dtype=jnp.float32) * s, 'out_b': jnp.zeros((E,), dtype=jnp.float32), 'rel_pe': jax.random.normal(ks[3], (2 * K + 1, D), dtype=jnp.float32) * (1.0 / math.sqrt(D))}
    _L2_attn_all = _L2_attn_setup()
    _L2_attn_in = {k: v for k, v in _L2_attn_all.items() if k in ('in_proj_weight', 'in_proj_bias', 'out_w', 'out_b', 'rel_pe')}
    del _L2_attn_all

    def _L2_xattn_setup():
        import jax, jax.numpy as jnp
        import numpy as np
        DIM = 128
        HEADS = 16
        HEAD_DIM = DIM // HEADS
        SCALE = HEAD_DIM ** (-0.5)
        key = jax.random.key(seed)
        ks = jax.random.split(key, 13)
        B, Nq, Nk = (4, 256, 256)
        s = DIM ** (-0.5)
        return {'query': jax.random.normal(ks[0], (B, Nq, DIM), jnp.float32), 'key': jax.random.normal(ks[1], (B, Nk, DIM), jnp.float32), 'value': jax.random.normal(ks[2], (B, Nk, DIM), jnp.float32), 'qpos': jax.random.randint(ks[3], (B, Nq), 0, Nq), 'kpos': jax.random.randint(ks[4], (B, Nk), 0, Nk), 'Wq': jax.random.normal(ks[5], (DIM, DIM), jnp.float32) * s, 'bq': jnp.zeros((DIM,), jnp.float32), 'Wk': jax.random.normal(ks[6], (DIM, DIM), jnp.float32) * s, 'bk': jnp.zeros((DIM,), jnp.float32), 'Wv': jax.random.normal(ks[7], (DIM, DIM), jnp.float32) * s, 'bv': jnp.zeros((DIM,), jnp.float32), 'Wo': jax.random.normal(ks[8], (DIM, DIM), jnp.float32) * s, 'bo': jnp.zeros((DIM,), jnp.float32)}
    _L2_xattn_all = _L2_xattn_setup()
    _L2_xattn_in = {k: v for k, v in _L2_xattn_all.items() if k in ('Wq', 'bq', 'Wk', 'bk', 'Wv', 'bv', 'Wo', 'bo')}
    del _L2_xattn_all

    def _L2_ffn_setup():
        import jax, jax.numpy as jnp
        import numpy as np
        IN_F = 128
        OUT_F = 128
        N_EXPERTS = 8
        TOP_K = 2
        key = jax.random.key(seed)
        ks = jax.random.split(key, 5)
        scale_in = 1.0 / np.sqrt(IN_F)
        x = jax.random.normal(ks[0], (4, 256, IN_F), dtype=jnp.float32)
        W_experts = jax.random.uniform(ks[1], (N_EXPERTS, OUT_F, IN_F), jnp.float32, -scale_in, scale_in)
        b_experts = jax.random.uniform(ks[2], (N_EXPERTS, OUT_F), jnp.float32, -scale_in, scale_in)
        W_router = jax.random.uniform(ks[3], (N_EXPERTS, IN_F), jnp.float32, -scale_in, scale_in)
        b_router = jax.random.uniform(ks[4], (N_EXPERTS,), jnp.float32, -scale_in, scale_in)
        return {'x': x, 'W_experts': W_experts, 'b_experts': b_experts, 'W_router': W_router, 'b_router': b_router}
    _L2_ffn_all = _L2_ffn_setup()
    _L2_ffn_in = {k: v for k, v in _L2_ffn_all.items() if k in ('W_experts', 'b_experts', 'W_router', 'b_router')}
    del _L2_ffn_all

    def _L3_attn_setup():
        import jax, jax.numpy as jnp
        import numpy as np
        DIM = 128
        HEADS = 16
        DIM_HEAD = 64
        SOFTCAP = 50.0
        key = jax.random.key(seed)
        k1, k2, k3, k4 = jax.random.split(key, 4)
        b, n = (2, 256)
        dim_inner = HEADS * DIM_HEAD
        x = jax.random.normal(k1, (b, n, DIM), dtype=jnp.float32)
        w_qkv = jax.random.normal(k2, (DIM, 3 * dim_inner), dtype=jnp.float32) * 0.02
        w_gates = jax.random.normal(k3, (DIM, HEADS), dtype=jnp.float32) * 0.02
        w_out = jax.random.normal(k4, (dim_inner, DIM), dtype=jnp.float32) * 0.02
        return {'x': x, 'w_qkv': w_qkv, 'w_gates': w_gates, 'w_out': w_out}
    _L3_attn_all = _L3_attn_setup()
    _L3_attn_in = {k: v for k, v in _L3_attn_all.items() if k in ('w_qkv', 'w_gates', 'w_out')}
    del _L3_attn_all

    def _L3_xattn_setup():
        import jax, jax.numpy as jnp
        import numpy as np
        Q_DIM, KV_DIM = (128, 128)
        H, HD, KVC, QC, R = (16, 64, 32, 48, 64)
        LOOKBACK = 2
        B, LQ, LK = (4, 256, 64)

        def _rope(x, pos):
            r = x.shape[-1]
            half = r // 2
            inv = 1.0 / 10000.0 ** (jnp.arange(half, dtype=jnp.float32) / half)
            ang = pos[..., None].astype(jnp.float32) * inv
            cos, sin = (jnp.cos(ang), jnp.sin(ang))
            x1, x2 = (x[..., :half], x[..., half:])
            return jnp.concatenate([x1 * cos - x2 * sin, x1 * sin + x2 * cos], axis=-1)
        key = jax.random.key(seed)
        ks = jax.random.split(key, 11)
        w = lambda k, shape: jax.random.normal(k, shape, jnp.float32) / np.sqrt(shape[0]).astype(np.float32)
        return {'q': jax.random.normal(ks[0], (B, LQ, Q_DIM), jnp.float32), 'kv': jax.random.normal(ks[1], (B, LK, KV_DIM), jnp.float32), 'seg_id': jnp.sort(jax.random.randint(ks[2], (B, LQ), 0, LK), axis=-1), 'w_kv_comp': w(ks[3], (KV_DIM, KVC)), 'w_q_down': w(ks[4], (Q_DIM, QC)), 'w_q_up': w(ks[5], (QC, H * HD)), 'w_q_rope': w(ks[6], (QC, H * R)), 'w_k_up': w(ks[7], (KVC, H * HD)), 'w_k_rope': w(ks[8], (KVC, R)), 'w_v_up': w(ks[9], (KVC, H * HD)), 'w_out': w(ks[10], (H * HD, Q_DIM))}
    _L3_xattn_all = _L3_xattn_setup()
    _L3_xattn_in = {k: v for k, v in _L3_xattn_all.items() if k in ('w_kv_comp', 'w_q_down', 'w_q_up', 'w_q_rope', 'w_k_up', 'w_k_rope', 'w_v_up', 'w_out')}
    del _L3_xattn_all

    def _L3_ffn_setup():
        import jax, jax.numpy as jnp
        import numpy as np
        LN_EPS = 1e-05

        def entmax15(z):
            z = z / 2.0
            z = z - jnp.max(z, axis=-1, keepdims=True)
            zs = -jnp.sort(-z, axis=-1)
            k = jnp.arange(1, z.shape[-1] + 1, dtype=z.dtype)
            mean = jnp.cumsum(zs, axis=-1) / k
            meansq = jnp.cumsum(zs * zs, axis=-1) / k
            ss = k * (meansq - jnp.square(mean))
            delta = (1.0 - ss) / k
            tau = mean - jnp.sqrt(jnp.clip(delta, 0.0))
            support = jnp.sum((tau <= zs).astype(jnp.int32), axis=-1, keepdims=True)
            tau_star = jnp.take_along_axis(tau, support - 1, axis=-1)
            return jnp.square(jnp.clip(z - tau_star, 0.0))

        def layernorm_noaffine(v):
            m = jnp.mean(v, axis=-1, keepdims=True)
            var = jnp.mean(jnp.square(v - m), axis=-1, keepdims=True)
            return (v - m) / jnp.sqrt(var + LN_EPS)

        def cp_mumoe(x, gate, Win, Wout):
            ones = jnp.ones(x.shape[:-1] + (1,), x.dtype)
            xb = jnp.concatenate([x, ones], axis=-1)
            z = jnp.einsum('btd,dr->btr', xb, Win) * gate
            return jnp.einsum('btr,or->bto', z, Wout)
        key = jax.random.key(seed)
        ks = jax.random.split(key, 8)
        B, T, D, O, D2, E, R = (8, 256, 128, 512, 128, 16, 64)
        s = lambda k, shape, scale: jax.random.normal(k, shape, jnp.float32) * scale
        return {'x': s(ks[0], (B, T, D), 1.0), 'proj': s(ks[1], (D, E), D ** (-0.5)), 'C1': s(ks[2], (E, R), E ** (-0.5)), 'Win1': s(ks[3], (D + 1, R), D ** (-0.5)), 'Wout1': s(ks[4], (O, R), R ** (-0.5)), 'C2': s(ks[5], (E, R), E ** (-0.5)), 'Win2': s(ks[6], (O + 1, R), O ** (-0.5)), 'Wout2': s(ks[7], (D2, R), R ** (-0.5))}
    _L3_ffn_all = _L3_ffn_setup()
    _L3_ffn_in = {k: v for k, v in _L3_ffn_all.items() if k in ('proj', 'C1', 'Win1', 'Wout1', 'C2', 'Win2', 'Wout2')}
    del _L3_ffn_all
    return {'x': x, 'ctx_1024': ctx_1024, 'itok_BxS2_0_2047': itok_BxS2_0_2047, 'itok_BxS_0_511': itok_BxS_0_511, 'mask_BxS2_bk0': mask_BxS2_bk0, 'L0_attn_x_r': _L0_attn_in['x_r'], 'L0_attn_x_w': _L0_attn_in['x_w'], 'L0_attn_x_k': _L0_attn_in['x_k'], 'L0_attn_x_v': _L0_attn_in['x_v'], 'L0_attn_x_a': _L0_attn_in['x_a'], 'L0_attn_x_g': _L0_attn_in['x_g'], 'L0_attn_w0': _L0_attn_in['w0'], 'L0_attn_w1': _L0_attn_in['w1'], 'L0_attn_w2': _L0_attn_in['w2'], 'L0_attn_a0': _L0_attn_in['a0'], 'L0_attn_a1': _L0_attn_in['a1'], 'L0_attn_a2': _L0_attn_in['a2'], 'L0_attn_v0': _L0_attn_in['v0'], 'L0_attn_v1': _L0_attn_in['v1'], 'L0_attn_v2': _L0_attn_in['v2'], 'L0_attn_g1': _L0_attn_in['g1'], 'L0_attn_g2': _L0_attn_in['g2'], 'L0_attn_k_k': _L0_attn_in['k_k'], 'L0_attn_k_a': _L0_attn_in['k_a'], 'L0_attn_r_k': _L0_attn_in['r_k'], 'L0_attn_Wr': _L0_attn_in['Wr'], 'L0_attn_Wk': _L0_attn_in['Wk'], 'L0_attn_Wv': _L0_attn_in['Wv'], 'L0_attn_Wo': _L0_attn_in['Wo'], 'L0_attn_ln_w': _L0_attn_in['ln_w'], 'L0_attn_ln_b': _L0_attn_in['ln_b'], 'L0_xattn_ln_x_g': _L0_xattn_in['ln_x_g'], 'L0_xattn_ln_x_b': _L0_xattn_in['ln_x_b'], 'L0_xattn_ln_l_g': _L0_xattn_in['ln_l_g'], 'L0_xattn_ln_l_b': _L0_xattn_in['ln_l_b'], 'L0_xattn_q_gamma': _L0_xattn_in['q_gamma'], 'L0_xattn_k_gamma': _L0_xattn_in['k_gamma'], 'L0_xattn_W_q': _L0_xattn_in['W_q'], 'L0_xattn_W_kv': _L0_xattn_in['W_kv'], 'L0_xattn_W_out': _L0_xattn_in['W_out'], 'L0_xattn_b_out': _L0_xattn_in['b_out'], 'L0_ffn_router_w': _L0_ffn_in['router_w'], 'L0_ffn_router_bias': _L0_ffn_in['router_bias'], 'L0_ffn_gate_w': _L0_ffn_in['gate_w'], 'L0_ffn_up_w': _L0_ffn_in['up_w'], 'L0_ffn_down_w': _L0_ffn_in['down_w'], 'L0_ffn_sgate_w': _L0_ffn_in['sgate_w'], 'L0_ffn_sup_w': _L0_ffn_in['sup_w'], 'L0_ffn_sdown_w': _L0_ffn_in['sdown_w'], 'L1_attn_w_Q': _L1_attn_in['w_Q'], 'L1_attn_w_K': _L1_attn_in['w_K'], 'L1_attn_w_V': _L1_attn_in['w_V'], 'L1_xattn_Wq': _L1_xattn_in['Wq'], 'L1_xattn_bq': _L1_xattn_in['bq'], 'L1_xattn_Wk': _L1_xattn_in['Wk'], 'L1_xattn_bk': _L1_xattn_in['bk'], 'L1_xattn_Wv': _L1_xattn_in['Wv'], 'L1_xattn_bv': _L1_xattn_in['bv'], 'L1_xattn_Wo': _L1_xattn_in['Wo'], 'L1_xattn_bo': _L1_xattn_in['bo'], 'L1_ffn_Wqkv': _L1_ffn_in['Wqkv'], 'L1_ffn_q_scale': _L1_ffn_in['q_scale'], 'L1_ffn_k_scale': _L1_ffn_in['k_scale'], 'L1_ffn_Wo': _L1_ffn_in['Wo'], 'L1_ffn_ln_g': _L1_ffn_in['ln_g'], 'L1_ffn_ln_b': _L1_ffn_in['ln_b'], 'L1_ffn_W1': _L1_ffn_in['W1'], 'L1_ffn_b1': _L1_ffn_in['b1'], 'L1_ffn_W2': _L1_ffn_in['W2'], 'L1_ffn_b2': _L1_ffn_in['b2'], 'L2_attn_in_proj_weight': _L2_attn_in['in_proj_weight'], 'L2_attn_in_proj_bias': _L2_attn_in['in_proj_bias'], 'L2_attn_out_w': _L2_attn_in['out_w'], 'L2_attn_out_b': _L2_attn_in['out_b'], 'L2_attn_rel_pe': _L2_attn_in['rel_pe'], 'L2_xattn_Wq': _L2_xattn_in['Wq'], 'L2_xattn_bq': _L2_xattn_in['bq'], 'L2_xattn_Wk': _L2_xattn_in['Wk'], 'L2_xattn_bk': _L2_xattn_in['bk'], 'L2_xattn_Wv': _L2_xattn_in['Wv'], 'L2_xattn_bv': _L2_xattn_in['bv'], 'L2_xattn_Wo': _L2_xattn_in['Wo'], 'L2_xattn_bo': _L2_xattn_in['bo'], 'L2_ffn_W_experts': _L2_ffn_in['W_experts'], 'L2_ffn_b_experts': _L2_ffn_in['b_experts'], 'L2_ffn_W_router': _L2_ffn_in['W_router'], 'L2_ffn_b_router': _L2_ffn_in['b_router'], 'L3_attn_w_qkv': _L3_attn_in['w_qkv'], 'L3_attn_w_gates': _L3_attn_in['w_gates'], 'L3_attn_w_out': _L3_attn_in['w_out'], 'L3_xattn_w_kv_comp': _L3_xattn_in['w_kv_comp'], 'L3_xattn_w_q_down': _L3_xattn_in['w_q_down'], 'L3_xattn_w_q_up': _L3_xattn_in['w_q_up'], 'L3_xattn_w_q_rope': _L3_xattn_in['w_q_rope'], 'L3_xattn_w_k_up': _L3_xattn_in['w_k_up'], 'L3_xattn_w_k_rope': _L3_xattn_in['w_k_rope'], 'L3_xattn_w_v_up': _L3_xattn_in['w_v_up'], 'L3_xattn_w_out': _L3_xattn_in['w_out'], 'L3_ffn_proj': _L3_ffn_in['proj'], 'L3_ffn_C1': _L3_ffn_in['C1'], 'L3_ffn_Win1': _L3_ffn_in['Win1'], 'L3_ffn_Wout1': _L3_ffn_in['Wout1'], 'L3_ffn_C2': _L3_ffn_in['C2'], 'L3_ffn_Win2': _L3_ffn_in['Win2'], 'L3_ffn_Wout2': _L3_ffn_in['Wout2']}

def reference(x, ctx_1024, itok_BxS2_0_2047, itok_BxS_0_511, mask_BxS2_bk0, L0_attn_x_r, L0_attn_x_w, L0_attn_x_k, L0_attn_x_v, L0_attn_x_a, L0_attn_x_g, L0_attn_w0, L0_attn_w1, L0_attn_w2, L0_attn_a0, L0_attn_a1, L0_attn_a2, L0_attn_v0, L0_attn_v1, L0_attn_v2, L0_attn_g1, L0_attn_g2, L0_attn_k_k, L0_attn_k_a, L0_attn_r_k, L0_attn_Wr, L0_attn_Wk, L0_attn_Wv, L0_attn_Wo, L0_attn_ln_w, L0_attn_ln_b, L0_xattn_ln_x_g, L0_xattn_ln_x_b, L0_xattn_ln_l_g, L0_xattn_ln_l_b, L0_xattn_q_gamma, L0_xattn_k_gamma, L0_xattn_W_q, L0_xattn_W_kv, L0_xattn_W_out, L0_xattn_b_out, L0_ffn_router_w, L0_ffn_router_bias, L0_ffn_gate_w, L0_ffn_up_w, L0_ffn_down_w, L0_ffn_sgate_w, L0_ffn_sup_w, L0_ffn_sdown_w, L1_attn_w_Q, L1_attn_w_K, L1_attn_w_V, L1_xattn_Wq, L1_xattn_bq, L1_xattn_Wk, L1_xattn_bk, L1_xattn_Wv, L1_xattn_bv, L1_xattn_Wo, L1_xattn_bo, L1_ffn_Wqkv, L1_ffn_q_scale, L1_ffn_k_scale, L1_ffn_Wo, L1_ffn_ln_g, L1_ffn_ln_b, L1_ffn_W1, L1_ffn_b1, L1_ffn_W2, L1_ffn_b2, L2_attn_in_proj_weight, L2_attn_in_proj_bias, L2_attn_out_w, L2_attn_out_b, L2_attn_rel_pe, L2_xattn_Wq, L2_xattn_bq, L2_xattn_Wk, L2_xattn_bk, L2_xattn_Wv, L2_xattn_bv, L2_xattn_Wo, L2_xattn_bo, L2_ffn_W_experts, L2_ffn_b_experts, L2_ffn_W_router, L2_ffn_b_router, L3_attn_w_qkv, L3_attn_w_gates, L3_attn_w_out, L3_xattn_w_kv_comp, L3_xattn_w_q_down, L3_xattn_w_q_up, L3_xattn_w_q_rope, L3_xattn_w_k_up, L3_xattn_w_k_rope, L3_xattn_w_v_up, L3_xattn_w_out, L3_ffn_proj, L3_ffn_C1, L3_ffn_Win1, L3_ffn_Wout1, L3_ffn_C2, L3_ffn_Win2, L3_ffn_Wout2):
    import jax
    import jax.numpy as jnp

    def _L0_attn_ref(x, x_r, x_w, x_k, x_v, x_a, x_g, w0, w1, w2, a0, a1, a2, v0, v1, v2, g1, g2, k_k, k_a, r_k, Wr, Wk, Wv, Wo, ln_w, ln_b):
        import jax, jax.numpy as jnp
        import numpy as np
        B, T, C = (4, 128, 128)
        HS = 64
        H = C // HS
        D_W, D_A, D_V, D_G = (64, 64, 32, 128)
        EPS = 0.00064

        def _wkv(r, w, k, v, a, b):
            Bv, Tv, Cv = r.shape
            rs = lambda t: t.reshape(Bv, Tv, H, HS)
            r, k, v, a, b = (rs(r), rs(k), rs(v), rs(a), rs(b))
            wd = jnp.exp(-jnp.exp(rs(w)))

            def step(S, xs):
                r_, w_, k_, v_, a_, b_ = xs
                sa = jnp.einsum('bhij,bhj->bhi', S, a_)
                S = S * w_[:, :, None, :] + sa[..., None] * b_[:, :, None, :] + v_[..., None] * k_[:, :, None, :]
                y = jnp.einsum('bhij,bhj->bhi', S, r_)
                return (S, y)
            xs = tuple((jnp.swapaxes(t, 0, 1) for t in (r, wd, k, v, a, b)))
            S0 = jnp.zeros((Bv, H, HS, HS), r.dtype)
            _, ys = jax.lax.scan(step, S0, xs)
            return jnp.swapaxes(ys, 0, 1).reshape(Bv, Tv, Cv)

        def _forward(x, x_r, x_w, x_k, x_v, x_a, x_g, w0, w1, w2, a0, a1, a2, v0, v1, v2, g1, g2, k_k, k_a, r_k, Wr, Wk, Wv, Wo, ln_w, ln_b):
            Bv, Tv, Cv = x.shape
            xx = jnp.concatenate([jnp.zeros_like(x[:, :1]), x[:, :-1]], axis=1) - x
            xr = x + xx * x_r
            xw = x + xx * x_w
            xk = x + xx * x_k
            xv = x + xx * x_v
            xa = x + xx * x_a
            xg = x + xx * x_g
            r = xr @ Wr
            w = -jax.nn.softplus(-(w0 + jnp.tanh(xw @ w1) @ w2)) - 0.5
            k = xk @ Wk
            v = xv @ Wv
            v_first = jax.lax.stop_gradient(v)
            v = v + (v_first - v) * jax.nn.sigmoid(v0 + xv @ v1 @ v2)
            a = jax.nn.sigmoid(a0 + xa @ a1 @ a2)
            g = jax.nn.sigmoid(xg @ g1) @ g2
            kk = k * k_k
            kkh = kk.reshape(Bv, Tv, H, HS)
            kkh = kkh / jnp.maximum(jnp.linalg.norm(kkh, axis=-1, keepdims=True), 1e-12)
            kk = kkh.reshape(Bv, Tv, Cv)
            k = k * (1 + (a - 1) * k_a)
            y = _wkv(r, w, k, v, -kk, kk * a)
            yh = y.reshape(Bv, Tv, H, HS)
            mu = jnp.mean(yh, axis=-1, keepdims=True)
            var = jnp.var(yh, axis=-1, keepdims=True)
            y = ((yh - mu) / jnp.sqrt(var + EPS)).reshape(Bv, Tv, Cv) * ln_w + ln_b
            rt = (r.reshape(Bv, Tv, H, HS) * k.reshape(Bv, Tv, H, HS) * r_k).sum(-1, keepdims=True) * v.reshape(Bv, Tv, H, HS)
            y = y + rt.reshape(Bv, Tv, Cv)
            return y * g @ Wo
        return _forward(x, x_r, x_w, x_k, x_v, x_a, x_g, w0, w1, w2, a0, a1, a2, v0, v1, v2, g1, g2, k_k, k_a, r_k, Wr, Wk, Wv, Wo, ln_w, ln_b)

    def _L0_xattn_ref(x, latents, mask, ln_x_g, ln_x_b, ln_l_g, ln_l_b, q_gamma, k_gamma, W_q, W_kv, W_out, b_out):
        import jax, jax.numpy as jnp
        import numpy as np
        DIM = 128
        DIM_LATENT = 128
        DIM_HEAD = 64
        INNER = max(DIM, DIM_LATENT)
        HEADS = INNER // DIM_HEAD
        SCALE = DIM_HEAD ** (-0.5)
        LN_EPS = 1e-05
        RMS_EPS = 1e-08

        def layernorm(x, g, b):
            mu = jnp.mean(x, axis=-1, keepdims=True)
            var = jnp.mean(jnp.square(x - mu), axis=-1, keepdims=True)
            return (x - mu) * jax.lax.rsqrt(var + LN_EPS) * g + b

        def rmsnorm(x, gamma):
            n = jnp.linalg.norm(x, axis=-1, keepdims=True) * x.shape[-1] ** (-0.5)
            return x / jnp.maximum(n, RMS_EPS) * gamma
        b, n, _ = x.shape
        nl = latents.shape[1]
        xn = layernorm(x, ln_x_g, ln_x_b)
        ln = layernorm(latents, ln_l_g, ln_l_b)
        q = ln @ W_q
        kv = jnp.concatenate([xn @ W_kv, ln @ W_kv], axis=1)
        k, v = (kv[..., :INNER], kv[..., INNER:])
        to_heads = lambda t: t.reshape(t.shape[0], t.shape[1], HEADS, DIM_HEAD).transpose(0, 2, 1, 3)
        q, k, v = (to_heads(q), to_heads(k), to_heads(v))
        qn = rmsnorm(q, q_gamma) * SCALE
        kn = rmsnorm(k, k_gamma)
        sim = jnp.einsum('bhid,bhjd->bhij', qn, kn)
        full_mask = jnp.pad(mask, ((0, 0), (0, nl)), constant_values=True)
        neg = -jnp.finfo(sim.dtype).max
        sim = jnp.where(full_mask[:, None, None, :], sim, neg)
        attn = jax.nn.softmax(sim.astype(jnp.float32), axis=-1).astype(sim.dtype)
        out = jnp.einsum('bhij,bhjd->bhid', attn, v)
        out = out.transpose(0, 2, 1, 3).reshape(b, nl, INNER)
        return out @ W_out + b_out

    def _L0_ffn_ref(x, router_w, router_bias, gate_w, up_w, down_w, sgate_w, sup_w, sdown_w):
        import jax, jax.numpy as jnp
        import numpy as np
        TOPK = 4
        B, T, D = x.shape
        flat = x.reshape(B * T, D)
        logits = flat.astype(jnp.float32) @ router_w.T + router_bias
        scores = jax.nn.softmax(logits, axis=-1)
        topk_scores, topk_idx = jax.lax.top_k(scores, TOPK)
        topk_scores = topk_scores / jnp.clip(topk_scores.sum(axis=-1, keepdims=True), 1e-12, None)
        h = jax.nn.silu(jnp.einsum('nd,ehd->neh', flat, gate_w)) * jnp.einsum('nd,ehd->neh', flat, up_w)
        expert_out = jnp.einsum('neh,edh->ned', h, down_w)
        sel = jnp.take_along_axis(expert_out, topk_idx[:, :, None], axis=1)
        out = (sel * topk_scores.astype(flat.dtype)[:, :, None]).sum(axis=1)
        out = out + jax.nn.silu(flat @ sgate_w.T) * (flat @ sup_w.T) @ sdown_w.T
        return out.reshape(B, T, D)

    def _L1_attn_ref(x, w_Q, w_K, w_V):
        import jax, jax.numpy as jnp
        import numpy as np
        B, T, E, H = (2, 256, 128, 16)
        HD = E // H

        def _xavier(key, shape):
            limit = float(np.sqrt(6.0 / (shape[0] + shape[1])))
            return jax.random.uniform(key, shape, dtype=jnp.float32, minval=-limit, maxval=limit)
        Bs, Ts, Es = x.shape
        q = (x @ w_Q).reshape(Bs, Ts, H, HD).transpose(0, 2, 1, 3)
        k = (x @ w_K).reshape(Bs, Ts, H, HD).transpose(0, 2, 1, 3)
        v = (x @ w_V).reshape(Bs, Ts, H, HD).transpose(0, 2, 1, 3)
        scores = jnp.einsum('bhtd,bhsd->bhts', q, k) / jnp.sqrt(jnp.asarray(HD, x.dtype))
        probs = jax.nn.softmax(scores, axis=-1)
        attn = jnp.einsum('bhts,bhsd->bhtd', probs, v)
        return attn.transpose(0, 2, 1, 3).reshape(Bs, Ts, H * HD)

    def _L1_xattn_ref(query, key, value, Wq, bq, Wk, bk, Wv, bv, Wo, bo):
        import jax, jax.numpy as jnp
        import numpy as np
        D_MODEL = 128
        N_HEADS = 16
        D_HEAD = D_MODEL // N_HEADS
        B, Lq, _ = query.shape
        Lk = key.shape[1]
        scale = D_HEAD ** (-0.5)
        q = (query @ Wq + bq).reshape(B, Lq, N_HEADS, D_HEAD).transpose(0, 2, 1, 3)
        k = (key @ Wk + bk).reshape(B, Lk, N_HEADS, D_HEAD).transpose(0, 2, 1, 3)
        v = (value @ Wv + bv).reshape(B, Lk, N_HEADS, D_HEAD).transpose(0, 2, 1, 3)
        scores = jnp.einsum('bhqd,bhkd->bhqk', q, k) * scale
        causal = jnp.triu(jnp.ones((Lq, Lk), dtype=bool), k=1)
        scores = jnp.where(causal, -jnp.inf, scores)
        attn = jax.nn.softmax(scores, axis=-1)
        out = jnp.einsum('bhqk,bhkd->bhqd', attn, v)
        out = out.transpose(0, 2, 1, 3).reshape(B, Lq, D_MODEL)
        return out @ Wo + bo

    def _L1_ffn_ref(x, Wqkv, q_scale, k_scale, Wo, ln_g, ln_b, W1, b1, W2, b2):
        import jax, jax.numpy as jnp
        import numpy as np
        DIM = 128
        DEPTH = 6
        HEADS = 16
        DIM_HEAD = 64
        WINDOW = 32
        INNER = HEADS * DIM_HEAD
        DIM_INNER = int(DIM * 4 * 2 / 3)
        QK_SCALE = 8.0

        def shift_tokens(t):
            a, s = jnp.split(t, 2, -1)
            s = jnp.pad(s, ((0, 0), (1, 0), (0, 0)))[:, :-1]
            return jnp.concatenate([a, s], -1)

        def l2norm(t):
            return t / jnp.maximum(jnp.linalg.norm(t, axis=-1, keepdims=True), 1e-12)

        def rotate_half(x):
            x1, x2 = jnp.split(x, 2, -1)
            return jnp.concatenate([-x2, x1], -1)

        def rotary_tables(n):
            half = jnp.arange(0, DIM_HEAD, 2, dtype=jnp.float32)
            inv_freq = 1.0 / 10000.0 ** (half / DIM_HEAD)
            t = jnp.arange(n, dtype=jnp.float32)
            freqs = t[:, None] * inv_freq[None, :]
            freqs = jnp.concatenate([freqs, freqs], -1)
            base_scale = (half + 0.4 * DIM_HEAD) / (1.4 * DIM_HEAD)
            power = (t - n // 2) / (WINDOW // 2)
            scale = base_scale[None, :] ** power[:, None]
            scale = jnp.concatenate([scale, scale], -1)
            return (freqs, scale)

        def local_attention(q, k, v):
            b, h, n, d = q.shape
            w = WINDOW
            nw = n // w
            bq = q.reshape(b, h, nw, w, d)
            bk = k.reshape(b, h, nw, w, d)
            bv = v.reshape(b, h, nw, w, d)

            def look(t):
                p = jnp.pad(t, ((0, 0), (0, 0), (1, 0), (0, 0), (0, 0)))
                return jnp.concatenate([p[:, :, :nw], p[:, :, 1:]], axis=3)
            bk2, bv2 = (look(bk), look(bv))
            seq = jnp.arange(n).reshape(nw, w)
            seq_p = jnp.pad(seq, ((1, 0), (0, 0)), constant_values=-1)
            jt = jnp.concatenate([seq_p[:nw], seq_p[1:]], axis=1)
            it = seq[:, :, None]
            jb = jt[:, None, :]
            mask = (it < jb) | (it > jb + w) | (jb == -1)
            sim = jnp.einsum('bhwie,bhwje->bhwij', bq, bk2) * QK_SCALE
            sim = jnp.where(mask, -jnp.finfo(sim.dtype).max, sim)
            attn = jax.nn.softmax(sim, -1)
            out = jnp.einsum('bhwij,bhwje->bhwie', attn, bv2)
            return out.reshape(b, h, n, d)

        def attn_layer(x, Wqkv, qs, ksc, Wo):
            b, n, _ = x.shape
            qkv = x @ Wqkv
            q, k, v = jnp.split(qkv, 3, -1)
            sh = lambda t: t.reshape(b, n, HEADS, DIM_HEAD).transpose(0, 2, 1, 3)
            q, k, v = (sh(q), sh(k), sh(v))
            q = l2norm(q) * qs
            k = l2norm(k) * ksc
            freqs, scale = rotary_tables(n)
            cos, sin = (jnp.cos(freqs), jnp.sin(freqs))
            q = q * cos * scale + rotate_half(q) * sin * scale
            inv = 1.0 / scale
            k = k * cos * inv + rotate_half(k) * sin * inv
            out = local_attention(q, k, v)
            out = out.transpose(0, 2, 1, 3).reshape(b, n, INNER)
            return out @ Wo

        def ffn_layer(x, g, bln, W1, b1, W2, b2):
            mu = x.mean(-1, keepdims=True)
            var = ((x - mu) ** 2).mean(-1, keepdims=True)
            xn = (x - mu) / jnp.sqrt(var + 1e-05) * g + bln
            hg = xn @ W1 + b1
            a, gate = jnp.split(hg, 2, -1)
            return a * jax.nn.gelu(gate, approximate=False) @ W2 + b2
        for i in range(DEPTH):
            x = attn_layer(shift_tokens(x), Wqkv[i], q_scale[i], k_scale[i], Wo[i]) + x
            x = ffn_layer(shift_tokens(x), ln_g[i], ln_b[i], W1[i], b1[i], W2[i], b2[i]) + x
        return x

    def _L2_attn_ref(q, in_proj_weight, in_proj_bias, out_w, out_b, rel_pe):
        import jax, jax.numpy as jnp
        import numpy as np
        import math
        B, L, E, H, K = (4, 128, 128, 16, 64)
        D = E // H

        def _attend(q, in_proj_weight, in_proj_bias, out_w, out_b, rel_pe):
            b, l, e = q.shape
            h, d = (H, D)
            qkv = q @ in_proj_weight.T + in_proj_bias
            qh, kh, vh = jnp.split(qkv, 3, axis=-1)
            qh = qh.reshape(b, l, h, d).transpose(0, 2, 1, 3)
            kh = kh.reshape(b, l, h, d).transpose(0, 2, 1, 3)
            vh = vh.reshape(b, l, h, d).transpose(0, 2, 1, 3)
            qh = qh / math.sqrt(d)
            scores = jnp.einsum('bhid,bhjd->bhij', qh, kh)
            pos = jnp.arange(l)
            rel = jnp.clip(pos[None, :] - pos[:, None], -K, K) + K
            bias_r = jnp.einsum('bhid,rd->bhir', qh, rel_pe)
            bias = jnp.take_along_axis(bias_r, jnp.broadcast_to(rel[None, None], (b, h, l, l)), axis=-1)
            attn = jax.nn.softmax(scores + bias, axis=-1)
            out = jnp.einsum('bhij,bhjd->bhid', attn, vh)
            out = out.transpose(0, 2, 1, 3).reshape(b, l, e)
            return out @ out_w.T + out_b
        return _attend(q, in_proj_weight, in_proj_bias, out_w, out_b, rel_pe)

    def _L2_xattn_ref(query, key, value, qpos, kpos, Wq, bq, Wk, bk, Wv, bv, Wo, bo):
        import jax, jax.numpy as jnp
        import numpy as np
        DIM = 128
        HEADS = 16
        HEAD_DIM = DIM // HEADS
        SCALE = HEAD_DIM ** (-0.5)
        B, Nq, C = query.shape

        def split_heads(x):
            return x.reshape(x.shape[0], x.shape[1], HEADS, HEAD_DIM).transpose(0, 2, 1, 3)
        q = split_heads(query @ Wq + bq)
        k = split_heads(key @ Wk + bk)
        v = split_heads(value @ Wv + bv)
        attn = jnp.einsum('bhqd,bhkd->bhqk', q, k) * SCALE
        attn = jax.nn.softmax(attn, axis=-1)
        x = jnp.einsum('bhqk,bhkd->bhqd', attn, v)
        x = x.transpose(0, 2, 1, 3).reshape(B, Nq, C)
        return x @ Wo + bo

    def _L2_ffn_ref(x, W_experts, b_experts, W_router, b_router):
        import jax, jax.numpy as jnp
        import numpy as np
        IN_F = 128
        OUT_F = 128
        N_EXPERTS = 8
        TOP_K = 2
        router_logits = jnp.einsum('bsd,ed->bse', x, W_router) + b_router
        router_weights = jax.nn.softmax(router_logits, axis=-1)
        if TOP_K < N_EXPERTS:
            topk_w, topk_idx = jax.lax.top_k(router_weights, TOP_K)
            sparse = jnp.zeros_like(router_weights)
            router_weights = jnp.take_along_axis(sparse, topk_idx, axis=-1)
            router_weights = sparse.at[..., :].set(0.0)
            b_idx = jnp.arange(sparse.shape[0])[:, None, None]
            s_idx = jnp.arange(sparse.shape[1])[None, :, None]
            router_weights = sparse.at[b_idx, s_idx, topk_idx].set(topk_w)
        expert_out = jnp.einsum('bsd,eod->bseo', x, W_experts) + b_experts
        return jnp.einsum('bseo,bse->bso', expert_out, router_weights)

    def _L3_attn_ref(x, w_qkv, w_gates, w_out):
        import jax, jax.numpy as jnp
        import numpy as np
        DIM = 128
        HEADS = 16
        DIM_HEAD = 64
        SOFTCAP = 50.0
        b, n, _ = x.shape
        scale = DIM_HEAD ** (-0.5)
        qkv = jnp.einsum('bnf,fe->bne', x, w_qkv).reshape(b, n, 3, HEADS, DIM_HEAD)
        qkv = jnp.moveaxis(qkv, 2, 0)
        q, k, v = jnp.moveaxis(qkv, 3, 2)
        q = q * scale
        sim = jnp.einsum('bhid,bhjd->bhij', q, k)
        sim = SOFTCAP * jnp.tanh(sim / SOFTCAP)
        mask_value = -jnp.finfo(sim.dtype).max
        causal_mask = jnp.triu(jnp.ones((n, n), dtype=bool), 1)
        sim = jnp.where(causal_mask, mask_value, sim)
        attn = jax.nn.softmax(sim, axis=-1)
        out = jnp.einsum('bhij,bhjd->bhid', attn, v)
        gates = jax.nn.sigmoid(jnp.einsum('bnf,fh->bhn', x, w_gates))[..., None]
        out = out * gates
        out = jnp.transpose(out, (0, 2, 1, 3)).reshape(b, n, HEADS * DIM_HEAD)
        return jnp.einsum('bne,ef->bnf', out, w_out)

    def _L3_xattn_ref(q, kv, seg_id, w_kv_comp, w_q_down, w_q_up, w_q_rope, w_k_up, w_k_rope, w_v_up, w_out):
        import jax, jax.numpy as jnp
        import numpy as np
        Q_DIM, KV_DIM = (128, 128)
        H, HD, KVC, QC, R = (16, 64, 32, 48, 64)
        LOOKBACK = 2
        B, LQ, LK = (4, 256, 64)

        def _rope(x, pos):
            r = x.shape[-1]
            half = r // 2
            inv = 1.0 / 10000.0 ** (jnp.arange(half, dtype=jnp.float32) / half)
            ang = pos[..., None].astype(jnp.float32) * inv
            cos, sin = (jnp.cos(ang), jnp.sin(ang))
            x1, x2 = (x[..., :half], x[..., half:])
            return jnp.concatenate([x1 * cos - x2 * sin, x1 * sin + x2 * cos], axis=-1)
        b, lq, _ = q.shape
        lk = kv.shape[1]
        kv_c = kv @ w_kv_comp
        qc = q @ w_q_down
        q_nope = (qc @ w_q_up).reshape(b, lq, H, HD)
        q_rope = (qc @ w_q_rope).reshape(b, lq, H, R)
        q_rope = _rope(q_rope, jnp.arange(lq)[None, :, None])
        k_nope = (kv_c @ w_k_up).reshape(b, lk, H, HD)
        k_rope = _rope(kv_c @ w_k_rope, jnp.arange(lk)[None, :])
        v = (kv_c @ w_v_up).reshape(b, lk, H, HD)
        scale = 1.0 / np.sqrt(HD + R).astype(np.float32)
        scores = (jnp.einsum('bqhd,bkhd->bhqk', q_nope, k_nope) + jnp.einsum('bqhr,bkr->bhqk', q_rope, k_rope)) * scale
        k_idx = jnp.arange(lk)[None, None, :]
        q_seg = seg_id[:, :, None]
        good = (k_idx <= q_seg) & (k_idx >= q_seg - LOOKBACK)
        neg = jnp.finfo(scores.dtype).min
        scores = jnp.where(good[:, None, :, :], scores, neg)
        attn = jax.nn.softmax(scores, axis=-1)
        out = jnp.einsum('bhqk,bkhd->bqhd', attn, v).reshape(b, lq, H * HD)
        return out @ w_out

    def _L3_ffn_ref(x, proj, C1, Win1, Wout1, C2, Win2, Wout2):
        import jax, jax.numpy as jnp
        import numpy as np
        LN_EPS = 1e-05

        def entmax15(z):
            z = z / 2.0
            z = z - jnp.max(z, axis=-1, keepdims=True)
            zs = -jnp.sort(-z, axis=-1)
            k = jnp.arange(1, z.shape[-1] + 1, dtype=z.dtype)
            mean = jnp.cumsum(zs, axis=-1) / k
            meansq = jnp.cumsum(zs * zs, axis=-1) / k
            ss = k * (meansq - jnp.square(mean))
            delta = (1.0 - ss) / k
            tau = mean - jnp.sqrt(jnp.clip(delta, 0.0))
            support = jnp.sum((tau <= zs).astype(jnp.int32), axis=-1, keepdims=True)
            tau_star = jnp.take_along_axis(tau, support - 1, axis=-1)
            return jnp.square(jnp.clip(z - tau_star, 0.0))

        def layernorm_noaffine(v):
            m = jnp.mean(v, axis=-1, keepdims=True)
            var = jnp.mean(jnp.square(v - m), axis=-1, keepdims=True)
            return (v - m) / jnp.sqrt(var + LN_EPS)

        def cp_mumoe(x, gate, Win, Wout):
            ones = jnp.ones(x.shape[:-1] + (1,), x.dtype)
            xb = jnp.concatenate([x, ones], axis=-1)
            z = jnp.einsum('btd,dr->btr', xb, Win) * gate
            return jnp.einsum('btr,or->bto', z, Wout)
        a = entmax15(layernorm_noaffine(jnp.einsum('btd,de->bte', x, proj)))
        g1 = jnp.einsum('bte,er->btr', a, C1)
        h = cp_mumoe(x, g1, Win1, Wout1)
        h = jax.nn.gelu(h, approximate=False)
        g2 = jnp.einsum('bte,er->btr', a, C2)
        return cp_mumoe(h, g2, Win2, Wout2)
    x = _layernorm(x + _L0_attn_ref(x, L0_attn_x_r, L0_attn_x_w, L0_attn_x_k, L0_attn_x_v, L0_attn_x_a, L0_attn_x_g, L0_attn_w0, L0_attn_w1, L0_attn_w2, L0_attn_a0, L0_attn_a1, L0_attn_a2, L0_attn_v0, L0_attn_v1, L0_attn_v2, L0_attn_g1, L0_attn_g2, L0_attn_k_k, L0_attn_k_a, L0_attn_r_k, L0_attn_Wr, L0_attn_Wk, L0_attn_Wv, L0_attn_Wo, L0_attn_ln_w, L0_attn_ln_b), axis=-1)
    x = _layernorm(x + _L0_xattn_ref(ctx_1024, x, mask_BxS2_bk0, L0_xattn_ln_x_g, L0_xattn_ln_x_b, L0_xattn_ln_l_g, L0_xattn_ln_l_b, L0_xattn_q_gamma, L0_xattn_k_gamma, L0_xattn_W_q, L0_xattn_W_kv, L0_xattn_W_out, L0_xattn_b_out), axis=-1)
    x = _layernorm(x + _L0_ffn_ref(x, L0_ffn_router_w, L0_ffn_router_bias, L0_ffn_gate_w, L0_ffn_up_w, L0_ffn_down_w, L0_ffn_sgate_w, L0_ffn_sup_w, L0_ffn_sdown_w), axis=-1)
    x = _layernorm(x + _L1_attn_ref(x, L1_attn_w_Q, L1_attn_w_K, L1_attn_w_V), axis=-1)
    x = _layernorm(x + _L1_xattn_ref(x, ctx_1024, ctx_1024, L1_xattn_Wq, L1_xattn_bq, L1_xattn_Wk, L1_xattn_bk, L1_xattn_Wv, L1_xattn_bv, L1_xattn_Wo, L1_xattn_bo), axis=-1)
    x = _layernorm(x + _L1_ffn_ref(x, L1_ffn_Wqkv, L1_ffn_q_scale, L1_ffn_k_scale, L1_ffn_Wo, L1_ffn_ln_g, L1_ffn_ln_b, L1_ffn_W1, L1_ffn_b1, L1_ffn_W2, L1_ffn_b2), axis=-1)
    x = _layernorm(x + _L2_attn_ref(x, L2_attn_in_proj_weight, L2_attn_in_proj_bias, L2_attn_out_w, L2_attn_out_b, L2_attn_rel_pe), axis=-1)
    x = _layernorm(x + _L2_xattn_ref(x, ctx_1024, ctx_1024, itok_BxS2_0_2047, itok_BxS2_0_2047, L2_xattn_Wq, L2_xattn_bq, L2_xattn_Wk, L2_xattn_bk, L2_xattn_Wv, L2_xattn_bv, L2_xattn_Wo, L2_xattn_bo), axis=-1)
    x = _layernorm(x + _L2_ffn_ref(x, L2_ffn_W_experts, L2_ffn_b_experts, L2_ffn_W_router, L2_ffn_b_router), axis=-1)
    x = _layernorm(x + _L3_attn_ref(x, L3_attn_w_qkv, L3_attn_w_gates, L3_attn_w_out), axis=-1)
    x = _layernorm(x + _L3_xattn_ref(x, ctx_1024, itok_BxS_0_511, L3_xattn_w_kv_comp, L3_xattn_w_q_down, L3_xattn_w_q_up, L3_xattn_w_q_rope, L3_xattn_w_k_up, L3_xattn_w_k_rope, L3_xattn_w_v_up, L3_xattn_w_out), axis=-1)
    x = _layernorm(x + _L3_ffn_ref(x, L3_ffn_proj, L3_ffn_C1, L3_ffn_Win1, L3_ffn_Wout1, L3_ffn_C2, L3_ffn_Win2, L3_ffn_Wout2), axis=-1)
    return x

_drawn_inputs = setup_inputs


def setup_inputs(seed=0):
    import zlib

    import numpy as np

    out = dict(_drawn_inputs(seed))
    spreads = {'L0_attn_ln_w': (1.0, 0.2),
     'L0_attn_ln_b': (0.0, 0.1),
     'L0_xattn_ln_x_g': (1.0, 0.6),
     'L0_xattn_ln_x_b': (0.0, 0.349),
     'L0_xattn_ln_l_g': (1.0, 0.2),
     'L0_xattn_ln_l_b': (0.0, 0.1),
     'L0_xattn_q_gamma': (1.0, 0.2),
     'L0_xattn_k_gamma': (1.0, 0.2),
     'L0_xattn_b_out': (0.0, 0.1),
     'L0_ffn_router_bias': (0.0, 0.1),
     'L1_xattn_bq': (0.0, 0.278),
     'L1_xattn_bk': (0.0, 2.0),
     'L1_xattn_bv': (0.0, 0.1),
     'L1_xattn_bo': (0.0, 0.1),
     'L1_ffn_q_scale': (1.0, 0.6),
     'L1_ffn_k_scale': (1.0, 0.6),
     'L1_ffn_ln_g': (1.0, 0.6),
     'L1_ffn_ln_b': (0.0, 0.8),
     'L1_ffn_b1': (0.0, 0.602),
     'L1_ffn_b2': (0.0, 0.1),
     'L2_attn_in_proj_bias': (0.0, 0.1),
     'L2_attn_out_b': (0.0, 0.1),
     'L2_xattn_bq': (0.0, 0.306),
     'L2_xattn_bk': (0.0, 2.0),
     'L2_xattn_bv': (0.0, 0.1),
     'L2_xattn_bo': (0.0, 0.1)}
    factors = {'L0_attn_x_r': 5.479,
     'L0_attn_x_w': 8.0,
     'L0_attn_x_k': 4.537,
     'L0_attn_x_v': 5.432,
     'L0_attn_x_a': 8.0,
     'L0_attn_x_g': 8.0,
     'L0_attn_w0': 8.0,
     'L0_attn_w1': 4.61,
     'L0_attn_w2': 3.782,
     'L0_attn_a0': 64.0,
     'L0_attn_a1': 7.323,
     'L0_attn_a2': 6.553,
     'L0_attn_k_a': 6.067,
     'L1_ffn_W1': 3.444,
     'L1_ffn_W2': 3.424,
     'L2_attn_rel_pe': 2.811,
     'L2_ffn_b_experts': 4.184,
     'L3_attn_w_gates': 8.0,
     'L3_ffn_proj': 3.646,
     'L3_ffn_C1': 3.996,
     'L3_ffn_Win1': 4.176,
     'L3_ffn_Wout1': 4.01,
     'L3_ffn_C2': 3.47,
     'L3_ffn_Win2': 3.537,
     'L3_ffn_Wout2': 3.488}
    for name, (base, spread) in spreads.items():
        noise = np.random.default_rng([zlib.crc32(name.encode()), seed]).standard_normal(out[name].shape)
        drawn = base * np.exp(spread * noise) if base else spread * noise
        out[name] = jnp.asarray(drawn.astype(out[name].dtype))
    for name, factor in factors.items():
        out[name] = (out[name] * factor).astype(out[name].dtype)
    return out
```

```python
from contextlib import ExitStack, contextmanager

import numpy as np

import concourse.bass as bass
from concourse import mybir

F32 = mybir.dt.float32
I32 = mybir.dt.int32
ALU = mybir.AluOpType
ACT = mybir.ActivationFunctionType
AX = mybir.AxisListType.X

P = 128
B = 2
S = 512
N = B * S
TILES = N // P
SK = 154
KT = 77
CT = B * SK
BIG = 3.0e37
BLK = 512
NB = N // BLK
LN_EPS = 1e-5
H16, D8 = 16, 8
D64 = 64
INNER = 1024
WC = INNER // P
DEPTH = 6
DI = 341
WIN = 32
REL = 64
EXT = 384


def shape_constants():
    p = np.arange(P)
    c = {}
    c["ident"] = np.eye(P)
    c["mean"] = np.full((P, P), 1.0 / P)
    c["head64"] = (p[:, None] // D64 == p[None, :] // D64) * 1.0
    c["headmask"] = (p[:, None] // D8 == np.arange(H16)[None, :]) * 1.0
    c["pick2"] = (p[:, None] // D64 == np.arange(2)[None, :]) * 1.0
    up = np.zeros((P, 2, WC, 2 * H16))
    for side in range(2):
        for k in range(WC):
            for q in range(P):
                up[q, side, k, H16 * side + 2 * k + q // D64] = 1.0
    c["toheads"] = up.reshape(P, 2 * WC, 2 * H16)
    c["fromheads"] = up.reshape(P, 2 * WC, 2 * H16).transpose(2, 1, 0)
    pick = np.zeros((P, 32, P))
    for e in range(32):
        pick[e, e, :] = 1.0
    c["pickrow"] = pick
    rot = np.zeros((P, P))
    for h in range(2):
        for d in range(32):
            rot[64 * h + 32 + d, 64 * h + d] = -1.0
            rot[64 * h + d, 64 * h + 32 + d] = 1.0
    c["rot"] = rot
    half = np.arange(0, D64, 2, dtype=np.float64)
    inv = (1.0 / 10000.0 ** (half / D64)).astype(np.float32)
    t = np.arange(S, dtype=np.float32)
    fr = (t[:, None] * inv[None, :]).astype(np.float32).astype(np.float64)
    base = (half + 0.4 * D64) / (1.4 * D64)
    sc = base[None, :] ** ((t[:, None] - S // 2) / (WIN // 2))
    wide = lambda a: np.concatenate([a, a, a, a], 1).T
    c["cos"], c["sin"] = wide(np.cos(fr)), wide(np.sin(fr))
    c["qcos"], c["qsin"] = wide(np.cos(fr) * sc), wide(np.sin(fr) * sc)
    c["kcos"], c["ksin"] = wide(np.cos(fr) / sc), wide(np.sin(fr) / sc)
    i, j = p[:, None], np.arange(P + WIN)[None, :] - WIN
    band = (j <= i) & (j >= i - WIN)
    c["band"] = np.stack([np.where(band & (j >= 0), 0, -BIG), np.where(band, 0, -BIG)], 1)
    k = np.arange(SK)[None, :]
    c["xcausal"] = np.stack([np.where(k <= i, 0, -BIG), np.where(k <= i + P, 0, -BIG)], 1)
    c["keyno"] = np.broadcast_to(k * 1.0, (P, SK))
    c["upper"] = (p[:, None] <= p[None, :]) * 1.0
    c["supper"] = (p[:, None] < p[None, :]) * 1.0
    lv = []
    for m in (1, 2, 4, 8, 16, 32, 64):
        same = p[:, None] // (2 * m) == p[None, :] // (2 * m)
        lv.append(same * (p[:, None] % (2 * m) < m) * (p[None, :] % (2 * m) >= m) * 1.0)
    c["levels"] = np.stack(lv, 1)
    c["restart128"] = np.broadcast_to((np.arange(N) % P != 0) * 1.0, (P, N))
    c["restart16"] = np.broadcast_to((p % 16 != 0) * 1.0, (P, P))
    c["rank"] = np.broadcast_to(p % 16 + 1.0, (P, P))
    c["invrank"] = np.broadcast_to(1.0 / (p % 16 + 1.0), (P, P))
    c["cols"] = np.broadcast_to(np.array([LN_EPS, 6.4e-4, 1.0, 0.0]), (P, 4))
    return {n: np.ascontiguousarray(a, dtype=np.float32) for n, a in c.items()}


class Core:

    def __init__(self, nc, io):
        self.nc, self.io = nc, io
        self.ps = nc.alloc_psum_tensor("ps", [P, 8, BLK], F32)
        self.stale = []
        self.const = {}
        self.count = 0
        self.orders = []
        self.fetched = {}

    def buffer(self, mem, shape, name="work", dtype=F32):
        self.count += 1
        return mem.enter_context(self.nc.sbuf_tensor(f"{name}_{self.count}", list(shape), dtype))[:]

    def bank(self, i, n=1):
        return self.ps[:, i:i + n, :].rearrange("p b c -> p (b c)")

    @contextmanager
    def stage(self, *names):
        nc = self.nc
        self.count += 1
        sems = [nc.alloc_semaphore(f"{n}_{self.count}") for n in names]
        stale, self.stale = self.stale, []
        with nc.Block(no_gpsimd_drain=True) as block:
            orders, self.orders = self.orders, []
            if orders:
                @block.sync
                def _(sp):
                    for tag, dst, src in orders:
                        sp.dma_start(dst, src).then_inc(self.fetched[tag][0], 16)
            if stale:
                @block.gpsimd
                def _(pool):
                    for s in stale:
                        pool.sem_clear(s)
            yield (block, *sems)
        for s in stale:
            nc.release_semaphore(s)
        self.stale = sems

    def fetch(self, tag, pairs):
        self.fetched[tag] = (self.nc.alloc_semaphore("fetched_" + tag), 16 * len(pairs))
        self.orders += [(tag, dst, src) for dst, src in pairs]

    def need(self, *tags):
        with self.stage() as (block,):
            @block.sync
            def _(sp):
                for tag in tags:
                    sp.wait_ge(*self.fetched[tag])

    def settle(self):
        with self.stage():
            pass


def chained(eng, sem):
    done = [0]

    def link(ins):
        done[0] += 1
        ins.then_inc(sem, 1)
        eng.wait_ge(sem, done[0])
    return link


def load(core, pairs):
    with core.stage("loaded_by_sync", "loaded_by_act") as (block, by_sync, by_act):
        @block.sync
        def _(sp):
            for dst, src in pairs[0::2]:
                sp.dma_start(dst, src).then_inc(by_sync, 16)
            sp.wait_ge(by_sync, 16 * len(pairs[0::2]))

        if pairs[1::2]:
            @block.scalar
            def _(act):
                for dst, src in pairs[1::2]:
                    act.dma_start(dst, src).then_inc(by_act, 16)
                act.wait_ge(by_act, 16 * len(pairs[1::2]))


def products(core, jobs, ring=8):
    nc = core.nc
    by_act = [j % 2 == 0 or jobs[j][2] is not None for j in range(len(jobs))]
    acts = lambda j: sum(by_act[:j + 1])
    dves = lambda j: j + 1 - acts(j)

    def spot(j):
        out = jobs[j][0]
        m, n = out.shape[0], int(np.prod(out.shape[1:]))
        v = core.bank(j % ring)[0:m, 0:n]
        if len(out.shape) == 3:
            v = v.rearrange("p (a b) -> p a b", a=out.shape[1])
        return v

    with core.stage("product_done", "emptied_by_act", "emptied_by_dve") as (block, product_done, emptied_a, emptied_v):
        @block.tensor
        def _(pe):
            for j, (out, terms, *_) in enumerate(jobs):
                if j >= ring:
                    if by_act[j - ring]:
                        pe.wait_ge(emptied_a, acts(j - ring))
                    else:
                        pe.wait_ge(emptied_v, dves(j - ring))
                for k, (lhsT, rhs) in enumerate(terms):
                    mm = nc.tensor.matmul(spot(j), lhsT, rhs, start=(k == 0), stop=(k == len(terms) - 1))
                mm.then_inc(product_done, 1)

        @block.scalar
        def _(act):
            for j, (out, terms, func, scale, bias) in enumerate(jobs):
                if by_act[j]:
                    act.wait_ge(product_done, j + 1)
                    nc.scalar.activation(out, spot(j), func or ACT.Identity, scale=scale,
                                         bias=0.0 if bias is None else bias).then_inc(emptied_a, 1)

        @block.vector
        def _(dve):
            for j, (out, terms, func, scale, bias) in enumerate(jobs):
                if not by_act[j]:
                    dve.wait_ge(product_done, j + 1)
                    if bias is None:
                        ins = nc.vector.tensor_scalar(out, spot(j), scale, None, ALU.mult)
                    else:
                        ins = nc.vector.tensor_scalar(out, spot(j), scale, bias, ALU.mult, ALU.add)
                    ins.then_inc(emptied_v, 1)


def transposes(core, jobs, ring=8):
    nc = core.nc

    def spot(j, k):
        a = jobs[j][1][k]
        w = a.shape[0]
        return core.bank(j % ring)[0:a.shape[1], w * k:w * k + w]

    def whole(j):
        out, ins = jobs[j]
        v = core.bank(j % ring)[0:out.shape[0], 0:len(ins) * ins[0].shape[0]]
        if len(out.shape) == 3:
            v = v.rearrange("p (a b) -> p a b", a=out.shape[1])
        return v

    with core.stage("turned", "copied_by_act", "copied_by_dve") as (block, turned, copied_a, copied_v):
        @block.tensor
        def _(pe):
            for j, (out, ins) in enumerate(jobs):
                if j >= ring:
                    pe.wait_ge(copied_v if j % 2 else copied_a, (j - ring) // 2 + 1)
                for k, a in enumerate(ins):
                    mm = nc.tensor.transpose(spot(j, k), a, core.const["ident"][0:a.shape[0], 0:a.shape[0]])
                mm.then_inc(turned, 1)

        @block.scalar
        def _(act):
            for j in range(0, len(jobs), 2):
                act.wait_ge(turned, j + 1)
                nc.scalar.copy(jobs[j][0], whole(j)).then_inc(copied_a, 1)

        if len(jobs) > 1:
            @block.vector
            def _(dve):
                for j in range(1, len(jobs), 2):
                    dve.wait_ge(turned, j + 1)
                    nc.vector.tensor_copy(jobs[j][0], whole(j)).then_inc(copied_v, 1)


def normalise(core, src, dst, blocks, gain=None, shift=None, terms=None, bias=None, relu_eps=None):
    nc = core.nc
    eps = core.const["cols"][:, 0:1]
    with ExitStack() as mem:
        width = sum(b - a for a, b in blocks)
        centred = core.buffer(mem, [P, width])
        square = core.buffer(mem, [P, width])
        block, projected, summed, mean_done, centred_done, squared, var_done, rooted, dve_step, normed = \
            mem.enter_context(core.stage("projected", "residual_added", "mean_done", "centred", "squared", "var_done",
                                         "std_done", "dve_step", "normed"))

        def cols(t, k):
            a, b = blocks[k]
            return t[:, a:b]

        def own(t, k):
            a = blocks[0][0]
            return t[:, blocks[k][0] - a:blocks[k][1] - a]

        def bank(k, what):
            return core.bank(3 * (k % 2) + what)[:, 0:blocks[k][1] - blocks[k][0]]

        @block.tensor
        def _(pe):
            for k in range(len(blocks)):
                if k >= 2:
                    pe.wait_ge(normed, k - 1)
                if terms:
                    for i, (lhsT, rhs) in enumerate(terms):
                        mm = nc.tensor.matmul(bank(k, 0), lhsT, cols(rhs, k), start=(i == 0), stop=(i == len(terms) - 1))
                    mm.then_inc(projected, 1)
            for k in range(len(blocks)):
                if terms:
                    pe.wait_ge(summed, k + 1)
                nc.tensor.matmul(bank(k, 1), core.const["mean"][:], cols(src, k), start=True, stop=True).then_inc(mean_done, 1)
            for k in range(len(blocks)):
                pe.wait_ge(squared, k + 1)
                nc.tensor.matmul(bank(k, 2), core.const["mean"][:], own(square, k), start=True, stop=True).then_inc(var_done, 1)

        @block.scalar
        def _(act):
            for k in range(len(blocks)):
                act.wait_ge(centred_done, k + 1)
                nc.scalar.activation(own(square, k), own(centred, k), ACT.Square).then_inc(squared, 1)
            for k in range(len(blocks)):
                act.wait_ge(var_done, k + 1)
                nc.scalar.activation(own(square, k), bank(k, 2), ACT.Sqrt, bias=eps).then_inc(rooted, 1)

        @block.vector
        def _(dve):
            link = chained(dve, dve_step)
            if terms:
                for k in range(len(blocks)):
                    dve.wait_ge(projected, k + 1)
                    if bias is None:
                        nc.vector.tensor_tensor(cols(src, k), bank(k, 0), cols(src, k), ALU.add).then_inc(summed, 1)
                    else:
                        nc.vector.scalar_tensor_tensor(cols(src, k), bank(k, 0), bias, cols(src, k), ALU.add, ALU.add) \
                            .then_inc(summed, 1)
                dve.wait_ge(summed, len(blocks))
            for k in range(len(blocks)):
                dve.wait_ge(mean_done, k + 1)
                nc.vector.tensor_tensor(own(centred, k), cols(src, k), bank(k, 1), ALU.subtract).then_inc(centred_done, 1)
            dve.wait_ge(centred_done, len(blocks))
            for k in range(len(blocks)):
                dve.wait_ge(rooted, k + 1)
                link(nc.vector.reciprocal(own(square, k), own(square, k)))
                ins = nc.vector.tensor_tensor(cols(dst, k), own(centred, k), own(square, k), ALU.mult)
                if gain is not None:
                    link(ins)
                    ins = nc.vector.tensor_scalar(cols(dst, k), cols(dst, k), gain, shift, ALU.mult, ALU.add)
                ins.then_inc(normed, 1)


XBLOCKS = [(0, BLK), (BLK, N)]


def attend(core, units, keytiles, out_width, outs, scale, tiles, parts_of=None, nk=None, lead=0, stream=None):
    nc = core.nc
    heads = len([u for u in units if u[0] == units[0][0]])
    U = len(units)
    wide = nk > BLK
    sb = 2 if wide else 1
    kt = len(keytiles)
    tb = 1 if kt <= 4 else 2
    SR = 2
    TR = 1 if wide else 2
    oband = 8 - SR * sb - TR * tb
    ob = -(-heads * out_width // BLK)
    OR = max(1, oband // ob)

    def score(u):
        return core.bank((u % SR) * sb, sb)[:, 0:nk]

    def turned_at(u):
        return core.bank(SR * sb + (u % TR) * tb, tb)

    def outp(t):
        return core.bank(SR * sb + TR * tb + (t % OR) * ob, ob)[:, 0:heads * out_width]

    with ExitStack() as mem:
        prob = core.buffer(mem, [P, 2, lead + nk], "prob")
        turned = core.buffer(mem, [P, 2, kt * P])
        top = core.buffer(mem, [P, 2, 2], "top")
        tops = core.buffer(mem, [P, 4], "tops")
        masked = core.buffer(mem, [P, 2, nk], "masked") if parts_of else None
        rs = core.buffer(mem, [P, 2, heads])
        block, scores_ready, max_found, max_negated, probs_ready, probs_turned, copied_v, copied_a, \
            values_done, sums_inverted, tile_out, lead_cleared, parts_added, *streamed = mem.enter_context(core.stage(
                "scores_ready", "max_found", "max_negated", "probs_ready", "probs_turned", "turned_copied_dve",
                "turned_copied_act", "values_done", "sums_inverted", "tile_out", "lead_cleared", "parts_added", "streamed_even", "streamed_odd"))
        groups = [(0, kt, P)] if len({n for _, n in keytiles}) == 1 else [
            (0, len([n for _, n in keytiles if n == P]), P), (len([n for _, n in keytiles if n == P]), kt, keytiles[-1][1])]
        if len(groups) == 1:
            groups = [(0, kt, keytiles[0][1])]

        def copied(eng, u):
            if u % 2 == 0:
                eng.wait_ge(copied_v, u // 2 + 1)
            else:
                eng.wait_ge(copied_a, u // 2 + 1)


        if stream:
            @block.sync
            def _(sp):
                for i in range(U // heads):
                    if i >= 2:
                        sp.wait_ge(max_found, heads * (i - 1))
                    for dst, src in stream(i):
                        sp.dma_start(dst, src).then_inc(streamed[i % 2], 16)

        @block.tensor
        def _(pe):
            def scores(u):
                if u >= SR:
                    pe.wait_ge(probs_ready, u - SR + 1)
                for col, lhsT, rhs, first, last in units[u][2]:
                    mm = nc.tensor.matmul(score(u)[:, col:col + rhs.shape[-1]], lhsT, rhs, start=first, stop=last)
                mm.then_inc(scores_ready, 1)

            def turn(u):
                pe.wait_ge(probs_ready, u + 1)
                if u >= TR:
                    copied(pe, u - TR)
                for k, (a, n) in enumerate(keytiles):
                    mm = nc.tensor.transpose(turned_at(u)[0:n, P * k:P * k + P], prob[:, u % 2, a:a + n], core.const["ident"][:])
                mm.then_inc(probs_turned, 1)

            def values(u):
                t, h = units[u][0], u % heads
                copied(pe, u)
                if h == 0 and u // heads >= OR:
                    pe.wait_ge(tile_out, u // heads - OR + 1)
                for k, (a, n) in enumerate(keytiles):
                    mm = nc.tensor.matmul(outp(u // heads)[:, h * out_width:(h + 1) * out_width],
                                          turned[0:n, u % 2, P * k:P * k + P], units[u][3][k],
                                          start=(k == 0), stop=(k == kt - 1))
                mm.then_inc(values_done, 1)

            scores(0)
            for u in range(U):
                if u + 1 < U:
                    scores(u + 1)
                turn(u)
                if u >= 1:
                    values(u - 1)
            values(U - 1)

        @block.scalar
        def _(act):
            def spread(u):
                act.wait_ge(probs_turned, u + 1)
                if u >= 2:
                    act.wait_ge(values_done, u - 1)
                for a, b, m in groups:
                    ins = nc.scalar.copy(turned[0:m, u % 2, P * a:P * b], turned_at(u)[0:m, P * a:P * b])
                ins.then_inc(copied_a, 1)

            for u in range(U):
                act.wait_ge(max_negated, u + 1)
                if u >= 2:
                    act.wait_ge(probs_turned, u - 1)
                if u % heads == 0 and u // heads >= 2:
                    act.wait_ge(tile_out, u // heads - 1)
                src = masked[:, u % 2, :] if parts_of and parts_of(units[u]) else score(u)
                nc.scalar.activation(prob[:, u % 2, lead:], src, ACT.Exp, bias=top[:, u % 2, 1:2], scale=scale,
                                     accum_out=rs[:, (u // heads) % 2, u % heads:u % heads + 1]).then_inc(probs_ready, 1)
                if u >= 1 and u % 2 == 0:
                    spread(u - 1)
            spread(U - 1)

        @block.vector
        def _(dve):
            def finish(i):
                dve.wait_ge(probs_ready, heads * (i + 1))
                nc.vector.reciprocal(rs[:, i % 2, :], rs[:, i % 2, :]).then_inc(sums_inverted, 1)
                dve.wait_ge(sums_inverted, i + 1)
                dve.wait_ge(values_done, heads * (i + 1))
                nc.vector.tensor_tensor(
                    outs(tiles[i]).rearrange("p (h d) -> p h d", h=heads),
                    outp(i).rearrange("p (h d) -> p h d", h=heads),
                    rs[:, i % 2, :].unsqueeze(2).broadcast_to([P, heads, out_width]), ALU.mult).then_inc(tile_out, 1)

            def spread(u):
                dve.wait_ge(probs_turned, u + 1)
                if u >= 2:
                    dve.wait_ge(values_done, u - 1)
                for a, b, m in groups:
                    ins = nc.vector.tensor_copy(turned[0:m, u % 2, P * a:P * b], turned_at(u)[0:m, P * a:P * b])
                ins.then_inc(copied_v, 1)

            added = 0
            if lead:
                nc.vector.memset(prob[:, :, 0:lead], 0.0).then_inc(lead_cleared, 1)
                dve.wait_ge(lead_cleared, 1)
            for u in range(U):
                dve.wait_ge(scores_ready, u + 1)
                if u >= 2:
                    dve.wait_ge(probs_ready, u - 1)
                if stream and u % heads == 0:
                    dve.wait_ge(streamed[u // heads % 2], 16 * len(stream(0)) * (u // heads // 2 + 1))
                parts = parts_of(units[u]) if parts_of else []
                if not parts:
                    nc.vector.reduce_max(top[:, u % 2, 0:1], score(u), AX).then_inc(max_found, 1)
                else:
                    for k, (a, b, what) in enumerate(parts):
                        best = top[:, u % 2, 0:1] if len(parts) == 1 else tops[:, k:k + 1]
                        if what.shape[-1] == 1:
                            ins = nc.vector.tensor_scalar(masked[:, u % 2, a:b], score(u)[:, a:b], what, -BIG, ALU.add, ALU.max,
                                                          accum_out=best)
                        else:
                            ins = nc.vector.tensor_tensor_reduce(masked[:, u % 2, a:b], score(u)[:, a:b], what, 1.0, -BIG,
                                                                 ALU.add, ALU.max, best)
                        if len(parts) > 1:
                            ins.then_inc(parts_added, 1)
                            added += 1
                    if len(parts) > 1:
                        dve.wait_ge(parts_added, added)
                        ins = nc.vector.reduce_max(top[:, u % 2, 0:1], tops[:, 0:len(parts)], AX)
                    ins.then_inc(max_found, 1)
                dve.wait_ge(max_found, u + 1)
                nc.vector.tensor_scalar(top[:, u % 2, 1:2], top[:, u % 2, 0:1], -scale, None, ALU.mult).then_inc(max_negated, 1)
                if u % 2 == 1:
                    spread(u - 1)
                if u >= 1 and u % heads == min(2, heads - 1) and u // heads >= 1:
                    finish(u // heads - 1)
            finish(U // heads - 1)


def plain(out, terms, func=None, scale=1.0, bias=None):
    return out, terms, func, scale, bias


def by_block(outT, W, srcT, func=None, scale=1.0, bias=None, n=N):
    m = W.shape[1]
    return [plain(outT[0:m, a:min(a + BLK, n)], [(W[:], srcT[0:W.shape[0], a:min(a + BLK, n)])], func, scale, bias)
            for a in range(0, n, BLK)]


def l0_attn(core):
    nc, io = core.nc, core.io
    x = core.xT
    with ExitStack() as mem:
        sb = lambda shape, name="work": core.buffer(mem, shape, name)
        mix = sb([P, 6])
        vec = sb([P, 7])
        W = {n: sb([P, P]) for n in ("Wr", "Wk", "Wv", "Wo", "g1", "g2")}
        down = sb([P, 160])
        up = sb([D64, 3, P])
        rows = sb([P, 2, P])
        load(core, [(mix[:], io["mix"]), (vec[:, 0:6], io["vec"]), (down[:], io["down"]), (up[:], io["up"])]
             + [(W[n][:], io["L0_attn_" + n]) for n in W]
             + [(rows[:, 0, :], io["L0_attn_ln_w"].unsqueeze(0).broadcast_to([P, P])),
                (rows[:, 1, :], io["L0_attn_ln_b"].unsqueeze(0).broadcast_to([P, P]))])
        load(core, core.consts(mem, "supper", "upper", "levels", "restart128", "pick2"))
        xm = [sb([P, N]) for _ in range(6)]
        xr, xw, xk, xv, xa, xg = xm
        with core.stage("shifted", "dve_step") as (block, shifted, dve_step):
            @block.vector
            def _(dve):
                link = chained(dve, dve_step)
                v = xg[:].rearrange("p (b s) -> p b s", b=B)
                xx = x[:].rearrange("p (b s) -> p b s", b=B)
                nc.vector.tensor_scalar(v[:, :, 0:1], xx[:, :, 0:1], -1.0, None, ALU.mult).then_inc(shifted, 1)
                nc.vector.tensor_tensor(v[:, :, 1:S], xx[:, :, 0:S - 1], xx[:, :, 1:S], ALU.subtract).then_inc(shifted, 1)
                dve.wait_ge(shifted, 2)
                for i in range(6):
                    link(nc.vector.scalar_tensor_tensor(xm[i][:], xg[:], mix[:, i:i + 1], x[:], ALU.mult, ALU.add))
        r, k, v_tok, v = sb([P, N]), sb([P, N]), sb([P, TILES, P]), sb([P, N])
        mid = sb([P, 4, N])
        tok = lambda a, t: a[:, P * t:P * t + P]
        jobs = by_block(r, W["Wr"], xr) + by_block(k, W["Wk"], xk) + by_block(v, W["Wv"], xv)
        jobs += by_block(mid[:, 0, :], down[:, 0:64], xw, ACT.Tanh) + by_block(mid[:, 1, :], down[:, 64:128], xa)
        jobs += by_block(mid[:, 2, :], down[:, 128:160], xv) + by_block(mid[:, 3, :], W["g1"], xg, ACT.Sigmoid)
        products(core, jobs)
        jobs = by_block(xw, up[:, 0, :], mid[0:64, 0, :], ACT.Sigmoid, 1.0, vec[:, 0:1])
        jobs += by_block(xa, up[:, 1, :], mid[0:64, 1, :], ACT.Sigmoid, 1.0, vec[:, 1:2])
        jobs += by_block(xv, up[0:32, 2, :], mid[0:32, 2, :], ACT.Sigmoid, 1.0, vec[:, 2:3])
        products(core, jobs)
        g_tok = sb([P, TILES, P])
        kk, sq, keff, beta, alpha, rt = xk, xr, mid[:, 0, :], mid[:, 1, :], sb([P, N]), sb([P, N])
        cum, dec, mids, ends = sb([P, N]), sb([P, N]), sb([P, TILES]), sb([P, TILES])
        reset, hd, rkr = core.const["restart128"], core.const["head64"], mid[:, 2, :]
        with core.stage("dve_step", "kk_squared", "norms_done", "rooted", "decay_ready", "act_step") as \
                (block, dve_step, kk_squared, norms_done, rooted, decay_ready, act_step):
            @block.vector
            def _(dve):
                link = chained(dve, dve_step)
                link(nc.vector.tensor_scalar(kk[:], k[:], vec[:, 3:4], None, ALU.mult))
                nc.vector.tensor_tensor(sq[:], kk[:], kk[:], ALU.mult).then_inc(kk_squared, 1)
                link(nc.vector.tensor_tensor(alpha[:], v[:], v[:], ALU.subtract))
                link(nc.vector.tensor_tensor(alpha[:], alpha[:], xv[:], ALU.mult))
                link(nc.vector.tensor_tensor(v[:], v[:], alpha[:], ALU.add))
                link(nc.vector.tensor_scalar(dec[:], xw[:], -float(np.exp(-0.5)), None, ALU.mult))
                link(nc.vector.tensor_tensor_scan(cum[:], reset[:], dec[:], 0.0, ALU.mult, ALU.add))
                c3 = cum[:].rearrange("p (t q) -> p t q", t=TILES)
                link(nc.vector.tensor_copy(mids[:].unsqueeze(2), c3[:, :, 63:64]))
                link(nc.vector.tensor_tensor(c3, c3, mids[:].unsqueeze(2).broadcast_to([P, TILES, P]), ALU.subtract))
                link(nc.vector.tensor_copy(ends[:].unsqueeze(2), c3[:, :, P - 1:P]))
                nc.vector.tensor_tensor(dec[:], cum[:], dec[:], ALU.subtract).then_inc(decay_ready, 1)
                link(nc.vector.tensor_scalar(keff, xa[:], 1.0, vec[:, 4:5], ALU.subtract, ALU.mult))
                link(nc.vector.tensor_scalar(keff, keff, 1.0, None, ALU.add))
                link(nc.vector.tensor_tensor(keff, keff, k[:], ALU.mult))
                link(nc.vector.scalar_tensor_tensor(rkr, r[:], vec[:, 5:6], keff, ALU.mult, ALU.mult))
                dve.wait_ge(rooted, 2)
                link(nc.vector.tensor_scalar(sq[:], sq[:], 1e-12, None, ALU.max))
                link(nc.vector.reciprocal(sq[:], sq[:]))
                link(nc.vector.tensor_tensor(kk[:], kk[:], sq[:], ALU.mult))
                link(nc.vector.tensor_tensor(beta, kk[:], xa[:], ALU.mult))
                dve.wait_ge(act_step, 4)
                link(nc.vector.scalar_tensor_tensor(alpha[:], kk[:], -1.0, dec[:], ALU.mult, ALU.mult))
                link(nc.vector.tensor_tensor(rt[:], r[:], cum[:], ALU.mult))
                link(nc.vector.reciprocal(cum[:], cum[:]))
                link(nc.vector.tensor_tensor(beta, beta, cum[:], ALU.mult))
                link(nc.vector.tensor_tensor(keff, keff, cum[:], ALU.mult))

            @block.tensor
            def _(pe):
                pe.wait_ge(kk_squared, 1)
                for n in range(NB):
                    nc.tensor.matmul(core.bank(n), hd[:], sq[:, BLK * n:BLK * n + BLK], start=True, stop=True) \
                        .then_inc(norms_done, 1)

            @block.scalar
            def _(act):
                for n in range(NB):
                    act.wait_ge(norms_done, n + 1)
                    if n == 0:
                        act.wait_ge(norms_done, 2)
                    nc.scalar.activation(sq[:, BLK * n:BLK * n + BLK], core.bank(n), ACT.Sqrt).then_inc(rooted, 1)
                act.wait_ge(decay_ready, 1)
                for a in (cum, dec, mids, ends):
                    nc.scalar.activation(a[:], a[:], ACT.Exp).then_inc(act_step, 1)
        rk_tok = sb([P, TILES, 2])
        k_tok, b_tok = W_ = sb([P, TILES, P]), sb([P, TILES, P])
        jobs = [plain(g_tok[:, t:t + 4, :].rearrange("p t f -> p (t f)")[:, P * i:P * i + P], [(mid[:, 3, P * (t + i):P * (t + i) + P], W["g2"][:])])
                for t in (0, 4) for i in range(4)]
        jobs += [plain(rk_tok[:, t, :], [(rkr[:, P * t:P * t + P], core.const["pick2"][:])]) for t in range(TILES)]
        products(core, jobs)
        transposes(core, [(dst[:, t:t + 4, :], [src[:, P * (t + i):P * (t + i) + P] for i in range(4)])
                          for dst, src in ((v_tok, v), (k_tok, keff), (b_tok, beta)) for t in (0, 4)])
        G = 16
        U_, M_, Y_, T_ = (sb([P, G, P]) for _ in range(4))
        akT, rbT, rkT = (sb([P, G, P]) for _ in range(3))
        at = lambda a, u: a[D64 * (u // TILES):D64 * (u // TILES) + D64, P * (u % TILES):P * (u % TILES) + P]
        four = lambda a, g: a[:, 4 * g:4 * g + 4, :]
        bank4 = lambda i: core.bank(i).rearrange("p (u q) -> p u q", u=4)
        row4 = lambda m: m.unsqueeze(1).broadcast_to([P, 4, P])
        pairs = [(beta, alpha, U_, core.const["supper"]), (keff, alpha, akT, core.const["supper"]),
                 (beta, rt, rbT, core.const["upper"]), (keff, rt, rkT, core.const["upper"])]
        with core.stage("cross_done", "cross_masked", "ones_set") as (block, cross_done, cross_masked, ones_set):
            @block.tensor
            def _(pe):
                for i in range(16):
                    left, right = pairs[i // 4][0:2]
                    if i >= 8:
                        pe.wait_ge(cross_masked, i - 7)
                    for j in range(4):
                        u = 4 * (i % 4) + j
                        mm = nc.tensor.matmul(core.bank(i % 8)[:, P * j:P * j + P], at(left, u), at(right, u), start=True, stop=True)
                    mm.then_inc(cross_done, 1)

            @block.vector
            def _(dve):
                for i in range(16):
                    _, _, dst, mask = pairs[i // 4]
                    dve.wait_ge(cross_done, i + 1)
                    nc.vector.tensor_tensor(four(dst, i % 4), bank4(i % 8), row4(mask[:]), ALU.mult).then_inc(cross_masked, 1)
                for g in range(4):
                    nc.vector.tensor_copy(four(M_, g), row4(core.const["ident"][:])).then_inc(ones_set, 1)
                    nc.vector.tensor_copy(four(Y_, g), row4(core.const["ident"][:])).then_inc(ones_set, 1)
        UL = sb([P, 2, 4, P])
        LV = 7
        with core.stage("level_masked", "lm_done", "lm_copied", "grown", "inverse_added") as \
                (block, level_masked, lm_done, lm_copied, grown, added):
            @block.tensor
            def _(pe):
                for s in range(4 * LV):
                    g = s % 4
                    pe.wait_ge(level_masked, s + 1)
                    if s >= 4:
                        pe.wait_ge(added, 2 * (s - 3))
                    for j in range(4):
                        mm = nc.tensor.matmul(core.bank(s % 2)[:, P * j:P * j + P], UL[:, s % 2, j, :], M_[:, 4 * g + j, :], start=True, stop=True)
                    mm.then_inc(lm_done, 1)
                    pe.wait_ge(lm_copied, s + 1)
                    if s >= 2:
                        pe.wait_ge(added, 2 * (s - 1))
                    for j in range(4):
                        nc.tensor.matmul(core.bank(2 + s % 2)[:, P * j:P * j + P], Y_[:, 4 * g + j, :], T_[:, 4 * g + j, :], start=True, stop=True)
                    for j in range(4):
                        mm = nc.tensor.matmul(core.bank(4 + s % 2)[:, P * j:P * j + P], T_[:, 4 * g + j, :], Y_[:, 4 * g + j, :], start=True, stop=True)
                    mm.then_inc(grown, 1)

            @block.scalar
            def _(act):
                for s in range(4 * LV):
                    act.wait_ge(lm_done, s + 1)
                    if s >= 4:
                        act.wait_ge(grown, s - 3)
                    nc.scalar.copy(four(T_, s % 4), bank4(s % 2)).then_inc(lm_copied, 1)

            @block.vector
            def _(dve):
                def mask(s):
                    if s >= 2:
                        dve.wait_ge(lm_done, s - 1)
                    nc.vector.tensor_tensor(UL[:, s % 2], four(U_, s % 4), row4(core.const["levels"][:, s // 4, :]), ALU.mult) \
                        .then_inc(level_masked, 1)
                mask(0)
                for s in range(4 * LV):
                    if s + 1 < 4 * LV:
                        mask(s + 1)
                    dve.wait_ge(grown, s + 1)
                    for i, a in enumerate((M_, Y_)):
                        nc.vector.tensor_tensor(four(a, s % 4), bank4(2 + 2 * i + s % 2), four(a, s % 4), ALU.add).then_inc(added, 1)
        state = sb([P, B, D64])
        W_sb, SA = sb([P, 4, D64]), sb([P, 4, D64])
        y = sb([P, TILES, P])
        comb = sb([P, TILES])
        CH = S // P
        with core.stage("state_ready", "w_done", "w_copied", "sa_done", "sa_copied", "step_done", "y_copied", "dve_step") as \
                (block, state_ready, w_done, w_copied, sa_done, sa_copied, step_done, y_copied, dve_step):
            lane = lambda i: (i % 2, i // 2)
            unit = lambda c, i: TILES * (i // 2) + CH * (i % 2) + c
            hp = lambda i: slice(D64 * (i // 2), D64 * (i // 2) + D64)

            @block.tensor
            def _(pe):
                for c in range(CH):
                    pe.wait_ge(state_ready, c + 1)
                    for i in range(4):
                        b, h = lane(i)
                        u, o = unit(c, i), core.bank(h)[:, D64 * b:D64 * b + D64]
                        nc.tensor.matmul(o, at(alpha, u), state[hp(i), b, :], start=True, stop=False)
                        mm = nc.tensor.matmul(o, akT[:, u, :], v_tok[:, CH * b + c, hp(i)], start=False, stop=True)
                    mm.then_inc(w_done, 1)
                    pe.wait_ge(w_copied, c + 1)
                    for i in range(4):
                        mm = nc.tensor.matmul(core.bank(2)[:, D64 * i:D64 * i + D64], Y_[:, unit(c, i), :], W_sb[:, i, :],
                                              start=True, stop=True)
                    mm.then_inc(sa_done, 1)
                    pe.wait_ge(sa_copied, c + 1)
                    for i in range(4):
                        b, h = lane(i)
                        t = CH * b + c
                        o = core.bank(3 + h)[hp(i), D64 * b:D64 * b + D64]
                        nc.tensor.matmul(o, b_tok[:, t, hp(i)], SA[:, i, :], start=True, stop=False)
                        nc.tensor.matmul(o, k_tok[:, t, hp(i)], v_tok[:, t, hp(i)], start=False, stop=True)
                    for i in range(4):
                        b, h = lane(i)
                        u, o = unit(c, i), core.bank(5 + h)[:, D64 * b:D64 * b + D64]
                        nc.tensor.matmul(o, at(rt, u), state[hp(i), b, :], start=True, stop=False)
                        nc.tensor.matmul(o, rbT[:, u, :], SA[:, i, :], start=False, stop=False)
                        mm = nc.tensor.matmul(o, rkT[:, u, :], v_tok[:, CH * b + c, hp(i)], start=False, stop=True)
                    mm.then_inc(step_done, 1)

            @block.vector
            def _(dve):
                link = chained(dve, dve_step)
                m3, e3 = (a[:].rearrange("p (b c) -> p b c", b=B) for a in (mids, ends))
                c3 = comb[:].rearrange("p (b c) -> p b c", b=B)
                link(nc.vector.memset(comb[:], 1.0))
                link(nc.vector.tensor_tensor(c3[:, :, 0:CH - 1], e3[:, :, 0:CH - 1], m3[:, :, 1:CH], ALU.mult))
                nc.vector.memset(state[:], 0.0).then_inc(state_ready, 1)
                for c in range(CH):
                    dve.wait_ge(w_done, c + 1)
                    nc.vector.tensor_copy(W_sb[:].rearrange("p (h b) d -> p h (b d)", h=2), core.ps[:, 0:2, 0:P]).then_inc(w_copied, 1)
                    dve.wait_ge(sa_done, c + 1)
                    nc.vector.tensor_copy(SA[:].rearrange("p a b -> p (a b)"), core.bank(2)[:, 0:256]).then_inc(sa_copied, 1)
                    dve.wait_ge(step_done, c + 1)
                    if c + 1 < CH:
                        for h in range(2):
                            q = slice(D64 * h, D64 * h + D64)
                            link(nc.vector.tensor_tensor(state[q].rearrange("p a b -> p (a b)"), core.bank(3 + h)[q, 0:P],
                                                         state[q].rearrange("p a b -> p (a b)"), ALU.add))
                        for b in range(B):
                            ins = nc.vector.tensor_scalar(state[:, b, :], state[:, b, :], comb[:, CH * b + c:CH * b + c + 1],
                                                          None, ALU.mult)
                            if b == 0:
                                link(ins)
                        ins.then_inc(state_ready, 1)
                    for b in range(B):
                        nc.vector.tensor_copy(y[:, CH * b + c, :].rearrange("p (h d) -> p h d", h=2), core.ps[:, 5:7, D64 * b:D64 * b + D64]).then_inc(y_copied, 1)
                    dve.wait_ge(y_copied, 2 * (c + 1))
        mean, var = sb([P, G]), sb([P, G])
        with core.stage("dve_step", "var_ready", "rooted") as (block, dve_step, var_ready, rooted):
            y3 = y[:].rearrange("p t (h d) -> p (t h) d", h=2)
            s3 = g3 = M_[:].rearrange("p u q -> p (u q)")[:, 0:N].rearrange("p (g d) -> p g d", g=G)
            per = lambda a: a[:].unsqueeze(2).broadcast_to([P, G, D64])

            @block.vector
            def _(dve):
                link = chained(dve, dve_step)
                link(nc.vector.reduce_sum(mean[:], y3, AX))
                link(nc.vector.tensor_scalar(mean[:], mean[:], 1.0 / D64, None, ALU.mult))
                link(nc.vector.tensor_tensor(y3, y3, per(mean), ALU.subtract))
                link(nc.vector.tensor_tensor(s3, y3, y3, ALU.mult))
                link(nc.vector.reduce_sum(var[:], s3, AX))
                nc.vector.tensor_scalar(var[:], var[:], 1.0 / D64, None, ALU.mult).then_inc(var_ready, 1)
                dve.wait_ge(rooted, 1)
                link(nc.vector.reciprocal(var[:], var[:]))
                link(nc.vector.tensor_tensor(y3, y3, per(var), ALU.mult))
                for row, op in ((0, ALU.mult), (1, ALU.add)):
                    link(nc.vector.tensor_tensor(y[:], y[:], rows[:, row, :].unsqueeze(1).broadcast_to([P, TILES, P]), op))
                v3 = v_tok[:].rearrange("p t (h d) -> p (t h) d", h=2)
                link(nc.vector.tensor_tensor(s3, v3, rk_tok[:].rearrange("p t h -> p (t h)").unsqueeze(2).broadcast_to([P, G, D64]),
                                             ALU.mult))
                link(nc.vector.tensor_tensor(y3, y3, s3, ALU.add))
                link(nc.vector.tensor_tensor(y[:], y[:], g_tok[:], ALU.mult))

            @block.scalar
            def _(act):
                act.wait_ge(var_ready, 1)
                nc.scalar.activation(var[:], var[:], ACT.Sqrt, bias=core.const["cols"][:, 1:2]).then_inc(rooted, 1)
        turn_tokens(core, xr, y)
        normalise(core, x, x, XBLOCKS, terms=[(W["Wo"][:], xr)])


def head_norm(core, a, width, gain, scale, floor):
    nc = core.nc
    blocks = [(c, min(c + BLK, width)) for c in range(0, width, BLK)]
    with ExitStack() as mem:
        sq = core.buffer(mem, [P, width])
        with core.stage("squared", "summed", "rooted", "dve_step") as (block, squared, summed, rooted, dve_step):
            @block.vector
            def _(dve):
                link = chained(dve, dve_step)
                for c0, c1 in blocks:
                    nc.vector.tensor_tensor(sq[:, c0:c1], a[:, c0:c1], a[:, c0:c1], ALU.mult).then_inc(squared, 1)
                for k, (c0, c1) in enumerate(blocks):
                    dve.wait_ge(rooted, k + 1)
                    link(nc.vector.tensor_scalar(sq[:, c0:c1], sq[:, c0:c1], floor, None, ALU.max))
                    link(nc.vector.reciprocal(sq[:, c0:c1], sq[:, c0:c1]))
                    link(nc.vector.scalar_tensor_tensor(a[:, c0:c1], a[:, c0:c1], gain, sq[:, c0:c1], ALU.mult, ALU.mult))

            @block.tensor
            def _(pe):
                for k, (c0, c1) in enumerate(blocks):
                    pe.wait_ge(squared, k + 1)
                    nc.tensor.matmul(core.bank(k)[:, 0:c1 - c0], core.const["head64"][:], sq[:, c0:c1], start=True, stop=True) \
                        .then_inc(summed, 1)

            @block.scalar
            def _(act):
                for k, (c0, c1) in enumerate(blocks):
                    act.wait_ge(summed, k + 1)
                    nc.scalar.activation(sq[:, c0:c1], core.bank(k)[:, 0:c1 - c0], ACT.Sqrt, scale=scale).then_inc(rooted, 1)


def column(src):
    return src.rearrange("(p o) -> p o", o=1)


XKEYS = [(0, KT), (KT, KT)]


def l0_xattn(core):
    nc, io = core.nc, core.io
    L = lambda n: io["L0_xattn_" + n]
    NK = S + SK
    with ExitStack() as mem:
        sb = lambda shape, name="work": core.buffer(mem, shape, name)
        Wq, Wkv, Wo = sb([P, P], "Wq"), sb([P, 2 * P], "Wkv"), sb([P, P], "Wo")
        vec = sb([P, 7], "vec")
        seen = core.buffer(mem, [P, B, SK], "seen", I32)
        core.fetch("l0x", [(Wq, L("W_q")), (Wkv, L("W_kv")), (Wo, L("W_out")), (vec, L("vec")),
                           (seen, io["mask"].unsqueeze(0).broadcast_to([P, B, SK]))])
        core.need("l0x")
        xn, cn, qT, kT = sb([P, N]), sb([P, CT]), sb([P, N], "qT"), sb([P, B, NK], "kT")
        v_tok, v_ctx, o_tok = sb([P, TILES, P], "v"), sb([KT, 4, P], "v_ctx"), sb([P, TILES, P], "o")
        normalise(core, core.xT, xn, XBLOCKS, vec[:, 2:3], vec[:, 3:4])
        normalise(core, core.ctx, cn, [(0, CT)], vec[:, 0:1], vec[:, 1:2])
        jobs = by_block(qT, Wq, xn)
        for b in range(B):
            jobs.append(plain(kT[:, b, 0:S], [(Wkv[:, 0:P], xn[:, S * b:S * b + S])]))
            jobs.append(plain(kT[:, b, S:NK], [(Wkv[:, 0:P], cn[:, SK * b:SK * b + SK])]))
        jobs += [plain(v_tok[:, t, :], [(xn[:, P * t:P * t + P], Wkv[:, P:2 * P])]) for t in range(TILES)]
        jobs += [plain(v_ctx[:, t, :], [(cn[:, KT * t:KT * t + KT], Wkv[:, P:2 * P])]) for t in range(4)]
        products(core, jobs)
        head_norm(core, qT, N, vec[:, 4:5], 1.0 / D64, 1e-8)
        head_norm(core, kT.rearrange("p b k -> p (b k)"), B * NK, vec[:, 5:6], 1.0 / D64, 1e-8)
        mask = sb([P, B, NK], "mask")
        with core.stage("dve_step") as (block, dve_step):
            @block.vector
            def _(dve):
                link = chained(dve, dve_step)
                link(nc.vector.memset(mask[:, :, 0:S], 0.0))
                link(nc.vector.tensor_scalar(mask[:, :, S:NK], seen, BIG, -BIG, ALU.mult, ALU.add))
        units = []
        for t in range(TILES):
            for h in range(2):
                hp, b = slice(D64 * h, D64 * h + D64), t // 4
                q = qT[hp, P * t:P * t + P]
                units.append((t, h, [(0, q, kT[hp, b, 0:S], True, True), (S, q, kT[hp, b, S:NK], True, True)],
                              [v_tok[:, 4 * b + i, hp] for i in range(4)] + [v_ctx[:, 2 * b + i, hp] for i in range(2)]))
        attend(core, units, [(P * i, P) for i in range(4)] + [(S, KT), (S + KT, KT)], D64, lambda t: o_tok[:, t, :],
               D64 ** -0.5, range(TILES), lambda u: [(0, NK, mask[:, u[0] // 4, :])], nk=NK)
        turn_tokens(core, xn, o_tok)
        normalise(core, core.xT, core.xT, XBLOCKS, terms=[(Wo, xn)], bias=vec[:, 6:7])


def top_weights(core, logits, experts, k, renormalise, w):
    nc = core.nc
    with ExitStack() as mem:
        m = core.buffer(mem, [P, TILES], "row")
        rest = core.buffer(mem, [P, TILES, experts], "rest")
        best = core.buffer(mem, [P, TILES, 8], "best")
        per = lambda a: a.unsqueeze(2).broadcast_to([P, TILES, experts])
        with core.stage("dve_step", "shifted", "act_done") as (block, dve_step, shifted, exp_done):
            @block.vector
            def _(dve):
                link = chained(dve, dve_step)
                link(nc.vector.reduce_max(m, logits, AX))
                nc.vector.tensor_tensor(logits, logits, per(m), ALU.subtract).then_inc(shifted, 1)
                dve.wait_ge(exp_done, 1)
                link(nc.vector.reduce_sum(m, logits, AX))
                link(nc.vector.reciprocal(m, m))
                link(nc.vector.tensor_tensor(logits, logits, per(m), ALU.mult))
                for t in range(TILES):
                    link(nc.vector.max(best[:, t, :], logits[:, t, :]))
                link(nc.vector.memset(best[:, :, k:8], -1.0))
                for t in range(TILES):
                    link(nc.vector.match_replace(rest[:, t, :], best[:, t, :], logits[:, t, :], -1.0))
                link(nc.vector.tensor_tensor(rest, rest, logits, ALU.not_equal))
                link(nc.vector.tensor_tensor(w, rest, logits, ALU.mult))
                if renormalise:
                    link(nc.vector.reduce_sum(m, w, AX))
                    link(nc.vector.tensor_scalar(m, m, 1e-12, None, ALU.max))
                    link(nc.vector.reciprocal(m, m))
                    link(nc.vector.tensor_tensor(w, w, per(m), ALU.mult))

            @block.scalar
            def _(act):
                act.wait_ge(shifted, 1)
                nc.scalar.activation(logits, logits, ACT.Exp).then_inc(exp_done, 1)


def l0_ffn(core):
    nc, io = core.nc, core.io
    E, SH = 32, 4
    x = core.xT
    with ExitStack() as mem:
        sb = lambda shape, name="work": core.buffer(mem, shape, name)
        gate, up, down = (sb([P, E + SH, P], n) for n in ("gate", "up", "down"))
        router, rbias = sb([P, E], "router"), sb([P, E], "router_bias")
        pick = sb([E, E, P], "pickrow")
        core.fetch("router", [(router, io["L0_ffn_router"]), (rbias, io["L0_ffn_router_bias"].unsqueeze(0).broadcast_to([P, E])),
                              (pick, io["c_pickrow"][0:E])])
        for g in range(0, E + SH, 4):
            core.fetch(f"experts{g}", [(t[:, g:g + 4, :], io["L0_ffn_" + n][:, g:g + 4, :])
                                       for t, n in ((gate, "gate"), (up, "up"), (down, "down"))])
        core.need("router")
        logits, w = sb([P, TILES, E], "logits"), sb([P, TILES, E], "weights")
        with core.stage("logits_done", "logits_out") as (block, logits_done, logits_out):
            @block.tensor
            def _(pe):
                for t in range(TILES):
                    mm = nc.tensor.matmul(core.bank(0)[:, E * t:E * t + E], x[:, P * t:P * t + P], router, start=True, stop=True)
                mm.then_inc(logits_done, 1)

            @block.vector
            def _(dve):
                dve.wait_ge(logits_done, 1)
                nc.vector.tensor_tensor(logits, core.bank(0)[:, 0:E * TILES].rearrange("p (t e) -> p t e", e=E),
                                        rbias.unsqueeze(1).broadcast_to([P, TILES, E]), ALU.add).then_inc(logits_out, 1)
        top_weights(core, logits, E, 4, True, w)
        wT = sb([E, N], "wT")
        transposes(core, [(wT[:, P * t:P * t + 4 * P], [w[:, t + i, :] for i in range(4)]) for t in (0, 4)])
        U, R = 2 * (E + SH), 2 * E
        act_out, hidden = sb([P, 2, BLK], "gated"), sb([P, 2, BLK], "hidden")
        cols = lambda i: slice(BLK * (i % 2), BLK * (i % 2) + BLK)
        with core.stage("inner_done", "silu_done", "hidden_ready", "down_done", "dve_step") as \
                (block, inner_done, silu_done, hidden_ready, down_done, dve_step):
            @block.tensor
            def _(pe):
                def inner(i):
                    e = i // 2
                    if i % 8 == 0:
                        pe.wait_ge(*core.fetched[f"experts{e}"])
                    if i >= 2:
                        pe.wait_ge(hidden_ready, i - 1)
                    nc.tensor.matmul(core.bank(i % 2), gate[:, e, :], x[:, cols(i)], start=True, stop=True)
                    mm = nc.tensor.matmul(core.bank(2 + i % 2), up[:, e, :], x[:, cols(i)], start=True, stop=True)
                    if i < R:
                        mm = nc.tensor.matmul(core.bank(4 + i % 2), pick[:, e, :], wT[:, cols(i)], start=True, stop=True)
                    mm.then_inc(inner_done, 1)

                def outer(i):
                    pe.wait_ge(hidden_ready, i + 1)
                    nc.tensor.matmul(core.bank(6 + i % 2), down[:, i // 2, :], hidden[:, i % 2, :], start=(i < 2),
                                     stop=(i >= U - 2)).then_inc(down_done, 1)

                inner(0)
                for i in range(1, U):
                    inner(i)
                    outer(i - 1)
                outer(U - 1)

            @block.scalar
            def _(act):
                for i in range(U):
                    act.wait_ge(inner_done, i + 1)
                    if i >= 2:
                        act.wait_ge(hidden_ready, i - 1)
                    nc.scalar.activation(act_out[:, i % 2, :], core.bank(i % 2), ACT.Silu).then_inc(silu_done, 1)

            @block.vector
            def _(dve):
                link = chained(dve, dve_step)
                for i in range(U):
                    dve.wait_ge(silu_done, i + 1)
                    if i >= 2:
                        dve.wait_ge(down_done, i - 1)
                    ins = nc.vector.tensor_tensor(hidden[:, i % 2, :], core.bank(2 + i % 2), act_out[:, i % 2, :], ALU.mult)
                    if i < R:
                        link(ins)
                        ins = nc.vector.tensor_tensor(hidden[:, i % 2, :], core.bank(4 + i % 2), hidden[:, i % 2, :], ALU.mult)
                    ins.then_inc(hidden_ready, 1)
                dve.wait_ge(down_done, U)
                for n in range(NB):
                    link(nc.vector.tensor_tensor(x[:, cols(n)], core.bank(6 + n), x[:, cols(n)], ALU.add))
        normalise(core, x, x, XBLOCKS)


def expand_heads(core, dst, src, width):
    nc = core.nc
    with core.stage("spread_dve", "spread_pool") as (block, by_dve, by_pool):
        @block.vector
        def _(dve):
            for h in range(H16):
                nc.vector.tensor_scalar(dst[:, h, :], src, core.const["headmask"][:, h:h + 1], None, ALU.mult).then_inc(by_dve, 1)
            dve.wait_ge(by_dve, H16)


def narrow_attention(core, qT, kTs, v, o_tok, keytiles, scale, width, parts_of=None, stream=None):
    with ExitStack() as mem:
        K = [core.buffer(mem, [P, H16, width], "k_heads") for _ in range(B)]
        for b in range(B):
            expand_heads(core, K[b], kTs[b], width)
        units = [(t, h, [(0, qT[:, P * t:P * t + P], K[t // 4][:, h, :], True, True)],
                  [v[t // 4][i][:, D8 * h:D8 * h + D8] for i in range(len(keytiles))])
                 for t in range(TILES) for h in range(H16)]
        attend(core, units, keytiles, D8, lambda t: o_tok[:, t, :], scale, range(TILES), parts_of, nk=width, stream=stream)


SELF_KEYS = [(P * i, P) for i in range(4)]


def l1_attn(core):
    io = core.io
    with ExitStack() as mem:
        sb = lambda shape, name="work": core.buffer(mem, shape, name)
        W = {n: sb([P, P], n) for n in ("w_Q", "w_K", "w_V")}
        core.fetch("l1a", core.consts(mem, "headmask") + [(W[n], io["L1_attn_" + n]) for n in W])
        core.need("l1a")
        qT, kT, v, o = sb([P, N], "qT"), sb([P, N], "kT"), sb([P, TILES, P], "v"), sb([P, TILES, P], "o")
        products(core, by_block(qT, W["w_Q"], core.xT) + by_block(kT, W["w_K"], core.xT)
                 + [plain(v[:, t, :], [(core.xT[:, P * t:P * t + P], W["w_V"])]) for t in range(TILES)])
        narrow_attention(core, qT, [kT[:, S * b:S * b + S] for b in range(B)], [[v[:, 4 * b + i, :] for i in range(4)] for b in range(B)],
                         o, SELF_KEYS, D8 ** -0.5, S)
        turn_tokens(core, qT, o)
        normalise(core, core.xT, core.xT, XBLOCKS, terms=[(core.const["ident"], qT)])


def narrow_cross(core, layer, causal):
    io = core.io
    with ExitStack() as mem:
        sb = lambda shape, name="work": core.buffer(mem, shape, name)
        W = {n: sb([P, P], n) for n in ("Wq", "Wk", "Wv", "Wo")}
        vec, bv = sb([P, 3], "vec"), sb([P, P], "bv")
        core.fetch(layer, core.consts(mem, "headmask", *(["xcausal"] if causal else [])) + [(W[n], io[layer + n]) for n in W]
                   + [(vec, io[layer + "vec"]), (bv, io[layer + "bv"].unsqueeze(0).broadcast_to([P, P]))])
        core.need(layer)
        qT, kT, v, o = sb([P, N], "qT"), sb([P, CT], "kT"), sb([KT, 4, P], "v"), sb([P, TILES, P], "o")
        products(core, by_block(qT, W["Wq"], core.xT, None, 1.0, vec[:, 0:1]) + by_block(kT, W["Wk"], core.ctx, None, 1.0, vec[:, 1:2], CT)
                 + [plain(v[:, i, :], [(core.ctx[:, KT * i:KT * i + KT], W["Wv"])]) for i in range(4)])
        with core.stage("bias_added") as (block, bias_added):
            @block.vector
            def _(dve):
                core.nc.vector.tensor_tensor(v, v, bv[0:KT].unsqueeze(1).broadcast_to([KT, 4, P]), ALU.add).then_inc(bias_added, 1)
        parts_of = (lambda u: [(0, SK, core.const["xcausal"][:, u[0] % 4, :])] if u[0] % 4 < 2 else []) if causal else None
        narrow_attention(core, qT, [kT[:, SK * b:SK * b + SK] for b in range(B)], [[v[:, 2 * b + i, :] for i in range(2)] for b in range(B)],
                         o, XKEYS, D8 ** -0.5, SK, parts_of)
        turn_tokens(core, qT, o)
        normalise(core, core.xT, core.xT, XBLOCKS, terms=[(W["Wo"], qT)], bias=vec[:, 2:3])


def l1_xattn(core):
    narrow_cross(core, "L1_xattn_", True)


def l2_xattn(core):
    narrow_cross(core, "L2_xattn_", False)


def add_projection(core, dst, terms, bias=None):
    nc = core.nc
    with core.stage("projected", "added") as (block, projected, added):
        @block.tensor
        def _(pe):
            for n in range(NB):
                for i, (lhsT, rhs) in enumerate(terms):
                    mm = nc.tensor.matmul(core.bank(n), lhsT, rhs[:, BLK * n:BLK * n + BLK], start=(i == 0), stop=(i == len(terms) - 1))
                mm.then_inc(projected, 1)

        @block.vector
        def _(dve):
            for n in range(NB):
                d = dst[:, BLK * n:BLK * n + BLK]
                dve.wait_ge(projected, n + 1)
                if bias is None:
                    nc.vector.tensor_tensor(d, core.bank(n), d, ALU.add).then_inc(added, 1)
                else:
                    nc.vector.scalar_tensor_tensor(d, core.bank(n), bias, d, ALU.add, ALU.add).then_inc(added, 1)


def shift_tokens(core, dst, src):
    nc = core.nc
    with core.stage("shifted", "copied") as (block, shifted, copied):
        @block.vector
        def _(dve):
            d, s = (a[D64:P].rearrange("p (b s) -> p b s", b=B) for a in (dst, src))
            nc.vector.memset(d[:, :, 0:1], 0.0).then_inc(shifted, 1)
            nc.vector.tensor_copy(d[:, :, 1:S], s[:, :, 0:S - 1]).then_inc(shifted, 1)

        @block.scalar
        def _(act):
            nc.scalar.copy(dst[0:D64], src[0:D64]).then_inc(copied, 1)


def rotate(core, units):
    nc = core.nc
    with ExitStack() as mem:
        cosed, sined = core.buffer(mem, [P, 2, BLK], "cosed"), core.buffer(mem, [P, 2, BLK], "sined")
        w = lambda u: units[u][0].shape[-1]
        with core.stage("norm_spread", "scaled", "turned", "cos_taken", "sin_taken", "rotated") as \
                (block, norm_spread, scaled, turned, cos_taken, sin_taken, rotated):
            @block.tensor
            def _(pe):
                def spread(u):
                    if units[u][3]:
                        if u >= 2:
                            pe.wait_ge(scaled, u - 1)
                        nc.tensor.matmul(core.bank(u % 2)[:, 0:w(u)], units[u][3][1], units[u][3][2], start=True, stop=True) \
                            .then_inc(norm_spread, 1)
                spread(0)
                for u in range(len(units)):
                    if u + 1 < len(units):
                        spread(u + 1)
                    if units[u][3]:
                        pe.wait_ge(scaled, u + 1)
                    if u >= 2:
                        pe.wait_ge(sin_taken, u - 1)
                    nc.tensor.matmul(core.bank(2 + u % 2)[:, 0:w(u)], core.const["rot"], units[u][0], start=True, stop=True).then_inc(turned, 1)

            @block.vector
            def _(dve):
                for u, (a, cos, sin, norm) in enumerate(units):
                    if norm:
                        dve.wait_ge(norm_spread, u + 1)
                        nc.vector.scalar_tensor_tensor(a, a, norm[0], core.bank(u % 2)[:, 0:w(u)], ALU.mult, ALU.mult).then_inc(scaled, 1)
                    dve.wait_ge(turned, u + 1)
                    if u >= 2:
                        dve.wait_ge(rotated, u - 1)
                    nc.vector.tensor_tensor(sined[:, u % 2, 0:w(u)], core.bank(2 + u % 2)[:, 0:w(u)], sin, ALU.mult).then_inc(sin_taken, 1)

            @block.gpsimd
            def _(pool):
                for u, (a, cos, sin, norm) in enumerate(units):
                    pool.wait_ge(turned, u + 1)
                    nc.gpsimd.tensor_tensor(cosed[:, u % 2, 0:w(u)], a, cos, ALU.mult).then_inc(cos_taken, 1)
                    pool.wait_ge(cos_taken, u + 1)
                    pool.wait_ge(sin_taken, u + 1)
                    nc.gpsimd.tensor_tensor(a, cosed[:, u % 2, 0:w(u)], sined[:, u % 2, 0:w(u)], ALU.add).then_inc(rotated, 1)
                pool.wait_ge(rotated, len(units))


def l1_ffn(core):
    nc, io = core.nc, core.io
    x = core.xT
    D = lambda n: io["L1_ffn_" + n]
    with ExitStack() as mem:
        sb = lambda shape, name="work": core.buffer(mem, shape, name)
        start = sb([P, N], "start")
        Wqkv, Wo, W1, W2, vec = sb([P, 3 * INNER], "Wqkv"), sb([P, WC, P], "Wo"), sb([P, 2 * DI], "W1"), sb([P, 3, P], "W2"), sb([P, 11], "vec")
        load(core, core.consts(mem, "toheads", "fromheads", "rot", "qcos", "qsin", "kcos", "ksin", "band"))
        with core.stage("copied") as (block, copied):
            @block.vector
            def _(dve):
                nc.vector.tensor_copy(start, x).then_inc(copied, 1)
        xs = sb([P, N], "shifted")
        core.settle()
        with nc.Fori(0, DEPTH) as i:
            load(core, [(Wqkv, D("Wqkv")[i]), (Wo, D("Wo")[i]), (W1, D("W1")[i]), (W2, D("W2")[i]), (vec, D("vec")[i])])
            shift_tokens(core, xs, x)
            with ExitStack() as inner:
                ib = lambda shape, name: core.buffer(inner, shape, name)
                q, k, v = ib([P, WC, N], "q"), ib([P, WC, B, WIN + S], "k"), ib([P, TILES, INNER], "v")
                with core.stage("cleared") as (block, cleared):
                    @block.vector
                    def _(dve):
                        nc.vector.memset(k[:, :, :, 0:WIN], 0.0).then_inc(cleared, 1)
                spots = [(side, c, b) for side in range(2) for c in range(WC) for b in range(B)]
                at = lambda side, c, b: q[:, c, S * b:S * b + S] if side == 0 else k[:, c, b, WIN:]
                jobs = [plain(at(side, c, b), [(Wqkv[:, INNER * side + P * c:INNER * side + P * c + P], xs[:, S * b:S * b + S])])
                        for side, c, b in spots]
                jobs += [plain(v[:, t, BLK * j:BLK * j + BLK], [(xs[:, P * t:P * t + P], Wqkv[:, 2 * INNER + BLK * j:2 * INNER + BLK * j + BLK])])
                         for t in range(TILES) for j in range(2)]
                products(core, jobs)
                norms, sq = ib([2 * H16, N], "norms"), ib([P, 4, S], "squares")
                with core.stage("squared", "summed", "rooted", "dve_step") as (block, squared, summed, rooted, dve_step):
                    @block.scalar
                    def _(act):
                        for s, (side, c, b) in enumerate(spots):
                            if s >= 4:
                                act.wait_ge(summed, s - 3)
                            nc.scalar.activation(sq[:, s % 4, :], at(side, c, b), ACT.Square).then_inc(squared, 1)
                        for b in range(B):
                            act.wait_ge(summed, len(spots))
                            nc.scalar.activation(norms[:, S * b:S * b + S], core.bank(b)[0:2 * H16], ACT.Sqrt).then_inc(rooted, 1)

                    @block.tensor
                    def _(pe):
                        for s, (side, c, b) in enumerate(spots):
                            pe.wait_ge(squared, s + 1)
                            nc.tensor.matmul(core.bank(b)[0:2 * H16], core.const["toheads"][:, WC * side + c, :], sq[:, s % 4, :],
                                             start=(s < B), stop=(s >= len(spots) - B)).then_inc(summed, 1)

                    @block.vector
                    def _(dve):
                        link = chained(dve, dve_step)
                        dve.wait_ge(rooted, B)
                        link(nc.vector.tensor_scalar(norms, norms, 1e-12, None, ALU.max))
                        link(nc.vector.reciprocal(norms, norms))
                rotate(core, [(at(side, c, b), *((core.const["qcos"], core.const["qsin"]) if side == 0 else (core.const["kcos"], core.const["ksin"])),
                               (vec[:, side:side + 1], core.const["fromheads"][:, WC * side + c, :], norms[:, S * b:S * b + S]))
                              for side, c, b in spots])
                o = ib([P, TILES, INNER], "o")
                units = []
                for t in range(TILES):
                    for h in range(H16):
                        b, j, c, hp = t // 4, t % 4, h // 2, slice(D64 * (h % 2), D64 * (h % 2) + D64)
                        own, before = v[:, t, D64 * h:D64 * h + D64], v[:, max(t - 1, 0), D64 * h:D64 * h + D64]
                        units.append((t, h, [(0, q[hp, c, P * t:P * t + P], k[hp, c, b, P * j:P * j + P + WIN], True, True)], [before, own]))
                attend(core, units, [(0, P), (P, P)], D64, lambda t: o[:, t, :], 8.0, range(TILES),
                       lambda u: [(0, P + WIN, core.const["band"][:, min(u[0] % 4, 1), :])], nk=P + WIN, lead=P - WIN)
                transposes(core, [(q[:, c, P * t:P * t + 4 * P], [o[:, t + i, P * c:P * c + P] for i in range(4)])
                                  for c in range(WC) for t in (0, 4)])
                add_projection(core, x, [(Wo[:, c, :], q[:, c, :]) for c in range(WC)])
            shift_tokens(core, xs, x)
            with ExitStack() as inner:
                xn, gelu, prod = (core.buffer(inner, s, n) for s, n in (([P, N], "xn"), ([P, 2, BLK], "gelu"), ([P, 3, N], "prod")))
                normalise(core, xs, xn, XBLOCKS, vec[:, 2:3], vec[:, 3:4])
                parts = [(j, min(P, DI - P * j), n) for j in range(3) for n in range(NB)]
                with core.stage("inner_done", "gelu_done", "gated") as (block, inner_done, gelu_done, gated):
                    @block.tensor
                    def _(pe):
                        for s, (j, m, n) in enumerate(parts):
                            if s >= 2:
                                pe.wait_ge(gated, s - 1)
                            for half in range(2):
                                mm = nc.tensor.matmul(core.bank(2 * (s % 2) + half)[0:m], W1[:, DI * half + P * j:DI * half + P * j + m],
                                                      xn[:, BLK * n:BLK * n + BLK], start=True, stop=True)
                            mm.then_inc(inner_done, 1)

                    @block.scalar
                    def _(act):
                        for s, (j, m, n) in enumerate(parts):
                            act.wait_ge(inner_done, s + 1)
                            if s >= 2:
                                act.wait_ge(gated, s - 1)
                            nc.scalar.activation(gelu[0:m, s % 2, :], core.bank(2 * (s % 2) + 1)[0:m], ACT.Gelu,
                                                 bias=vec[0:m, 8 + j:9 + j]).then_inc(gelu_done, 1)

                    @block.vector
                    def _(dve):
                        for s, (j, m, n) in enumerate(parts):
                            dve.wait_ge(gelu_done, s + 1)
                            nc.vector.scalar_tensor_tensor(prod[0:m, j, BLK * n:BLK * n + BLK], core.bank(2 * (s % 2))[0:m],
                                                           vec[0:m, 5 + j:6 + j], gelu[0:m, s % 2, :], ALU.add, ALU.mult).then_inc(gated, 1)
                add_projection(core, x, [(W2[0:m, j, :], prod[0:m, j, :]) for j, m in ((0, P), (1, P), (2, DI - 2 * P))], vec[:, 4:5])
            core.settle()
        normalise(core, x, x, XBLOCKS, terms=[(core.const["ident"], start)])


def l2_attn(core):
    nc, io = core.nc, core.io
    A = lambda n: io["L2_attn_" + n]
    WINDOW = 2 * P
    with ExitStack() as mem:
        sb = lambda shape, name="work": core.buffer(mem, shape, name)
        W, Wo, vec, bv, rel = sb([P, 3 * P], "Wqkv"), sb([P, P], "Wo"), sb([P, 3], "vec"), sb([P, P], "bv"), sb([P, EXT], "rel")
        core.fetch("l2a", core.consts(mem, "headmask") + [(W, A("W")), (Wo, A("Wo")), (vec, A("vec")), (rel, A("rel")),
                                                          (bv, A("bv").unsqueeze(0).broadcast_to([P, P]))])
        core.need("l2a")
        qT, kT, v, o = sb([P, N], "qT"), sb([P, N], "kT"), sb([P, TILES, P], "v"), sb([P, TILES, P], "o")
        products(core, by_block(qT, W[:, 0:P], core.xT, None, 1.0, vec[:, 0:1]) + by_block(kT, W[:, P:2 * P], core.xT, None, 1.0, vec[:, 1:2])
                 + [plain(v[:, t, :], [(core.xT[:, P * t:P * t + P], W[:, 2 * P:3 * P])]) for t in range(TILES)])
        edges = sb([P, TILES, H16, 2], "edges")
        scratch = nc.dram_tensor("relative", (TILES, P * H16 * EXT), F32, kind="Internal")
        with core.stage("dve_step") as (block, dve_step):
            @block.vector
            def _(dve):
                link = chained(dve, dve_step)
                link(nc.vector.tensor_tensor(v, v, bv.unsqueeze(1).broadcast_to([P, TILES, P]), ALU.add))
                link(nc.vector.tensor_scalar(qT, qT, float(1.0 / np.sqrt(D8)), None, ALU.mult))
        with ExitStack() as inner:
            heads = core.buffer(inner, [P, H16, EXT], "rel_heads")
            rows = core.buffer(inner, [P, 2, H16, EXT], "rows")
            expand_heads(core, heads, rel, EXT)
            with core.stage("bias_done", "out_by_act", "out_by_dve", "stored_even", "stored_odd", "edges_kept") as \
                    (block, bias_done, by_act, by_dve, stored_even, stored_odd, kept):
                stored = (stored_even, stored_odd)

                @block.tensor
                def _(pe):
                    for u in range(TILES * H16):
                        if u >= 8:
                            if u % 2:
                                pe.wait_ge(by_dve, (u - 8) // 2 + 1)
                            else:
                                pe.wait_ge(by_act, (u - 8) // 2 + 1)
                        t, h = u // H16, u % H16
                        nc.tensor.matmul(core.bank(u % 8)[:, 0:EXT], qT[:, P * t:P * t + P], heads[:, h, :], start=True, stop=True) \
                            .then_inc(bias_done, 1)

                @block.scalar
                def _(act):
                    for u in range(0, TILES * H16, 2):
                        t, h = u // H16, u % H16
                        act.wait_ge(bias_done, u + 1)
                        if h == 0 and t >= 2:
                            act.wait_ge(stored[t % 2], 16 * (t // 2))
                            act.wait_ge(kept, t - 1)
                        nc.scalar.copy(rows[:, t % 2, h, :], core.bank(u % 8)[:, 0:EXT]).then_inc(by_act, 1)

                @block.vector
                def _(dve):
                    for u in range(1, TILES * H16, 2):
                        t, h = u // H16, u % H16
                        dve.wait_ge(bias_done, u + 1)
                        if h == 1 and t >= 2:
                            dve.wait_ge(stored[t % 2], 16 * (t // 2))
                            dve.wait_ge(kept, t - 1)
                        nc.vector.tensor_copy(rows[:, t % 2, h, :], core.bank(u % 8)[:, 0:EXT]).then_inc(by_dve, 1)
                        if h == H16 - 1:
                            dve.wait_ge(by_act, H16 // 2 * (t + 1))
                            dve.wait_ge(by_dve, H16 // 2 * (t + 1))
                            nc.vector.tensor_copy(edges[:, t, :, :], rows[:, t % 2, :, 0:EXT - 1:EXT - 2]).then_inc(kept, 1)

                @block.sync
                def _(sp):
                    for t in range(TILES):
                        sp.wait_ge(by_act, H16 // 2 * (t + 1))
                        sp.wait_ge(by_dve, H16 // 2 * (t + 1))
                        sp.dma_start(scratch.ap()[t].rearrange("(p c) -> p c", p=P), rows[:, t % 2].rearrange("p h c -> p (h c)")) \
                            .then_inc(stored[t % 2], 16)
                    for one in stored:
                        sp.wait_ge(one, 8 * TILES)
        window = sb([P, 2, H16, WINDOW], "window")

        def parts(u):
            t, h = u[0], u[1]
            first = P * (t % 4) - REL
            a, b = max(first, 0), min(first + WINDOW, S)
            out = [(a, b, window[:, t % 2, h, a - first:b - first])]
            if a:
                out.append((0, a, edges[:, t, h, 0:1]))
            if b < S:
                out.append((b, S, edges[:, t, h, 1:2]))
            return out

        def stream(t):
            src = bass.AP(scratch, t * P * H16 * EXT + P - 1, [[H16 * EXT - 1, P], [EXT, H16], [1, WINDOW]])
            return [(window[:, t % 2], src)]

        narrow_attention(core, qT, [kT[:, S * b:S * b + S] for b in range(B)], [[v[:, 4 * b + i, :] for i in range(4)] for b in range(B)],
                         o, SELF_KEYS, 1.0, S, parts, stream)
        turn_tokens(core, qT, o)
        normalise(core, core.xT, core.xT, XBLOCKS, terms=[(Wo, qT)], bias=vec[:, 2:3])


def l2_ffn(core):
    nc, io = core.nc, core.io
    E = 8
    x = core.xT
    with ExitStack() as mem:
        sb = lambda shape, name="work": core.buffer(mem, shape, name)
        W, router, rbias, bias, pick = sb([P, E, P], "experts"), sb([P, E], "router"), sb([P, E], "rbias"), sb([E, P], "bias"), sb([E, E, P], "pick")
        core.fetch("l2f", [(W, io["L2_ffn_W"]), (router, io["L2_ffn_router"]), (rbias, io["L2_ffn_b_router"].unsqueeze(0).broadcast_to([P, E])),
                           (bias, io["L2_ffn_b_experts"]), (pick, io["c_pickrow"][0:E, 0:E])])
        core.need("l2f")
        logits, w, wT = sb([P, TILES, E], "logits"), sb([P, TILES, E], "weights"), sb([E, N], "wT")
        with core.stage("logits_done", "logits_out") as (block, logits_done, logits_out):
            @block.tensor
            def _(pe):
                for t in range(TILES):
                    mm = nc.tensor.matmul(core.bank(0)[:, E * t:E * t + E], x[:, P * t:P * t + P], router, start=True, stop=True)
                mm.then_inc(logits_done, 1)

            @block.vector
            def _(dve):
                dve.wait_ge(logits_done, 1)
                nc.vector.tensor_tensor(logits, core.bank(0)[:, 0:E * TILES].rearrange("p (t e) -> p t e", e=E),
                                        rbias.unsqueeze(1).broadcast_to([P, TILES, E]), ALU.add).then_inc(logits_out, 1)
        top_weights(core, logits, E, 2, False, w)
        transposes(core, [(wT[:, P * t:P * t + 4 * P], [w[:, t + i, :] for i in range(4)]) for t in (0, 4)])
        xw = sb([P, 2, BLK], "weighted")
        cols = lambda i: slice(BLK * (i % 2), BLK * (i % 2) + BLK)
        U = 2 * E
        with core.stage("weight_spread", "x_weighted", "expert_done", "dve_step") as (block, spread, weighted, expert_done, dve_step):
            @block.tensor
            def _(pe):
                def pick_row(i):
                    if i >= 2:
                        pe.wait_ge(weighted, i - 1)
                    nc.tensor.matmul(core.bank(i % 2), pick[:, i // 2, :], wT[:, cols(i)], start=True, stop=True).then_inc(spread, 1)
                for n in range(NB):
                    nc.tensor.matmul(core.bank(2 + n), bias, wT[:, cols(n)], start=True, stop=False)
                pick_row(0)
                for i in range(U):
                    if i + 1 < U:
                        pick_row(i + 1)
                    pe.wait_ge(weighted, i + 1)
                    nc.tensor.matmul(core.bank(2 + i % 2), W[:, i // 2, :], xw[:, i % 2, :], start=False, stop=(i >= U - 2)).then_inc(expert_done, 1)

            @block.vector
            def _(dve):
                for i in range(U):
                    dve.wait_ge(spread, i + 1)
                    if i >= 2:
                        dve.wait_ge(expert_done, i - 1)
                    nc.vector.tensor_tensor(xw[:, i % 2, :], core.bank(i % 2), x[:, cols(i)], ALU.mult).then_inc(weighted, 1)
                dve.wait_ge(weighted, U)
                dve.wait_ge(expert_done, U)
                link = chained(dve, dve_step)
                for n in range(NB):
                    link(nc.vector.tensor_tensor(x[:, cols(n)], core.bank(2 + n), x[:, cols(n)], ALU.add))
        normalise(core, x, x, XBLOCKS)


def l3_attn(core):
    nc, io = core.nc, core.io
    x = core.xT
    CAP = 50.0
    with ExitStack() as mem:
        sb = lambda shape, name="work": core.buffer(mem, shape, name)
        W, Wg, Wo = sb([P, 3 * INNER], "Wqkv"), sb([P, H16], "Wg"), sb([P, WC, P], "Wo")
        core.fetch("l3a", core.consts(mem, "upper") + [(W, io["L3_attn_w_qkv"]), (Wg, io["L3_attn_w_gates"]), (Wo, io["L3_attn_w_out"])])
        core.need("l3a")
        q, k = sb([P, WC, N], "q"), sb([P, WC, N], "k")
        o = sb([P, TILES, INNER], "o")
        gates = sb([P, TILES, H16], "gates")
        with ExitStack() as inner:
            v = core.buffer(inner, [P, TILES, H16, D64 + 1], "v_ones")
            with core.stage("ones_set") as (block, ones_set):
                @block.vector
                def _(dve):
                    nc.vector.memset(v[:, :, :, D64:D64 + 1], 1.0).then_inc(ones_set, 1)
            jobs = [plain(a[:, c, S * b:S * b + S], [(W[:, INNER * i + P * c:INNER * i + P * c + P], x[:, S * b:S * b + S])])
                    for i, a in enumerate((q, k)) for c in range(WC) for b in range(B)]
            jobs += [plain(v[:, t, 8 * j:8 * j + 8, 0:D64], [(x[:, P * t:P * t + P], W[:, 2 * INNER + BLK * j:2 * INNER + BLK * j + BLK])])
                     for t in range(TILES) for j in range(2)]
            jobs += [plain(gates[:, t, :], [(x[:, P * t:P * t + P], Wg)], ACT.Sigmoid) for t in range(TILES)]
            products(core, jobs)
            U = B * H16
            first = [0, 4 * P, 7 * P, 9 * P]
            prob = core.buffer(inner, [P, 2, 10 * P], "prob")
            inv = core.buffer(inner, [P, 2, 4], "inverse")
            with core.stage("scores_ready", "tanh_done", "exp_done", "masked", "values_done", "inverted", "head_out") as \
                    (block, scores_ready, tanh_done, exp_done, masked, values_done, inverted, head_out):
                @block.tensor
                def _(pe):
                    def scores(u):
                        b, h = u // H16, u % H16
                        hp, c = slice(D64 * (h % 2), D64 * (h % 2) + D64), h // 2
                        for j in range(4):
                            if u >= 1:
                                pe.wait_ge(tanh_done, 4 * (u - 1) + j + 1)
                            nc.tensor.matmul(core.bank(j)[:, 0:S - P * j], k[hp, c, S * b + P * j:S * b + P * j + P],
                                             q[hp, c, S * b + P * j:S * b + S], start=True, stop=True).then_inc(scores_ready, 1)

                    def values(u):
                        b, h = u // H16, u % H16
                        pe.wait_ge(masked, 4 * (u + 1))
                        if u >= 4:
                            pe.wait_ge(head_out, u - 3)
                        for i in range(4):
                            for j in range(i + 1):
                                mm = nc.tensor.matmul(core.bank(4 + u % 4)[:, (D64 + 1) * i:(D64 + 1) * (i + 1)],
                                                      prob[:, u % 2, first[j] + P * (i - j):first[j] + P * (i - j) + P],
                                                      v[:, 4 * b + j, h, :], start=(j == 0), stop=(j == i))
                        mm.then_inc(values_done, 1)

                    scores(0)
                    for u in range(U):
                        if u + 1 < U:
                            scores(u + 1)
                        values(u)

                @block.scalar
                def _(act):
                    for u in range(U):
                        for j in range(4):
                            act.wait_ge(scores_ready, 4 * u + j + 1)
                            if j == 0 and u >= 2:
                                act.wait_ge(values_done, u - 1)
                            nc.scalar.activation(prob[:, u % 2, first[j]:first[j] + S - P * j], core.bank(j)[:, 0:S - P * j], ACT.Tanh,
                                                 scale=D64 ** -0.5 / CAP).then_inc(tanh_done, 1)
                        act.wait_ge(tanh_done, 4 * (u + 1))
                        nc.scalar.activation(prob[:, u % 2, :], prob[:, u % 2, :], ACT.Exp, scale=CAP).then_inc(exp_done, 1)

                @block.vector
                def _(dve):
                    def finish(u):
                        b, h = u // H16, u % H16
                        out = core.bank(4 + u % 4)[:, 0:4 * (D64 + 1)].rearrange("p (i d) -> p i d", i=4)
                        dve.wait_ge(values_done, u + 1)
                        if u >= 2:
                            dve.wait_ge(head_out, u - 1)
                        r = inv[:, u % 2, :]
                        nc.vector.reciprocal(r.unsqueeze(2), out[:, :, D64:D64 + 1]).then_inc(inverted, 1)
                        dve.wait_ge(inverted, 2 * u + 1)
                        nc.vector.tensor_tensor(r, r, gates[:, 4 * b:4 * b + 4, h], ALU.mult).then_inc(inverted, 1)
                        dve.wait_ge(inverted, 2 * u + 2)
                        nc.vector.tensor_tensor(o[:, 4 * b:4 * b + 4, D64 * h:D64 * h + D64], out[:, :, 0:D64],
                                                r.unsqueeze(2).broadcast_to([P, 4, D64]), ALU.mult).then_inc(head_out, 1)
                    for u in range(U):
                        dve.wait_ge(exp_done, u + 1)
                        for j in range(4):
                            d = prob[:, u % 2, first[j]:first[j] + P]
                            nc.vector.tensor_tensor(d, d, core.const["upper"], ALU.mult).then_inc(masked, 1)
                        if u >= 1:
                            finish(u - 1)
                    finish(U - 1)
        transposes(core, [(q[:, c, P * t:P * t + 4 * P], [o[:, t + i, P * c:P * c + P] for i in range(4)]) for c in range(WC) for t in (0, 4)])
        normalise(core, x, x, XBLOCKS, terms=[(Wo[:, c, :], q[:, c, :]) for c in range(WC)])


def l3_xattn(core):
    nc, io = core.nc, core.io
    x = core.xT
    SCALE = float(np.float32(1.0) / np.sqrt(2 * D64).astype(np.float32))
    KVC, QC = 32, 48
    with ExitStack() as mem:
        sb = lambda shape, name="work": core.buffer(mem, shape, name)
        W = {n: sb(list(io["L3_xattn_" + n].shape), n) for n in ("w_kv_comp", "w_q_down", "w_q_up", "w_q_rope", "w_k_up", "w_k_rope", "w_v_up", "w_out")}
        seg = core.buffer(mem, [P, TILES], "segment", I32)
        core.fetch("l3x", core.consts(mem, "rot", "cos", "sin", "keyno") + [(W[n], io["L3_xattn_" + n]) for n in W]
                   + [(seg, io["segment"])])
        core.need("l3x")
        qn, qr, kn, kr = sb([P, WC, N], "q_nope"), sb([P, WC, N], "q_rope"), sb([P, WC, CT], "k_nope"), sb([P, CT], "k_rope")
        v, kvc, qc, o = sb([KT, 4, INNER], "v"), sb([KVC, CT], "kv_comp"), sb([QC, N], "q_down"), sb([P, TILES, INNER], "o")
        mask, segf = sb([P, TILES, SK], "mask"), sb([P, TILES], "segf")
        products(core, by_block(kvc, W["w_kv_comp"], core.ctx, n=CT) + by_block(qc, W["w_q_down"], x))
        jobs = []
        for c in range(WC):
            jobs += by_block(qn[:, c, :], W["w_q_up"][:, P * c:P * c + P], qc, None, SCALE) + by_block(qr[:, c, :], W["w_q_rope"][:, P * c:P * c + P], qc, None, SCALE)
            jobs += by_block(kn[:, c, :], W["w_k_up"][:, P * c:P * c + P], kvc, n=CT)
        jobs += by_block(kr, W["w_k_rope"], kvc, n=CT)
        jobs += [plain(v[:, i, BLK * j:BLK * j + BLK], [(kvc[:, KT * i:KT * i + KT], W["w_v_up"][:, BLK * j:BLK * j + BLK])]) for i in range(4) for j in range(2)]
        products(core, jobs)
        rotate(core, [(qr[:, c, S * b:S * b + S], core.const["cos"], core.const["sin"], None) for c in range(WC) for b in range(B)]
               + [(kr[:, SK * b:SK * b + SK], core.const["cos"][:, 0:SK], core.const["sin"][:, 0:SK], None) for b in range(B)])
        with core.stage("dve_step") as (block, dve_step):
            @block.vector
            def _(dve):
                link = chained(dve, dve_step)
                link(nc.vector.tensor_copy(segf, seg))
                near = sb([P, TILES, SK], "near")
                link(nc.vector.tensor_tensor(mask, core.const["keyno"].unsqueeze(1).broadcast_to([P, TILES, SK]),
                                             segf.unsqueeze(2).broadcast_to([P, TILES, SK]), ALU.subtract))
                link(nc.vector.tensor_scalar(near, mask, -2.0, None, ALU.is_ge))
                link(nc.vector.tensor_scalar(mask, mask, 0.0, None, ALU.is_le))
                link(nc.vector.tensor_tensor(mask, mask, near, ALU.mult))
                link(nc.vector.tensor_scalar(mask, mask, 1.0, BIG, ALU.subtract, ALU.mult))
        units = []
        for t in range(TILES):
            for h in range(H16):
                c, hp, b = h // 2, slice(D64 * (h % 2), D64 * (h % 2) + D64), t // 4
                units.append((t, h, [(0, qn[hp, c, P * t:P * t + P], kn[hp, c, SK * b:SK * b + SK], True, False),
                                     (0, qr[hp, c, P * t:P * t + P], kr[hp, SK * b:SK * b + SK], False, True)],
                              [v[:, 2 * b + i, D64 * h:D64 * h + D64] for i in range(2)]))
        attend(core, units, XKEYS, D64, lambda t: o[:, t, :], 1.0, range(TILES), lambda u: [(0, SK, mask[:, u[0], :])], nk=SK)
        transposes(core, [(qn[:, c, P * t:P * t + 4 * P], [o[:, t + i, P * c:P * c + P] for i in range(4)]) for c in range(WC) for t in (0, 4)])
        normalise(core, x, x, XBLOCKS, terms=[(W["w_out"][:, c, :], qn[:, c, :]) for c in range(WC)])


def l3_ffn(core):
    nc, io = core.nc, core.io
    x = core.xT
    E, R, O = 16, 64, 512
    with ExitStack() as mem:
        sb = lambda shape, name="work": core.buffer(mem, shape, name)
        F = lambda n: io["L3_ffn_" + n]
        names = {"proj": [P, E], "C": [E, 2, R], "Win1": [P, R], "Wout1": [R, O], "Win2": [P, 4, R], "Wout2": [R, P], "bias": [R, 2]}
        W = {n: sb(s, n) for n, s in names.items()}
        core.fetch("l3f", core.consts(mem, "restart16", "rank", "invrank") + [(W[n], F(n)) for n in W])
        core.need("l3f")
        z, zs, rest, cum, cq, t1, t2 = (sb([P, TILES, E], n) for n in ("z", "sorted", "rest", "mean", "meansq", "work", "tau"))
        m, s1 = sb([P, TILES], "row"), sb([P, TILES], "row2")
        per = lambda a: a.unsqueeze(2).broadcast_to([P, TILES, E])
        flat = lambda a: a.rearrange("p t e -> p (t e)")
        products(core, [plain(z[:, t, :], [(x[:, P * t:P * t + P], W["proj"])]) for t in range(TILES)])
        with core.stage("dve_step", "var_ready", "std_done", "delta_ready", "root_done") as (block, dve_step, var_ready, std_done, delta_ready, root_done):
            @block.vector
            def _(dve):
                link = chained(dve, dve_step)
                link(nc.vector.reduce_sum(m, z, AX))
                link(nc.vector.tensor_scalar(m, m, 1.0 / E, None, ALU.mult))
                link(nc.vector.tensor_tensor(z, z, per(m), ALU.subtract))
                link(nc.vector.tensor_tensor(t1, z, z, ALU.mult))
                link(nc.vector.reduce_sum(m, t1, AX))
                nc.vector.tensor_scalar(m, m, 1.0 / E, None, ALU.mult).then_inc(var_ready, 1)
                dve.wait_ge(std_done, 1)
                link(nc.vector.reciprocal(m, m))
                link(nc.vector.tensor_tensor(z, z, per(m), ALU.mult))
                link(nc.vector.tensor_scalar(z, z, 0.5, None, ALU.mult))
                link(nc.vector.reduce_max(m, z, AX))
                link(nc.vector.tensor_tensor(z, z, per(m), ALU.subtract))
                for t in range(TILES):
                    link(nc.vector.max(zs[:, t, 0:8], z[:, t, :]))
                for t in range(TILES):
                    link(nc.vector.match_replace(rest[:, t, :], zs[:, t, 0:8], z[:, t, :], -BIG))
                for t in range(TILES):
                    link(nc.vector.max(zs[:, t, 8:16], rest[:, t, :]))
                link(nc.vector.tensor_tensor(t1, zs, zs, ALU.mult))
                link(nc.vector.tensor_tensor_scan(flat(cum), core.const["restart16"], flat(zs), 0.0, ALU.mult, ALU.add))
                link(nc.vector.tensor_tensor_scan(flat(cq), core.const["restart16"], flat(t1), 0.0, ALU.mult, ALU.add))
                link(nc.vector.tensor_tensor(flat(cum), flat(cum), core.const["invrank"], ALU.mult))
                link(nc.vector.tensor_tensor(flat(cq), flat(cq), core.const["invrank"], ALU.mult))
                link(nc.vector.tensor_tensor(t1, cum, cum, ALU.mult))
                link(nc.vector.tensor_tensor(t1, cq, t1, ALU.subtract))
                link(nc.vector.tensor_tensor(flat(t1), flat(t1), core.const["rank"], ALU.mult))
                link(nc.vector.tensor_scalar(t1, t1, -1.0, 1.0, ALU.mult, ALU.add))
                link(nc.vector.tensor_tensor(flat(t1), flat(t1), core.const["invrank"], ALU.mult))
                nc.vector.tensor_scalar(t1, t1, 0.0, None, ALU.max).then_inc(delta_ready, 1)
                dve.wait_ge(root_done, 1)
                link(nc.vector.tensor_tensor(t2, cum, t1, ALU.subtract))
                link(nc.vector.tensor_tensor(t1, t2, zs, ALU.is_le))
                link(nc.vector.reduce_sum(m, t1, AX))
                link(nc.vector.tensor_tensor(t1, core.const["rank"].rearrange("p (t e) -> p t e", e=E), per(m), ALU.is_equal))
                link(nc.vector.tensor_tensor(t1, t1, t2, ALU.mult))
                link(nc.vector.reduce_sum(m, t1, AX))
                link(nc.vector.tensor_tensor(z, z, per(m), ALU.subtract))
                link(nc.vector.tensor_scalar(z, z, 0.0, None, ALU.max))
                link(nc.vector.tensor_tensor(z, z, z, ALU.mult))

            @block.scalar
            def _(act):
                act.wait_ge(var_ready, 1)
                nc.scalar.activation(m, m, ACT.Sqrt, bias=core.const["cols"][:, 0:1]).then_inc(std_done, 1)
                act.wait_ge(delta_ready, 1)
                nc.scalar.activation(t1, t1, ACT.Sqrt).then_inc(root_done, 1)
        aT, g, z1, h, z2 = sb([E, N], "weights"), sb([R, 2, N], "gates"), sb([R, N], "z1"), sb([P, 4, N], "h"), sb([R, N], "z2")
        transposes(core, [(aT[:, P * t:P * t + 4 * P], [z[:, t + i, :] for i in range(4)]) for t in (0, 4)])
        products(core, by_block(g[:, 0, :], W["C"][:, 0, :], aT) + by_block(g[:, 1, :], W["C"][:, 1, :], aT)
                 + by_block(z1, W["Win1"], x, None, 1.0, W["bias"][:, 0:1]))

        def gated(a, i):
            with core.stage("gated") as (block, done):
                @block.vector
                def _(dve):
                    nc.vector.tensor_tensor(a, a, g[:, i, :], ALU.mult).then_inc(done, 1)
        gated(z1, 0)
        products(core, [j for c in range(4) for j in by_block(h[:, c, :], W["Wout1"][:, P * c:P * c + P], z1, ACT.Gelu)])
        products(core, [plain(z2[:, BLK * n:BLK * n + BLK], [(W["Win2"][:, c, :], h[:, c, BLK * n:BLK * n + BLK]) for c in range(4)], None, 1.0, W["bias"][:, 1:2])
                        for n in range(NB)])
        gated(z2, 1)
        normalise(core, x, x, XBLOCKS, terms=[(W["Wout2"], z2)])


def turn_tokens(core, dstT, src):
    transposes(core, [(dstT[:, P * t:P * t + 4 * P], [src[:, t + i, :] for i in range(4)]) for t in range(0, src.shape[1], 4)])


def network(nc, io, depth=99):
    core = Core(nc, io)
    with ExitStack() as mem:
        sb = lambda shape, name="work": core.buffer(mem, shape, name)
        core.xT = sb([P, N])
        core.ctx = sb([P, CT])
        c = {n: sb(list(io["c_" + n].shape)) for n in ("ident", "mean", "head64", "cols")}
        for n, t in c.items():
            core.const[n] = t
        with nc.sbuf_tensor("x_tok", [P, TILES, P], F32) as x_tok, nc.sbuf_tensor("c_tok", [KT, 4, P], F32) as c_tok:
            load(core, [(c[n][:], io["c_" + n]) for n in c] + [
                (x_tok[:], io["x"].rearrange("b (t p) f -> p (b t) f", p=P)),
                (c_tok[:], io["ctx_1024"].rearrange("b (t p) f -> p (b t) f", p=KT))])
            turn_tokens(core, core.xT, x_tok)
            transposes(core, [(core.ctx[:], [c_tok[:, i, :] for i in range(4)])])

        def consts(m, *names):
            ts = {n: core.buffer(m, io["c_" + n].shape, n) for n in names}
            for n, t in ts.items():
                core.const[n] = t
            return [(t[:], io["c_" + n]) for n, t in ts.items()]
        core.consts = consts

        for i, layer in enumerate(LAYERS[:depth]):
            layer(core)

        with nc.sbuf_tensor("y_tok", [P, TILES, P], F32) as y:
            transposes(core, [(y[:, t:t + 4, :], [core.xT[:, P * (t + i):P * (t + i) + P] for i in range(4)]) for t in (0, 4)])
            with core.stage("stored") as (block, stored):
                @block.sync
                def _(sp):
                    sp.dma_start(io["out"].rearrange("b (t p) f -> p (b t) f", p=P), y[:]).then_inc(stored, 16)
                    sp.wait_ge(stored, 16)


LAYERS = [l0_attn, l0_xattn, l0_ffn, l1_attn, l1_xattn, l1_ffn, l2_attn, l2_xattn, l2_ffn, l3_attn, l3_xattn, l3_ffn]


def layouts(inputs):
    a = {n: np.asarray(v) for n, v in inputs.items()}
    i = {"x": a["x"], "ctx_1024": a["ctx_1024"]}
    L = lambda n: a["L0_attn_" + n]
    i["mix"] = np.stack([L("x_" + n)[0, 0] for n in "rwkvag"], 1)
    i["vec"] = np.stack([L(n)[0, 0] for n in ("w0", "a0", "v0", "k_k", "k_a")] + [L("r_k").reshape(P)], 1)
    i["down"] = np.concatenate([L("w1"), L("a1"), L("v1")], 1)
    i["up"] = np.stack([L("w2"), L("a2"), np.concatenate([L("v2"), np.zeros((32, P), np.float32)])], 1)
    for n in ("Wr", "Wk", "Wv", "Wo", "g1", "g2", "ln_w", "ln_b"):
        i["L0_attn_" + n] = L(n)
    i["mask"] = a["mask_BxS2_bk0"].astype(np.int32)
    X = lambda n: a["L0_xattn_" + n]
    for n in ("W_q", "W_kv", "W_out"):
        i["L0_xattn_" + n] = X(n)
    i["L0_xattn_vec"] = np.stack([X("ln_x_g"), X("ln_x_b"), X("ln_l_g"), X("ln_l_b"), np.concatenate([X("q_gamma")] * 2),
                                  np.concatenate([X("k_gamma")] * 2), X("b_out")], 1)
    F = lambda n: a["L0_ffn_" + n]
    i["L0_ffn_router"], i["L0_ffn_router_bias"] = F("router_w").T, F("router_bias")
    i["L0_ffn_gate"] = np.concatenate([F("gate_w"), F("sgate_w").reshape(4, P, P)], 0).transpose(2, 0, 1)
    i["L0_ffn_up"] = np.concatenate([F("up_w"), F("sup_w").reshape(4, P, P)], 0).transpose(2, 0, 1)
    i["L0_ffn_down"] = np.concatenate([F("down_w"), F("sdown_w").reshape(P, 4, P).transpose(1, 0, 2)], 0).transpose(2, 0, 1)
    for n in ("w_Q", "w_K", "w_V"):
        i["L1_attn_" + n] = a["L1_attn_" + n]
    for l in ("L1_xattn_", "L2_xattn_"):
        for n in ("Wq", "Wk", "Wv", "Wo", "bv"):
            i[l + n] = a[l + n]
        i[l + "vec"] = np.stack([a[l + n] for n in ("bq", "bk", "bo")], 1)
    F = lambda n: a["L1_ffn_" + n]
    chunks = lambda w: w.reshape(*w.shape[:-2], WC, P, P).swapaxes(-3, -2)
    pad = lambda w, n, axis: np.concatenate([w, np.zeros(w.shape[:axis] + (n - w.shape[axis],) + w.shape[axis + 1:], w.dtype)], axis)
    i["L1_ffn_Wqkv"], i["L1_ffn_Wo"], i["L1_ffn_W1"] = F("Wqkv"), chunks(F("Wo")), F("W1")
    i["L1_ffn_W2"] = pad(F("W2"), 3 * P, 1).reshape(DEPTH, 3, P, P).transpose(0, 2, 1, 3)
    b1 = pad(F("b1").reshape(DEPTH, 2, DI), 3 * P, 2).reshape(DEPTH, 6, P).transpose(0, 2, 1)
    i["L1_ffn_vec"] = np.concatenate([np.stack([np.tile(F("q_scale"), 2), np.tile(F("k_scale"), 2), F("ln_g"), F("ln_b"), F("b2")], 2), b1], 2)
    A = lambda n: a["L2_attn_" + n]
    i["L2_attn_W"], i["L2_attn_Wo"] = A("in_proj_weight").T, A("out_w").T
    bias = A("in_proj_bias").reshape(3, P)
    i["L2_attn_vec"], i["L2_attn_bv"] = np.stack([bias[0], bias[1], A("out_b")], 1), bias[2]
    i["L2_attn_rel"] = np.tile(A("rel_pe")[np.clip(np.arange(EXT) - (P - 1), 0, 2 * REL)].T, (H16, 1))
    i["L2_ffn_W"] = a["L2_ffn_W_experts"].transpose(2, 0, 1)
    i["L2_ffn_router"], i["L2_ffn_b_router"], i["L2_ffn_b_experts"] = a["L2_ffn_W_router"].T, a["L2_ffn_b_router"], a["L2_ffn_b_experts"]
    i["L3_attn_w_qkv"], i["L3_attn_w_gates"], i["L3_attn_w_out"] = a["L3_attn_w_qkv"], a["L3_attn_w_gates"], chunks(a["L3_attn_w_out"])
    for n in ("w_kv_comp", "w_q_down", "w_q_up", "w_q_rope", "w_k_up", "w_v_up"):
        i["L3_xattn_" + n] = a["L3_xattn_" + n]
    i["L3_xattn_w_k_rope"] = np.concatenate([a["L3_xattn_w_k_rope"]] * 2, 1)
    i["L3_xattn_w_out"] = chunks(a["L3_xattn_w_out"])
    i["segment"] = a["itok_BxS_0_511"].reshape(TILES, P).T
    F3 = lambda n: a["L3_ffn_" + n]
    i["L3_ffn_proj"], i["L3_ffn_C"] = F3("proj"), np.stack([F3("C1"), F3("C2")], 1)
    i["L3_ffn_Win1"], i["L3_ffn_Wout1"], i["L3_ffn_Wout2"] = F3("Win1")[:P], F3("Wout1").T, F3("Wout2").T
    i["L3_ffn_Win2"] = F3("Win2")[:512].reshape(4, P, 64).transpose(1, 0, 2)
    i["L3_ffn_bias"] = np.stack([F3("Win1")[P], F3("Win2")[512]], 1)
    i.update({"c_" + n: v for n, v in shape_constants().items()})
    return {n: np.ascontiguousarray(v) for n, v in i.items()}


def build(nc, arrays, depth=99):
    io = {n: nc.dram_tensor("in_" + n, v.shape, mybir.dt.from_np(v.dtype), kind="ExternalInput").ap()
          for n, v in arrays.items()}
    io["out"] = nc.dram_tensor("out", (B, S, P), F32, kind="ExternalOutput").ap()
    network(nc, io, depth)


def kernel(**inputs):
    import concourse.bacc as bacc
    from concourse.bass_utils import run_bass_kernel_spmd

    arrays = layouts(inputs)
    nc = bacc.Bacc("TRN2", target_bir_lowering=False, num_devices=1)
    build(nc, arrays)
    result = run_bass_kernel_spmd(nc, [{"in_" + n: v for n, v in arrays.items()}], core_ids=[0])
    return result.results[0]["out"]
```

```python
from contextlib import ExitStack, contextmanager

import numpy as np

import concourse.bass as bass
from concourse import mybir

F32 = mybir.dt.float32
I32 = mybir.dt.int32
BF16 = mybir.dt.bfloat16
ALU = mybir.AluOpType
ACT = mybir.ActivationFunctionType
AX = mybir.AxisListType.X

P = 128
B = 2
S = 512
N = B * S
TILES = N // P
SK = 154
KT = 77
CT = B * SK
BIG = 3.0e37
BLK = 512
NB = N // BLK
LN_EPS = 1e-5
H16, D8 = 16, 8
D64 = 64
INNER = 1024
WC = INNER // P
DEPTH = 6
DI = 341
WIN = 32
REL = 64
WROWS = 96
STARTS = [0, 96, 192, 288, 384, 416]
WINDOWS = len(STARTS)
EXT = 384


def shape_constants():
    p = np.arange(P)
    c = {}
    c["ident"] = np.eye(P)
    c["mean"] = np.full((P, P), 1.0 / P)
    c["head64"] = (p[:, None] // D64 == p[None, :] // D64) * 1.0
    c["headmask"] = (p[:, None] // D8 == np.arange(H16)[None, :]) * 1.0
    c["pick2"] = (p[:, None] // D64 == np.arange(2)[None, :]) * 1.0
    up = np.zeros((P, 2, WC, 2 * H16))
    for side in range(2):
        for k in range(WC):
            for q in range(P):
                up[q, side, k, H16 * side + 2 * k + q // D64] = 1.0
    c["toheads"] = up.reshape(P, 2 * WC, 2 * H16)
    c["fromheads"] = up.reshape(P, 2 * WC, 2 * H16).transpose(2, 1, 0)
    c["modulo32"] = (p[:96, None] % 32 == np.arange(32)[None, :]) * 1.0
    rot = np.zeros((P, P))
    for h in range(2):
        for d in range(32):
            rot[64 * h + 32 + d, 64 * h + d] = -1.0
            rot[64 * h + d, 64 * h + 32 + d] = 1.0
    c["rot"] = rot
    half = np.arange(0, D64, 2, dtype=np.float64)
    inv = (1.0 / 10000.0 ** (half / D64)).astype(np.float32)
    t = np.arange(S, dtype=np.float32)
    fr = (t[:, None] * inv[None, :]).astype(np.float32).astype(np.float64)
    base = (half + 0.4 * D64) / (1.4 * D64)
    sc = base[None, :] ** ((t[:, None] - S // 2) / (WIN // 2))
    def rotary(scale):
        a = np.stack([np.concatenate([np.cos(fr)] * 2, 1), np.concatenate([-np.sin(fr), np.sin(fr)], 1)], 1)
        return (a * np.concatenate([scale, scale], 1)[:, None, :]).reshape(4, P, 2, D64).transpose(1, 0, 2, 3)
    c["rotary"] = rotary(np.ones_like(sc))
    c["xpos"] = np.stack([rotary(sc), rotary(1.0 / sc)], 1)
    wide = lambda a: np.concatenate([a, a, a, a], 1).T
    c["cos"], c["sin"] = wide(np.cos(fr))[:, :SK], wide(np.sin(fr))[:, :SK]
    i, j = np.arange(WROWS)[:, None], np.arange(P)[None, :]
    band = (j >= i) & (j <= i + WIN)
    c["band"] = np.stack([np.where(band & (j >= WIN), 0, -BIG), np.where(band, 0, -BIG)], 1)
    c["slide"] = np.concatenate([np.zeros((P, WROWS)), np.eye(P), np.zeros((P, WROWS))], 1)
    i = p[:, None]
    k = np.arange(SK)[None, :]
    c["xcausal"] = np.stack([np.where(k <= i, 0, -BIG), np.where(k <= i + P, 0, -BIG)], 1)
    c["keyno"] = np.broadcast_to(k * 1.0, (P, SK))
    c["upper"] = (p[:, None] <= p[None, :]) * 1.0
    c["supper"] = (p[:, None] < p[None, :]) * 1.0
    lv = []
    for m in (1, 2, 4, 8, 16, 32, 64):
        same = p[:, None] // (2 * m) == p[None, :] // (2 * m)
        lv.append(same * (p[:, None] % (2 * m) < m) * (p[None, :] % (2 * m) >= m) * 1.0)
    c["levels"] = np.stack(lv, 1)
    c["restart128"] = np.broadcast_to((np.arange(N) % P != 0) * 1.0, (P, N))
    c["restart16"] = np.broadcast_to((p % 16 != 0) * 1.0, (P, P))
    c["rank"] = np.broadcast_to(p % 16 + 1.0, (P, P))
    c["invrank"] = np.broadcast_to(1.0 / (p % 16 + 1.0), (P, P))
    c["cols"] = np.broadcast_to(np.array([LN_EPS, 6.4e-4, 1.0, 0.0]), (P, 4))
    return {n: np.ascontiguousarray(a, dtype=np.float32) for n, a in c.items()}


class Core:

    def __init__(self, nc, io):
        self.nc, self.io = nc, io
        self.ps = nc.alloc_psum_tensor("ps", [P, 8, BLK], F32)
        self.stale = []
        self.const = {}
        self.count = 0
        self.orders = []
        self.fetched = {}

    def buffer(self, mem, shape, name="work", dtype=F32):
        self.count += 1
        return mem.enter_context(self.nc.sbuf_tensor(f"{name}_{self.count}", list(shape), dtype))[:]

    def bank(self, i, n=1):
        return self.ps[:, i:i + n, :].rearrange("p b c -> p (b c)")

    @contextmanager
    def stage(self, *names):
        nc = self.nc
        self.count += 1
        sems = [nc.alloc_semaphore(f"{n}_{self.count}") for n in names]
        stale, self.stale = self.stale, []
        with nc.Block(no_gpsimd_drain=True) as block:
            orders, self.orders = self.orders, []
            if orders:
                @block.sync
                def _(sp):
                    for tag, dst, src in orders:
                        sp.dma_start(dst, src).then_inc(self.fetched[tag][0], 16)
            if stale:
                @block.gpsimd
                def _(pool):
                    for s in stale:
                        pool.sem_clear(s)
            yield (block, *sems)
        for s in stale:
            nc.release_semaphore(s)
        self.stale = sems

    def fetch(self, tag, pairs):
        self.fetched[tag] = (self.nc.alloc_semaphore("fetched_" + tag), 16 * len(pairs))
        self.orders += [(tag, dst, src) for dst, src in pairs]

    def need(self, *tags, zeros=()):
        with self.stage("cleared_by_dve", "cleared_by_pool") as (block, by_dve, by_pool):
            if zeros:
                @block.vector
                def _(dve):
                    for a in zeros[0::2]:
                        self.nc.vector.memset(a, 0.0).then_inc(by_dve, 1)

                @block.gpsimd
                def _(pool):
                    for a in zeros[1::2]:
                        self.nc.gpsimd.memset(a, 0.0).then_inc(by_pool, 1)
                    pool.wait_ge(by_pool, len(zeros[1::2]))

            @block.sync
            def _(sp):
                for tag in tags:
                    sp.wait_ge(*self.fetched[tag])

    def settle(self):
        with self.stage():
            pass


def chained(eng, sem):
    done = [0]

    def link(ins):
        done[0] += 1
        ins.then_inc(sem, 1)
        eng.wait_ge(sem, done[0])
    return link


def load(core, pairs):
    with core.stage("loaded_by_sync", "loaded_by_act") as (block, by_sync, by_act):
        @block.sync
        def _(sp):
            for dst, src in pairs[0::2]:
                sp.dma_start(dst, src).then_inc(by_sync, 16)
            sp.wait_ge(by_sync, 16 * len(pairs[0::2]))

        if pairs[1::2]:
            @block.scalar
            def _(act):
                for dst, src in pairs[1::2]:
                    act.dma_start(dst, src).then_inc(by_act, 16)
                act.wait_ge(by_act, 16 * len(pairs[1::2]))


def load_meanwhile(block, loaded, pairs):
    @block.sync
    def _(sp):
        for dst, src in pairs:
            sp.dma_start(dst, src).then_inc(loaded, 16)
        sp.wait_ge(loaded, 16 * len(pairs))


def products(core, jobs, ring=8):
    nc = core.nc
    by_act = [j % 2 == 0 or jobs[j][2] is not None for j in range(len(jobs))]
    acts = lambda j: sum(by_act[:j + 1])
    dves = lambda j: j + 1 - acts(j)

    def halves(j):
        out = jobs[j][0]
        return list(zip(out, (spot(j)[0:D64], spot(j)[D64:P]))) if isinstance(out, tuple) else [(out, spot(j))]

    def spot(j):
        out = jobs[j][0]
        if isinstance(out, tuple):
            return core.bank(j % ring)[:, 0:out[0].shape[-1]]
        m, n = out.shape[0], int(np.prod(out.shape[1:]))
        v = core.bank(j % ring)[0:m, 0:n]
        if len(out.shape) == 3:
            v = v.rearrange("p (a b) -> p a b", a=out.shape[1])
        return v

    with core.stage("product_done", "emptied_by_act", "emptied_by_dve") as (block, product_done, emptied_a, emptied_v):
        @block.tensor
        def _(pe):
            for j, (out, terms, *_) in enumerate(jobs):
                if j >= ring:
                    if by_act[j - ring]:
                        pe.wait_ge(emptied_a, acts(j - ring))
                    else:
                        pe.wait_ge(emptied_v, dves(j - ring))
                for k, (lhsT, rhs) in enumerate(terms):
                    mm = nc.tensor.matmul(spot(j), lhsT, rhs, start=(k == 0), stop=(k == len(terms) - 1))
                mm.then_inc(product_done, 1)

        @block.scalar
        def _(act):
            for j, (out, terms, func, scale, bias) in enumerate(jobs):
                if by_act[j]:
                    act.wait_ge(product_done, j + 1)
                    for dst, src in halves(j):
                        ins = nc.scalar.activation(dst, src, func or ACT.Identity, scale=scale, bias=0.0 if bias is None else bias)
                    ins.then_inc(emptied_a, 1)

        @block.vector
        def _(dve):
            for j, (out, terms, func, scale, bias) in enumerate(jobs):
                if not by_act[j]:
                    dve.wait_ge(product_done, j + 1)
                    for dst, src in halves(j):
                        if bias is None:
                            ins = nc.vector.tensor_scalar(dst, src, scale, None, ALU.mult)
                        else:
                            ins = nc.vector.tensor_scalar(dst, src, scale, bias, ALU.mult, ALU.add)
                    ins.then_inc(emptied_v, 1)


def transposes(core, jobs, ring=8):
    nc = core.nc

    def spot(j, k):
        a = jobs[j][1][k]
        w = a.shape[0]
        return core.bank(j % ring)[0:a.shape[1], w * k:w * k + w]

    def whole(j):
        out, ins = jobs[j]
        v = core.bank(j % ring)[0:out.shape[0], 0:len(ins) * ins[0].shape[0]]
        if len(out.shape) == 3:
            v = v.rearrange("p (a b) -> p a b", a=out.shape[1])
            if len(ins) == out.shape[1]:
                v = v[:, :, ins[0].shape[0] - out.shape[2]:]
        return v

    with core.stage("turned", "copied_by_act", "copied_by_dve") as (block, turned, copied_a, copied_v):
        @block.tensor
        def _(pe):
            for j, (out, ins) in enumerate(jobs):
                if j >= ring:
                    pe.wait_ge(copied_v if j % 2 else copied_a, (j - ring) // 2 + 1)
                for k, a in enumerate(ins):
                    mm = nc.tensor.transpose(spot(j, k), a, core.const["ident"][0:a.shape[0], 0:a.shape[0]])
                mm.then_inc(turned, 1)

        @block.scalar
        def _(act):
            for j in range(0, len(jobs), 2):
                act.wait_ge(turned, j + 1)
                nc.scalar.copy(jobs[j][0], whole(j)).then_inc(copied_a, 1)

        if len(jobs) > 1:
            @block.vector
            def _(dve):
                for j in range(1, len(jobs), 2):
                    dve.wait_ge(turned, j + 1)
                    nc.vector.tensor_copy(jobs[j][0], whole(j)).then_inc(copied_v, 1)


def normalise(core, src, dst, blocks, gain=None, shift=None, terms=None, bias=None, relu_eps=None):
    nc = core.nc
    eps = core.const["cols"][:, 0:1]
    with ExitStack() as mem:
        width = sum(b - a for a, b in blocks)
        centred = core.buffer(mem, [P, width])
        square = core.buffer(mem, [P, width])
        block, projected, summed, mean_done, centred_done, squared, var_done, rooted, dve_step, normed = \
            mem.enter_context(core.stage("projected", "residual_added", "mean_done", "centred", "squared", "var_done",
                                         "std_done", "dve_step", "normed"))

        def cols(t, k):
            a, b = blocks[k]
            return t[:, a:b]

        def own(t, k):
            a = blocks[0][0]
            return t[:, blocks[k][0] - a:blocks[k][1] - a]

        def bank(k, what):
            return core.bank(3 * (k % 2) + what)[:, 0:blocks[k][1] - blocks[k][0]]

        @block.tensor
        def _(pe):
            for k in range(len(blocks)):
                if k >= 2:
                    pe.wait_ge(normed, k - 1)
                if terms:
                    for i, (lhsT, rhs) in enumerate(terms):
                        mm = nc.tensor.matmul(bank(k, 0), lhsT, columns(rhs, *blocks[k]), start=(i == 0), stop=(i == len(terms) - 1))
                    mm.then_inc(projected, 1)
            for k in range(len(blocks)):
                if terms:
                    pe.wait_ge(summed, k + 1)
                nc.tensor.matmul(bank(k, 1), core.const["mean"][:], cols(src, k), start=True, stop=True).then_inc(mean_done, 1)
            for k in range(len(blocks)):
                pe.wait_ge(squared, k + 1)
                nc.tensor.matmul(bank(k, 2), core.const["mean"][:], own(square, k), start=True, stop=True).then_inc(var_done, 1)

        @block.scalar
        def _(act):
            for k in range(len(blocks)):
                act.wait_ge(centred_done, k + 1)
                nc.scalar.activation(own(square, k), own(centred, k), ACT.Square).then_inc(squared, 1)
            for k in range(len(blocks)):
                act.wait_ge(var_done, k + 1)
                nc.scalar.activation(own(square, k), bank(k, 2), ACT.Sqrt, bias=eps).then_inc(rooted, 1)

        @block.vector
        def _(dve):
            link = chained(dve, dve_step)
            if terms:
                for k in range(len(blocks)):
                    dve.wait_ge(projected, k + 1)
                    if bias is None:
                        nc.vector.tensor_tensor(cols(src, k), bank(k, 0), cols(src, k), ALU.add).then_inc(summed, 1)
                    else:
                        nc.vector.scalar_tensor_tensor(cols(src, k), bank(k, 0), bias, cols(src, k), ALU.add, ALU.add) \
                            .then_inc(summed, 1)
                dve.wait_ge(summed, len(blocks))
            for k in range(len(blocks)):
                dve.wait_ge(mean_done, k + 1)
                nc.vector.tensor_tensor(own(centred, k), cols(src, k), bank(k, 1), ALU.subtract).then_inc(centred_done, 1)
            dve.wait_ge(centred_done, len(blocks))
            for k in range(len(blocks)):
                dve.wait_ge(rooted, k + 1)
                link(nc.vector.reciprocal(own(square, k), own(square, k)))
                ins = nc.vector.tensor_tensor(cols(dst, k), own(centred, k), own(square, k), ALU.mult)
                if gain is not None:
                    link(ins)
                    ins = nc.vector.tensor_scalar(cols(dst, k), cols(dst, k), gain, shift, ALU.mult, ALU.add)
                ins.then_inc(normed, 1)


XBLOCKS = [(0, BLK), (BLK, N)]


def attend(core, units, keytiles, out_width, outs, scale, parts_of=None, nk=None, lead=0, stream=None, scale_of=None,
           meanwhile=(), R=P, act_copies=True):
    nc = core.nc
    heads = len([u for u in units if u[0] == units[0][0]])
    kt = len(keytiles)
    G = max(g for g in (1, 2, 4) if g == 1 or (g * nk <= BLK and g * kt * R <= BLK))
    groups = [units[i:i + G] for i in range(0, len(units), G)]
    n = len(groups)
    sb = -(-G * nk // BLK)
    tb = -(-G * kt * R // BLK)
    SR, TR = (3, 3) if sb == 1 else (2, 1)
    RING = 3
    ahead = SR - 1
    hb = min(heads, BLK // out_width)
    per = hb // G
    full = len([k for _, k in keytiles if k == P])
    runs = [(0, kt, keytiles[0][1])] if full in (0, kt) else [(0, full, P), (full, kt, keytiles[-1][1])]

    def score(i):
        return core.bank((i % SR) * sb, sb)[0:R, 0:G * nk].rearrange("p (g k) -> p g k", g=G)

    def turned_at(i):
        return core.bank(SR * sb + (i % TR) * tb, tb)[:, 0:G * kt * R].rearrange("p (g k) -> p g k", g=G)

    def outp(block):
        return core.bank(6 + block % 2)[0:R, 0:hb * out_width].rearrange("p (h d) -> p h d", h=hb)

    with ExitStack() as mem:
        prob = core.buffer(mem, [R, RING, G, lead + nk], "prob")
        turned = core.buffer(mem, [P, RING, G, kt * R], "turned")
        top = core.buffer(mem, [R, RING, 2, G], "top")
        tops = core.buffer(mem, [R, 4], "tops")
        masked = core.buffer(mem, [R, RING, G, nk], "masked") if parts_of else None
        sums = core.buffer(mem, [R, 2, hb], "sums")
        block, scores_ready, max_found, max_negated, probs_ready, probs_turned, copied_v, copied_a, values_done, \
            sums_inverted, block_out, lead_cleared, parts_added, *streamed, loaded = mem.enter_context(core.stage(
                "scores_ready", "max_found", "max_negated", "probs_ready", "probs_turned", "turned_copied_dve",
                "turned_copied_act", "values_done", "sums_inverted", "block_out", "lead_cleared", "parts_added",
                "streamed_even", "streamed_odd", "loaded"))

        def copies_on_act(i):
            return act_copies and i % 2 == 1

        def copied(eng, i):
            if act_copies:
                eng.wait_ge(copied_a if i % 2 else copied_v, i // 2 + 1)
            else:
                eng.wait_ge(copied_v, i + 1)

        def spread(eng, copy, done, i):
            eng.wait_ge(probs_turned, i + 1)
            if i >= RING:
                eng.wait_ge(values_done, i - RING + 1)
            for a, b, m in runs:
                ins = copy(turned[0:m, i % RING, :, R * a:R * b], turned_at(i)[0:m, :, R * a:R * b])
            ins.then_inc(done, 1)

        if meanwhile:
            load_meanwhile(block, loaded, meanwhile)

        if stream:
            @block.sync
            def _(sp):
                for t in range(n * G // heads):
                    if t >= 2:
                        sp.wait_ge(max_found, heads // G * (t - 1))
                    for dst, src in stream(t):
                        sp.dma_start(dst, src).then_inc(streamed[t % 2], 16)

        @block.tensor
        def _(pe):
            def scores(i):
                if i >= SR:
                    pe.wait_ge(probs_ready, i - SR + 1)
                for g, (t, h, terms, _) in enumerate(groups[i]):
                    for col, lhsT, rhs, first, last in terms:
                        mm = nc.tensor.matmul(score(i)[:, g, col:col + rhs.shape[-1]], lhsT, rhs, start=first, stop=last)
                mm.then_inc(scores_ready, 1)

            def turn(i):
                pe.wait_ge(probs_ready, i + 1)
                if i >= TR:
                    copied(pe, i - TR)
                for g in range(G):
                    for k, (a, m) in enumerate(keytiles):
                        mm = nc.tensor.transpose(turned_at(i)[0:m, g, R * k:R * k + R], prob[:, i % RING, g, a:a + m],
                                                 core.const["ident"][0:R, 0:R])
                mm.then_inc(probs_turned, 1)

            def values(i):
                copied(pe, i)
                if i % per == 0 and i // per >= 2:
                    pe.wait_ge(block_out, i // per - 1)
                for g, (t, h, _, vals) in enumerate(groups[i]):
                    for k, (a, m) in enumerate(keytiles):
                        mm = nc.tensor.matmul(outp(i // per)[:, h % hb, :], turned[0:m, i % RING, g, R * k:R * k + R], vals[k],
                                              start=(k == 0), stop=(k == kt - 1))
                mm.then_inc(values_done, 1)

            for i in range(ahead):
                scores(i)
            for i in range(n):
                if i + ahead < n:
                    scores(i + ahead)
                turn(i)
                if i >= 1:
                    values(i - 1)
            values(n - 1)

        @block.scalar
        def _(act):
            for i in range(n):
                act.wait_ge(max_negated, i + 1)
                if i >= RING:
                    act.wait_ge(probs_turned, i - RING + 1)
                if i % per == 0 and i // per >= 2:
                    act.wait_ge(block_out, i // per - 1)
                for g, unit in enumerate(groups[i]):
                    src = masked[:, i % RING, g, :] if parts_of and parts_of(unit) else score(i)[:, g, :]
                    ins = nc.scalar.activation(prob[:, i % RING, g, lead:], src, ACT.Exp, bias=top[:, i % RING, 1, g:g + 1],
                                               scale=scale_of(groups[i])[:, g:g + 1] if scale_of else scale,
                                               accum_out=sums[:, i // per % 2, unit[1] % hb:unit[1] % hb + 1])
                ins.then_inc(probs_ready, 1)
                if i >= ahead and copies_on_act(i - ahead):
                    spread(act, nc.scalar.copy, copied_a, i - ahead)
            for i in range(n - ahead, n):
                if copies_on_act(i):
                    spread(act, nc.scalar.copy, copied_a, i)

        @block.vector
        def _(dve):
            def finish(k):
                dve.wait_ge(probs_ready, per * (k + 1))
                nc.vector.reciprocal(sums[:, k % 2, :], sums[:, k % 2, :]).then_inc(sums_inverted, 1)
                dve.wait_ge(sums_inverted, k + 1)
                dve.wait_ge(values_done, per * (k + 1))
                t, h = groups[per * k][0][0], groups[per * k][0][1] // hb * hb
                out = outs(t)[:, h * out_width:(h + hb) * out_width].rearrange("p (h d) -> p h d", h=hb)
                nc.vector.tensor_tensor(out, outp(k), sums[:, k % 2, :].unsqueeze(2).broadcast_to([R, hb, out_width]), ALU.mult) \
                    .then_inc(block_out, 1)

            added = 0
            if lead:
                nc.vector.memset(prob[:, :, :, 0:lead], 0.0).then_inc(lead_cleared, 1)
                dve.wait_ge(lead_cleared, 1)
            for i in range(n):
                dve.wait_ge(scores_ready, i + 1)
                if i >= RING:
                    dve.wait_ge(probs_ready, i - RING + 1)
                tile = i * G // heads
                if stream and i * G % heads == 0:
                    dve.wait_ge(streamed[tile % 2], 16 * len(stream(0)) * (tile // 2 + 1))
                best = top[:, i % RING, 0, :]
                if not (parts_of and parts_of(groups[i][0])):
                    ins = nc.vector.reduce_max(best, score(i), AX)
                else:
                    for g, unit in enumerate(groups[i]):
                        parts = parts_of(unit)
                        for k, (a, b, what) in enumerate(parts):
                            to = best[:, g:g + 1] if len(parts) == 1 else tops[:, k:k + 1]
                            into = masked[:, i % RING, g, a:b]
                            if what.shape[-1] == 1:
                                ins = nc.vector.tensor_scalar(into, score(i)[:, g, a:b], what, -BIG, ALU.add, ALU.max, accum_out=to)
                            else:
                                ins = nc.vector.tensor_tensor_reduce(into, score(i)[:, g, a:b], what, 1.0, -BIG, ALU.add, ALU.max, to)
                            if len(parts) > 1:
                                ins.then_inc(parts_added, 1)
                                added += 1
                        if len(parts) > 1:
                            dve.wait_ge(parts_added, added)
                            ins = nc.vector.reduce_max(best[:, g:g + 1], tops[:, 0:len(parts)], AX)
                ins.then_inc(max_found, 1)
                dve.wait_ge(max_found, i + 1)
                if scale_of:
                    ins = nc.vector.scalar_tensor_tensor(top[:, i % RING, 1, :], best, -1.0, scale_of(groups[i]), ALU.mult, ALU.mult)
                else:
                    ins = nc.vector.tensor_scalar(top[:, i % RING, 1, :], best, -scale, None, ALU.mult)
                ins.then_inc(max_negated, 1)
                if i >= ahead and not copies_on_act(i - ahead):
                    spread(dve, nc.vector.tensor_copy, copied_v, i - ahead)
                if i >= per + ahead and (i - ahead) % per == 0:
                    finish((i - ahead) // per - 1)
            for i in range(n - ahead, n):
                if not copies_on_act(i):
                    spread(dve, nc.vector.tensor_copy, copied_v, i)
            for k in range((n - 1 - ahead) // per, n // per):
                finish(k)


def columns(a, lo, hi):
    return a[:, lo:hi] if len(a.shape) == 2 else a[:, lo // P:hi // P, :]


def plain(out, terms, func=None, scale=1.0, bias=None):
    return out, terms, func, scale, bias


def by_block(outT, W, srcT, func=None, scale=1.0, bias=None, n=N):
    m = W.shape[1]
    return [plain(outT[0:m, a:min(a + BLK, n)], [(W[:], srcT[0:W.shape[0], a:min(a + BLK, n)])], func, scale, bias)
            for a in range(0, n, BLK)]


def l0_attn(core):
    nc, io = core.nc, core.io
    x = core.xT
    with ExitStack() as mem:
        sb = lambda shape, name="work": core.buffer(mem, shape, name)
        mix = sb([P, 6])
        vec = sb([P, 7])
        W = {n: sb([P, P]) for n in ("Wr", "Wk", "Wv", "Wo", "g1", "g2")}
        down = sb([P, 160])
        up = sb([D64, 3, P])
        rows = sb([P, 2, P])
        load(core, [(mix[:], io["mix"]), (vec[:, 0:6], io["vec"]), (down[:], io["down"]), (up[:], io["up"])]
             + [(W[n][:], io["L0_attn_" + n]) for n in W]
             + [(rows[:, 0, :], io["L0_attn_ln_w"].unsqueeze(0).broadcast_to([P, P])),
                (rows[:, 1, :], io["L0_attn_ln_b"].unsqueeze(0).broadcast_to([P, P]))])
        load(core, core.consts(mem, "head64", "supper", "upper", "levels", "restart128", "pick2"))
        xm = [sb([P, N]) for _ in range(6)]
        xr, xw, xk, xv, xa, xg = xm
        with core.stage("shifted", "dve_step") as (block, shifted, dve_step):
            @block.vector
            def _(dve):
                link = chained(dve, dve_step)
                v = xg[:].rearrange("p (b s) -> p b s", b=B)
                xx = x[:].rearrange("p (b s) -> p b s", b=B)
                nc.vector.tensor_scalar(v[:, :, 0:1], xx[:, :, 0:1], -1.0, None, ALU.mult).then_inc(shifted, 1)
                nc.vector.tensor_tensor(v[:, :, 1:S], xx[:, :, 0:S - 1], xx[:, :, 1:S], ALU.subtract).then_inc(shifted, 1)
                dve.wait_ge(shifted, 2)
                for i in range(6):
                    link(nc.vector.scalar_tensor_tensor(xm[i][:], xg[:], mix[:, i:i + 1], x[:], ALU.mult, ALU.add))
        r, k, v_tok, v = sb([P, N]), sb([P, N]), sb([P, TILES, P]), sb([P, N])
        mid = sb([P, 4, N])
        tok = lambda a, t: a[:, P * t:P * t + P]
        jobs = by_block(r, W["Wr"], xr) + by_block(k, W["Wk"], xk) + by_block(v, W["Wv"], xv)
        jobs += by_block(mid[:, 0, :], down[:, 0:64], xw, ACT.Tanh) + by_block(mid[:, 1, :], down[:, 64:128], xa)
        jobs += by_block(mid[:, 2, :], down[:, 128:160], xv) + by_block(mid[:, 3, :], W["g1"], xg, ACT.Sigmoid)
        products(core, jobs)
        jobs = by_block(xw, up[:, 0, :], mid[0:64, 0, :], ACT.Sigmoid, 1.0, vec[:, 0:1])
        jobs += by_block(xa, up[:, 1, :], mid[0:64, 1, :], ACT.Sigmoid, 1.0, vec[:, 1:2])
        jobs += by_block(xv, up[0:32, 2, :], mid[0:32, 2, :], ACT.Sigmoid, 1.0, vec[:, 2:3])
        products(core, jobs)
        g_tok = sb([P, TILES, P])
        kk, sq, keff, beta, alpha, rt = xk, xr, mid[:, 0, :], mid[:, 1, :], sb([P, N]), sb([P, N])
        cum, dec, mids, ends = sb([P, N]), sb([P, N]), sb([P, TILES]), sb([P, TILES])
        reset, hd, rkr = core.const["restart128"], core.const["head64"], mid[:, 2, :]
        with core.stage("dve_step", "kk_squared", "norms_done", "rooted", "decay_ready", "act_step") as \
                (block, dve_step, kk_squared, norms_done, rooted, decay_ready, act_step):
            @block.vector
            def _(dve):
                link = chained(dve, dve_step)
                link(nc.vector.tensor_scalar(kk[:], k[:], vec[:, 3:4], None, ALU.mult))
                nc.vector.tensor_tensor(sq[:], kk[:], kk[:], ALU.mult).then_inc(kk_squared, 1)
                link(nc.vector.tensor_tensor(alpha[:], v[:], v[:], ALU.subtract))
                link(nc.vector.tensor_tensor(alpha[:], alpha[:], xv[:], ALU.mult))
                link(nc.vector.tensor_tensor(v[:], v[:], alpha[:], ALU.add))
                link(nc.vector.tensor_scalar(dec[:], xw[:], -float(np.exp(-0.5)), None, ALU.mult))
                link(nc.vector.tensor_tensor_scan(cum[:], reset[:], dec[:], 0.0, ALU.mult, ALU.add))
                c3 = cum[:].rearrange("p (t q) -> p t q", t=TILES)
                link(nc.vector.tensor_copy(mids[:].unsqueeze(2), c3[:, :, 63:64]))
                link(nc.vector.tensor_tensor(c3, c3, mids[:].unsqueeze(2).broadcast_to([P, TILES, P]), ALU.subtract))
                link(nc.vector.tensor_copy(ends[:].unsqueeze(2), c3[:, :, P - 1:P]))
                nc.vector.tensor_tensor(dec[:], cum[:], dec[:], ALU.subtract).then_inc(decay_ready, 1)
                link(nc.vector.tensor_scalar(keff, xa[:], 1.0, vec[:, 4:5], ALU.subtract, ALU.mult))
                link(nc.vector.tensor_scalar(keff, keff, 1.0, None, ALU.add))
                link(nc.vector.tensor_tensor(keff, keff, k[:], ALU.mult))
                link(nc.vector.scalar_tensor_tensor(rkr, r[:], vec[:, 5:6], keff, ALU.mult, ALU.mult))
                dve.wait_ge(rooted, 2)
                link(nc.vector.tensor_scalar(sq[:], sq[:], 1e-12, None, ALU.max))
                link(nc.vector.reciprocal(sq[:], sq[:]))
                link(nc.vector.tensor_tensor(kk[:], kk[:], sq[:], ALU.mult))
                link(nc.vector.tensor_tensor(beta, kk[:], xa[:], ALU.mult))
                dve.wait_ge(act_step, 4)
                link(nc.vector.scalar_tensor_tensor(alpha[:], kk[:], -1.0, dec[:], ALU.mult, ALU.mult))
                link(nc.vector.tensor_tensor(rt[:], r[:], cum[:], ALU.mult))
                link(nc.vector.reciprocal(cum[:], cum[:]))
                link(nc.vector.tensor_tensor(beta, beta, cum[:], ALU.mult))
                link(nc.vector.tensor_tensor(keff, keff, cum[:], ALU.mult))

            @block.tensor
            def _(pe):
                pe.wait_ge(kk_squared, 1)
                for n in range(NB):
                    nc.tensor.matmul(core.bank(n), hd[:], sq[:, BLK * n:BLK * n + BLK], start=True, stop=True) \
                        .then_inc(norms_done, 1)

            @block.scalar
            def _(act):
                for n in range(NB):
                    act.wait_ge(norms_done, n + 1)
                    if n == 0:
                        act.wait_ge(norms_done, 2)
                    nc.scalar.activation(sq[:, BLK * n:BLK * n + BLK], core.bank(n), ACT.Sqrt).then_inc(rooted, 1)
                act.wait_ge(decay_ready, 1)
                for a in (cum, dec, mids, ends):
                    nc.scalar.activation(a[:], a[:], ACT.Exp).then_inc(act_step, 1)
        rk_tok = sb([P, TILES, 2])
        k_tok, b_tok = W_ = sb([P, TILES, P]), sb([P, TILES, P])
        jobs = [plain(g_tok[:, t:t + 4, :].rearrange("p t f -> p (t f)")[:, P * i:P * i + P], [(mid[:, 3, P * (t + i):P * (t + i) + P], W["g2"][:])])
                for t in (0, 4) for i in range(4)]
        jobs += [plain(rk_tok[:, t, :], [(rkr[:, P * t:P * t + P], core.const["pick2"][:])]) for t in range(TILES)]
        products(core, jobs)
        transposes(core, [(dst[:, t:t + 4, :], [src[:, P * (t + i):P * (t + i) + P] for i in range(4)])
                          for dst, src in ((v_tok, v), (k_tok, keff), (b_tok, beta)) for t in (0, 4)])
        G = 16
        U_, M_, Y_, T_ = (sb([P, G, P]) for _ in range(4))
        akT, rbT, rkT = (sb([P, G, P]) for _ in range(3))
        at = lambda a, u: a[D64 * (u // TILES):D64 * (u // TILES) + D64, P * (u % TILES):P * (u % TILES) + P]
        four = lambda a, g: a[:, 4 * g:4 * g + 4, :]
        bank4 = lambda i: core.bank(i).rearrange("p (u q) -> p u q", u=4)
        row4 = lambda m: m.unsqueeze(1).broadcast_to([P, 4, P])
        pairs = [(beta, alpha, U_, core.const["supper"]), (keff, alpha, akT, core.const["supper"]),
                 (beta, rt, rbT, core.const["upper"]), (keff, rt, rkT, core.const["upper"])]
        with core.stage("cross_done", "cross_masked", "ones_set") as (block, cross_done, cross_masked, ones_set):
            @block.tensor
            def _(pe):
                for i in range(16):
                    left, right = pairs[i // 4][0:2]
                    if i >= 8:
                        pe.wait_ge(cross_masked, i - 7)
                    for j in range(4):
                        u = 4 * (i % 4) + j
                        mm = nc.tensor.matmul(core.bank(i % 8)[:, P * j:P * j + P], at(left, u), at(right, u), start=True, stop=True)
                    mm.then_inc(cross_done, 1)

            @block.vector
            def _(dve):
                for i in range(16):
                    _, _, dst, mask = pairs[i // 4]
                    dve.wait_ge(cross_done, i + 1)
                    nc.vector.tensor_tensor(four(dst, i % 4), bank4(i % 8), row4(mask[:]), ALU.mult).then_inc(cross_masked, 1)
                for g in range(4):
                    nc.vector.tensor_copy(four(M_, g), row4(core.const["ident"][:])).then_inc(ones_set, 1)
                    nc.vector.tensor_copy(four(Y_, g), row4(core.const["ident"][:])).then_inc(ones_set, 1)
        UL = sb([P, 2, 4, P])
        LV = 7
        with core.stage("level_masked", "lm_done", "lm_copied", "grown", "inverse_added") as \
                (block, level_masked, lm_done, lm_copied, grown, added):
            @block.tensor
            def _(pe):
                for s in range(4 * LV):
                    g = s % 4
                    pe.wait_ge(level_masked, s + 1)
                    if s >= 4:
                        pe.wait_ge(added, 2 * (s - 3))
                    for j in range(4):
                        mm = nc.tensor.matmul(core.bank(s % 2)[:, P * j:P * j + P], UL[:, s % 2, j, :], M_[:, 4 * g + j, :], start=True, stop=True)
                    mm.then_inc(lm_done, 1)
                    pe.wait_ge(lm_copied, s + 1)
                    if s >= 2:
                        pe.wait_ge(added, 2 * (s - 1))
                    for j in range(4):
                        nc.tensor.matmul(core.bank(2 + s % 2)[:, P * j:P * j + P], Y_[:, 4 * g + j, :], T_[:, 4 * g + j, :], start=True, stop=True)
                    for j in range(4):
                        mm = nc.tensor.matmul(core.bank(4 + s % 2)[:, P * j:P * j + P], T_[:, 4 * g + j, :], Y_[:, 4 * g + j, :], start=True, stop=True)
                    mm.then_inc(grown, 1)

            @block.scalar
            def _(act):
                for s in range(4 * LV):
                    act.wait_ge(lm_done, s + 1)
                    if s >= 4:
                        act.wait_ge(grown, s - 3)
                    nc.scalar.copy(four(T_, s % 4), bank4(s % 2)).then_inc(lm_copied, 1)

            @block.vector
            def _(dve):
                def mask(s):
                    if s >= 2:
                        dve.wait_ge(lm_done, s - 1)
                    nc.vector.tensor_tensor(UL[:, s % 2], four(U_, s % 4), row4(core.const["levels"][:, s // 4, :]), ALU.mult) \
                        .then_inc(level_masked, 1)
                mask(0)
                for s in range(4 * LV):
                    if s + 1 < 4 * LV:
                        mask(s + 1)
                    dve.wait_ge(grown, s + 1)
                    for i, a in enumerate((M_, Y_)):
                        nc.vector.tensor_tensor(four(a, s % 4), bank4(2 + 2 * i + s % 2), four(a, s % 4), ALU.add).then_inc(added, 1)
        state = sb([P, B, D64])
        W_sb, SA = sb([P, 4, D64]), sb([P, 4, D64])
        y = sb([P, TILES, P])
        comb = sb([P, TILES])
        CH = S // P
        with core.stage("state_ready", "w_done", "w_copied", "sa_done", "sa_copied", "step_done", "y_copied", "dve_step") as \
                (block, state_ready, w_done, w_copied, sa_done, sa_copied, step_done, y_copied, dve_step):
            lane = lambda i: (i % 2, i // 2)
            unit = lambda c, i: TILES * (i // 2) + CH * (i % 2) + c
            hp = lambda i: slice(D64 * (i // 2), D64 * (i // 2) + D64)

            @block.tensor
            def _(pe):
                for c in range(CH):
                    pe.wait_ge(state_ready, c + 1)
                    for i in range(4):
                        b, h = lane(i)
                        u, o = unit(c, i), core.bank(h)[:, D64 * b:D64 * b + D64]
                        nc.tensor.matmul(o, at(alpha, u), state[hp(i), b, :], start=True, stop=False)
                        mm = nc.tensor.matmul(o, akT[:, u, :], v_tok[:, CH * b + c, hp(i)], start=False, stop=True)
                    mm.then_inc(w_done, 1)
                    pe.wait_ge(w_copied, c + 1)
                    for i in range(4):
                        mm = nc.tensor.matmul(core.bank(2)[:, D64 * i:D64 * i + D64], Y_[:, unit(c, i), :], W_sb[:, i, :],
                                              start=True, stop=True)
                    mm.then_inc(sa_done, 1)
                    pe.wait_ge(sa_copied, c + 1)
                    for i in range(4):
                        b, h = lane(i)
                        t = CH * b + c
                        o = core.bank(3 + h)[hp(i), D64 * b:D64 * b + D64]
                        nc.tensor.matmul(o, b_tok[:, t, hp(i)], SA[:, i, :], start=True, stop=False)
                        nc.tensor.matmul(o, k_tok[:, t, hp(i)], v_tok[:, t, hp(i)], start=False, stop=True)
                    for i in range(4):
                        b, h = lane(i)
                        u, o = unit(c, i), core.bank(5 + h)[:, D64 * b:D64 * b + D64]
                        nc.tensor.matmul(o, at(rt, u), state[hp(i), b, :], start=True, stop=False)
                        nc.tensor.matmul(o, rbT[:, u, :], SA[:, i, :], start=False, stop=False)
                        mm = nc.tensor.matmul(o, rkT[:, u, :], v_tok[:, CH * b + c, hp(i)], start=False, stop=True)
                    mm.then_inc(step_done, 1)

            @block.vector
            def _(dve):
                link = chained(dve, dve_step)
                m3, e3 = (a[:].rearrange("p (b c) -> p b c", b=B) for a in (mids, ends))
                c3 = comb[:].rearrange("p (b c) -> p b c", b=B)
                link(nc.vector.memset(comb[:], 1.0))
                link(nc.vector.tensor_tensor(c3[:, :, 0:CH - 1], e3[:, :, 0:CH - 1], m3[:, :, 1:CH], ALU.mult))
                nc.vector.memset(state[:], 0.0).then_inc(state_ready, 1)
                for c in range(CH):
                    dve.wait_ge(w_done, c + 1)
                    nc.vector.tensor_copy(W_sb[:].rearrange("p (h b) d -> p h (b d)", h=2), core.ps[:, 0:2, 0:P]).then_inc(w_copied, 1)
                    dve.wait_ge(sa_done, c + 1)
                    nc.vector.tensor_copy(SA[:].rearrange("p a b -> p (a b)"), core.bank(2)[:, 0:256]).then_inc(sa_copied, 1)
                    dve.wait_ge(step_done, c + 1)
                    if c + 1 < CH:
                        for h in range(2):
                            q = slice(D64 * h, D64 * h + D64)
                            link(nc.vector.tensor_tensor(state[q].rearrange("p a b -> p (a b)"), core.bank(3 + h)[q, 0:P],
                                                         state[q].rearrange("p a b -> p (a b)"), ALU.add))
                        for b in range(B):
                            ins = nc.vector.tensor_scalar(state[:, b, :], state[:, b, :], comb[:, CH * b + c:CH * b + c + 1],
                                                          None, ALU.mult)
                            if b == 0:
                                link(ins)
                        ins.then_inc(state_ready, 1)
                    for b in range(B):
                        nc.vector.tensor_copy(y[:, CH * b + c, :].rearrange("p (h d) -> p h d", h=2), core.ps[:, 5:7, D64 * b:D64 * b + D64]).then_inc(y_copied, 1)
                    dve.wait_ge(y_copied, 2 * (c + 1))
        mean, var = sb([P, G]), sb([P, G])
        with core.stage("dve_step", "var_ready", "rooted") as (block, dve_step, var_ready, rooted):
            y3 = y[:].rearrange("p t (h d) -> p (t h) d", h=2)
            s3 = g3 = M_[:].rearrange("p u q -> p (u q)")[:, 0:N].rearrange("p (g d) -> p g d", g=G)
            per = lambda a: a[:].unsqueeze(2).broadcast_to([P, G, D64])

            @block.vector
            def _(dve):
                link = chained(dve, dve_step)
                link(nc.vector.reduce_sum(mean[:], y3, AX))
                link(nc.vector.tensor_scalar(mean[:], mean[:], 1.0 / D64, None, ALU.mult))
                link(nc.vector.tensor_tensor(y3, y3, per(mean), ALU.subtract))
                link(nc.vector.tensor_tensor(s3, y3, y3, ALU.mult))
                link(nc.vector.reduce_sum(var[:], s3, AX))
                nc.vector.tensor_scalar(var[:], var[:], 1.0 / D64, None, ALU.mult).then_inc(var_ready, 1)
                dve.wait_ge(rooted, 1)
                link(nc.vector.reciprocal(var[:], var[:]))
                link(nc.vector.tensor_tensor(y3, y3, per(var), ALU.mult))
                for row, op in ((0, ALU.mult), (1, ALU.add)):
                    link(nc.vector.tensor_tensor(y[:], y[:], rows[:, row, :].unsqueeze(1).broadcast_to([P, TILES, P]), op))
                v3 = v_tok[:].rearrange("p t (h d) -> p (t h) d", h=2)
                link(nc.vector.tensor_tensor(s3, v3, rk_tok[:].rearrange("p t h -> p (t h)").unsqueeze(2).broadcast_to([P, G, D64]),
                                             ALU.mult))
                link(nc.vector.tensor_tensor(y3, y3, s3, ALU.add))
                link(nc.vector.tensor_tensor(y[:], y[:], g_tok[:], ALU.mult))

            @block.scalar
            def _(act):
                act.wait_ge(var_ready, 1)
                nc.scalar.activation(var[:], var[:], ACT.Sqrt, bias=core.const["cols"][:, 1:2]).then_inc(rooted, 1)
        turn_tokens(core, xr, y)
        normalise(core, x, x, XBLOCKS, terms=[(W["Wo"][:], xr)])


def head_norm(core, a, width, gain, scale, floor):
    nc = core.nc
    blocks = [(c, min(c + BLK, width)) for c in range(0, width, BLK)]
    with ExitStack() as mem:
        sq = core.buffer(mem, [P, width])
        with core.stage("squared", "summed", "rooted", "dve_step") as (block, squared, summed, rooted, dve_step):
            @block.vector
            def _(dve):
                link = chained(dve, dve_step)
                for c0, c1 in blocks:
                    nc.vector.tensor_tensor(sq[:, c0:c1], a[:, c0:c1], a[:, c0:c1], ALU.mult).then_inc(squared, 1)
                for k, (c0, c1) in enumerate(blocks):
                    dve.wait_ge(rooted, k + 1)
                    link(nc.vector.tensor_scalar(sq[:, c0:c1], sq[:, c0:c1], floor, None, ALU.max))
                    link(nc.vector.reciprocal(sq[:, c0:c1], sq[:, c0:c1]))
                    link(nc.vector.scalar_tensor_tensor(a[:, c0:c1], a[:, c0:c1], gain, sq[:, c0:c1], ALU.mult, ALU.mult))

            @block.tensor
            def _(pe):
                for k, (c0, c1) in enumerate(blocks):
                    pe.wait_ge(squared, k + 1)
                    nc.tensor.matmul(core.bank(k)[:, 0:c1 - c0], core.const["head64"][:], sq[:, c0:c1], start=True, stop=True) \
                        .then_inc(summed, 1)

            @block.scalar
            def _(act):
                for k, (c0, c1) in enumerate(blocks):
                    act.wait_ge(summed, k + 1)
                    nc.scalar.activation(sq[:, c0:c1], core.bank(k)[:, 0:c1 - c0], ACT.Sqrt, scale=scale).then_inc(rooted, 1)


def column(src):
    return src.rearrange("(p o) -> p o", o=1)


XKEYS = [(0, KT), (KT, KT)]


def l0_xattn(core):
    nc, io = core.nc, core.io
    L = lambda n: io["L0_xattn_" + n]
    NK = S + SK
    with ExitStack() as mem:
        sb = lambda shape, name="work": core.buffer(mem, shape, name)
        Wq, Wkv, Wo = sb([P, P], "Wq"), sb([P, 2 * P], "Wkv"), sb([P, P], "Wo")
        vec = sb([P, 7], "vec")
        seen = core.buffer(mem, [P, B, SK], "seen", I32)
        core.fetch("l0x", core.consts(mem, "head64") + [(Wq, L("W_q")), (Wkv, L("W_kv")), (Wo, L("W_out")), (vec, L("vec")),
                           (seen, io["mask"].unsqueeze(0).broadcast_to([P, B, SK]))])
        core.need("l0x")
        xn, cn, qT, kT = sb([P, N]), sb([P, CT]), sb([P, N], "qT"), sb([P, B, NK], "kT")
        k = sb([P, 2, B, NK], "keys")
        v_tok, v_ctx, o_tok = sb([P, TILES, P], "v"), sb([KT, 4, P], "v_ctx"), sb([P, TILES, P], "o")
        normalise(core, core.xT, xn, XBLOCKS, vec[:, 2:3], vec[:, 3:4])
        normalise(core, core.ctx, cn, [(0, CT)], vec[:, 0:1], vec[:, 1:2])
        jobs = by_block(qT, Wq, xn)
        for b in range(B):
            jobs.append(plain(kT[:, b, 0:S], [(Wkv[:, 0:P], xn[:, S * b:S * b + S])]))
            jobs.append(plain(kT[:, b, S:NK], [(Wkv[:, 0:P], cn[:, SK * b:SK * b + SK])]))
        jobs += [plain(v_tok[:, t, :], [(xn[:, P * t:P * t + P], Wkv[:, P:2 * P])]) for t in range(TILES)]
        jobs += [plain(v_ctx[:, t, :], [(cn[:, KT * t:KT * t + KT], Wkv[:, P:2 * P])]) for t in range(4)]
        products(core, jobs)
        head_norm(core, qT, N, vec[:, 4:5], 1.0 / D64, 1e-8)
        head_norm(core, kT.rearrange("p b k -> p (b k)"), B * NK, vec[:, 5:6], 1.0 / D64, 1e-8)
        mask = sb([P, B, NK], "mask")
        with core.stage("dve_step", "keys_copied") as (block, dve_step, keys_copied):
            @block.scalar
            def _(act):
                for h, hp in ((0, slice(0, D64)), (1, slice(D64, P))):
                    nc.scalar.copy(k[hp, h], kT[hp]).then_inc(keys_copied, 1)

            @block.vector
            def _(dve):
                link = chained(dve, dve_step)
                link(nc.vector.memset(k[0:D64, 1], 0.0))
                link(nc.vector.memset(k[D64:P, 0], 0.0))
                link(nc.vector.memset(mask[:, :, 0:S], 0.0))
                link(nc.vector.tensor_scalar(mask[:, :, S:NK], seen, BIG, -BIG, ALU.mult, ALU.add))
        units = []
        for t in range(TILES):
            for h in range(2):
                hp, b = slice(D64 * h, D64 * h + D64), t // 4
                q = qT[:, P * t:P * t + P]
                units.append((t, h, [(0, q, k[:, h, b, 0:S], True, True), (S, q, k[:, h, b, S:NK], True, True)],
                              [v_tok[:, 4 * b + i, hp] for i in range(4)] + [v_ctx[:, 2 * b + i, hp] for i in range(2)]))
        attend(core, units, [(P * i, P) for i in range(4)] + [(S, KT), (S + KT, KT)], D64, lambda t: o_tok[:, t, :],
               D64 ** -0.5, lambda u: [(0, NK, mask[:, u[0] // 4, :])], nk=NK)
        turn_tokens(core, xn, o_tok)
        normalise(core, core.xT, core.xT, XBLOCKS, terms=[(Wo, xn)], bias=vec[:, 6:7])


def top_weights(core, logits, experts, k, renormalise, w):
    nc = core.nc
    with ExitStack() as mem:
        m = core.buffer(mem, [P, TILES], "row")
        rest = core.buffer(mem, [P, TILES, experts], "rest")
        best = core.buffer(mem, [P, TILES, 8], "best")
        per = lambda a: a.unsqueeze(2).broadcast_to([P, TILES, experts])
        with core.stage("dve_step", "shifted", "act_done") as (block, dve_step, shifted, exp_done):
            @block.vector
            def _(dve):
                link = chained(dve, dve_step)
                link(nc.vector.reduce_max(m, logits, AX))
                nc.vector.tensor_tensor(logits, logits, per(m), ALU.subtract).then_inc(shifted, 1)
                dve.wait_ge(exp_done, 1)
                link(nc.vector.reduce_sum(m, logits, AX))
                link(nc.vector.reciprocal(m, m))
                link(nc.vector.tensor_tensor(logits, logits, per(m), ALU.mult))
                for t in range(TILES):
                    link(nc.vector.max(best[:, t, :], logits[:, t, :]))
                link(nc.vector.memset(best[:, :, k:8], -1.0))
                for t in range(TILES):
                    link(nc.vector.match_replace(rest[:, t, :], best[:, t, :], logits[:, t, :], -1.0))
                link(nc.vector.tensor_tensor(rest, rest, logits, ALU.not_equal))
                link(nc.vector.tensor_tensor(w, rest, logits, ALU.mult))
                if renormalise:
                    link(nc.vector.reduce_sum(m, w, AX))
                    link(nc.vector.tensor_scalar(m, m, 1e-12, None, ALU.max))
                    link(nc.vector.reciprocal(m, m))
                    link(nc.vector.tensor_tensor(w, w, per(m), ALU.mult))

            @block.scalar
            def _(act):
                act.wait_ge(shifted, 1)
                nc.scalar.activation(logits, logits, ACT.Exp).then_inc(exp_done, 1)


def spread_rows(core, mem, w, experts):
    nc = core.nc
    pick, parts = core.buffer(mem, [96, experts, P], "pick", BF16), core.buffer(mem, [96, N], "parts", BF16)
    with ExitStack() as inner:
        ones = core.buffer(inner, [96, 32], "ones")
        rest, short = core.buffer(inner, [P, TILES, experts], "rest"), core.buffer(inner, [P, TILES, experts], "short", BF16)
        cut = core.buffer(inner, [P, TILES, 96], "cut")
        with core.stage("ones_in", "pick_made", "dve_step") as (block, ones_in, pick_made, dve_step):
            @block.sync
            def _(sp):
                sp.dma_start(ones, core.io["c_modulo32"]).then_inc(ones_in, 16)

            @block.scalar
            def _(act):
                act.wait_ge(ones_in, 16)
                nc.scalar.copy(pick, ones[:, 0:experts].unsqueeze(2).broadcast_to([96, experts, P])).then_inc(pick_made, 1)

            @block.vector
            def _(dve):
                link = chained(dve, dve_step)
                link(nc.vector.tensor_copy(rest, w))
                if experts < 32:
                    link(nc.vector.memset(cut, 0.0))
                for i in range(3):
                    part = cut[:, :, 32 * i:32 * i + experts]
                    link(nc.vector.tensor_copy(short, rest))
                    link(nc.vector.tensor_copy(part, short))
                    if i < 2:
                        link(nc.vector.tensor_tensor(rest, rest, part, ALU.subtract))
        transposes(core, [(parts[:, P * t:P * t + 4 * P], [cut[:, t + i, :] for i in range(4)]) for t in (0, 4)])
    return pick, parts


def l0_ffn(core):
    nc, io = core.nc, core.io
    E, SH = 32, 4
    x = core.xT
    with ExitStack() as mem:
        sb = lambda shape, name="work": core.buffer(mem, shape, name)
        gate, up, down = (sb([P, E + SH, P], n) for n in ("gate", "up", "down"))
        router, rbias = sb([P, E], "router"), sb([P, E], "router_bias")
        core.fetch("router", [(router, io["L0_ffn_router"]), (rbias, io["L0_ffn_router_bias"].unsqueeze(0).broadcast_to([P, E]))])
        for g in range(0, E + SH, 4):
            core.fetch(f"experts{g}", [(t[:, g:g + 4, :], io["L0_ffn_" + n][:, g:g + 4, :])
                                       for t, n in ((gate, "gate"), (up, "up"), (down, "down"))])
        core.need("router")
        logits, w = sb([P, TILES, E], "logits"), sb([P, TILES, E], "weights")
        with core.stage("logits_done", "logits_out") as (block, logits_done, logits_out):
            @block.tensor
            def _(pe):
                for t in range(TILES):
                    mm = nc.tensor.matmul(core.bank(0)[:, E * t:E * t + E], x[:, P * t:P * t + P], router, start=True, stop=True)
                mm.then_inc(logits_done, 1)

            @block.vector
            def _(dve):
                dve.wait_ge(logits_done, 1)
                nc.vector.tensor_tensor(logits, core.bank(0)[:, 0:E * TILES].rearrange("p (t e) -> p t e", e=E),
                                        rbias.unsqueeze(1).broadcast_to([P, TILES, E]), ALU.add).then_inc(logits_out, 1)
        top_weights(core, logits, E, 4, True, w)
        pick, parts = spread_rows(core, mem, w, E)
        U, R = 2 * (E + SH), 2 * E
        act_out, hidden = sb([P, 2, BLK], "gated"), sb([P, 2, BLK], "hidden")
        cols = lambda i: slice(BLK * (i % 2), BLK * (i % 2) + BLK)
        with core.stage("inner_done", "silu_done", "hidden_ready", "down_done", "dve_step") as \
                (block, inner_done, silu_done, hidden_ready, down_done, dve_step):
            @block.tensor
            def _(pe):
                def inner(i):
                    e = i // 2
                    if i % 8 == 0:
                        pe.wait_ge(*core.fetched[f"experts{e}"])
                    if i >= 2:
                        pe.wait_ge(hidden_ready, i - 1)
                    nc.tensor.matmul(core.bank(i % 2), gate[:, e, :], x[:, cols(i)], start=True, stop=True)
                    mm = nc.tensor.matmul(core.bank(2 + i % 2), up[:, e, :], x[:, cols(i)], start=True, stop=True)
                    if i < R:
                        mm = nc.tensor.matmul(core.bank(4 + i % 2), pick[:, e, :], parts[:, cols(i)], start=True, stop=True)
                    mm.then_inc(inner_done, 1)

                def outer(i):
                    pe.wait_ge(hidden_ready, i + 1)
                    nc.tensor.matmul(core.bank(6 + i % 2), down[:, i // 2, :], hidden[:, i % 2, :], start=(i < 2),
                                     stop=(i >= U - 2)).then_inc(down_done, 1)

                inner(0)
                for i in range(1, U):
                    inner(i)
                    outer(i - 1)
                outer(U - 1)

            @block.scalar
            def _(act):
                for i in range(U):
                    act.wait_ge(inner_done, i + 1)
                    if i >= 2:
                        act.wait_ge(hidden_ready, i - 1)
                    nc.scalar.activation(act_out[:, i % 2, :], core.bank(i % 2), ACT.Silu).then_inc(silu_done, 1)

            @block.vector
            def _(dve):
                link = chained(dve, dve_step)
                for i in range(U):
                    dve.wait_ge(silu_done, i + 1)
                    if i >= 2:
                        dve.wait_ge(down_done, i - 1)
                    ins = nc.vector.tensor_tensor(hidden[:, i % 2, :], core.bank(2 + i % 2), act_out[:, i % 2, :], ALU.mult)
                    if i < R:
                        link(ins)
                        ins = nc.vector.tensor_tensor(hidden[:, i % 2, :], core.bank(4 + i % 2), hidden[:, i % 2, :], ALU.mult)
                    ins.then_inc(hidden_ready, 1)
                dve.wait_ge(down_done, U)
                for n in range(NB):
                    link(nc.vector.tensor_tensor(x[:, cols(n)], core.bank(6 + n), x[:, cols(n)], ALU.add))
        normalise(core, x, x, XBLOCKS)


def expand_heads(core, dst, src, width):
    nc = core.nc
    with core.stage("spread_dve", "spread_pool") as (block, by_dve, by_pool):
        @block.vector
        def _(dve):
            for h in range(H16):
                nc.vector.tensor_scalar(dst[:, h, :], src, core.const["headmask"][:, h:h + 1], None, ALU.mult).then_inc(by_dve, 1)
            dve.wait_ge(by_dve, H16)


def narrow_attention(core, qT, kTs, v, o_tok, keytiles, scale, width, parts_of=None, stream=None):
    with ExitStack() as mem:
        K = [core.buffer(mem, [P, H16, width], "k_heads") for _ in range(B)]
        for b in range(B):
            expand_heads(core, K[b], kTs[b], width)
        units = [(t, h, [(0, qT[:, P * t:P * t + P], K[t // 4][:, h, :], True, True)],
                  [v[t // 4][i][:, D8 * h:D8 * h + D8] for i in range(len(keytiles))])
                 for t in range(TILES) for h in range(H16)]
        attend(core, units, keytiles, D8, lambda t: o_tok[:, t, :], scale, parts_of, nk=width, stream=stream)


SELF_KEYS = [(P * i, P) for i in range(4)]


def l1_attn(core):
    io = core.io
    with ExitStack() as mem:
        sb = lambda shape, name="work": core.buffer(mem, shape, name)
        W = {n: sb([P, P], n) for n in ("w_Q", "w_K", "w_V")}
        core.fetch("l1a", core.consts(mem, "headmask") + [(W[n], io["L1_attn_" + n]) for n in W])
        core.need("l1a")
        qT, kT, v, o = sb([P, N], "qT"), sb([P, N], "kT"), sb([P, TILES, P], "v"), sb([P, TILES, P], "o")
        products(core, by_block(qT, W["w_Q"], core.xT) + by_block(kT, W["w_K"], core.xT)
                 + [plain(v[:, t, :], [(core.xT[:, P * t:P * t + P], W["w_V"])]) for t in range(TILES)])
        narrow_attention(core, qT, [kT[:, S * b:S * b + S] for b in range(B)], [[v[:, 4 * b + i, :] for i in range(4)] for b in range(B)],
                         o, SELF_KEYS, D8 ** -0.5, S)
        turn_tokens(core, qT, o)
        normalise(core, core.xT, core.xT, XBLOCKS, terms=[(core.const["ident"], qT)])


def narrow_cross(core, layer, causal):
    io = core.io
    with ExitStack() as mem:
        sb = lambda shape, name="work": core.buffer(mem, shape, name)
        W = {n: sb([P, P], n) for n in ("Wq", "Wk", "Wv", "Wo")}
        vec, bv = sb([P, 3], "vec"), sb([P, P], "bv")
        core.fetch(layer, core.consts(mem, "headmask", *(["xcausal"] if causal else [])) + [(W[n], io[layer + n]) for n in W]
                   + [(vec, io[layer + "vec"]), (bv, io[layer + "bv"].unsqueeze(0).broadcast_to([P, P]))])
        core.need(layer)
        qT, kT, v, o = sb([P, N], "qT"), sb([P, CT], "kT"), sb([KT, 4, P], "v"), sb([P, TILES, P], "o")
        products(core, by_block(qT, W["Wq"], core.xT, None, 1.0, vec[:, 0:1]) + by_block(kT, W["Wk"], core.ctx, None, 1.0, vec[:, 1:2], CT)
                 + [plain(v[:, i, :], [(core.ctx[:, KT * i:KT * i + KT], W["Wv"])]) for i in range(4)])
        with core.stage("bias_added") as (block, bias_added):
            @block.vector
            def _(dve):
                core.nc.vector.tensor_tensor(v, v, bv[0:KT].unsqueeze(1).broadcast_to([KT, 4, P]), ALU.add).then_inc(bias_added, 1)
        parts_of = (lambda u: [(0, SK, core.const["xcausal"][:, u[0] % 4, :])] if u[0] % 4 < 2 else []) if causal else None
        narrow_attention(core, qT, [kT[:, SK * b:SK * b + SK] for b in range(B)], [[v[:, 2 * b + i, :] for i in range(2)] for b in range(B)],
                         o, XKEYS, D8 ** -0.5, SK, parts_of)
        turn_tokens(core, qT, o)
        normalise(core, core.xT, core.xT, XBLOCKS, terms=[(W["Wo"], qT)], bias=vec[:, 2:3])


def l1_xattn(core):
    narrow_cross(core, "L1_xattn_", True)


def l2_xattn(core):
    narrow_cross(core, "L2_xattn_", False)


def add_projection(core, dst, terms, bias=None):
    nc = core.nc
    with core.stage("projected", "added") as (block, projected, added):
        @block.tensor
        def _(pe):
            for n in range(NB):
                for i, (lhsT, rhs) in enumerate(terms):
                    mm = nc.tensor.matmul(core.bank(n), lhsT, columns(rhs, BLK * n, BLK * n + BLK), start=(i == 0), stop=(i == len(terms) - 1))
                mm.then_inc(projected, 1)

        @block.vector
        def _(dve):
            for n in range(NB):
                d = dst[:, BLK * n:BLK * n + BLK]
                dve.wait_ge(projected, n + 1)
                if bias is None:
                    nc.vector.tensor_tensor(d, core.bank(n), d, ALU.add).then_inc(added, 1)
                else:
                    nc.vector.scalar_tensor_tensor(d, core.bank(n), bias, d, ALU.add, ALU.add).then_inc(added, 1)


def shift_tokens(core, dst, src, zeros=None):
    nc = core.nc
    with core.stage("shifted", "copied") as (block, shifted, copied):
        s = src.rearrange("p (b s) -> p b s", b=B)

        @block.vector
        def _(dve):
            if zeros is not None:
                nc.vector.memset(zeros, 0.0).then_inc(shifted, 1)
            nc.vector.memset(dst[D64:P, :, 0:1], 0.0).then_inc(shifted, 1)
            nc.vector.tensor_copy(dst[D64:P, :, 1:S], s[D64:P, :, 0:S - 1]).then_inc(shifted, 1)

        @block.scalar
        def _(act):
            nc.scalar.copy(dst[0:D64], s[0:D64]).then_inc(copied, 1)


def rotate(core, units):
    nc = core.nc
    with ExitStack() as mem:
        cosed, sined = core.buffer(mem, [P, 2, BLK], "cosed"), core.buffer(mem, [P, 2, BLK], "sined")
        w = lambda u: units[u][0].shape[-1]
        with core.stage("norm_spread", "scaled", "turned", "cos_taken", "sin_taken", "rotated") as \
                (block, norm_spread, scaled, turned, cos_taken, sin_taken, rotated):
            @block.tensor
            def _(pe):
                def spread(u):
                    if units[u][3]:
                        if u >= 2:
                            pe.wait_ge(scaled, u - 1)
                        nc.tensor.matmul(core.bank(u % 2)[:, 0:w(u)], units[u][3][1], units[u][3][2], start=True, stop=True) \
                            .then_inc(norm_spread, 1)
                spread(0)
                for u in range(len(units)):
                    if u + 1 < len(units):
                        spread(u + 1)
                    if units[u][3]:
                        pe.wait_ge(scaled, u + 1)
                    if u >= 2:
                        pe.wait_ge(sin_taken, u - 1)
                    nc.tensor.matmul(core.bank(2 + u % 2)[:, 0:w(u)], core.const["rot"], units[u][0], start=True, stop=True).then_inc(turned, 1)

            @block.vector
            def _(dve):
                for u, (a, cos, sin, norm) in enumerate(units):
                    if norm:
                        dve.wait_ge(norm_spread, u + 1)
                        nc.vector.scalar_tensor_tensor(a, a, norm[0], core.bank(u % 2)[:, 0:w(u)], ALU.mult, ALU.mult).then_inc(scaled, 1)
                    dve.wait_ge(turned, u + 1)
                    if u >= 2:
                        dve.wait_ge(rotated, u - 1)
                    nc.vector.tensor_tensor(sined[:, u % 2, 0:w(u)], core.bank(2 + u % 2)[:, 0:w(u)], sin, ALU.mult).then_inc(sin_taken, 1)

            @block.gpsimd
            def _(pool):
                for u, (a, cos, sin, norm) in enumerate(units):
                    pool.wait_ge(turned, u + 1)
                    nc.gpsimd.tensor_tensor(cosed[:, u % 2, 0:w(u)], a, cos, ALU.mult).then_inc(cos_taken, 1)
                    pool.wait_ge(cos_taken, u + 1)
                    pool.wait_ge(sin_taken, u + 1)
                    nc.gpsimd.tensor_tensor(a, cosed[:, u % 2, 0:w(u)], sined[:, u % 2, 0:w(u)], ALU.add).then_inc(rotated, 1)
                pool.wait_ge(rotated, len(units))


def local_projections(core, Wqkv, gains, table, xs, q, k, v, q_factor):
    nc = core.nc
    with ExitStack() as mem:
        sb = lambda shape, name: core.buffer(mem, shape, name)
        lengths = sb([P, 2, TILES, H16], "lengths")
        square, cosed, sined = sb([P, 2, INNER], "square"), sb([P, 4, INNER], "cosed"), sb([P, INNER], "sined")
        block, tables_ready, q_made, k_made, v_made, squared, rotated, summed, floored, rooted, inverted, added, scaled, \
            q_turned, k_turned, q_copied, k_copied, v_copied, slid = mem.enter_context(core.stage(
                "tables_ready", "queries_made", "keys_made", "values_made", "squared", "rotated", "summed", "floored", "rooted",
                "lengths_inverted", "added", "keys_scaled", "queries_turned", "keys_turned", "queries_copied", "keys_copied", "values_copied", "slid"))
        first_window = lambda t: t + (t + 1) // 2
        made_sem = (q_made, k_made, v_made)
        made = lambda kind: core.bank(2 * kind, 2)
        back = core.bank(6, 2)
        by_head = lambda a: a.rearrange("p (h d) -> p h d", h=H16)

        @block.tensor
        def _(pe):
            def project(t, kind):
                if t >= 1:
                    if kind == 2:
                        pe.wait_ge(v_copied, t)
                    else:
                        pe.wait_ge(rotated, 2 * (t - 1) + kind + 1)
                b, first = (t // WINDOWS, STARTS[t % WINDOWS]) if kind == 2 else (t // 4, WIN + P * (t % 4))
                for half in range(2):
                    mm = nc.tensor.matmul(made(kind)[:, BLK * half:BLK * half + BLK], xs[:, b, first:first + P],
                                          Wqkv[:, INNER * kind + BLK * half:INNER * kind + BLK * half + BLK], start=True, stop=True)
                mm.then_inc(made_sem[kind], 1)

            def turn(s, done):
                for c in range(WC):
                    mm = nc.tensor.transpose(back[:, P * c:P * c + P], cosed[:, s % 4, P * c:P * c + P], core.const["ident"])
                mm.then_inc(done, 1)

            def turn_queries(t):
                pe.wait_ge(added, 2 * t + 1)
                if t >= 2:
                    pe.wait_ge(k_copied, t - 1)
                elif t == 1:
                    pe.wait_ge(q_copied, 1)
                turn(2 * t, q_turned)

            def turn_keys(t):
                pe.wait_ge(scaled, t + 1)
                if t < TILES - 1:
                    pe.wait_ge(q_copied, t + 2)
                else:
                    pe.wait_ge(k_copied, t)
                turn(2 * t + 1, k_turned)

            project(0, 0)
            project(0, 1)
            for t in range(TILES):
                if t + 1 < TILES:
                    project(t + 1, 0)
                project(first_window(t), 2)
                turn_queries(t)
                if t % 2 == 0:
                    project(first_window(t) + 1, 2)
                if t + 1 < TILES:
                    project(t + 1, 1)
                if t >= 1:
                    turn_keys(t - 1)
            turn_keys(TILES - 1)
            pe.wait_ge(inverted, TILES + 1)
            for w in range(B * WINDOWS):
                tile, row = 4 * (w // WINDOWS) + STARTS[w % WINDOWS] // P, STARTS[w % WINDOWS] % P
                pieces = [(tile, row)] + ([(tile + 1, row - P)] if row + WROWS > P else [])
                for i, (t, offset) in enumerate(pieces):
                    mm = nc.tensor.matmul(core.bank(0)[0:WROWS, H16 * w:H16 * w + H16], core.const["slide"][:, WROWS + offset:2 * WROWS + offset],
                                          lengths[:, 0, t, :], start=(i == 0), stop=(i == len(pieces) - 1))
            mm.then_inc(slid, 1)

        @block.scalar
        def _(act):
            def make_square(t, kind):
                act.wait_ge(made_sem[kind], t + 1)
                if t >= 1:
                    act.wait_ge(summed, 2 * (t - 1) + kind + 1)
                nc.scalar.activation(square[:, kind, :], made(kind), ACT.Square).then_inc(squared, 1)

            def copy_values(t):
                act.wait_ge(v_made, t + 1)
                nc.scalar.copy(v[:, t, :], made(2)).then_inc(v_copied, 1)

            def copy_queries(t):
                act.wait_ge(q_turned, t + 1)
                nc.scalar.copy(q[:, :, P * t:P * t + P], back.rearrange("p (c q) -> p c q", c=WC)).then_inc(q_copied, 1)

            def copy_keys(t):
                act.wait_ge(k_turned, t + 1)
                for odd in range(2):
                    half = slice(D64 * odd, D64 * odd + D64)
                    ins = nc.scalar.copy(k[half, odd::2, t // 4, WIN + P * (t % 4):WIN + P * (t % 4) + P],
                                         back[half].rearrange("p (c q) -> p c q", c=WC))
                ins.then_inc(k_copied, 1)

            make_square(0, 0)
            make_square(0, 1)
            for t in range(TILES):
                if t + 1 < TILES:
                    make_square(t + 1, 0)
                copy_values(first_window(t))
                copy_queries(t)
                if t % 2 == 0:
                    copy_values(first_window(t) + 1)
                if t + 1 < TILES:
                    make_square(t + 1, 1)
                act.wait_ge(summed, 2 * t + 2)
                nc.scalar.activation(lengths[:, 1, t, :], lengths[:, 1, t, :], ACT.Sqrt).then_inc(rooted, 1)
                if t >= 1:
                    copy_keys(t - 1)
            nc.scalar.activation(lengths[:, 0], lengths[:, 0], ACT.Sqrt).then_inc(rooted, 1)
            copy_keys(TILES - 1)

        @block.vector
        def _(dve):
            for side in range(2):
                nc.vector.tensor_tensor(table[:, side], table[:, side],
                                        gains[:, side].unsqueeze(1).broadcast_to([P, 4, 2, D64]), ALU.mult).then_inc(tables_ready, 1)
            dve.wait_ge(tables_ready, 2)

            def invert_keys(t):
                dve.wait_ge(rooted, t + 1)
                one = lengths[:, 1, t, :]
                nc.vector.tensor_scalar(one, one, 1e-12, None, ALU.max).then_inc(floored, 1)
                dve.wait_ge(floored, t + 1)
                nc.vector.reciprocal(one, one).then_inc(inverted, 1)

            for s in range(2 * TILES):
                t, kind = s // 2, s % 2
                dve.wait_ge(squared, s + 1)
                if s >= 4:
                    dve.wait_ge(k_turned if kind else q_turned, t - 1)
                a = by_head(made(kind))
                tab = lambda i, lo, hi: table[:, kind, t % 4, i, lo:hi].unsqueeze(1).broadcast_to([P, H16, hi - lo])
                nc.vector.tensor_tensor(by_head(cosed[:, s % 4, :]), a, tab(0, 0, D64), ALU.mult)
                if s >= 1:
                    dve.wait_ge(added, s)
                sines = by_head(sined)
                nc.vector.tensor_tensor(sines[:, :, 0:32], a[:, :, 32:64], tab(1, 0, 32), ALU.mult)
                nc.vector.tensor_tensor(sines[:, :, 32:64], a[:, :, 0:32], tab(1, 32, 64), ALU.mult).then_inc(rotated, 1)
                nc.vector.reduce_sum(lengths[:, kind, t, :], by_head(square[:, kind, :]), AX).then_inc(summed, 1)
                if kind == 0 and t >= 1:
                    invert_keys(t - 1)
            invert_keys(TILES - 1)
            dve.wait_ge(rooted, TILES + 1)
            all_q = lengths[:, 0]
            nc.vector.tensor_scalar(all_q, all_q, 1e-12, None, ALU.max).then_inc(floored, 1)
            dve.wait_ge(floored, TILES + 1)
            nc.vector.reciprocal(all_q, all_q).then_inc(inverted, 1)
            dve.wait_ge(slid, 1)
            nc.vector.tensor_scalar(q_factor.rearrange("p w h -> p (w h)"), core.bank(0)[0:WROWS, 0:B * WINDOWS * H16], 8.0, None, ALU.mult) \
                .then_inc(floored, 1)

        @block.gpsimd
        def _(pool):
            def scale_keys(t):
                pool.wait_ge(added, 2 * t + 2)
                pool.wait_ge(inverted, t + 1)
                keys = by_head(cosed[:, (2 * t + 1) % 4, :])
                nc.gpsimd.tensor_tensor(keys, keys, lengths[:, 1, t, :].unsqueeze(2).broadcast_to([P, H16, D64]), ALU.mult).then_inc(scaled, 1)

            for s in range(2 * TILES):
                pool.wait_ge(rotated, s + 1)
                nc.gpsimd.tensor_tensor(cosed[:, s % 4, :], cosed[:, s % 4, :], sined, ALU.add).then_inc(added, 1)
                if s >= 2 and s % 2 == 0:
                    scale_keys(s // 2 - 1)
            scale_keys(TILES - 1)


def l1_ffn(core):
    nc, io = core.nc, core.io
    x = core.xT
    D = lambda n: io["L1_ffn_" + n]
    with ExitStack() as mem:
        sb = lambda shape, name="work": core.buffer(mem, shape, name)
        start = nc.dram_tensor("l1_ffn_start", (P, N), F32, kind="Internal").ap()
        Wqkv = sb([P, 3 * INNER], "Wqkv")
        table, gains = sb([P, 2, 4, 2, D64], "table"), sb([P, 2, 2, D64], "gains")
        k = sb([P, H16, B, WIN + S], "keys")
        first_weights = lambda depths, d: [(table, io["c_xpos"]), (Wqkv, D("Wqkv")[depths][d]), (gains, D("gains")[depths][d].unsqueeze(0).broadcast_to([P, 2, 2, D64]))]
        load(core, core.consts(mem, "band", "slide") + first_weights(slice(0, 1), 0))
        with core.stage("stored", "cleared") as (block, stored, cleared):
            @block.vector
            def _(dve):
                nc.vector.memset(k[:, 0:H16 // 2], 0.0).then_inc(cleared, 1)

            @block.gpsimd
            def _(pool):
                nc.gpsimd.memset(k[:, H16 // 2:], 0.0).then_inc(cleared, 1)
                pool.wait_ge(cleared, 2)

            @block.sync
            def _(sp):
                sp.dma_start(start, x).then_inc(stored, 16)
                sp.wait_ge(stored, 16)
        core.settle()
        with nc.Fori(0, DEPTH) as i:
            with ExitStack() as inner:
                ib = lambda shape, name: core.buffer(inner, shape, name)
                q, v = ib([P, WC, N], "q"), ib([P, B * WINDOWS, INNER], "v")
                q_factor = ib([WROWS, B * WINDOWS, H16], "q_factor")
                with ExitStack() as early:
                    xs = core.buffer(early, [P, B, WIN + S], "shifted")
                    shift_tokens(core, xs[:, :, WIN:], x, xs[:, :, 0:WIN])
                    local_projections(core, Wqkv, gains, table, xs, q, k, v, q_factor)
                Wo, W1, W2, vec = ib([P, WC, P], "Wo"), ib([P, 2 * DI], "W1"), ib([P, 3, P], "W2"), ib([P, 9], "vec")
                units = []
                for w in range(B * WINDOWS):
                    for h in range(H16):
                        b, first = w // WINDOWS, STARTS[w % WINDOWS]
                        units.append((w, h, [(0, q[:, h // 2, S * b + first:S * b + first + WROWS], k[:, h, b, first:first + P], True, True)],
                                      [v[:, w, D64 * h:D64 * h + D64]]))
                attend(core, units, [(0, P)], D64, lambda w: v[0:WROWS, w, :], 1.0,
                       lambda u: [(0, P, core.const["band"][:, min(u[0] % WINDOWS, 1), :])], nk=P,
                       scale_of=lambda g: q_factor[:, g[0][0], g[0][1]:g[-1][1] + 1],
                       meanwhile=[(Wo, D("Wo")[i]), (W1, D("W1")[i]), (W2, D("W2")[i]), (vec, D("vec")[i])]
                       + first_weights(slice(1, DEPTH + 1), i),
                       R=WROWS, act_copies=False)
                end = lambda w: S * (w // WINDOWS) + STARTS[w % WINDOWS] + WROWS
                new = lambda w: WROWS if w % WINDOWS == 0 else STARTS[w % WINDOWS] - STARTS[w % WINDOWS - 1]
                transposes(core, [(q[:, c:c + 4, end(w) - new(w):end(w)], [v[0:WROWS, w, P * (c + i):P * (c + i) + P] for i in range(4)])
                                  for w in range(B * WINDOWS) for c in (0, 4)])
                add_projection(core, x, [(Wo[:, c, :], q[:, c, :]) for c in range(WC)])
                xs, xn, gelu, prod = q[:, 0, :], q[:, 1, :], q[:, 2, :].rearrange("p (b s) -> p b s", b=2), q[:, 3:6, :]
                shift_tokens(core, xs.rearrange("p (b s) -> p b s", b=B), x)
                normalise(core, xs, xn, XBLOCKS, vec[:, 0:1], vec[:, 1:2])
                parts = [(j, min(P, DI - P * j), n) for j in range(3) for n in range(NB)]
                with core.stage("inner_done", "gelu_done", "gated") as (block, inner_done, gelu_done, gated):
                    @block.tensor
                    def _(pe):
                        for s, (j, m, n) in enumerate(parts):
                            if s >= 2:
                                pe.wait_ge(gated, s - 1)
                            for half in range(2):
                                mm = nc.tensor.matmul(core.bank(2 * (s % 2) + half)[0:m], W1[:, DI * half + P * j:DI * half + P * j + m],
                                                      xn[:, BLK * n:BLK * n + BLK], start=True, stop=True)
                            mm.then_inc(inner_done, 1)

                    @block.scalar
                    def _(act):
                        for s, (j, m, n) in enumerate(parts):
                            act.wait_ge(inner_done, s + 1)
                            if s >= 2:
                                act.wait_ge(gated, s - 1)
                            nc.scalar.activation(gelu[0:m, s % 2, :], core.bank(2 * (s % 2) + 1)[0:m], ACT.Gelu,
                                                 bias=vec[0:m, 6 + j:7 + j]).then_inc(gelu_done, 1)

                    @block.vector
                    def _(dve):
                        for s, (j, m, n) in enumerate(parts):
                            dve.wait_ge(gelu_done, s + 1)
                            nc.vector.scalar_tensor_tensor(prod[0:m, j, BLK * n:BLK * n + BLK], core.bank(2 * (s % 2))[0:m],
                                                           vec[0:m, 3 + j:4 + j], gelu[0:m, s % 2, :], ALU.add, ALU.mult).then_inc(gated, 1)
                add_projection(core, x, [(W2[0:m, j, :], prod[0:m, j, :]) for j, m in ((0, P), (1, P), (2, DI - 2 * P))], vec[:, 2:3])
            core.settle()
        before = sb([P, N], "before")
        load(core, [(before, start)])
        normalise(core, x, x, XBLOCKS, terms=[(core.const["ident"], before)])


def l2_attn(core):
    nc, io = core.nc, core.io
    A = lambda n: io["L2_attn_" + n]
    WINDOW = 2 * P
    with ExitStack() as mem:
        sb = lambda shape, name="work": core.buffer(mem, shape, name)
        W, Wo, vec, bv, rel = sb([P, 3 * P], "Wqkv"), sb([P, P], "Wo"), sb([P, 3], "vec"), sb([P, P], "bv"), sb([P, EXT], "rel")
        core.fetch("l2a", core.consts(mem, "headmask") + [(W, A("W")), (Wo, A("Wo")), (vec, A("vec")), (rel, A("rel")),
                                                          (bv, A("bv").unsqueeze(0).broadcast_to([P, P]))])
        core.need("l2a")
        qT, kT, v, o = sb([P, N], "qT"), sb([P, N], "kT"), sb([P, TILES, P], "v"), sb([P, TILES, P], "o")
        products(core, by_block(qT, W[:, 0:P], core.xT, None, 1.0, vec[:, 0:1]) + by_block(kT, W[:, P:2 * P], core.xT, None, 1.0, vec[:, 1:2])
                 + [plain(v[:, t, :], [(core.xT[:, P * t:P * t + P], W[:, 2 * P:3 * P])]) for t in range(TILES)])
        edges = sb([P, TILES, H16, 2], "edges")
        scratch = nc.dram_tensor("relative", (TILES, P * H16 * EXT), F32, kind="Internal")
        with core.stage("dve_step") as (block, dve_step):
            @block.vector
            def _(dve):
                link = chained(dve, dve_step)
                link(nc.vector.tensor_tensor(v, v, bv.unsqueeze(1).broadcast_to([P, TILES, P]), ALU.add))
                link(nc.vector.tensor_scalar(qT, qT, float(1.0 / np.sqrt(D8)), None, ALU.mult))
        with ExitStack() as inner:
            heads = core.buffer(inner, [P, H16, EXT], "rel_heads")
            rows = core.buffer(inner, [P, 2, H16, EXT], "rows")
            expand_heads(core, heads, rel, EXT)
            with core.stage("bias_done", "out_by_act", "out_by_dve", "stored_even", "stored_odd", "edges_kept") as \
                    (block, bias_done, by_act, by_dve, stored_even, stored_odd, kept):
                stored = (stored_even, stored_odd)

                @block.tensor
                def _(pe):
                    for u in range(TILES * H16):
                        if u >= 8:
                            if u % 2:
                                pe.wait_ge(by_dve, (u - 8) // 2 + 1)
                            else:
                                pe.wait_ge(by_act, (u - 8) // 2 + 1)
                        t, h = u // H16, u % H16
                        nc.tensor.matmul(core.bank(u % 8)[:, 0:EXT], qT[:, P * t:P * t + P], heads[:, h, :], start=True, stop=True) \
                            .then_inc(bias_done, 1)

                @block.scalar
                def _(act):
                    for u in range(0, TILES * H16, 2):
                        t, h = u // H16, u % H16
                        act.wait_ge(bias_done, u + 1)
                        if h == 0 and t >= 2:
                            act.wait_ge(stored[t % 2], 16 * (t // 2))
                            act.wait_ge(kept, t - 1)
                        nc.scalar.copy(rows[:, t % 2, h, :], core.bank(u % 8)[:, 0:EXT]).then_inc(by_act, 1)

                @block.vector
                def _(dve):
                    for u in range(1, TILES * H16, 2):
                        t, h = u // H16, u % H16
                        dve.wait_ge(bias_done, u + 1)
                        if h == 1 and t >= 2:
                            dve.wait_ge(stored[t % 2], 16 * (t // 2))
                            dve.wait_ge(kept, t - 1)
                        nc.vector.tensor_copy(rows[:, t % 2, h, :], core.bank(u % 8)[:, 0:EXT]).then_inc(by_dve, 1)
                        if h == H16 - 1:
                            dve.wait_ge(by_act, H16 // 2 * (t + 1))
                            dve.wait_ge(by_dve, H16 // 2 * (t + 1))
                            nc.vector.tensor_copy(edges[:, t, :, :], rows[:, t % 2, :, 0:EXT - 1:EXT - 2]).then_inc(kept, 1)

                @block.sync
                def _(sp):
                    for t in range(TILES):
                        sp.wait_ge(by_act, H16 // 2 * (t + 1))
                        sp.wait_ge(by_dve, H16 // 2 * (t + 1))
                        sp.dma_start(scratch.ap()[t].rearrange("(p c) -> p c", p=P), rows[:, t % 2].rearrange("p h c -> p (h c)")) \
                            .then_inc(stored[t % 2], 16)
                    for one in stored:
                        sp.wait_ge(one, 8 * TILES)
        window = sb([P, 2, H16, WINDOW], "window")

        def parts(u):
            t, h = u[0], u[1]
            first = P * (t % 4) - REL
            a, b = max(first, 0), min(first + WINDOW, S)
            out = [(a, b, window[:, t % 2, h, a - first:b - first])]
            if a:
                out.append((0, a, edges[:, t, h, 0:1]))
            if b < S:
                out.append((b, S, edges[:, t, h, 1:2]))
            return out

        def stream(t):
            src = bass.AP(scratch, t * P * H16 * EXT + P - 1, [[H16 * EXT - 1, P], [EXT, H16], [1, WINDOW]])
            return [(window[:, t % 2], src)]

        narrow_attention(core, qT, [kT[:, S * b:S * b + S] for b in range(B)], [[v[:, 4 * b + i, :] for i in range(4)] for b in range(B)],
                         o, SELF_KEYS, 1.0, S, parts, stream)
        turn_tokens(core, qT, o)
        normalise(core, core.xT, core.xT, XBLOCKS, terms=[(Wo, qT)], bias=vec[:, 2:3])


def l2_ffn(core):
    nc, io = core.nc, core.io
    E = 8
    x = core.xT
    with ExitStack() as mem:
        sb = lambda shape, name="work": core.buffer(mem, shape, name)
        W, router, rbias, bias = sb([P, E, P], "experts"), sb([P, E], "router"), sb([P, E], "rbias"), sb([E, P], "bias")
        core.fetch("l2f", [(W, io["L2_ffn_W"]), (router, io["L2_ffn_router"]), (rbias, io["L2_ffn_b_router"].unsqueeze(0).broadcast_to([P, E])),
                           (bias, io["L2_ffn_b_experts"])])
        core.need("l2f")
        logits, w, wT = sb([P, TILES, E], "logits"), sb([P, TILES, E], "weights"), sb([E, N], "wT")
        with core.stage("logits_done", "logits_out") as (block, logits_done, logits_out):
            @block.tensor
            def _(pe):
                for t in range(TILES):
                    mm = nc.tensor.matmul(core.bank(0)[:, E * t:E * t + E], x[:, P * t:P * t + P], router, start=True, stop=True)
                mm.then_inc(logits_done, 1)

            @block.vector
            def _(dve):
                dve.wait_ge(logits_done, 1)
                nc.vector.tensor_tensor(logits, core.bank(0)[:, 0:E * TILES].rearrange("p (t e) -> p t e", e=E),
                                        rbias.unsqueeze(1).broadcast_to([P, TILES, E]), ALU.add).then_inc(logits_out, 1)
        top_weights(core, logits, E, 2, False, w)
        transposes(core, [(wT[:, P * t:P * t + 4 * P], [w[:, t + i, :] for i in range(4)]) for t in (0, 4)])
        pick, parts = spread_rows(core, mem, w, E)
        xw = sb([P, 2, BLK], "weighted")
        cols = lambda i: slice(BLK * (i % 2), BLK * (i % 2) + BLK)
        U = 2 * E
        with core.stage("weight_spread", "x_weighted", "expert_done", "dve_step") as (block, spread, weighted, expert_done, dve_step):
            @block.tensor
            def _(pe):
                def pick_row(i):
                    if i >= 2:
                        pe.wait_ge(weighted, i - 1)
                    nc.tensor.matmul(core.bank(i % 2), pick[:, i // 2, :], parts[:, cols(i)], start=True, stop=True).then_inc(spread, 1)
                for n in range(NB):
                    nc.tensor.matmul(core.bank(2 + n), bias, wT[:, cols(n)], start=True, stop=False)
                pick_row(0)
                for i in range(U):
                    if i + 1 < U:
                        pick_row(i + 1)
                    pe.wait_ge(weighted, i + 1)
                    nc.tensor.matmul(core.bank(2 + i % 2), W[:, i // 2, :], xw[:, i % 2, :], start=False, stop=(i >= U - 2)).then_inc(expert_done, 1)

            @block.vector
            def _(dve):
                for i in range(U):
                    dve.wait_ge(spread, i + 1)
                    if i >= 2:
                        dve.wait_ge(expert_done, i - 1)
                    nc.vector.tensor_tensor(xw[:, i % 2, :], core.bank(i % 2), x[:, cols(i)], ALU.mult).then_inc(weighted, 1)
                dve.wait_ge(weighted, U)
                dve.wait_ge(expert_done, U)
                link = chained(dve, dve_step)
                for n in range(NB):
                    link(nc.vector.tensor_tensor(x[:, cols(n)], core.bank(2 + n), x[:, cols(n)], ALU.add))
        normalise(core, x, x, XBLOCKS)


def l3_attn(core):
    nc, io = core.nc, core.io
    x = core.xT
    CAP = 50.0
    with ExitStack() as mem:
        sb = lambda shape, name="work": core.buffer(mem, shape, name)
        W, Wg, Wo = sb([P, 3 * INNER], "Wqkv"), sb([P, H16], "Wg"), sb([P, WC, P], "Wo")
        core.fetch("l3a", core.consts(mem, "upper") + [(W, io["L3_attn_w_qkv"]), (Wg, io["L3_attn_w_gates"]), (Wo, io["L3_attn_w_out"])])
        q, k = sb([P, WC, N], "q"), sb([P, H16, N], "k")
        v = sb([P, TILES, H16, D64 + 1], "v_ones")
        core.need("l3a", zeros=[k[0:D64, 1::2, :], k[D64:P, 0::2, :]])
        o = sb([P, TILES, WC, P], "o")
        gates = sb([P, TILES, H16], "gates")
        with ExitStack() as inner:
            with core.stage("ones_set") as (block, ones_set):
                @block.vector
                def _(dve):
                    nc.vector.memset(v[:, :, :, D64:D64 + 1], 1.0).then_inc(ones_set, 1)
            blocks = [slice(S * b, S * b + S) for b in range(B)]
            jobs = [plain(q[:, c, n], [(W[:, P * c:P * c + P], x[:, n])]) for c in range(WC) for n in blocks]
            jobs += [plain((k[0:D64, 2 * c, n], k[D64:P, 2 * c + 1, n]), [(W[:, INNER + P * c:INNER + P * c + P], x[:, n])])
                     for c in range(WC) for n in blocks]
            jobs += [plain(v[:, t, 8 * j:8 * j + 8, 0:D64], [(x[:, P * t:P * t + P], W[:, 2 * INNER + BLK * j:2 * INNER + BLK * j + BLK])])
                     for t in range(TILES) for j in range(2)]
            jobs += [plain(gates[:, t, :], [(x[:, P * t:P * t + P], Wg)], ACT.Sigmoid) for t in range(TILES)]
            products(core, jobs)
            U = B * H16
            first = [0, 4 * P, 7 * P, 9 * P]
            prob = core.buffer(inner, [P, 2, 10 * P], "prob")
            inv = core.buffer(inner, [P, 2, 4], "inverse")
            with core.stage("scores_ready", "tanh_done", "exp_done", "masked", "values_done", "inverted", "head_out") as \
                    (block, scores_ready, tanh_done, exp_done, masked, values_done, inverted, head_out):
                @block.tensor
                def _(pe):
                    def scores(u):
                        b, h = u // H16, u % H16
                        for j in range(4):
                            if u >= 1:
                                pe.wait_ge(tanh_done, 4 * (u - 1) + j + 1)
                            nc.tensor.matmul(core.bank(j)[:, 0:S - P * j], k[:, h, S * b + P * j:S * b + P * j + P],
                                             q[:, h // 2, S * b + P * j:S * b + S], start=True, stop=True).then_inc(scores_ready, 1)

                    def values(u):
                        b, h = u // H16, u % H16
                        pe.wait_ge(masked, 4 * (u + 1))
                        if u >= 4:
                            pe.wait_ge(head_out, u - 3)
                        for i in range(4):
                            for j in range(i + 1):
                                mm = nc.tensor.matmul(core.bank(4 + u % 4)[:, (D64 + 1) * i:(D64 + 1) * (i + 1)],
                                                      prob[:, u % 2, first[j] + P * (i - j):first[j] + P * (i - j) + P],
                                                      v[:, 4 * b + j, h, :], start=(j == 0), stop=(j == i))
                        mm.then_inc(values_done, 1)

                    scores(0)
                    for u in range(U):
                        if u + 1 < U:
                            scores(u + 1)
                        values(u)

                @block.scalar
                def _(act):
                    for u in range(U):
                        for j in range(4):
                            act.wait_ge(scores_ready, 4 * u + j + 1)
                            if j == 0 and u >= 2:
                                act.wait_ge(values_done, u - 1)
                            nc.scalar.activation(prob[:, u % 2, first[j]:first[j] + S - P * j], core.bank(j)[:, 0:S - P * j], ACT.Tanh,
                                                 scale=D64 ** -0.5 / CAP).then_inc(tanh_done, 1)
                        act.wait_ge(tanh_done, 4 * (u + 1))
                        nc.scalar.activation(prob[:, u % 2, :], prob[:, u % 2, :], ACT.Exp, scale=CAP).then_inc(exp_done, 1)

                @block.vector
                def _(dve):
                    def finish(u):
                        b, h = u // H16, u % H16
                        out = core.bank(4 + u % 4)[:, 0:4 * (D64 + 1)].rearrange("p (i d) -> p i d", i=4)
                        dve.wait_ge(values_done, u + 1)
                        if u >= 2:
                            dve.wait_ge(head_out, u - 1)
                        r = inv[:, u % 2, :]
                        nc.vector.reciprocal(r.unsqueeze(2), out[:, :, D64:D64 + 1]).then_inc(inverted, 1)
                        dve.wait_ge(inverted, 2 * u + 1)
                        nc.vector.tensor_tensor(r, r, gates[:, 4 * b:4 * b + 4, h], ALU.mult).then_inc(inverted, 1)
                        dve.wait_ge(inverted, 2 * u + 2)
                        nc.vector.tensor_tensor(o[:, 4 * b:4 * b + 4, h // 2, D64 * (h % 2):D64 * (h % 2) + D64], out[:, :, 0:D64],
                                                r.unsqueeze(2).broadcast_to([P, 4, D64]), ALU.mult).then_inc(head_out, 1)
                    for u in range(U):
                        dve.wait_ge(exp_done, u + 1)
                        for j in range(4):
                            d = prob[:, u % 2, first[j]:first[j] + P]
                            nc.vector.tensor_tensor(d, d, core.const["upper"], ALU.mult).then_inc(masked, 1)
                        if u >= 1:
                            finish(u - 1)
                    finish(U - 1)
        turn_heads(core, o)
        normalise(core, x, x, XBLOCKS, terms=[(Wo[:, c, :], o[:, :, c, :]) for c in range(WC)])


def rotary_queries(core, W, qc, q):
    nc = core.nc
    U, HU = 2 * TILES, H16 // 2
    with ExitStack() as mem:
        sb = lambda shape, name: core.buffer(mem, shape, name)
        rows, sined = sb([P, 3, HU, P], "rows"), sb([P, 2, HU, D64], "sined")
        block, projected, plain_copied, rotated, added, turned, copied = mem.enter_context(
            core.stage("projected", "nope_copied", "rotated", "added", "turned", "turned_copied"))
        made = lambda u: core.bank(2 * (u % 2), 2).rearrange("p (h d) -> p h d", h=HU)
        back = lambda u: core.bank(4 + 2 * (u % 2), 2)

        @block.tensor
        def _(pe):
            def turn(u):
                pe.wait_ge(added, u + 1)
                if u >= 2:
                    pe.wait_ge(copied, u - 1)
                for h in range(HU):
                    mm = nc.tensor.transpose(back(u)[:, P * h:P * h + P], rows[:, u % 3, h, :], core.const["ident"])
                mm.then_inc(turned, 1)

            for u in range(U):
                t, first = u // 2, INNER * (u % 2)
                if u >= 2:
                    pe.wait_ge(rotated, u - 1)
                for half in range(2):
                    mm = nc.tensor.matmul(core.bank(2 * (u % 2) + half), qc[:, P * t:P * t + P],
                                          W[:, first + BLK * half:first + BLK * half + BLK], start=True, stop=True)
                mm.then_inc(projected, 1)
                if u >= 1:
                    turn(u - 1)
            turn(U - 1)

        @block.scalar
        def _(act):
            def copy_back(u):
                act.wait_ge(turned, u + 1)
                nc.scalar.copy(q[:, u // 2, HU * (u % 2):HU * (u % 2) + HU, :].rearrange("p h q -> p (h q)"), back(u)).then_inc(copied, 1)

            for u in range(U):
                act.wait_ge(projected, u + 1)
                if u >= 3:
                    act.wait_ge(turned, u - 2)
                nc.scalar.copy(rows[:, u % 3, :, 0:D64], made(u)[:, :, 0:D64]).then_inc(plain_copied, 1)
                if u >= 2:
                    copy_back(u - 2)
            copy_back(U - 2)
            copy_back(U - 1)

        @block.vector
        def _(dve):
            for u in range(U):
                dve.wait_ge(plain_copied, u + 1)
                if u >= 2:
                    dve.wait_ge(added, u - 1)
                a = made(u)
                tab = lambda i, lo, hi: core.const["rotary"][:, u // 2 % 4, i, lo:hi].unsqueeze(1).broadcast_to([P, HU, hi - lo])
                nc.vector.tensor_tensor(rows[:, u % 3, :, D64:P], a[:, :, D64:P], tab(0, 0, 64), ALU.mult)
                nc.vector.tensor_tensor(sined[:, u % 2, :, 0:32], a[:, :, D64 + 32:P], tab(1, 0, 32), ALU.mult)
                nc.vector.tensor_tensor(sined[:, u % 2, :, 32:64], a[:, :, D64:D64 + 32], tab(1, 32, 64), ALU.mult).then_inc(rotated, 1)

        @block.gpsimd
        def _(pool):
            for u in range(U):
                pool.wait_ge(rotated, u + 1)
                rope = rows[:, u % 3, :, D64:P]
                nc.gpsimd.tensor_tensor(rope, rope, sined[:, u % 2], ALU.add).then_inc(added, 1)


def l3_xattn(core):
    nc, io = core.nc, core.io
    x = core.xT
    SCALE = float(np.float32(1.0) / np.sqrt(2 * D64).astype(np.float32))
    with ExitStack() as mem:
        sb = lambda shape, name="work": core.buffer(mem, shape, name)
        W = {n: sb(list(io["L3_xattn_" + n].shape), n) for n in ("w_kv_comp", "w_q_down", "w_q", "w_k_up", "w_k_rope", "w_v_up", "w_out")}
        seg = core.buffer(mem, [P, TILES], "segment", I32)
        core.fetch("l3x", core.consts(mem, "rot", "cos", "sin", "keyno", "rotary") + [(W[n], io["L3_xattn_" + n]) for n in W]
                   + [(seg, io["segment"])])
        core.need("l3x")
        q, k, kr = sb([P, TILES, H16, P], "queries"), sb([P, H16, CT], "keys"), sb([P, CT], "k_rope")
        v, kvc, qc, o = sb([KT, 4, INNER], "v"), sb([P, CT], "kv_comp"), sb([P, N], "q_down"), sb([P, TILES, WC, P], "o")
        mask, segf, near = sb([P, TILES, SK], "mask"), sb([P, TILES], "segf"), sb([P, TILES, SK], "near")
        products(core, by_block(kvc, W["w_kv_comp"], core.ctx, n=CT) + by_block(qc, W["w_q_down"], x))
        jobs = by_block(kr, W["w_k_rope"], kvc, n=CT)
        jobs += [plain(k[0:D64, h, :], [(W["w_k_up"][:, D64 * h:D64 * h + D64], kvc)]) for h in range(H16)]
        jobs += [plain(v[:, i, BLK * j:BLK * j + BLK], [(kvc[:, KT * i:KT * i + KT], W["w_v_up"][:, BLK * j:BLK * j + BLK])]) for i in range(4) for j in range(2)]
        products(core, jobs)
        rotate(core, [(kr[:, SK * b:SK * b + SK], core.const["cos"], core.const["sin"], None) for b in range(B)])
        with core.stage("dve_step", "keys_spread") as (block, dve_step, keys_spread):
            @block.scalar
            def _(act):
                for h in range(H16):
                    nc.scalar.copy(k[D64:P, h, :], kr[D64:P]).then_inc(keys_spread, 1)

            @block.vector
            def _(dve):
                link = chained(dve, dve_step)
                link(nc.vector.tensor_copy(segf, seg))
                link(nc.vector.tensor_tensor(mask, core.const["keyno"].unsqueeze(1).broadcast_to([P, TILES, SK]),
                                             segf.unsqueeze(2).broadcast_to([P, TILES, SK]), ALU.subtract))
                link(nc.vector.tensor_scalar(near, mask, -2.0, None, ALU.is_ge))
                link(nc.vector.tensor_scalar(mask, mask, 0.0, None, ALU.is_le))
                link(nc.vector.tensor_tensor(mask, mask, near, ALU.mult))
                link(nc.vector.tensor_scalar(mask, mask, 1.0, BIG, ALU.subtract, ALU.mult))
        rotary_queries(core, W["w_q"], qc, q)
        units = [(t, h, [(0, q[:, t, h, :], k[:, h, SK * (t // 4):SK * (t // 4) + SK], True, True)],
                  [v[:, 2 * (t // 4) + i, D64 * h:D64 * h + D64] for i in range(2)]) for t in range(TILES) for h in range(H16)]
        attend(core, units, XKEYS, D64, lambda t: o[:, t].rearrange("p c q -> p (c q)"), SCALE, lambda u: [(0, SK, mask[:, u[0], :])], nk=SK)
        turn_heads(core, o)
        normalise(core, x, x, XBLOCKS, terms=[(W["w_out"][:, c, :], o[:, :, c, :]) for c in range(WC)])


def turn_heads(core, a):
    transposes(core, [(a[:, t, c:c + 4, :], [a[:, t, c + i, :] for i in range(4)]) for t in range(TILES) for c in (0, 4)])


def l3_ffn(core):
    nc, io = core.nc, core.io
    x = core.xT
    E, R, O = 16, 64, 512
    with ExitStack() as mem:
        sb = lambda shape, name="work": core.buffer(mem, shape, name)
        F = lambda n: io["L3_ffn_" + n]
        names = {"proj": [P, E], "C": [E, 2, R], "Win1": [P, R], "Wout1": [R, O], "Win2": [P, 4, R], "Wout2": [R, P], "bias": [R, 2]}
        W = {n: sb(s, n) for n, s in names.items()}
        core.fetch("l3f", core.consts(mem, "restart16", "rank", "invrank") + [(W[n], F(n)) for n in W])
        core.need("l3f")
        z, zs, rest, cum, cq, t1, t2 = (sb([P, TILES, E], n) for n in ("z", "sorted", "rest", "mean", "meansq", "work", "tau"))
        m, s1 = sb([P, TILES], "row"), sb([P, TILES], "row2")
        per = lambda a: a.unsqueeze(2).broadcast_to([P, TILES, E])
        flat = lambda a: a.rearrange("p t e -> p (t e)")
        products(core, [plain(z[:, t, :], [(x[:, P * t:P * t + P], W["proj"])]) for t in range(TILES)])
        with core.stage("dve_step", "var_ready", "std_done", "delta_ready", "root_done") as (block, dve_step, var_ready, std_done, delta_ready, root_done):
            @block.vector
            def _(dve):
                link = chained(dve, dve_step)
                link(nc.vector.reduce_sum(m, z, AX))
                link(nc.vector.tensor_scalar(m, m, 1.0 / E, None, ALU.mult))
                link(nc.vector.tensor_tensor(z, z, per(m), ALU.subtract))
                link(nc.vector.tensor_tensor(t1, z, z, ALU.mult))
                link(nc.vector.reduce_sum(m, t1, AX))
                nc.vector.tensor_scalar(m, m, 1.0 / E, None, ALU.mult).then_inc(var_ready, 1)
                dve.wait_ge(std_done, 1)
                link(nc.vector.reciprocal(m, m))
                link(nc.vector.tensor_tensor(z, z, per(m), ALU.mult))
                link(nc.vector.tensor_scalar(z, z, 0.5, None, ALU.mult))
                link(nc.vector.reduce_max(m, z, AX))
                link(nc.vector.tensor_tensor(z, z, per(m), ALU.subtract))
                for t in range(TILES):
                    link(nc.vector.max(zs[:, t, 0:8], z[:, t, :]))
                for t in range(TILES):
                    link(nc.vector.match_replace(rest[:, t, :], zs[:, t, 0:8], z[:, t, :], -BIG))
                for t in range(TILES):
                    link(nc.vector.max(zs[:, t, 8:16], rest[:, t, :]))
                link(nc.vector.tensor_tensor(t1, zs, zs, ALU.mult))
                link(nc.vector.tensor_tensor_scan(flat(cum), core.const["restart16"], flat(zs), 0.0, ALU.mult, ALU.add))
                link(nc.vector.tensor_tensor_scan(flat(cq), core.const["restart16"], flat(t1), 0.0, ALU.mult, ALU.add))
                link(nc.vector.tensor_tensor(flat(cum), flat(cum), core.const["invrank"], ALU.mult))
                link(nc.vector.tensor_tensor(flat(cq), flat(cq), core.const["invrank"], ALU.mult))
                link(nc.vector.tensor_tensor(t1, cum, cum, ALU.mult))
                link(nc.vector.tensor_tensor(t1, cq, t1, ALU.subtract))
                link(nc.vector.tensor_tensor(flat(t1), flat(t1), core.const["rank"], ALU.mult))
                link(nc.vector.tensor_scalar(t1, t1, -1.0, 1.0, ALU.mult, ALU.add))
                link(nc.vector.tensor_tensor(flat(t1), flat(t1), core.const["invrank"], ALU.mult))
                nc.vector.tensor_scalar(t1, t1, 0.0, None, ALU.max).then_inc(delta_ready, 1)
                dve.wait_ge(root_done, 1)
                link(nc.vector.tensor_tensor(t2, cum, t1, ALU.subtract))
                link(nc.vector.tensor_tensor(t1, t2, zs, ALU.is_le))
                link(nc.vector.reduce_sum(m, t1, AX))
                link(nc.vector.tensor_tensor(t1, core.const["rank"].rearrange("p (t e) -> p t e", e=E), per(m), ALU.is_equal))
                link(nc.vector.tensor_tensor(t1, t1, t2, ALU.mult))
                link(nc.vector.reduce_sum(m, t1, AX))
                link(nc.vector.tensor_tensor(z, z, per(m), ALU.subtract))
                link(nc.vector.tensor_scalar(z, z, 0.0, None, ALU.max))
                link(nc.vector.tensor_tensor(z, z, z, ALU.mult))

            @block.scalar
            def _(act):
                act.wait_ge(var_ready, 1)
                nc.scalar.activation(m, m, ACT.Sqrt, bias=core.const["cols"][:, 0:1]).then_inc(std_done, 1)
                act.wait_ge(delta_ready, 1)
                nc.scalar.activation(t1, t1, ACT.Sqrt).then_inc(root_done, 1)
        aT, g, z1, h, z2 = sb([E, N], "weights"), sb([R, 2, N], "gates"), sb([R, N], "z1"), sb([P, 4, N], "h"), sb([R, N], "z2")
        transposes(core, [(aT[:, P * t:P * t + 4 * P], [z[:, t + i, :] for i in range(4)]) for t in (0, 4)])
        products(core, by_block(g[:, 0, :], W["C"][:, 0, :], aT) + by_block(g[:, 1, :], W["C"][:, 1, :], aT)
                 + by_block(z1, W["Win1"], x, None, 1.0, W["bias"][:, 0:1]))

        def gated(a, i):
            with core.stage("gated") as (block, done):
                @block.vector
                def _(dve):
                    nc.vector.tensor_tensor(a, a, g[:, i, :], ALU.mult).then_inc(done, 1)
        gated(z1, 0)
        products(core, [j for c in range(4) for j in by_block(h[:, c, :], W["Wout1"][:, P * c:P * c + P], z1, ACT.Gelu)])
        products(core, [plain(z2[:, BLK * n:BLK * n + BLK], [(W["Win2"][:, c, :], h[:, c, BLK * n:BLK * n + BLK]) for c in range(4)], None, 1.0, W["bias"][:, 1:2])
                        for n in range(NB)])
        gated(z2, 1)
        normalise(core, x, x, XBLOCKS, terms=[(W["Wout2"], z2)])


def turn_tokens(core, dstT, src):
    transposes(core, [(dstT[:, P * t:P * t + 4 * P], [src[:, t + i, :] for i in range(4)]) for t in range(0, src.shape[1], 4)])


def network(nc, io, depth=99):
    core = Core(nc, io)
    with ExitStack() as mem:
        sb = lambda shape, name="work": core.buffer(mem, shape, name)
        core.xT = sb([P, N])
        core.ctx = sb([P, CT])
        c = {n: sb(list(io["c_" + n].shape)) for n in ("ident", "mean", "cols")}
        for n, t in c.items():
            core.const[n] = t
        with nc.sbuf_tensor("x_tok", [P, TILES, P], F32) as x_tok, nc.sbuf_tensor("c_tok", [KT, 4, P], F32) as c_tok:
            load(core, [(c[n][:], io["c_" + n]) for n in c] + [
                (x_tok[:], io["x"].rearrange("b (t p) f -> p (b t) f", p=P)),
                (c_tok[:], io["ctx_1024"].rearrange("b (t p) f -> p (b t) f", p=KT))])
            turn_tokens(core, core.xT, x_tok)
            transposes(core, [(core.ctx[:], [c_tok[:, i, :] for i in range(4)])])

        def consts(m, *names):
            ts = {n: core.buffer(m, io["c_" + n].shape, n) for n in names}
            for n, t in ts.items():
                core.const[n] = t
            return [(t[:], io["c_" + n]) for n, t in ts.items()]
        core.consts = consts

        for i, layer in enumerate(LAYERS[:depth]):
            layer(core)

        with nc.sbuf_tensor("y_tok", [P, TILES, P], F32) as y:
            transposes(core, [(y[:, t:t + 4, :], [core.xT[:, P * (t + i):P * (t + i) + P] for i in range(4)]) for t in (0, 4)])
            with core.stage("stored") as (block, stored):
                @block.sync
                def _(sp):
                    sp.dma_start(io["out"].rearrange("b (t p) f -> p (b t) f", p=P), y[:]).then_inc(stored, 16)
                    sp.wait_ge(stored, 16)


LAYERS = [l0_attn, l0_xattn, l0_ffn, l1_attn, l1_xattn, l1_ffn, l2_attn, l2_xattn, l2_ffn, l3_attn, l3_xattn, l3_ffn]


def layouts(inputs):
    a = {n: np.asarray(v) for n, v in inputs.items()}
    i = {"x": a["x"], "ctx_1024": a["ctx_1024"]}
    L = lambda n: a["L0_attn_" + n]
    i["mix"] = np.stack([L("x_" + n)[0, 0] for n in "rwkvag"], 1)
    i["vec"] = np.stack([L(n)[0, 0] for n in ("w0", "a0", "v0", "k_k", "k_a")] + [L("r_k").reshape(P)], 1)
    i["down"] = np.concatenate([L("w1"), L("a1"), L("v1")], 1)
    i["up"] = np.stack([L("w2"), L("a2"), np.concatenate([L("v2"), np.zeros((32, P), np.float32)])], 1)
    for n in ("Wr", "Wk", "Wv", "Wo", "g1", "g2", "ln_w", "ln_b"):
        i["L0_attn_" + n] = L(n)
    i["mask"] = a["mask_BxS2_bk0"].astype(np.int32)
    X = lambda n: a["L0_xattn_" + n]
    for n in ("W_q", "W_kv", "W_out"):
        i["L0_xattn_" + n] = X(n)
    i["L0_xattn_vec"] = np.stack([X("ln_x_g"), X("ln_x_b"), X("ln_l_g"), X("ln_l_b"), np.concatenate([X("q_gamma")] * 2),
                                  np.concatenate([X("k_gamma")] * 2), X("b_out")], 1)
    F = lambda n: a["L0_ffn_" + n]
    i["L0_ffn_router"], i["L0_ffn_router_bias"] = F("router_w").T, F("router_bias")
    i["L0_ffn_gate"] = np.concatenate([F("gate_w"), F("sgate_w").reshape(4, P, P)], 0).transpose(2, 0, 1)
    i["L0_ffn_up"] = np.concatenate([F("up_w"), F("sup_w").reshape(4, P, P)], 0).transpose(2, 0, 1)
    i["L0_ffn_down"] = np.concatenate([F("down_w"), F("sdown_w").reshape(P, 4, P).transpose(1, 0, 2)], 0).transpose(2, 0, 1)
    for n in ("w_Q", "w_K", "w_V"):
        i["L1_attn_" + n] = a["L1_attn_" + n]
    for l in ("L1_xattn_", "L2_xattn_"):
        for n in ("Wq", "Wk", "Wv", "Wo", "bv"):
            i[l + n] = a[l + n]
        i[l + "vec"] = np.stack([a[l + n] for n in ("bq", "bk", "bo")], 1)
    F = lambda n: a["L1_ffn_" + n]
    chunks = lambda w: w.reshape(*w.shape[:-2], WC, P, P).swapaxes(-3, -2)
    pad = lambda w, n, axis: np.concatenate([w, np.zeros(w.shape[:axis] + (n - w.shape[axis],) + w.shape[axis + 1:], w.dtype)], axis)
    one_more = lambda w: np.concatenate([w, w[:1]])
    i["L1_ffn_Wqkv"], i["L1_ffn_Wo"], i["L1_ffn_W1"] = one_more(F("Wqkv")), chunks(F("Wo")), F("W1")
    i["L1_ffn_W2"] = pad(F("W2"), 3 * P, 1).reshape(DEPTH, 3, P, P).transpose(0, 2, 1, 3)
    b1 = pad(F("b1").reshape(DEPTH, 2, DI), 3 * P, 2).reshape(DEPTH, 6, P).transpose(0, 2, 1)
    i["L1_ffn_vec"] = np.concatenate([np.stack([F("ln_g"), F("ln_b"), F("b2")], 2), b1], 2)
    g = np.stack([F("q_scale"), F("k_scale")], 1)
    i["L1_ffn_gains"] = one_more(np.stack([g, np.roll(g, D64 // 2, 2)], 2))
    A = lambda n: a["L2_attn_" + n]
    i["L2_attn_W"], i["L2_attn_Wo"] = A("in_proj_weight").T, A("out_w").T
    bias = A("in_proj_bias").reshape(3, P)
    i["L2_attn_vec"], i["L2_attn_bv"] = np.stack([bias[0], bias[1], A("out_b")], 1), bias[2]
    i["L2_attn_rel"] = np.tile(A("rel_pe")[np.clip(np.arange(EXT) - (P - 1), 0, 2 * REL)].T, (H16, 1))
    i["L2_ffn_W"] = a["L2_ffn_W_experts"].transpose(2, 0, 1)
    i["L2_ffn_router"], i["L2_ffn_b_router"], i["L2_ffn_b_experts"] = a["L2_ffn_W_router"].T, a["L2_ffn_b_router"], a["L2_ffn_b_experts"]
    i["L3_attn_w_qkv"], i["L3_attn_w_gates"], i["L3_attn_w_out"] = a["L3_attn_w_qkv"], a["L3_attn_w_gates"], chunks(a["L3_attn_w_out"])
    X3 = lambda n: a["L3_xattn_" + n]
    i["L3_xattn_w_kv_comp"], i["L3_xattn_w_q_down"] = pad(X3("w_kv_comp"), P, 1), pad(X3("w_q_down"), P, 1)
    by_head = np.stack([X3(n).reshape(-1, H16, D64) for n in ("w_q_up", "w_q_rope")], 2)
    i["L3_xattn_w_q"] = pad(by_head.reshape(-1, 2 * INNER), P, 0)
    i["L3_xattn_w_k_up"], i["L3_xattn_w_v_up"] = pad(X3("w_k_up"), P, 0), pad(X3("w_v_up"), P, 0)
    i["L3_xattn_w_k_rope"] = pad(np.concatenate([X3("w_k_rope")] * 2, 1), P, 0)
    i["L3_xattn_w_out"] = chunks(X3("w_out"))
    i["segment"] = a["itok_BxS_0_511"].reshape(TILES, P).T
    F3 = lambda n: a["L3_ffn_" + n]
    i["L3_ffn_proj"], i["L3_ffn_C"] = F3("proj"), np.stack([F3("C1"), F3("C2")], 1)
    i["L3_ffn_Win1"], i["L3_ffn_Wout1"], i["L3_ffn_Wout2"] = F3("Win1")[:P], F3("Wout1").T, F3("Wout2").T
    i["L3_ffn_Win2"] = F3("Win2")[:512].reshape(4, P, 64).transpose(1, 0, 2)
    i["L3_ffn_bias"] = np.stack([F3("Win1")[P], F3("Win2")[512]], 1)
    i.update({"c_" + n: v for n, v in shape_constants().items()})
    return {n: np.ascontiguousarray(v) for n, v in i.items()}


def build(nc, arrays, depth=99):
    io = {n: nc.dram_tensor("in_" + n, v.shape, mybir.dt.from_np(v.dtype), kind="ExternalInput").ap()
          for n, v in arrays.items()}
    io["out"] = nc.dram_tensor("out", (B, S, P), F32, kind="ExternalOutput").ap()
    network(nc, io, depth)


def kernel(**inputs):
    import concourse.bacc as bacc
    from concourse.bass_utils import run_bass_kernel_spmd

    arrays = layouts(inputs)
    nc = bacc.Bacc("TRN2", target_bir_lowering=False, num_devices=1)
    build(nc, arrays)
    result = run_bass_kernel_spmd(nc, [{"in_" + n: v for n, v in arrays.items()}], core_ids=[0])
    return result.results[0]["out"]
```

```python
from contextlib import ExitStack, contextmanager

import numpy as np

import concourse.bass as bass
from concourse import mybir

F32 = mybir.dt.float32
I32 = mybir.dt.int32
BF16 = mybir.dt.bfloat16
ALU = mybir.AluOpType
ACT = mybir.ActivationFunctionType
AX = mybir.AxisListType.X

P = 128
B = 2
S = 512
N = B * S
TILES = N // P
SK = 154
KT = 77
CT = B * SK
BIG = 3.0e37
BLK = 512
NB = N // BLK
LN_EPS = 1e-5
H16, D8 = 16, 8
PAIRS = 9
D64 = 64
INNER = 1024
WC = INNER // P
DEPTH = 6
DI = 341
WIN = 32
REL = 64
WROWS = 96
STARTS = [0, 96, 192, 288, 384, 416]
WINDOWS = len(STARTS)
EXT = 384


def shape_constants():
    p = np.arange(P)
    c = {}
    c["ident"] = np.eye(P)
    c["mean"] = np.full((P, P), 1.0 / P)
    c["head64"] = (p[:, None] // D64 == p[None, :] // D64) * 1.0
    c["headmask"] = (p[:, None] // D8 == np.arange(H16)[None, :]) * 1.0
    c["keypart"] = (p[:PAIRS * D8, None] // D8 % 3 == np.arange(3)[None, :]) * 1.0
    c["pick2"] = (p[:, None] // D64 == np.arange(2)[None, :]) * 1.0
    c["modulo32"] = (p[:96, None] % 32 == np.arange(32)[None, :]) * 1.0
    rot = np.zeros((P, P))
    for h in range(2):
        for d in range(32):
            rot[64 * h + 32 + d, 64 * h + d] = -1.0
            rot[64 * h + d, 64 * h + 32 + d] = 1.0
    c["rot"] = rot
    half = np.arange(0, D64, 2, dtype=np.float64)
    inv = (1.0 / 10000.0 ** (half / D64)).astype(np.float32)
    t = np.arange(S, dtype=np.float32)
    fr = (t[:, None] * inv[None, :]).astype(np.float32).astype(np.float64)
    base = (half + 0.4 * D64) / (1.4 * D64)
    sc = base[None, :] ** ((t[:, None] - S // 2) / (WIN // 2))
    def rotary(scale):
        a = np.stack([np.concatenate([np.cos(fr)] * 2, 1), np.concatenate([-np.sin(fr), np.sin(fr)], 1)], 1)
        return (a * np.concatenate([scale, scale], 1)[:, None, :]).reshape(4, P, 2, D64).transpose(1, 0, 2, 3)
    c["rotary"] = rotary(np.ones_like(sc))
    c["xpos"] = np.stack([rotary(sc), rotary(1.0 / sc)], 1)
    wide = lambda a: np.concatenate([a, a, a, a], 1).T
    c["cos"], c["sin"] = wide(np.cos(fr))[:, :SK], wide(np.sin(fr))[:, :SK]
    i, j = np.arange(WROWS)[:, None], np.arange(P)[None, :]
    band = (j >= i) & (j <= i + WIN)
    c["band"] = np.stack([np.where(band & (j >= WIN), 0, -BIG), np.where(band, 0, -BIG)], 1)
    c["slide"] = np.concatenate([np.zeros((P, WROWS)), np.eye(P), np.zeros((P, WROWS))], 1)
    i = p[:, None]
    k = np.arange(SK)[None, :]
    c["xcausal"] = np.stack([np.where(k <= i, 0, -BIG), np.where(k <= i + P, 0, -BIG)], 1)
    c["keyno"] = np.broadcast_to(k * 1.0, (P, SK))
    c["upper"] = (p[:, None] <= p[None, :]) * 1.0
    c["supper"] = (p[:, None] < p[None, :]) * 1.0
    lv = []
    for m in (1, 2, 4, 8, 16, 32, 64):
        same = p[:, None] // (2 * m) == p[None, :] // (2 * m)
        lv.append(same * (p[:, None] % (2 * m) < m) * (p[None, :] % (2 * m) >= m) * 1.0)
    c["levels"] = np.stack(lv, 1)
    c["restart128"] = np.broadcast_to((np.arange(N) % P != 0) * 1.0, (P, N))
    c["restart16"] = np.broadcast_to((p % 16 != 0) * 1.0, (P, P))
    c["rank"] = np.broadcast_to(p % 16 + 1.0, (P, P))
    c["invrank"] = np.broadcast_to(1.0 / (p % 16 + 1.0), (P, P))
    c["cols"] = np.broadcast_to(np.array([LN_EPS, 6.4e-4, 1.0, 0.0]), (P, 4))
    return {n: np.ascontiguousarray(a, dtype=np.float32) for n, a in c.items()}


class Core:

    def __init__(self, nc, io):
        self.nc, self.io = nc, io
        self.ps = nc.alloc_psum_tensor("ps", [P, 8, BLK], F32)
        self.stale = []
        self.const = {}
        self.count = 0
        self.orders = []
        self.fetched = {}
        self.ahead = {}
        self.later = []

    def buffer(self, mem, shape, name="work", dtype=F32):
        self.count += 1
        return mem.enter_context(self.nc.sbuf_tensor(f"{name}_{self.count}", list(shape), dtype))[:]

    def bank(self, i, n=1):
        return self.ps[:, i:i + n, :].rearrange("p b c -> p (b c)")

    @contextmanager
    def stage(self, *names):
        nc = self.nc
        self.count += 1
        sems = [nc.alloc_semaphore(f"{n}_{self.count}") for n in names]
        stale, self.stale = self.stale, []
        with nc.Block(no_gpsimd_drain=True) as block:
            orders, self.orders = self.orders, []
            if orders:
                @block.sync
                def _(sp):
                    for tag, dst, src in orders:
                        sp.dma_start(dst, src).then_inc(self.fetched[tag][0], 16)
            if stale:
                @block.gpsimd
                def _(pool):
                    for s in stale:
                        pool.sem_clear(s)
            yield (block, *sems)
        for s in stale:
            nc.release_semaphore(s)
        self.stale = sems

    def fetch(self, tag, pairs):
        self.fetched[tag] = (self.nc.alloc_semaphore("fetched_" + tag), 16 * len(pairs))
        self.orders += [(tag, dst, src) for dst, src in pairs]

    def weights(self, tag, mem, make):
        return self.ahead.pop(tag) if tag in self.ahead else make(self, mem)

    def reserve(self, tag, mem, make):
        orders, self.orders = self.orders, []
        self.ahead[tag] = make(self, mem)
        self.orders, self.later = orders, self.later + self.orders

    def start_ahead(self):
        self.orders, self.later = self.orders + self.later, []

    def need(self, *tags, zeros=()):
        with self.stage("cleared_by_dve", "cleared_by_pool") as (block, by_dve, by_pool):
            if zeros:
                @block.vector
                def _(dve):
                    for a in zeros[0::2]:
                        self.nc.vector.memset(a, 0.0).then_inc(by_dve, 1)

                @block.gpsimd
                def _(pool):
                    for a in zeros[1::2]:
                        self.nc.gpsimd.memset(a, 0.0).then_inc(by_pool, 1)
                    pool.wait_ge(by_pool, len(zeros[1::2]))

            @block.sync
            def _(sp):
                for tag in tags:
                    sp.wait_ge(*self.fetched[tag])

    def settle(self):
        with self.stage():
            pass


def chained(eng, sem):
    done = [0]

    def link(ins):
        done[0] += 1
        ins.then_inc(sem, 1)
        eng.wait_ge(sem, done[0])
    return link


def load(core, pairs):
    with core.stage("loaded_by_sync", "loaded_by_act") as (block, by_sync, by_act):
        @block.sync
        def _(sp):
            for dst, src in pairs[0::2]:
                sp.dma_start(dst, src).then_inc(by_sync, 16)
            sp.wait_ge(by_sync, 16 * len(pairs[0::2]))

        if pairs[1::2]:
            @block.scalar
            def _(act):
                for dst, src in pairs[1::2]:
                    act.dma_start(dst, src).then_inc(by_act, 16)
                act.wait_ge(by_act, 16 * len(pairs[1::2]))


def load_meanwhile(block, loaded, pairs):
    @block.sync
    def _(sp):
        for dst, src in pairs:
            sp.dma_start(dst, src).then_inc(loaded, 16)
        sp.wait_ge(loaded, 16 * len(pairs))


def products(core, jobs, ring=8):
    nc = core.nc
    by_act = [j % 2 == 0 or jobs[j][2] is not None for j in range(len(jobs))]
    acts = lambda j: sum(by_act[:j + 1])
    dves = lambda j: j + 1 - acts(j)

    def halves(j):
        out = jobs[j][0]
        return list(zip(out, (spot(j)[0:D64], spot(j)[D64:P]))) if isinstance(out, tuple) else [(out, spot(j))]

    def spot(j):
        out = jobs[j][0]
        if isinstance(out, tuple):
            return core.bank(j % ring)[:, 0:out[0].shape[-1]]
        m, n = out.shape[0], int(np.prod(out.shape[1:]))
        v = core.bank(j % ring)[0:m, 0:n]
        if len(out.shape) == 3:
            v = v.rearrange("p (a b) -> p a b", a=out.shape[1])
        return v

    with core.stage("product_done", "emptied_by_act", "emptied_by_dve") as (block, product_done, emptied_a, emptied_v):
        @block.tensor
        def _(pe):
            for j, (out, terms, *_) in enumerate(jobs):
                if j >= ring:
                    if by_act[j - ring]:
                        pe.wait_ge(emptied_a, acts(j - ring))
                    else:
                        pe.wait_ge(emptied_v, dves(j - ring))
                for k, (lhsT, rhs) in enumerate(terms):
                    mm = nc.tensor.matmul(spot(j), lhsT, rhs, start=(k == 0), stop=(k == len(terms) - 1))
                mm.then_inc(product_done, 1)

        @block.scalar
        def _(act):
            for j, (out, terms, func, scale, bias) in enumerate(jobs):
                if by_act[j]:
                    act.wait_ge(product_done, j + 1)
                    for dst, src in halves(j):
                        ins = nc.scalar.activation(dst, src, func or ACT.Identity, scale=scale, bias=0.0 if bias is None else bias)
                    ins.then_inc(emptied_a, 1)

        @block.vector
        def _(dve):
            for j, (out, terms, func, scale, bias) in enumerate(jobs):
                if not by_act[j]:
                    dve.wait_ge(product_done, j + 1)
                    for dst, src in halves(j):
                        if bias is None:
                            ins = nc.vector.tensor_scalar(dst, src, scale, None, ALU.mult)
                        else:
                            ins = nc.vector.tensor_scalar(dst, src, scale, bias, ALU.mult, ALU.add)
                    ins.then_inc(emptied_v, 1)


def transposes(core, jobs, ring=8, dst=None, terms=()):
    nc = core.nc

    def spot(j, k):
        a = jobs[j][1][k]
        w = a.shape[0]
        return core.bank(j % ring)[0:a.shape[1], w * k:w * k + w]

    def whole(j):
        out, ins = jobs[j]
        v = core.bank(j % ring)[0:out.shape[0], 0:len(ins) * ins[0].shape[0]]
        if len(out.shape) == 3:
            v = v.rearrange("p (a b) -> p a b", a=out.shape[1])
            if len(ins) == out.shape[1]:
                v = v[:, :, ins[0].shape[0] - out.shape[2]:]
        return v

    with core.stage("turned", "copied_by_act", "copied_by_dve", "projected", "added") as (block, turned, copied_a, copied_v, projected, added):
        @block.tensor
        def _(pe):
            for j, (out, ins) in enumerate(jobs):
                if j >= ring:
                    pe.wait_ge(copied_v if j % 2 else copied_a, (j - ring) // 2 + 1)
                for k, a in enumerate(ins):
                    mm = nc.tensor.transpose(spot(j, k), a, core.const["ident"][0:a.shape[0], 0:a.shape[0]])
                mm.then_inc(turned, 1)
            for n in range(NB if terms else 0):
                made = len(jobs) // NB * (n + 1)
                pe.wait_ge(copied_a, made // 2)
                pe.wait_ge(copied_v, made // 2)
                for i, (lhsT, rhs) in enumerate(terms):
                    mm = nc.tensor.matmul(core.bank(ring + n), lhsT, columns(rhs, BLK * n, BLK * n + BLK), start=(i == 0), stop=(i == len(terms) - 1))
                mm.then_inc(projected, 1)

        @block.scalar
        def _(act):
            for j in range(0, len(jobs), 2):
                act.wait_ge(turned, j + 1)
                nc.scalar.copy(jobs[j][0], whole(j)).then_inc(copied_a, 1)

        if len(jobs) > 1:
            @block.vector
            def _(dve):
                for j in range(1, len(jobs), 2):
                    dve.wait_ge(turned, j + 1)
                    nc.vector.tensor_copy(jobs[j][0], whole(j)).then_inc(copied_v, 1)
                for n in range(NB if terms else 0):
                    dve.wait_ge(projected, n + 1)
                    d = dst[:, BLK * n:BLK * n + BLK]
                    nc.vector.tensor_tensor(d, core.bank(ring + n), d, ALU.add).then_inc(added, 1)


def normalise(core, src, dst, blocks, gain=None, shift=None, terms=None, bias=None):
    nc = core.nc
    eps = core.const["cols"][:, 0:1]
    with ExitStack() as mem:
        width = sum(b - a for a, b in blocks)
        centred = core.buffer(mem, [P, width], "centred")
        square = core.buffer(mem, [P, width], "square")
        step = P if width % P == 0 else KT
        tiles = [[(c, c + step) for c in range(0, b - a, step)] for a, b in blocks]
        scale = core.buffer(mem, [P, len(blocks), 4], "scale")
        block, projected, summed, mean_done, centred_done, squared, var_done, rooted, inverted, spread, scaled, normed = \
            mem.enter_context(core.stage("projected", "residual_added", "mean_done", "centred", "squared", "var_done",
                                         "std_done", "std_inverted", "spread", "scaled", "normed"))

        def cols(t, k):
            a, b = blocks[k]
            return t[:, a:b]

        def own(t, k):
            a = blocks[0][0]
            return t[:, blocks[k][0] - a:blocks[k][1] - a]

        def bank(k, what):
            return core.bank(4 * (k % 2) + what)[:, 0:blocks[k][1] - blocks[k][0]]

        def by_tile(k):
            return scale[0:tiles[k][0][1], k, 0:len(tiles[k])], core.bank(4 * (k % 2) + 2)[0:tiles[k][0][1], 0:len(tiles[k])]

        @block.tensor
        def _(pe):
            for k in range(len(blocks)):
                if terms:
                    for i, (lhsT, rhs) in enumerate(terms):
                        mm = nc.tensor.matmul(bank(k, 0), lhsT, columns(rhs, *blocks[k]), start=(i == 0), stop=(i == len(terms) - 1))
                    mm.then_inc(projected, 1)
            for k in range(len(blocks)):
                if terms:
                    pe.wait_ge(summed, k + 1)
                nc.tensor.matmul(bank(k, 1), core.const["mean"][:], cols(src, k), start=True, stop=True).then_inc(mean_done, 1)
            for k in range(len(blocks)):
                pe.wait_ge(squared, k + 1)
                for i, (a, b) in enumerate(tiles[k]):
                    mm = nc.tensor.matmul(core.bank(4 * (k % 2) + 2)[0:b - a, i:i + 1], own(square, k)[:, a:b], core.const["mean"][:, 0:1],
                                          start=True, stop=True)
                mm.then_inc(var_done, 1)
            for k in range(len(blocks)):
                pe.wait_ge(inverted, k + 1)
                for i, (a, b) in enumerate(tiles[k]):
                    mm = nc.tensor.matmul(bank(k, 3)[:, a:b], scale[0:b - a, k, i:i + 1].broadcast_to([b - a, P]),
                                          core.const["ident"][0:b - a, 0:b - a], start=True, stop=True)
                mm.then_inc(spread, 1)

        @block.scalar
        def _(act):
            for k in range(len(blocks)):
                act.wait_ge(centred_done, k + 1)
                nc.scalar.activation(own(square, k), own(centred, k), ACT.Square).then_inc(squared, 1)
            for k in range(len(blocks)):
                act.wait_ge(var_done, k + 1)
                to, var = by_tile(k)
                nc.scalar.activation(to, var, ACT.Sqrt, bias=eps[0:to.shape[0]]).then_inc(rooted, 1)
            if gain is not None:
                for k in range(len(blocks)):
                    act.wait_ge(scaled, k + 1)
                    nc.scalar.activation(cols(dst, k), own(centred, k), ACT.Identity, scale=gain, bias=shift).then_inc(normed, 1)

        @block.vector
        def _(dve):
            if terms:
                for k in range(len(blocks)):
                    dve.wait_ge(projected, k + 1)
                    if bias is None:
                        nc.vector.tensor_tensor(cols(src, k), bank(k, 0), cols(src, k), ALU.add).then_inc(summed, 1)
                    else:
                        nc.vector.scalar_tensor_tensor(cols(src, k), bank(k, 0), bias, cols(src, k), ALU.add, ALU.add) \
                            .then_inc(summed, 1)
                dve.wait_ge(summed, len(blocks))
            for k in range(len(blocks)):
                dve.wait_ge(mean_done, k + 1)
                nc.vector.tensor_tensor(own(centred, k), cols(src, k), bank(k, 1), ALU.subtract).then_inc(centred_done, 1)
            dve.wait_ge(centred_done, len(blocks))
            for k in range(len(blocks)):
                dve.wait_ge(rooted, k + 1)
                one = by_tile(k)[0]
                nc.vector.reciprocal(one, one).then_inc(inverted, 1)
            for k in range(len(blocks)):
                dve.wait_ge(spread, k + 1)
                if gain is None:
                    nc.vector.tensor_tensor(cols(dst, k), own(centred, k), bank(k, 3), ALU.mult).then_inc(normed, 1)
                else:
                    if k == 0:
                        dve.wait_ge(squared, len(blocks))
                    nc.vector.tensor_tensor(own(centred, k), own(centred, k), bank(k, 3), ALU.mult).then_inc(scaled, 1)


XBLOCKS = [(0, BLK), (BLK, N)]


def attend(core, units, keytiles, out_width, outs, scale, parts_of=None, nk=None, stream=None, scale_of=None,
           meanwhile=(), R=P, act_copies=True, all_values=False, lag=1):
    nc = core.nc
    heads = len([u for u in units if u[0] == units[0][0]])
    kt = len(keytiles)
    G = max(g for g in (1, 2, 4) if g == 1 or (g * nk <= BLK and g * kt * R <= BLK))
    groups = [units[i:i + G] for i in range(0, len(units), G)]
    n = len(groups)
    sb = -(-G * nk // BLK)
    tb = -(-G * kt * R // BLK)
    SR, TR = (3, 3) if sb == 1 else (2, 1)
    RING = 3
    ahead = SR - 1
    hb = 4 if all_values else min(heads, BLK // out_width)
    per = hb // G
    full = len([k for _, k in keytiles if k == P])
    runs = [(0, kt, keytiles[0][1])] if full in (0, kt) else [(0, full, P), (full, kt, keytiles[-1][1])]

    def score(i):
        return core.bank((i % SR) * sb, sb)[0:R, 0:G * nk].rearrange("p (g k) -> p g k", g=G)

    def turned_at(i):
        return core.bank(SR * sb + (i % TR) * tb, tb)[:, 0:G * kt * R].rearrange("p (g k) -> p g k", g=G)

    def outp(block):
        if all_values:
            own = out_width * (block * hb % heads)
            return core.bank(6 + block % 2)[0:R].rearrange("p (h d) -> p h d", h=hb)[:, :, own:own + out_width]
        return core.bank(6 + block % 2)[0:R, 0:hb * out_width].rearrange("p (h d) -> p h d", h=hb)

    def product_spot(block, h):
        if all_values:
            first = (P - out_width) * (h % hb)
            return core.bank(6 + block % 2)[0:R, first:first + P]
        return outp(block)[:, h % hb, :]

    with ExitStack() as mem:
        prob = core.buffer(mem, [R, RING, G, nk], "prob")
        turned = core.buffer(mem, [P, RING, G, kt * R], "turned")
        top = core.buffer(mem, [R, RING, 2, G], "top")
        tops = core.buffer(mem, [R, 4], "tops")
        masked = core.buffer(mem, [R, RING, G, nk], "masked") if parts_of else None
        sums = core.buffer(mem, [R, 2, hb], "sums")
        block, scores_ready, max_found, max_negated, probs_ready, probs_turned, copied_v, copied_a, values_done, \
            sums_inverted, block_out, parts_added, *streamed, loaded = mem.enter_context(core.stage(
                "scores_ready", "max_found", "max_negated", "probs_ready", "probs_turned", "turned_copied_dve",
                "turned_copied_act", "values_done", "sums_inverted", "block_out", "parts_added",
                "streamed_even", "streamed_odd", "loaded"))

        def copies_on_act(i):
            return act_copies and i % 2 == 1

        def copied(eng, i):
            if act_copies:
                eng.wait_ge(copied_a if i % 2 else copied_v, i // 2 + 1)
            else:
                eng.wait_ge(copied_v, i + 1)

        def spread(eng, copy, done, i):
            eng.wait_ge(probs_turned, i + 1)
            if i >= RING:
                eng.wait_ge(values_done, i - RING + 1)
            for a, b, m in runs:
                ins = copy(turned[0:m, i % RING, :, R * a:R * b], turned_at(i)[0:m, :, R * a:R * b])
            ins.then_inc(done, 1)

        if meanwhile:
            load_meanwhile(block, loaded, meanwhile)

        if stream:
            @block.sync
            def _(sp):
                for t in range(n * G // heads):
                    if t >= 2:
                        sp.wait_ge(max_found, heads // G * (t - 1))
                    for dst, src in stream(t):
                        sp.dma_start(dst, src).then_inc(streamed[t % 2], 16)

        @block.tensor
        def _(pe):
            def scores(i):
                if i >= SR:
                    pe.wait_ge(probs_ready, i - SR + 1)
                for g, (t, h, terms, _) in enumerate(groups[i]):
                    for col, lhsT, rhs, first, last in terms:
                        mm = nc.tensor.matmul(score(i)[:, g, col:col + rhs.shape[-1]], lhsT, rhs, start=first, stop=last)
                mm.then_inc(scores_ready, 1)

            def turn(i):
                pe.wait_ge(probs_ready, i + 1)
                if i >= TR:
                    copied(pe, i - TR)
                for g in range(G):
                    for k, (a, m) in enumerate(keytiles):
                        mm = nc.tensor.transpose(turned_at(i)[0:m, g, R * k:R * k + R], prob[:, i % RING, g, a:a + m],
                                                 core.const["ident"][0:R, 0:R])
                mm.then_inc(probs_turned, 1)

            def values(i):
                copied(pe, i)
                if i % per == 0 and i // per >= 2:
                    pe.wait_ge(block_out, i // per - 1)
                for g, (t, h, _, vals) in enumerate(groups[i]):
                    for k, (a, m) in enumerate(keytiles):
                        mm = nc.tensor.matmul(product_spot(i // per, h), turned[0:m, i % RING, g, R * k:R * k + R], vals[k],
                                              start=(k == 0), stop=(k == kt - 1))
                mm.then_inc(values_done, 1)

            for i in range(ahead):
                scores(i)
            for i in range(n):
                if i + ahead < n:
                    scores(i + ahead)
                turn(i)
                if i >= lag:
                    values(i - lag)
            for i in range(n - lag, n):
                values(i)

        @block.scalar
        def _(act):
            for i in range(n):
                act.wait_ge(max_negated, i + 1)
                if i >= RING:
                    act.wait_ge(probs_turned, i - RING + 1)
                if i % per == 0 and i // per >= 2:
                    act.wait_ge(block_out, i // per - 1)
                for g, unit in enumerate(groups[i]):
                    src = masked[:, i % RING, g, :] if parts_of and parts_of(unit) else score(i)[:, g, :]
                    ins = nc.scalar.activation(prob[:, i % RING, g, :], src, ACT.Exp, bias=top[:, i % RING, 1, g:g + 1],
                                               scale=scale_of(groups[i])[:, g:g + 1] if scale_of else scale,
                                               accum_out=sums[:, i // per % 2, unit[1] % hb:unit[1] % hb + 1])
                ins.then_inc(probs_ready, 1)
                if i >= ahead and copies_on_act(i - ahead):
                    spread(act, nc.scalar.copy, copied_a, i - ahead)
            for i in range(n - ahead, n):
                if copies_on_act(i):
                    spread(act, nc.scalar.copy, copied_a, i)

        @block.vector
        def _(dve):
            def finish(k):
                dve.wait_ge(probs_ready, per * (k + 1))
                nc.vector.reciprocal(sums[:, k % 2, :], sums[:, k % 2, :]).then_inc(sums_inverted, 1)
                dve.wait_ge(sums_inverted, k + 1)
                dve.wait_ge(values_done, per * (k + 1))
                t, h = groups[per * k][0][0], groups[per * k][0][1] // hb * hb
                out = outs(t)[:, h * out_width:(h + hb) * out_width].rearrange("p (h d) -> p h d", h=hb)
                nc.vector.tensor_tensor(out, outp(k), sums[:, k % 2, :].unsqueeze(2).broadcast_to([R, hb, out_width]), ALU.mult) \
                    .then_inc(block_out, 1)

            added = 0
            for i in range(n):
                dve.wait_ge(scores_ready, i + 1)
                if i >= RING:
                    dve.wait_ge(probs_ready, i - RING + 1)
                tile = i * G // heads
                if stream and i * G % heads == 0:
                    dve.wait_ge(streamed[tile % 2], 16 * len(stream(0)) * (tile // 2 + 1))
                best = top[:, i % RING, 0, :]
                if not (parts_of and parts_of(groups[i][0])):
                    ins = nc.vector.reduce_max(best, score(i), AX)
                else:
                    for g, unit in enumerate(groups[i]):
                        parts = parts_of(unit)
                        for k, (a, b, what) in enumerate(parts):
                            to = best[:, g:g + 1] if len(parts) == 1 else tops[:, k:k + 1]
                            into = masked[:, i % RING, g, a:b]
                            if what.shape[-1] == 1:
                                ins = nc.vector.tensor_scalar(into, score(i)[:, g, a:b], what, -BIG, ALU.add, ALU.max, accum_out=to)
                            else:
                                ins = nc.vector.tensor_tensor_reduce(into, score(i)[:, g, a:b], what, 1.0, -BIG, ALU.add, ALU.max, to)
                            if len(parts) > 1:
                                ins.then_inc(parts_added, 1)
                                added += 1
                        if len(parts) > 1:
                            dve.wait_ge(parts_added, added)
                            ins = nc.vector.reduce_max(best[:, g:g + 1], tops[:, 0:len(parts)], AX)
                ins.then_inc(max_found, 1)
                dve.wait_ge(max_found, i + 1)
                if scale_of:
                    ins = nc.vector.scalar_tensor_tensor(top[:, i % RING, 1, :], best, -1.0, scale_of(groups[i]), ALU.mult, ALU.mult)
                else:
                    ins = nc.vector.tensor_scalar(top[:, i % RING, 1, :], best, -scale, None, ALU.mult)
                ins.then_inc(max_negated, 1)
                if i >= ahead and not copies_on_act(i - ahead):
                    spread(dve, nc.vector.tensor_copy, copied_v, i - ahead)
                if i >= per + ahead and (i - ahead) % per == 0:
                    finish((i - ahead) // per - 1)
            for i in range(n - ahead, n):
                if not copies_on_act(i):
                    spread(dve, nc.vector.tensor_copy, copied_v, i)
            for k in range((n - 1 - ahead) // per, n // per):
                finish(k)


def columns(a, lo, hi):
    return a[:, lo:hi] if len(a.shape) == 2 else a[:, lo // P:hi // P, :]


def plain(out, terms, func=None, scale=1.0, bias=None):
    return out, terms, func, scale, bias


def by_block(outT, W, srcT, func=None, scale=1.0, bias=None, n=N):
    m = W.shape[1]
    return [plain(outT[0:m, a:min(a + BLK, n)], [(W[:], srcT[0:W.shape[0], a:min(a + BLK, n)])], func, scale, bias)
            for a in range(0, n, BLK)]


def l0_attn(core):
    nc, io = core.nc, core.io
    x = core.xT
    with ExitStack() as mem:
        sb = lambda shape, name="work": core.buffer(mem, shape, name)
        mix = sb([P, 6])
        vec = sb([P, 7])
        W = {n: sb([P, P]) for n in ("Wr", "Wk", "Wv", "Wo", "g1", "g2")}
        down = sb([P, 160])
        up = sb([D64, 3, P])
        rows = sb([P, 2, P])
        load(core, [(mix[:], io["mix"]), (vec[:, 0:6], io["vec"]), (down[:], io["down"]), (up[:], io["up"])]
             + [(W[n][:], io["L0_attn_" + n]) for n in W]
             + [(rows[:, 0, :], io["L0_attn_ln_w"].unsqueeze(0).broadcast_to([P, P])),
                (rows[:, 1, :], io["L0_attn_ln_b"].unsqueeze(0).broadcast_to([P, P]))])
        load(core, core.consts(mem, "supper", "upper", "levels", "restart128", "pick2"))
        xm = [sb([P, N]) for _ in range(6)]
        xr, xw, xk, xv, xa, xg = xm
        with core.stage("shifted", "dve_step") as (block, shifted, dve_step):
            @block.vector
            def _(dve):
                link = chained(dve, dve_step)
                v = xg[:].rearrange("p (b s) -> p b s", b=B)
                xx = x[:].rearrange("p (b s) -> p b s", b=B)
                nc.vector.tensor_scalar(v[:, :, 0:1], xx[:, :, 0:1], -1.0, None, ALU.mult).then_inc(shifted, 1)
                nc.vector.tensor_tensor(v[:, :, 1:S], xx[:, :, 0:S - 1], xx[:, :, 1:S], ALU.subtract).then_inc(shifted, 1)
                dve.wait_ge(shifted, 2)
                for i in range(6):
                    link(nc.vector.scalar_tensor_tensor(xm[i][:], xg[:], mix[:, i:i + 1], x[:], ALU.mult, ALU.add))
        r, k, v_tok, v = sb([P, N]), sb([P, N]), sb([P, TILES, P]), sb([P, N])
        mid = sb([P, 4, N])
        tok = lambda a, t: a[:, P * t:P * t + P]
        jobs = by_block(r, W["Wr"], xr) + by_block(k, W["Wk"], xk) + by_block(v, W["Wv"], xv)
        jobs += by_block(mid[:, 0, :], down[:, 0:64], xw, ACT.Tanh) + by_block(mid[:, 1, :], down[:, 64:128], xa)
        jobs += by_block(mid[:, 2, :], down[:, 128:160], xv) + by_block(mid[:, 3, :], W["g1"], xg, ACT.Sigmoid)
        products(core, jobs)
        jobs = by_block(xw, up[:, 0, :], mid[0:64, 0, :], ACT.Sigmoid, 1.0, vec[:, 0:1])
        jobs += by_block(xa, up[:, 1, :], mid[0:64, 1, :], ACT.Sigmoid, 1.0, vec[:, 1:2])
        jobs += by_block(xv, up[0:32, 2, :], mid[0:32, 2, :], ACT.Sigmoid, 1.0, vec[:, 2:3])
        products(core, jobs)
        g_tok = sb([P, TILES, P])
        kk, sq, keff, beta, alpha, rt = xk, xr, mid[:, 0, :], mid[:, 1, :], sb([P, N]), sb([P, N])
        cum, dec, mids, ends = sb([P, N]), sb([P, N]), sb([P, TILES]), sb([P, TILES])
        undecay = sb([P, N], "undecay")
        reset, hd, rkr = core.const["restart128"], core.const["head64"], mid[:, 2, :]
        with core.stage("dve_step", "kk_squared", "norms_done", "rooted", "decay_ready", "act_step", "v_mixed") as \
                (block, dve_step, kk_squared, norms_done, rooted, decay_ready, act_step, v_mixed):
            @block.vector
            def _(dve):
                link = chained(dve, dve_step)
                link(nc.vector.tensor_scalar(kk[:], k[:], vec[:, 3:4], None, ALU.mult))
                nc.vector.tensor_tensor(sq[:], kk[:], kk[:], ALU.mult).then_inc(kk_squared, 1)
                link(nc.vector.tensor_scalar(dec[:], xw[:], -float(np.exp(-0.5)), None, ALU.mult))
                link(nc.vector.tensor_tensor_scan(cum[:], reset[:], dec[:], 0.0, ALU.mult, ALU.add))
                c3 = cum[:].rearrange("p (t q) -> p t q", t=TILES)
                link(nc.vector.tensor_copy(mids[:].unsqueeze(2), c3[:, :, 63:64]))
                link(nc.vector.tensor_tensor(c3, c3, mids[:].unsqueeze(2).broadcast_to([P, TILES, P]), ALU.subtract))
                link(nc.vector.tensor_copy(ends[:].unsqueeze(2), c3[:, :, P - 1:P]))
                nc.vector.tensor_tensor(dec[:], cum[:], dec[:], ALU.subtract).then_inc(decay_ready, 1)
                link(nc.vector.tensor_scalar(keff, xa[:], 1.0, vec[:, 4:5], ALU.subtract, ALU.mult))
                link(nc.vector.tensor_scalar(keff, keff, 1.0, None, ALU.add))
                link(nc.vector.tensor_tensor(keff, keff, k[:], ALU.mult))
                link(nc.vector.scalar_tensor_tensor(rkr, r[:], vec[:, 5:6], keff, ALU.mult, ALU.mult))
                dve.wait_ge(rooted, 2)
                link(nc.vector.tensor_scalar(sq[:], sq[:], 1e-12, None, ALU.max))
                link(nc.vector.reciprocal(sq[:], sq[:]))
                link(nc.vector.tensor_tensor(kk[:], kk[:], sq[:], ALU.mult))
                link(nc.vector.tensor_tensor(beta, kk[:], xa[:], ALU.mult))
                dve.wait_ge(act_step, 5)
                dve.wait_ge(v_mixed, 3)
                link(nc.vector.scalar_tensor_tensor(alpha[:], kk[:], -1.0, dec[:], ALU.mult, ALU.mult))
                link(nc.vector.tensor_tensor(rt[:], r[:], cum[:], ALU.mult))
                link(nc.vector.tensor_tensor(beta, beta, undecay[:], ALU.mult))
                link(nc.vector.tensor_tensor(keff, keff, undecay[:], ALU.mult))

            @block.gpsimd
            def _(pool):
                link = chained(pool, v_mixed)
                link(nc.gpsimd.tensor_tensor(alpha[:], v[:], v[:], ALU.subtract))
                link(nc.gpsimd.tensor_tensor(alpha[:], alpha[:], xv[:], ALU.mult))
                link(nc.gpsimd.tensor_tensor(v[:], v[:], alpha[:], ALU.add))

            @block.tensor
            def _(pe):
                pe.wait_ge(kk_squared, 1)
                for n in range(NB):
                    nc.tensor.matmul(core.bank(n), hd[:], sq[:, BLK * n:BLK * n + BLK], start=True, stop=True) \
                        .then_inc(norms_done, 1)

            @block.scalar
            def _(act):
                for n in range(NB):
                    act.wait_ge(norms_done, n + 1)
                    if n == 0:
                        act.wait_ge(norms_done, 2)
                    nc.scalar.activation(sq[:, BLK * n:BLK * n + BLK], core.bank(n), ACT.Sqrt).then_inc(rooted, 1)
                act.wait_ge(decay_ready, 1)
                nc.scalar.activation(undecay[:], cum[:], ACT.Exp, scale=-1.0).then_inc(act_step, 1)
                act.wait_ge(act_step, 1)
                for a in (cum, dec, mids, ends):
                    nc.scalar.activation(a[:], a[:], ACT.Exp).then_inc(act_step, 1)
        rk_tok = sb([P, TILES, 2])
        k_tok, b_tok = W_ = sb([P, TILES, P]), sb([P, TILES, P])
        jobs = [plain(g_tok[:, t:t + 4, :].rearrange("p t f -> p (t f)")[:, P * i:P * i + P], [(mid[:, 3, P * (t + i):P * (t + i) + P], W["g2"][:])])
                for t in (0, 4) for i in range(4)]
        jobs += [plain(rk_tok[:, t, :], [(rkr[:, P * t:P * t + P], core.const["pick2"][:])]) for t in range(TILES)]
        products(core, jobs)
        transposes(core, [(dst[:, t:t + 4, :], [src[:, P * (t + i):P * (t + i) + P] for i in range(4)])
                          for dst, src in ((v_tok, v), (k_tok, keff), (b_tok, beta)) for t in (0, 4)])
        G = 16
        U_, M_, Y_, T_ = (sb([P, G, P]) for _ in range(4))
        akT, rbT, rkT = (sb([P, G, P]) for _ in range(3))
        at = lambda a, u: a[D64 * (u // TILES):D64 * (u // TILES) + D64, P * (u % TILES):P * (u % TILES) + P]
        four = lambda a, g: a[:, 4 * g:4 * g + 4, :]
        bank4 = lambda i: core.bank(i).rearrange("p (u q) -> p u q", u=4)
        row4 = lambda m: m.unsqueeze(1).broadcast_to([P, 4, P])
        pairs = [(beta, alpha, U_, core.const["supper"]), (keff, alpha, akT, core.const["supper"]),
                 (beta, rt, rbT, core.const["upper"]), (keff, rt, rkT, core.const["upper"])]
        with core.stage("cross_done", "cross_masked", "ones_set") as (block, cross_done, cross_masked, ones_set):
            @block.tensor
            def _(pe):
                for i in range(16):
                    left, right = pairs[i // 4][0:2]
                    if i >= 8:
                        pe.wait_ge(cross_masked, i - 7)
                    for j in range(4):
                        u = 4 * (i % 4) + j
                        mm = nc.tensor.matmul(core.bank(i % 8)[:, P * j:P * j + P], at(left, u), at(right, u), start=True, stop=True)
                    mm.then_inc(cross_done, 1)

            @block.vector
            def _(dve):
                for i in range(16):
                    _, _, dst, mask = pairs[i // 4]
                    dve.wait_ge(cross_done, i + 1)
                    nc.vector.tensor_tensor(four(dst, i % 4), bank4(i % 8), row4(mask[:]), ALU.mult).then_inc(cross_masked, 1)
                for g in range(4):
                    nc.vector.tensor_copy(four(M_, g), row4(core.const["ident"][:])).then_inc(ones_set, 1)
                    nc.vector.tensor_copy(four(Y_, g), row4(core.const["ident"][:])).then_inc(ones_set, 1)
        UL = sb([P, 3, 4, P])
        LV = 7
        core.start_ahead()
        with core.stage("level_masked", "lm_done", "lm_copied", "grown", "inverse_added") as \
                (block, level_masked, lm_done, lm_copied, grown, added):
            @block.tensor
            def _(pe):
                def level_product(s):
                    pe.wait_ge(level_masked, s + 1)
                    if s >= 4:
                        pe.wait_ge(added, 2 * (s - 3))
                    for j in range(4):
                        mm = nc.tensor.matmul(core.bank(s % 2)[:, P * j:P * j + P], UL[:, s % 3, j, :], M_[:, 4 * (s % 4) + j, :],
                                              start=True, stop=True)
                    mm.then_inc(lm_done, 1)

                level_product(0)
                for s in range(4 * LV):
                    g = s % 4
                    if s + 1 < 4 * LV:
                        level_product(s + 1)
                    pe.wait_ge(lm_copied, s + 1)
                    if s >= 2:
                        pe.wait_ge(added, 2 * (s - 1))
                    for j in range(4):
                        nc.tensor.matmul(core.bank(2 + s % 2)[:, P * j:P * j + P], Y_[:, 4 * g + j, :], T_[:, 4 * g + j, :], start=True, stop=True)
                    for j in range(4):
                        mm = nc.tensor.matmul(core.bank(4 + s % 2)[:, P * j:P * j + P], T_[:, 4 * g + j, :], Y_[:, 4 * g + j, :], start=True, stop=True)
                    mm.then_inc(grown, 1)

            @block.scalar
            def _(act):
                for s in range(4 * LV):
                    act.wait_ge(lm_done, s + 1)
                    if s >= 4:
                        act.wait_ge(grown, s - 3)
                    nc.scalar.copy(four(T_, s % 4), bank4(s % 2)).then_inc(lm_copied, 1)

            @block.vector
            def _(dve):
                def mask(s):
                    if s >= 3:
                        dve.wait_ge(lm_done, s - 2)
                    nc.vector.tensor_tensor(UL[:, s % 3], four(U_, s % 4), row4(core.const["levels"][:, s // 4, :]), ALU.mult) \
                        .then_inc(level_masked, 1)
                mask(0)
                mask(1)
                for s in range(4 * LV):
                    if s + 2 < 4 * LV:
                        mask(s + 2)
                    dve.wait_ge(grown, s + 1)
                    for i, a in enumerate((M_, Y_)):
                        nc.vector.tensor_tensor(four(a, s % 4), bank4(2 + 2 * i + s % 2), four(a, s % 4), ALU.add).then_inc(added, 1)
        state = sb([P, B, D64])
        W_sb, SA = sb([P, 4, D64]), sb([P, 4, D64])
        y = sb([P, TILES, P])
        comb = sb([P, TILES])
        CH = S // P
        with core.stage("state_ready", "w_done", "w_copied", "sa_done", "sa_copied", "step_done", "y_copied", "dve_step") as \
                (block, state_ready, w_done, w_copied, sa_done, sa_copied, step_done, y_copied, dve_step):
            lane = lambda i: (i % 2, i // 2)
            unit = lambda c, i: TILES * (i // 2) + CH * (i % 2) + c
            hp = lambda i: slice(D64 * (i // 2), D64 * (i // 2) + D64)

            @block.tensor
            def _(pe):
                for c in range(CH):
                    pe.wait_ge(state_ready, c + 1)
                    for i in range(4):
                        b, h = lane(i)
                        u, o = unit(c, i), core.bank(h)[:, D64 * b:D64 * b + D64]
                        nc.tensor.matmul(o, at(alpha, u), state[hp(i), b, :], start=True, stop=False)
                        mm = nc.tensor.matmul(o, akT[:, u, :], v_tok[:, CH * b + c, hp(i)], start=False, stop=True)
                    mm.then_inc(w_done, 1)
                    pe.wait_ge(w_copied, c + 1)
                    for i in range(4):
                        mm = nc.tensor.matmul(core.bank(2)[:, D64 * i:D64 * i + D64], Y_[:, unit(c, i), :], W_sb[:, i, :],
                                              start=True, stop=True)
                    mm.then_inc(sa_done, 1)
                    pe.wait_ge(sa_copied, c + 1)
                    for i in range(4):
                        b, h = lane(i)
                        t = CH * b + c
                        o = core.bank(3 + h)[hp(i), D64 * b:D64 * b + D64]
                        nc.tensor.matmul(o, b_tok[:, t, hp(i)], SA[:, i, :], start=True, stop=False)
                        nc.tensor.matmul(o, k_tok[:, t, hp(i)], v_tok[:, t, hp(i)], start=False, stop=True)
                    for i in range(4):
                        b, h = lane(i)
                        u, o = unit(c, i), core.bank(5 + h)[:, D64 * b:D64 * b + D64]
                        nc.tensor.matmul(o, at(rt, u), state[hp(i), b, :], start=True, stop=False)
                        nc.tensor.matmul(o, rbT[:, u, :], SA[:, i, :], start=False, stop=False)
                        mm = nc.tensor.matmul(o, rkT[:, u, :], v_tok[:, CH * b + c, hp(i)], start=False, stop=True)
                    mm.then_inc(step_done, 1)

            @block.vector
            def _(dve):
                link = chained(dve, dve_step)
                m3, e3 = (a[:].rearrange("p (b c) -> p b c", b=B) for a in (mids, ends))
                c3 = comb[:].rearrange("p (b c) -> p b c", b=B)
                link(nc.vector.memset(comb[:], 1.0))
                link(nc.vector.tensor_tensor(c3[:, :, 0:CH - 1], e3[:, :, 0:CH - 1], m3[:, :, 1:CH], ALU.mult))
                nc.vector.memset(state[:], 0.0).then_inc(state_ready, 1)
                for c in range(CH):
                    dve.wait_ge(w_done, c + 1)
                    nc.vector.tensor_copy(W_sb[:].rearrange("p (h b) d -> p h (b d)", h=2), core.ps[:, 0:2, 0:P]).then_inc(w_copied, 1)
                    dve.wait_ge(sa_done, c + 1)
                    nc.vector.tensor_copy(SA[:].rearrange("p a b -> p (a b)"), core.bank(2)[:, 0:256]).then_inc(sa_copied, 1)
                    dve.wait_ge(step_done, c + 1)
                    if c + 1 < CH:
                        for h in range(2):
                            q = slice(D64 * h, D64 * h + D64)
                            link(nc.vector.tensor_tensor(state[q].rearrange("p a b -> p (a b)"), core.bank(3 + h)[q, 0:P],
                                                         state[q].rearrange("p a b -> p (a b)"), ALU.add))
                        for b in range(B):
                            ins = nc.vector.tensor_scalar(state[:, b, :], state[:, b, :], comb[:, CH * b + c:CH * b + c + 1],
                                                          None, ALU.mult)
                            if b == 0:
                                link(ins)
                        ins.then_inc(state_ready, 1)
                    for b in range(B):
                        nc.vector.tensor_copy(y[:, CH * b + c, :].rearrange("p (h d) -> p h d", h=2), core.ps[:, 5:7, D64 * b:D64 * b + D64]).then_inc(y_copied, 1)
                    dve.wait_ge(y_copied, 2 * (c + 1))
        mean, var = sb([P, G]), sb([P, G])
        with core.stage("dve_step", "var_ready", "rooted") as (block, dve_step, var_ready, rooted):
            y3 = y[:].rearrange("p t (h d) -> p (t h) d", h=2)
            s3 = g3 = M_[:].rearrange("p u q -> p (u q)")[:, 0:N].rearrange("p (g d) -> p g d", g=G)
            per = lambda a: a[:].unsqueeze(2).broadcast_to([P, G, D64])

            @block.vector
            def _(dve):
                link = chained(dve, dve_step)
                link(nc.vector.reduce_sum(mean[:], y3, AX))
                link(nc.vector.tensor_scalar(mean[:], mean[:], 1.0 / D64, None, ALU.mult))
                link(nc.vector.tensor_tensor(y3, y3, per(mean), ALU.subtract))
                link(nc.vector.tensor_tensor(s3, y3, y3, ALU.mult))
                link(nc.vector.reduce_sum(var[:], s3, AX))
                nc.vector.tensor_scalar(var[:], var[:], 1.0 / D64, None, ALU.mult).then_inc(var_ready, 1)
                dve.wait_ge(rooted, 1)
                link(nc.vector.reciprocal(var[:], var[:]))
                link(nc.vector.tensor_tensor(y3, y3, per(var), ALU.mult))
                for row, op in ((0, ALU.mult), (1, ALU.add)):
                    link(nc.vector.tensor_tensor(y[:], y[:], rows[:, row, :].unsqueeze(1).broadcast_to([P, TILES, P]), op))
                v3 = v_tok[:].rearrange("p t (h d) -> p (t h) d", h=2)
                link(nc.vector.tensor_tensor(s3, v3, rk_tok[:].rearrange("p t h -> p (t h)").unsqueeze(2).broadcast_to([P, G, D64]),
                                             ALU.mult))
                link(nc.vector.tensor_tensor(y3, y3, s3, ALU.add))
                link(nc.vector.tensor_tensor(y[:], y[:], g_tok[:], ALU.mult))

            @block.scalar
            def _(act):
                act.wait_ge(var_ready, 1)
                nc.scalar.activation(var[:], var[:], ACT.Sqrt, bias=core.const["cols"][:, 1:2]).then_inc(rooted, 1)
        turn_tokens(core, xr, y)
        normalise(core, x, x, XBLOCKS, terms=[(W["Wo"][:], xr)])


def head_norm(core, a, width, gain, scale, floor):
    nc = core.nc
    blocks = [(c, min(c + BLK, width)) for c in range(0, width, BLK)]
    with ExitStack() as mem:
        sq = core.buffer(mem, [P, width])
        with core.stage("squared", "summed", "rooted", "dve_step") as (block, squared, summed, rooted, dve_step):
            @block.vector
            def _(dve):
                link = chained(dve, dve_step)
                for c0, c1 in blocks:
                    nc.vector.tensor_tensor(sq[:, c0:c1], a[:, c0:c1], a[:, c0:c1], ALU.mult).then_inc(squared, 1)
                for k, (c0, c1) in enumerate(blocks):
                    dve.wait_ge(rooted, k + 1)
                    link(nc.vector.tensor_scalar(sq[:, c0:c1], sq[:, c0:c1], floor, None, ALU.max))
                    link(nc.vector.reciprocal(sq[:, c0:c1], sq[:, c0:c1]))
                    link(nc.vector.scalar_tensor_tensor(a[:, c0:c1], a[:, c0:c1], gain, sq[:, c0:c1], ALU.mult, ALU.mult))

            @block.tensor
            def _(pe):
                for k, (c0, c1) in enumerate(blocks):
                    pe.wait_ge(squared, k + 1)
                    nc.tensor.matmul(core.bank(k)[:, 0:c1 - c0], core.const["head64"][:], sq[:, c0:c1], start=True, stop=True) \
                        .then_inc(summed, 1)

            @block.scalar
            def _(act):
                for k, (c0, c1) in enumerate(blocks):
                    act.wait_ge(summed, k + 1)
                    nc.scalar.activation(sq[:, c0:c1], core.bank(k)[:, 0:c1 - c0], ACT.Sqrt, scale=scale).then_inc(rooted, 1)


XKEYS = [(0, KT), (KT, KT)]


def l0_xattn_weights(core, mem):
    L = lambda n: core.io["L0_xattn_" + n]
    Wq, Wkv, Wo, vec = (core.buffer(mem, [P, n], "weights") for n in (P, 2 * P, P, 7))
    seen = core.buffer(mem, [P, B, SK], "seen", I32)
    core.fetch("l0x", [(Wq, L("W_q")), (Wkv, L("W_kv")), (Wo, L("W_out")), (vec, L("vec")),
                       (seen, core.io["mask"].unsqueeze(0).broadcast_to([P, B, SK]))])
    return Wq, Wkv, Wo, vec, seen


def l0_xattn(core):
    nc = core.nc
    NK = S + SK
    with ExitStack() as mem:
        sb = lambda shape, name="work": core.buffer(mem, shape, name)
        Wq, Wkv, Wo, vec, seen = core.weights("l0x", mem, l0_xattn_weights)
        core.need("l0x")
        xn, cn, qT, kT = sb([P, N]), sb([P, CT]), sb([P, N], "qT"), sb([P, B, NK], "kT")
        k = sb([P, 2, B, NK], "keys")
        v_tok, v_ctx, o_tok = sb([P, TILES, P], "v"), sb([KT, 4, P], "v_ctx"), sb([P, TILES, P], "o")
        normalise(core, core.xT, xn, XBLOCKS, vec[:, 2:3], vec[:, 3:4])
        normalise(core, core.ctx, cn, [(0, CT)], vec[:, 0:1], vec[:, 1:2])
        jobs = by_block(qT, Wq, xn)
        for b in range(B):
            jobs.append(plain(kT[:, b, 0:S], [(Wkv[:, 0:P], xn[:, S * b:S * b + S])]))
            jobs.append(plain(kT[:, b, S:NK], [(Wkv[:, 0:P], cn[:, SK * b:SK * b + SK])]))
        jobs += [plain(v_tok[:, t, :], [(xn[:, P * t:P * t + P], Wkv[:, P:2 * P])]) for t in range(TILES)]
        jobs += [plain(v_ctx[:, t, :], [(cn[:, KT * t:KT * t + KT], Wkv[:, P:2 * P])]) for t in range(4)]
        products(core, jobs)
        head_norm(core, qT, N, vec[:, 4:5], 1.0 / D64, 1e-8)
        head_norm(core, kT.rearrange("p b k -> p (b k)"), B * NK, vec[:, 5:6], 1.0 / D64, 1e-8)
        mask = sb([P, B, NK], "mask")
        with core.stage("dve_step", "keys_copied") as (block, dve_step, keys_copied):
            @block.scalar
            def _(act):
                for h, hp in ((0, slice(0, D64)), (1, slice(D64, P))):
                    nc.scalar.copy(k[hp, h], kT[hp]).then_inc(keys_copied, 1)

            @block.vector
            def _(dve):
                link = chained(dve, dve_step)
                link(nc.vector.memset(k[0:D64, 1], 0.0))
                link(nc.vector.memset(k[D64:P, 0], 0.0))
                link(nc.vector.memset(mask[:, :, 0:S], 0.0))
                link(nc.vector.tensor_scalar(mask[:, :, S:NK], seen, BIG, -BIG, ALU.mult, ALU.add))
        units = []
        for t in range(TILES):
            for h in range(2):
                hp, b = slice(D64 * h, D64 * h + D64), t // 4
                q = qT[:, P * t:P * t + P]
                units.append((t, h, [(0, q, k[:, h, b, 0:S], True, True), (S, q, k[:, h, b, S:NK], True, True)],
                              [v_tok[:, 4 * b + i, hp] for i in range(4)] + [v_ctx[:, 2 * b + i, hp] for i in range(2)]))
        attend(core, units, [(P * i, P) for i in range(4)] + [(S, KT), (S + KT, KT)], D64, lambda t: o_tok[:, t, :],
               D64 ** -0.5, lambda u: [(0, NK, mask[:, u[0] // 4, :])], nk=NK)
        turn_tokens(core, xn, o_tok)
        normalise(core, core.xT, core.xT, XBLOCKS, terms=[(Wo, xn)], bias=vec[:, 6:7])


def top_weights(core, logits, experts, k, renormalise, w):
    nc = core.nc
    with ExitStack() as mem:
        m = core.buffer(mem, [P, TILES], "row")
        rest = core.buffer(mem, [P, TILES, experts], "rest")
        best = core.buffer(mem, [P, TILES, 8], "best")
        per = lambda a: a.unsqueeze(2).broadcast_to([P, TILES, experts])
        with core.stage("dve_step", "shifted", "act_done") as (block, dve_step, shifted, exp_done):
            @block.vector
            def _(dve):
                link = chained(dve, dve_step)
                link(nc.vector.reduce_max(m, logits, AX))
                nc.vector.tensor_tensor(logits, logits, per(m), ALU.subtract).then_inc(shifted, 1)
                dve.wait_ge(exp_done, 1)
                link(nc.vector.reduce_sum(m, logits, AX))
                link(nc.vector.reciprocal(m, m))
                link(nc.vector.tensor_tensor(logits, logits, per(m), ALU.mult))
                for t in range(TILES):
                    link(nc.vector.max(best[:, t, :], logits[:, t, :]))
                link(nc.vector.memset(best[:, :, k:8], -1.0))
                for t in range(TILES):
                    link(nc.vector.match_replace(rest[:, t, :], best[:, t, :], logits[:, t, :], -1.0))
                link(nc.vector.tensor_tensor(rest, rest, logits, ALU.not_equal))
                link(nc.vector.tensor_tensor(w, rest, logits, ALU.mult))
                if renormalise:
                    link(nc.vector.reduce_sum(m, w, AX))
                    link(nc.vector.tensor_scalar(m, m, 1e-12, None, ALU.max))
                    link(nc.vector.reciprocal(m, m))
                    link(nc.vector.tensor_tensor(w, w, per(m), ALU.mult))

            @block.scalar
            def _(act):
                act.wait_ge(shifted, 1)
                nc.scalar.activation(logits, logits, ACT.Exp).then_inc(exp_done, 1)


def spread_rows(core, mem, w, experts):
    nc = core.nc
    pick, parts = core.buffer(mem, [96, experts, P], "pick", BF16), core.buffer(mem, [96, N], "parts", BF16)
    with ExitStack() as inner:
        ones = core.buffer(inner, [96, 32], "ones")
        rest, short = core.buffer(inner, [P, TILES, experts], "rest"), core.buffer(inner, [P, TILES, experts], "short", BF16)
        cut = core.buffer(inner, [P, TILES, 96], "cut")
        with core.stage("ones_in", "pick_made", "dve_step") as (block, ones_in, pick_made, dve_step):
            @block.sync
            def _(sp):
                sp.dma_start(ones, core.io["c_modulo32"]).then_inc(ones_in, 16)

            @block.scalar
            def _(act):
                act.wait_ge(ones_in, 16)
                nc.scalar.copy(pick, ones[:, 0:experts].unsqueeze(2).broadcast_to([96, experts, P])).then_inc(pick_made, 1)

            @block.vector
            def _(dve):
                link = chained(dve, dve_step)
                link(nc.vector.tensor_copy(rest, w))
                if experts < 32:
                    link(nc.vector.memset(cut, 0.0))
                for i in range(3):
                    part = cut[:, :, 32 * i:32 * i + experts]
                    link(nc.vector.tensor_copy(short, rest))
                    link(nc.vector.tensor_copy(part, short))
                    if i < 2:
                        link(nc.vector.tensor_tensor(rest, rest, part, ALU.subtract))
        transposes(core, [(parts[:, P * t:P * t + 4 * P], [cut[:, t + i, :] for i in range(4)]) for t in (0, 4)])
    return pick, parts


def l0_ffn(core):
    nc, io = core.nc, core.io
    E, SH = 32, 4
    x = core.xT
    with ExitStack() as mem:
        sb = lambda shape, name="work": core.buffer(mem, shape, name)
        gate, up, down = (sb([P, E + SH, P], n) for n in ("gate", "up", "down"))
        router, rbias = sb([P, E], "router"), sb([P, E], "router_bias")
        core.fetch("router", [(router, io["L0_ffn_router"]), (rbias, io["L0_ffn_router_bias"].unsqueeze(0).broadcast_to([P, E]))])
        fetch_experts = lambda g: core.fetch(f"experts{g}", [(t[:, g:g + 4, :], io["L0_ffn_" + n][:, g:g + 4, :])
                                                            for t, n in ((gate, "gate"), (up, "up"), (down, "down"))])
        fetch_experts(0)
        core.need("router")
        logits, w = sb([P, TILES, E], "logits"), sb([P, TILES, E], "weights")
        with core.stage("logits_done", "logits_out") as (block, logits_done, logits_out):
            @block.tensor
            def _(pe):
                for t in range(TILES):
                    mm = nc.tensor.matmul(core.bank(0)[:, E * t:E * t + E], x[:, P * t:P * t + P], router, start=True, stop=True)
                mm.then_inc(logits_done, 1)

            @block.vector
            def _(dve):
                dve.wait_ge(logits_done, 1)
                nc.vector.tensor_tensor(logits, core.bank(0)[:, 0:E * TILES].rearrange("p (t e) -> p t e", e=E),
                                        rbias.unsqueeze(1).broadcast_to([P, TILES, E]), ALU.add).then_inc(logits_out, 1)
        top_weights(core, logits, E, 4, True, w)
        pick, parts = spread_rows(core, mem, w, E)
        U, R = 2 * (E + SH), 2 * E
        act_out, hidden = sb([P, 2, BLK], "gated"), sb([P, 2, BLK], "hidden")
        for g in range(4, E + SH, 4):
            fetch_experts(g)
        core.start_ahead()
        cols = lambda i: slice(BLK * (i % 2), BLK * (i % 2) + BLK)
        with core.stage("inner_done", "silu_done", "hidden_ready", "down_done", "dve_step") as \
                (block, inner_done, silu_done, hidden_ready, down_done, dve_step):
            @block.tensor
            def _(pe):
                def inner(i):
                    e = i // 2
                    if i % 8 == 0:
                        pe.wait_ge(*core.fetched[f"experts{e}"])
                    if i >= 2:
                        pe.wait_ge(hidden_ready, i - 1)
                    nc.tensor.matmul(core.bank(i % 2), gate[:, e, :], x[:, cols(i)], start=True, stop=True)
                    mm = nc.tensor.matmul(core.bank(2 + i % 2), up[:, e, :], x[:, cols(i)], start=True, stop=True)
                    if i < R:
                        mm = nc.tensor.matmul(core.bank(4 + i % 2), pick[:, e, :], parts[:, cols(i)], start=True, stop=True)
                    mm.then_inc(inner_done, 1)

                def outer(i):
                    pe.wait_ge(hidden_ready, i + 1)
                    nc.tensor.matmul(core.bank(6 + i % 2), down[:, i // 2, :], hidden[:, i % 2, :], start=(i < 2),
                                     stop=(i >= U - 2)).then_inc(down_done, 1)

                inner(0)
                for i in range(1, U):
                    inner(i)
                    outer(i - 1)
                outer(U - 1)

            @block.scalar
            def _(act):
                for i in range(U):
                    act.wait_ge(inner_done, i + 1)
                    if i >= 2:
                        act.wait_ge(hidden_ready, i - 1)
                    nc.scalar.activation(act_out[:, i % 2, :], core.bank(i % 2), ACT.Silu).then_inc(silu_done, 1)

            @block.vector
            def _(dve):
                link = chained(dve, dve_step)
                for i in range(U):
                    dve.wait_ge(silu_done, i + 1)
                    if i >= 2:
                        dve.wait_ge(down_done, i - 1)
                    ins = nc.vector.tensor_tensor(hidden[:, i % 2, :], core.bank(2 + i % 2), act_out[:, i % 2, :], ALU.mult)
                    if i < R:
                        link(ins)
                        ins = nc.vector.tensor_tensor(hidden[:, i % 2, :], core.bank(4 + i % 2), hidden[:, i % 2, :], ALU.mult)
                    ins.then_inc(hidden_ready, 1)
                dve.wait_ge(down_done, U)
                for n in range(NB):
                    link(nc.vector.tensor_tensor(x[:, cols(n)], core.bank(6 + n), x[:, cols(n)], ALU.add))
        normalise(core, x, x, XBLOCKS)


def split_rows(core, rows, srcs):
    nc = core.nc
    with ExitStack() as mem:
        rest = [core.buffer(mem, [rows, src.shape[-1]], "rest") for _, src in srcs]
        with core.stage("first_part", "rest_ready", "second_part", "third_part") as (block, first, rest_ready, second, third):
            @block.scalar
            def _(act):
                for parts, src in srcs:
                    nc.scalar.copy(parts[:, 0, :], src).then_inc(first, 1)
                for i, (parts, src) in enumerate(srcs):
                    act.wait_ge(rest_ready, i + 1)
                    nc.scalar.copy(parts[:, 1, :], rest[i]).then_inc(second, 1)

            @block.vector
            def _(dve):
                for i, (parts, src) in enumerate(srcs):
                    dve.wait_ge(first, i + 1)
                    nc.vector.tensor_tensor(rest[i], src, parts[:, 0, :], ALU.subtract).then_inc(rest_ready, 1)
                for i, (parts, src) in enumerate(srcs):
                    dve.wait_ge(second, i + 1)
                    nc.vector.tensor_tensor(parts[:, 2, :], rest[i], parts[:, 1, :], ALU.subtract).then_inc(third, 1)


def stack_heads(core, mem, qT, kT):
    nc = core.nc
    core.count += 1
    stacks = [core.buffer(mem, [PAIRS * D8, H16, a.shape[-1]], n, BF16) for n, a in (("q_stack", qT), ("k_stack", kT))]
    with ExitStack() as inner:
        parts = [core.buffer(inner, [P, 3, a.shape[-1]], "parts", BF16) for a in (qT, kT)]
        split_rows(core, P, [(parts[0], qT), (parts[1], kT)])
        spread = [nc.dram_tensor(f"parts{side}_{core.count}", (3, P, a.shape[-1]), BF16, kind="Internal").ap() for side, a in enumerate((qT, kT))]
        with core.stage("queries_stored", "keys_stored", "queries_stacked", "keys_stacked") as (block, *sems):
            def move(eng, side):
                stored, stacked = sems[side], sems[2 + side]
                eng.dma_start(spread[side].rearrange("i p n -> p i n"), parts[side]).then_inc(stored, 16)
                eng.wait_ge(stored, 16)
                for c in range(PAIRS):
                    part = c % 3 if side else c // 3
                    eng.dma_start(stacks[side][D8 * c:D8 * c + D8], spread[side][part].rearrange("(h d) n -> d h n", d=D8)).then_inc(stacked, 16)
                eng.wait_ge(stacked, 16 * PAIRS)

            @block.sync
            def _(sp):
                move(sp, 0)

            @block.scalar
            def _(act):
                move(act, 1)
    return stacks


def expand_heads(core, dst, src, width):
    nc = core.nc
    with core.stage("spread") as (block, spread):
        @block.vector
        def _(dve):
            for h in range(H16):
                nc.vector.tensor_scalar(dst[:, h, :], src, core.const["headmask"][:, h:h + 1], None, ALU.mult).then_inc(spread, 1)


def narrow_attention(core, q, k, v, o_tok, keytiles, scale, width, parts_of=None, stream=None, lag=1):
    if not stream:
        core.start_ahead()
    units = [(t, h, [(0, q(h, P * t, P), k[:, h, width * (t // 4):width * (t // 4) + width], True, True)],
              v[t // 4])
             for t in range(TILES) for h in range(H16)]
    attend(core, units, keytiles, D8, lambda t: o_tok[:, t, :], scale, parts_of, nk=width, stream=stream, all_values=True, lag=lag)


SELF_KEYS = [(P * i, P) for i in range(4)]


def l1_attn_weights(core, mem):
    W = {n: core.buffer(mem, [P, P], n) for n in ("w_Q", "w_K", "w_V")}
    core.fetch("l1a", [(W[n], core.io["L1_attn_" + n]) for n in W])
    return W


def l1_attn(core):
    with ExitStack() as mem:
        sb = lambda shape, name="work": core.buffer(mem, shape, name)
        W = core.weights("l1a", mem, l1_attn_weights)
        core.need("l1a")
        qT, kT, v, o = sb([P, N], "qT"), sb([P, N], "kT"), sb([P, TILES, P], "v"), sb([P, TILES, P], "o")
        products(core, by_block(qT, W["w_Q"], core.xT) + by_block(kT, W["w_K"], core.xT)
                 + [plain(v[:, t, :], [(core.xT[:, P * t:P * t + P], W["w_V"])]) for t in range(TILES)])
        q, k = stack_heads(core, mem, qT, kT)
        narrow_attention(core, lambda h, a, n: q[:, h, a:a + n], k, [[v[:, 4 * b + i, :] for i in range(4)] for b in range(B)],
                         o, SELF_KEYS, D8 ** -0.5, S, lag=2)
        turn_tokens(core, qT, o)
        normalise(core, core.xT, core.xT, XBLOCKS, terms=[(core.const["ident"], qT)])


def narrow_cross_weights(layer, causal):
    def make(core, mem):
        io = core.io
        W = {n: core.buffer(mem, [P, P], n) for n in ("Wq", "Wk", "Wv", "Wo")}
        vec, bv = core.buffer(mem, [P, 3], "vec"), core.buffer(mem, [P, P], "bv")
        core.fetch(layer, core.consts(mem, "headmask", *(["xcausal"] if causal else [])) + [(W[n], io[layer + n]) for n in W]
                   + [(vec, io[layer + "vec"]), (bv, io[layer + "bv"].unsqueeze(0).broadcast_to([P, P]))])
        return W, vec, bv
    return make


def narrow_cross(core, layer, causal):
    with ExitStack() as mem:
        sb = lambda shape, name="work": core.buffer(mem, shape, name)
        W, vec, bv = core.weights(layer, mem, narrow_cross_weights(layer, causal))
        core.need(layer)
        qT, kT, v, o = sb([P, N], "qT"), sb([P, CT], "kT"), sb([KT, 4, P], "v"), sb([P, TILES, P], "o")
        products(core, by_block(qT, W["Wq"], core.xT, None, 1.0, vec[:, 0:1]) + by_block(kT, W["Wk"], core.ctx, None, 1.0, vec[:, 1:2], CT)
                 + [plain(v[:, i, :], [(core.ctx[:, KT * i:KT * i + KT], W["Wv"])]) for i in range(4)])
        with core.stage("bias_added") as (block, bias_added):
            @block.vector
            def _(dve):
                core.nc.vector.tensor_tensor(v, v, bv[0:KT].unsqueeze(1).broadcast_to([KT, 4, P]), ALU.add).then_inc(bias_added, 1)
        parts_of = (lambda u: [(0, SK, core.const["xcausal"][:, u[0] % 4, :])] if u[0] % 4 < 2 else []) if causal else None
        k = sb([P, H16, CT], "k_heads")
        expand_heads(core, k, kT, CT)
        narrow_attention(core, lambda h, a, n: qT[:, a:a + n], k, [[v[:, 2 * b + i, :] for i in range(2)] for b in range(B)],
                         o, XKEYS, D8 ** -0.5, SK, parts_of)
        turn_tokens(core, qT, o)
        normalise(core, core.xT, core.xT, XBLOCKS, terms=[(W["Wo"], qT)], bias=vec[:, 2:3])


def l1_xattn(core):
    narrow_cross(core, "L1_xattn_", True)


def l2_xattn(core):
    narrow_cross(core, "L2_xattn_", False)


def add_projection(core, dst, terms, bias=None):
    nc = core.nc
    with core.stage("projected", "added") as (block, projected, added):
        @block.tensor
        def _(pe):
            for n in range(NB):
                for i, (lhsT, rhs) in enumerate(terms):
                    mm = nc.tensor.matmul(core.bank(n), lhsT, columns(rhs, BLK * n, BLK * n + BLK), start=(i == 0), stop=(i == len(terms) - 1))
                mm.then_inc(projected, 1)

        @block.vector
        def _(dve):
            for n in range(NB):
                d = dst[:, BLK * n:BLK * n + BLK]
                dve.wait_ge(projected, n + 1)
                if bias is None:
                    nc.vector.tensor_tensor(d, core.bank(n), d, ALU.add).then_inc(added, 1)
                else:
                    nc.vector.scalar_tensor_tensor(d, core.bank(n), bias, d, ALU.add, ALU.add).then_inc(added, 1)


def shift_tokens(core, dst, src, zeros=None):
    nc = core.nc
    with core.stage("shifted", "copied") as (block, shifted, copied):
        s = src.rearrange("p (b s) -> p b s", b=B)

        @block.vector
        def _(dve):
            if zeros is not None:
                nc.vector.memset(zeros, 0.0).then_inc(shifted, 1)
            nc.vector.memset(dst[D64:P, :, 0:1], 0.0).then_inc(shifted, 1)
            nc.vector.tensor_copy(dst[D64:P, :, 1:S], s[D64:P, :, 0:S - 1]).then_inc(shifted, 1)

        @block.scalar
        def _(act):
            nc.scalar.copy(dst[0:D64], s[0:D64]).then_inc(copied, 1)


def rotate(core, units):
    nc = core.nc
    with ExitStack() as mem:
        cosed, sined = core.buffer(mem, [P, 2, BLK], "cosed"), core.buffer(mem, [P, 2, BLK], "sined")
        w = lambda u: units[u][0].shape[-1]
        with core.stage("turned", "cos_taken", "sin_taken", "rotated") as (block, turned, cos_taken, sin_taken, rotated):
            @block.tensor
            def _(pe):
                for u in range(len(units)):
                    if u >= 2:
                        pe.wait_ge(sin_taken, u - 1)
                    nc.tensor.matmul(core.bank(u % 2)[:, 0:w(u)], core.const["rot"], units[u][0], start=True, stop=True).then_inc(turned, 1)

            @block.vector
            def _(dve):
                for u, (a, cos, sin) in enumerate(units):
                    dve.wait_ge(turned, u + 1)
                    if u >= 2:
                        dve.wait_ge(rotated, u - 1)
                    nc.vector.tensor_tensor(sined[:, u % 2, 0:w(u)], core.bank(u % 2)[:, 0:w(u)], sin, ALU.mult).then_inc(sin_taken, 1)

            @block.gpsimd
            def _(pool):
                for u, (a, cos, sin) in enumerate(units):
                    pool.wait_ge(turned, u + 1)
                    nc.gpsimd.tensor_tensor(cosed[:, u % 2, 0:w(u)], a, cos, ALU.mult).then_inc(cos_taken, 1)
                    pool.wait_ge(cos_taken, u + 1)
                    pool.wait_ge(sin_taken, u + 1)
                    nc.gpsimd.tensor_tensor(a, cosed[:, u % 2, 0:w(u)], sined[:, u % 2, 0:w(u)], ALU.add).then_inc(rotated, 1)
                pool.wait_ge(rotated, len(units))


def local_projections(core, Wqkv, gains, table, xs, q, k, v, q_factor):
    nc = core.nc
    with ExitStack() as mem:
        sb = lambda shape, name: core.buffer(mem, shape, name)
        lengths = sb([P, 2, TILES, H16], "lengths")
        square, cosed, sined = sb([P, 2, INNER], "square"), sb([P, 4, INNER], "cosed"), sb([P, INNER], "sined")
        block, tables_ready, q_made, k_made, v_made, squared, rotated, summed, floored, rooted, inverted, added, scaled, \
            q_turned, k_turned, q_copied, k_copied, v_copied, slid = mem.enter_context(core.stage(
                "tables_ready", "queries_made", "keys_made", "values_made", "squared", "rotated", "summed", "floored", "rooted",
                "lengths_inverted", "added", "keys_scaled", "queries_turned", "keys_turned", "queries_copied", "keys_copied", "values_copied", "slid"))
        first_window = lambda t: t + (t + 1) // 2
        made_sem = (q_made, k_made, v_made)
        made = lambda kind: core.bank(2 * kind, 2)
        back = core.bank(6, 2)
        by_head = lambda a: a.rearrange("p (h d) -> p h d", h=H16)

        @block.tensor
        def _(pe):
            def project(t, kind):
                if t >= 1:
                    if kind == 2:
                        pe.wait_ge(v_copied, t)
                    else:
                        pe.wait_ge(rotated, 2 * (t - 1) + kind + 1)
                b, first = (t // WINDOWS, STARTS[t % WINDOWS]) if kind == 2 else (t // 4, WIN + P * (t % 4))
                for half in range(2):
                    mm = nc.tensor.matmul(made(kind)[:, BLK * half:BLK * half + BLK], xs[:, b, first:first + P],
                                          Wqkv[:, INNER * kind + BLK * half:INNER * kind + BLK * half + BLK], start=True, stop=True)
                mm.then_inc(made_sem[kind], 1)

            def turn(s, done):
                for c in range(WC):
                    mm = nc.tensor.transpose(back[:, P * c:P * c + P], cosed[:, s % 4, P * c:P * c + P], core.const["ident"])
                mm.then_inc(done, 1)

            def turn_queries(t):
                pe.wait_ge(added, 2 * t + 1)
                if t >= 2:
                    pe.wait_ge(k_copied, t - 1)
                elif t == 1:
                    pe.wait_ge(q_copied, 1)
                turn(2 * t, q_turned)

            def turn_keys(t):
                pe.wait_ge(scaled, t + 1)
                if t < TILES - 1:
                    pe.wait_ge(q_copied, t + 2)
                else:
                    pe.wait_ge(k_copied, t)
                turn(2 * t + 1, k_turned)

            project(0, 0)
            project(0, 1)
            for t in range(TILES):
                if t + 1 < TILES:
                    project(t + 1, 0)
                project(first_window(t), 2)
                turn_queries(t)
                if t % 2 == 0:
                    project(first_window(t) + 1, 2)
                if t + 1 < TILES:
                    project(t + 1, 1)
                if t >= 1:
                    turn_keys(t - 1)
            pe.wait_ge(inverted, TILES + 1)
            for w in range(B * WINDOWS):
                tile, row = 4 * (w // WINDOWS) + STARTS[w % WINDOWS] // P, STARTS[w % WINDOWS] % P
                pieces = [(tile, row)] + ([(tile + 1, row - P)] if row + WROWS > P else [])
                for i, (t, offset) in enumerate(pieces):
                    mm = nc.tensor.matmul(core.bank(0)[0:WROWS, H16 * w:H16 * w + H16], core.const["slide"][:, WROWS + offset:2 * WROWS + offset],
                                          lengths[:, 0, t, :], start=(i == 0), stop=(i == len(pieces) - 1))
            mm.then_inc(slid, 1)
            turn_keys(TILES - 1)

        @block.scalar
        def _(act):
            def make_square(t, kind):
                act.wait_ge(made_sem[kind], t + 1)
                if t >= 1:
                    act.wait_ge(summed, 2 * (t - 1) + kind + 1)
                nc.scalar.activation(square[:, kind, :], made(kind), ACT.Square).then_inc(squared, 1)

            def copy_values(t):
                act.wait_ge(v_made, t + 1)
                nc.scalar.copy(v[:, t, :], made(2)).then_inc(v_copied, 1)

            def copy_queries(t):
                act.wait_ge(q_turned, t + 1)
                nc.scalar.copy(q[:, :, P * t:P * t + P], back.rearrange("p (c q) -> p c q", c=WC)).then_inc(q_copied, 1)

            def copy_keys(t):
                act.wait_ge(k_turned, t + 1)
                for odd in range(2):
                    half = slice(D64 * odd, D64 * odd + D64)
                    ins = nc.scalar.copy(k[half, odd::2, t // 4, WIN + P * (t % 4):WIN + P * (t % 4) + P],
                                         back[half].rearrange("p (c q) -> p c q", c=WC))
                ins.then_inc(k_copied, 1)

            make_square(0, 0)
            make_square(0, 1)
            for t in range(TILES):
                if t + 1 < TILES:
                    make_square(t + 1, 0)
                copy_values(first_window(t))
                copy_queries(t)
                if t % 2 == 0:
                    copy_values(first_window(t) + 1)
                if t + 1 < TILES:
                    make_square(t + 1, 1)
                act.wait_ge(summed, 2 * t + 2)
                nc.scalar.activation(lengths[:, 1, t, :], lengths[:, 1, t, :], ACT.Sqrt).then_inc(rooted, 1)
                if t == TILES - 1:
                    nc.scalar.activation(lengths[:, 0], lengths[:, 0], ACT.Sqrt).then_inc(rooted, 1)
                if t >= 1:
                    copy_keys(t - 1)
            copy_keys(TILES - 1)

        @block.vector
        def _(dve):
            for side in range(2):
                nc.vector.tensor_tensor(table[:, side], table[:, side],
                                        gains[:, side].unsqueeze(1).broadcast_to([P, 4, 2, D64]), ALU.mult).then_inc(tables_ready, 1)
            dve.wait_ge(tables_ready, 2)

            def invert_keys(t):
                dve.wait_ge(rooted, t + 1)
                one = lengths[:, 1, t, :]
                nc.vector.tensor_scalar(one, one, 1e-12, None, ALU.max).then_inc(floored, 1)
                dve.wait_ge(floored, t + 1)
                nc.vector.reciprocal(one, one).then_inc(inverted, 1)

            for s in range(2 * TILES):
                t, kind = s // 2, s % 2
                dve.wait_ge(squared, s + 1)
                if s >= 4:
                    dve.wait_ge(k_turned if kind else q_turned, t - 1)
                a = by_head(made(kind))
                tab = lambda i, lo, hi: table[:, kind, t % 4, i, lo:hi].unsqueeze(1).broadcast_to([P, H16, hi - lo])
                nc.vector.tensor_tensor(by_head(cosed[:, s % 4, :]), a, tab(0, 0, D64), ALU.mult)
                if s >= 1:
                    dve.wait_ge(added, s)
                sines = by_head(sined)
                nc.vector.tensor_tensor(sines[:, :, 0:32], a[:, :, 32:64], tab(1, 0, 32), ALU.mult)
                nc.vector.tensor_tensor(sines[:, :, 32:64], a[:, :, 0:32], tab(1, 32, 64), ALU.mult).then_inc(rotated, 1)
                nc.vector.reduce_sum(lengths[:, kind, t, :], by_head(square[:, kind, :]), AX).then_inc(summed, 1)
                if kind == 0 and t >= 1:
                    invert_keys(t - 1)
            invert_keys(TILES - 1)
            dve.wait_ge(rooted, TILES + 1)
            all_q = lengths[:, 0]
            nc.vector.tensor_scalar(all_q, all_q, 1e-12, None, ALU.max).then_inc(floored, 1)
            dve.wait_ge(floored, TILES + 1)
            nc.vector.reciprocal(all_q, all_q).then_inc(inverted, 1)
            dve.wait_ge(slid, 1)
            nc.vector.tensor_scalar(q_factor.rearrange("p w h -> p (w h)"), core.bank(0)[0:WROWS, 0:B * WINDOWS * H16], 8.0, None, ALU.mult) \
                .then_inc(floored, 1)

        @block.gpsimd
        def _(pool):
            def scale_keys(t):
                pool.wait_ge(added, 2 * t + 2)
                pool.wait_ge(inverted, t + 1)
                keys = by_head(cosed[:, (2 * t + 1) % 4, :])
                nc.gpsimd.tensor_tensor(keys, keys, lengths[:, 1, t, :].unsqueeze(2).broadcast_to([P, H16, D64]), ALU.mult).then_inc(scaled, 1)

            for s in range(2 * TILES):
                pool.wait_ge(rotated, s + 1)
                nc.gpsimd.tensor_tensor(cosed[:, s % 4, :], cosed[:, s % 4, :], sined, ALU.add).then_inc(added, 1)
                if s >= 2 and s % 2 == 0:
                    scale_keys(s // 2 - 1)
            scale_keys(TILES - 1)


def l1_ffn_weights(core, mem):
    io = core.io
    Wqkv, table, gains = (core.buffer(mem, s, n) for s, n in (([P, 3 * INNER], "Wqkv"), ([P, 2, 4, 2, D64], "table"), ([P, 2, 2, D64], "gains")))

    def loads(depths, d):
        return [(table, io["c_xpos"]), (Wqkv, io["L1_ffn_Wqkv"][depths][d]),
                (gains, io["L1_ffn_gains"][depths][d].unsqueeze(0).broadcast_to([P, 2, 2, D64]))]
    core.fetch("l1f", core.consts(mem, "band", "slide") + loads(slice(0, 1), 0))
    return Wqkv, table, gains, loads


def l1_ffn(core):
    nc, io = core.nc, core.io
    x = core.xT
    D = lambda n: io["L1_ffn_" + n]
    with ExitStack() as mem:
        sb = lambda shape, name="work": core.buffer(mem, shape, name)
        start = nc.dram_tensor("l1_ffn_start", (P, N), F32, kind="Internal").ap()
        core.start_ahead()
        Wqkv, table, gains, first_weights = core.weights("l1f", mem, l1_ffn_weights)
        k = sb([P, H16, B, WIN + S], "keys")
        core.need("l1f")
        with core.stage("stored", "cleared") as (block, stored, cleared):
            @block.vector
            def _(dve):
                nc.vector.memset(k[:, 0:H16 // 2], 0.0).then_inc(cleared, 1)

            @block.gpsimd
            def _(pool):
                nc.gpsimd.memset(k[:, H16 // 2:], 0.0).then_inc(cleared, 1)
                pool.wait_ge(cleared, 2)

            @block.sync
            def _(sp):
                sp.dma_start(start, x).then_inc(stored, 16)
                sp.wait_ge(stored, 16)
        core.settle()
        with nc.Fori(0, DEPTH) as i:
            with ExitStack() as inner:
                ib = lambda shape, name: core.buffer(inner, shape, name)
                q, v = ib([P, WC, N], "q"), ib([P, B * WINDOWS, INNER], "v")
                q_factor = ib([WROWS, B * WINDOWS, H16], "q_factor")
                with ExitStack() as early:
                    xs = core.buffer(early, [P, B, WIN + S], "shifted")
                    shift_tokens(core, xs[:, :, WIN:], x, xs[:, :, 0:WIN])
                    local_projections(core, Wqkv, gains, table, xs, q, k, v, q_factor)
                Wo, W1, W2, vec = ib([P, WC, P], "Wo"), ib([P, 2 * DI], "W1"), ib([P, 3, P], "W2"), ib([P, 9], "vec")
                units = []
                for w in range(B * WINDOWS):
                    for h in range(H16):
                        b, first = w // WINDOWS, STARTS[w % WINDOWS]
                        units.append((w, h, [(0, q[:, h // 2, S * b + first:S * b + first + WROWS], k[:, h, b, first:first + P], True, True)],
                                      [v[:, w, D64 * h:D64 * h + D64]]))
                attend(core, units, [(0, P)], D64, lambda w: v[0:WROWS, w, :], 1.0,
                       lambda u: [(0, P, core.const["band"][:, min(u[0] % WINDOWS, 1), :])], nk=P,
                       scale_of=lambda g: q_factor[:, g[0][0], g[0][1]:g[-1][1] + 1],
                       meanwhile=[(Wo, D("Wo")[i]), (W1, D("W1")[i]), (W2, D("W2")[i]), (vec, D("vec")[i])]
                       + first_weights(slice(1, DEPTH + 1), i),
                       R=WROWS, act_copies=False)
                end = lambda w: S * (w // WINDOWS) + STARTS[w % WINDOWS] + WROWS
                new = lambda w: WROWS if w % WINDOWS == 0 else STARTS[w % WINDOWS] - STARTS[w % WINDOWS - 1]
                transposes(core, [(q[:, c:c + 4, end(w) - new(w):end(w)], [v[0:WROWS, w, P * (c + i):P * (c + i) + P] for i in range(4)])
                                  for w in range(B * WINDOWS) for c in (0, 4)], 6, x, [(Wo[:, c, :], q[:, c, :]) for c in range(WC)])
                xs, xn, gelu, prod = q[:, 0, :], q[:, 1, :], q[:, 2, :].rearrange("p (b s) -> p b s", b=2), q[:, 3:6, :]
                shift_tokens(core, xs.rearrange("p (b s) -> p b s", b=B), x)
                normalise(core, xs, xn, XBLOCKS, vec[:, 0:1], vec[:, 1:2])
                parts = [(j, min(P, DI - P * j), n) for j in range(3) for n in range(NB)]
                with core.stage("inner_done", "gelu_done", "gated") as (block, inner_done, gelu_done, gated):
                    @block.tensor
                    def _(pe):
                        for s, (j, m, n) in enumerate(parts):
                            if s >= 2:
                                pe.wait_ge(gated, s - 1)
                            for half in range(2):
                                mm = nc.tensor.matmul(core.bank(2 * (s % 2) + half)[0:m], W1[:, DI * half + P * j:DI * half + P * j + m],
                                                      xn[:, BLK * n:BLK * n + BLK], start=True, stop=True)
                            mm.then_inc(inner_done, 1)

                    @block.scalar
                    def _(act):
                        for s, (j, m, n) in enumerate(parts):
                            act.wait_ge(inner_done, s + 1)
                            if s >= 2:
                                act.wait_ge(gated, s - 1)
                            nc.scalar.activation(gelu[0:m, s % 2, :], core.bank(2 * (s % 2) + 1)[0:m], ACT.Gelu,
                                                 bias=vec[0:m, 6 + j:7 + j]).then_inc(gelu_done, 1)

                    @block.vector
                    def _(dve):
                        for s, (j, m, n) in enumerate(parts):
                            dve.wait_ge(gelu_done, s + 1)
                            nc.vector.scalar_tensor_tensor(prod[0:m, j, BLK * n:BLK * n + BLK], core.bank(2 * (s % 2))[0:m],
                                                           vec[0:m, 3 + j:4 + j], gelu[0:m, s % 2, :], ALU.add, ALU.mult).then_inc(gated, 1)
                add_projection(core, x, [(W2[0:m, j, :], prod[0:m, j, :]) for j, m in ((0, P), (1, P), (2, DI - 2 * P))], vec[:, 2:3])
            core.settle()
        before = sb([P, N], "before")
        load(core, [(before, start)])
        normalise(core, x, x, XBLOCKS, terms=[(core.const["ident"], before)])


def l2_attn(core):
    nc, io = core.nc, core.io
    A = lambda n: io["L2_attn_" + n]
    WINDOW = 2 * P
    STRIPS = P // 32
    with ExitStack() as mem:
        sb = lambda shape, name="work", dtype=F32: core.buffer(mem, shape, name, dtype)
        W, Wo, vec, bv, rel = sb([P, 3 * P], "Wqkv"), sb([P, P], "Wo"), sb([P, 3], "vec"), sb([P, P], "bv"), sb([PAIRS * D8, EXT], "rel")
        core.fetch("l2a", core.consts(mem, "keypart") + [(W, A("W")), (Wo, A("Wo")), (vec, A("vec")), (rel, A("rel")),
                                                          (bv, A("bv").unsqueeze(0).broadcast_to([P, P]))])
        core.need("l2a")
        qT, kT, v, o = sb([P, N], "qT"), sb([P, N], "kT"), sb([P, TILES, P], "v"), sb([P, TILES, P], "o")
        products(core, by_block(qT, W[:, 0:P], core.xT, None, 1.0, vec[:, 0:1]) + by_block(kT, W[:, P:2 * P], core.xT, None, 1.0, vec[:, 1:2])
                 + [plain(v[:, t, :], [(core.xT[:, P * t:P * t + P], W[:, 2 * P:3 * P])]) for t in range(TILES)])
        edges = sb([P, TILES, H16, 2], "edges")
        scratch = nc.dram_tensor("relative", (TILES, P * H16 * EXT), F32, kind="Internal")
        with core.stage("dve_step") as (block, dve_step):
            @block.vector
            def _(dve):
                link = chained(dve, dve_step)
                link(nc.vector.tensor_tensor(v, v, bv.unsqueeze(1).broadcast_to([P, TILES, P]), ALU.add))
                link(nc.vector.tensor_scalar(qT, qT, float(1.0 / np.sqrt(D8)), None, ALU.mult))
        q, k = stack_heads(core, mem, qT, kT)
        rel_parts, rel_stack = sb([PAIRS * D8, 3, EXT], "rel_parts", BF16), sb([PAIRS * D8, EXT], "rel_stack", BF16)
        split_rows(core, PAIRS * D8, [(rel_parts, rel)])
        with core.stage("dve_step") as (block, dve_step):
            @block.vector
            def _(dve):
                link = chained(dve, dve_step)
                which = core.const["keypart"]
                link(nc.vector.tensor_scalar(rel_stack, rel_parts[:, 0, :], which[:, 0:1], None, ALU.mult))
                for j in (1, 2):
                    link(nc.vector.scalar_tensor_tensor(rel_stack, rel_parts[:, j, :], which[:, j:j + 1], rel_stack, ALU.mult, ALU.add))
        with ExitStack() as inner:
            rows = core.buffer(inner, [P, 2, H16, EXT], "rows")
            with core.stage("bias_done", "out_by_act", "out_by_dve", "stored_even", "stored_odd", "edges_kept") as \
                    (block, bias_done, by_act, by_dve, stored_even, stored_odd, kept):
                stored = (stored_even, stored_odd)

                @block.tensor
                def _(pe):
                    for u in range(TILES * H16):
                        if u >= 8:
                            if u % 2:
                                pe.wait_ge(by_dve, (u - 8) // 2 + 1)
                            else:
                                pe.wait_ge(by_act, (u - 8) // 2 + 1)
                        t, h = u // H16, u % H16
                        nc.tensor.matmul(core.bank(u % 8)[:, 0:EXT], q[:, h, P * t:P * t + P], rel_stack, start=True, stop=True) \
                            .then_inc(bias_done, 1)

                @block.scalar
                def _(act):
                    for u in range(0, TILES * H16, 2):
                        t, h = u // H16, u % H16
                        act.wait_ge(bias_done, u + 1)
                        if h == 0 and t >= 2:
                            act.wait_ge(stored[t % 2], 16 * STRIPS * (t // 2))
                            act.wait_ge(kept, t - 1)
                        nc.scalar.copy(rows[:, t % 2, h, :], core.bank(u % 8)[:, 0:EXT]).then_inc(by_act, 1)

                @block.vector
                def _(dve):
                    for u in range(1, TILES * H16, 2):
                        t, h = u // H16, u % H16
                        dve.wait_ge(bias_done, u + 1)
                        if h == 1 and t >= 2:
                            dve.wait_ge(stored[t % 2], 16 * STRIPS * (t // 2))
                            dve.wait_ge(kept, t - 1)
                        nc.vector.tensor_copy(rows[:, t % 2, h, :], core.bank(u % 8)[:, 0:EXT]).then_inc(by_dve, 1)
                        if h == H16 - 1:
                            dve.wait_ge(by_act, H16 // 2 * (t + 1))
                            dve.wait_ge(by_dve, H16 // 2 * (t + 1))
                            nc.vector.tensor_copy(edges[:, t, :, :], rows[:, t % 2, :, 0:EXT - 1:EXT - 2]).then_inc(kept, 1)

                @block.sync
                def _(sp):
                    for t in range(TILES):
                        sp.wait_ge(by_act, H16 // 2 * (t + 1))
                        sp.wait_ge(by_dve, H16 // 2 * (t + 1))
                        for g in range(STRIPS):
                            strip, lo = slice(32 * g, 32 * g + 32), P - 32 * (g + 1)
                            sp.dma_start(scratch.ap()[t].rearrange("(p h c) -> p h c", p=P, h=H16)[strip, :, lo:lo + WINDOW + 32],
                                         rows[strip, t % 2, :, lo:lo + WINDOW + 32]).then_inc(stored[t % 2], 16)
                    for one in stored:
                        sp.wait_ge(one, 8 * STRIPS * TILES)
        window = sb([P, 2, H16, WINDOW], "window")

        def parts(u):
            t, h = u[0], u[1]
            first = P * (t % 4) - REL
            a, b = max(first, 0), min(first + WINDOW, S)
            out = [(a, b, window[:, t % 2, h, a - first:b - first])]
            if a:
                out.append((0, a, edges[:, t, h, 0:1]))
            if b < S:
                out.append((b, S, edges[:, t, h, 1:2]))
            return out

        def stream(t):
            src = bass.AP(scratch, t * P * H16 * EXT + P - 1, [[H16 * EXT - 1, P], [EXT, H16], [1, WINDOW]])
            return [(window[:, t % 2], src)]

        narrow_attention(core, lambda h, a, n: q[:, h, a:a + n], k, [[v[:, 4 * b + i, :] for i in range(4)] for b in range(B)],
                         o, SELF_KEYS, 1.0, S, parts, stream, lag=2)
        turn_tokens(core, qT, o)
        normalise(core, core.xT, core.xT, XBLOCKS, terms=[(Wo, qT)], bias=vec[:, 2:3])


def l2_ffn_weights(core, mem):
    io, E = core.io, 8
    W, router, rbias, bias = (core.buffer(mem, s, "experts") for s in ([P, E, P], [P, E], [P, E], [E, P]))
    core.fetch("l2f", [(W, io["L2_ffn_W"]), (router, io["L2_ffn_router"]), (rbias, io["L2_ffn_b_router"].unsqueeze(0).broadcast_to([P, E])),
                       (bias, io["L2_ffn_b_experts"])])
    return W, router, rbias, bias


def l2_ffn(core):
    nc = core.nc
    E = 8
    x = core.xT
    with ExitStack() as mem:
        sb = lambda shape, name="work": core.buffer(mem, shape, name)
        W, router, rbias, bias = core.weights("l2f", mem, l2_ffn_weights)
        core.need("l2f")
        logits, w, wT = sb([P, TILES, E], "logits"), sb([P, TILES, E], "weights"), sb([E, N], "wT")
        with core.stage("logits_done", "logits_out") as (block, logits_done, logits_out):
            @block.tensor
            def _(pe):
                for t in range(TILES):
                    mm = nc.tensor.matmul(core.bank(0)[:, E * t:E * t + E], x[:, P * t:P * t + P], router, start=True, stop=True)
                mm.then_inc(logits_done, 1)

            @block.vector
            def _(dve):
                dve.wait_ge(logits_done, 1)
                nc.vector.tensor_tensor(logits, core.bank(0)[:, 0:E * TILES].rearrange("p (t e) -> p t e", e=E),
                                        rbias.unsqueeze(1).broadcast_to([P, TILES, E]), ALU.add).then_inc(logits_out, 1)
        top_weights(core, logits, E, 2, False, w)
        transposes(core, [(wT[:, P * t:P * t + 4 * P], [w[:, t + i, :] for i in range(4)]) for t in (0, 4)])
        pick, parts = spread_rows(core, mem, w, E)
        xw = sb([P, 2, BLK], "weighted")
        cols = lambda i: slice(BLK * (i % 2), BLK * (i % 2) + BLK)
        U = 2 * E
        with core.stage("weight_spread", "x_weighted", "expert_done", "dve_step") as (block, spread, weighted, expert_done, dve_step):
            @block.tensor
            def _(pe):
                def pick_row(i):
                    if i >= 2:
                        pe.wait_ge(weighted, i - 1)
                    nc.tensor.matmul(core.bank(i % 2), pick[:, i // 2, :], parts[:, cols(i)], start=True, stop=True).then_inc(spread, 1)
                for n in range(NB):
                    nc.tensor.matmul(core.bank(2 + n), bias, wT[:, cols(n)], start=True, stop=False)
                pick_row(0)
                for i in range(U):
                    if i + 1 < U:
                        pick_row(i + 1)
                    pe.wait_ge(weighted, i + 1)
                    nc.tensor.matmul(core.bank(2 + i % 2), W[:, i // 2, :], xw[:, i % 2, :], start=False, stop=(i >= U - 2)).then_inc(expert_done, 1)

            @block.vector
            def _(dve):
                for i in range(U):
                    dve.wait_ge(spread, i + 1)
                    if i >= 2:
                        dve.wait_ge(expert_done, i - 1)
                    nc.vector.tensor_tensor(xw[:, i % 2, :], core.bank(i % 2), x[:, cols(i)], ALU.mult).then_inc(weighted, 1)
                dve.wait_ge(weighted, U)
                dve.wait_ge(expert_done, U)
                link = chained(dve, dve_step)
                for n in range(NB):
                    link(nc.vector.tensor_tensor(x[:, cols(n)], core.bank(2 + n), x[:, cols(n)], ALU.add))
        normalise(core, x, x, XBLOCKS)


def l3_attn_weights(core, mem):
    io = core.io
    W, Wg, Wo = (core.buffer(mem, s, "weights") for s in ([P, 3 * INNER], [P, H16], [P, WC, P]))
    core.fetch("l3a", core.consts(mem, "upper") + [(W, io["L3_attn_w_qkv"]), (Wg, io["L3_attn_w_gates"]), (Wo, io["L3_attn_w_out"])])
    return W, Wg, Wo


def l3_attn(core):
    nc = core.nc
    x = core.xT
    CAP = 50.0
    with ExitStack() as mem:
        sb = lambda shape, name="work": core.buffer(mem, shape, name)
        W, Wg, Wo = core.weights("l3a", mem, l3_attn_weights)
        q, k = sb([P, WC, N], "q"), sb([P, H16, N], "k")
        v = sb([P, TILES, H16, D64 + 1], "v_ones")
        core.need("l3a", zeros=[k[0:D64, 1::2, :], k[D64:P, 0::2, :]])
        o = sb([P, TILES, WC, P], "o")
        gates = sb([P, TILES, H16], "gates")
        with ExitStack() as inner:
            with core.stage("ones_set") as (block, ones_set):
                @block.vector
                def _(dve):
                    nc.vector.memset(v[:, :, :, D64:D64 + 1], 1.0).then_inc(ones_set, 1)
            blocks = [slice(S * b, S * b + S) for b in range(B)]
            jobs = [plain(q[:, c, n], [(W[:, P * c:P * c + P], x[:, n])]) for c in range(WC) for n in blocks]
            jobs += [plain((k[0:D64, 2 * c, n], k[D64:P, 2 * c + 1, n]), [(W[:, INNER + P * c:INNER + P * c + P], x[:, n])])
                     for c in range(WC) for n in blocks]
            jobs += [plain(v[:, t, 8 * j:8 * j + 8, 0:D64], [(x[:, P * t:P * t + P], W[:, 2 * INNER + BLK * j:2 * INNER + BLK * j + BLK])])
                     for t in range(TILES) for j in range(2)]
            jobs += [plain(gates[:, t, :], [(x[:, P * t:P * t + P], Wg)], ACT.Sigmoid) for t in range(TILES)]
            products(core, jobs)
            U = B * H16
            first = [0, 4 * P, 7 * P, 9 * P]
            prob = core.buffer(inner, [P, 2, 10 * P], "prob")
            inv = core.buffer(inner, [P, 2, 4], "inverse")
            with core.stage("scores_ready", "tanh_done", "exp_done", "masked", "values_done", "inverted", "head_out") as \
                    (block, scores_ready, tanh_done, exp_done, masked, values_done, inverted, head_out):
                @block.tensor
                def _(pe):
                    def scores(u):
                        b, h = u // H16, u % H16
                        for j in range(4):
                            if u >= 1:
                                pe.wait_ge(tanh_done, 4 * (u - 1) + j + 1)
                            nc.tensor.matmul(core.bank(j)[:, 0:S - P * j], k[:, h, S * b + P * j:S * b + P * j + P],
                                             q[:, h // 2, S * b + P * j:S * b + S], start=True, stop=True).then_inc(scores_ready, 1)

                    def values(u):
                        b, h = u // H16, u % H16
                        pe.wait_ge(masked, 4 * (u + 1))
                        if u >= 4:
                            pe.wait_ge(head_out, u - 3)
                        for i in range(4):
                            for j in range(i + 1):
                                mm = nc.tensor.matmul(core.bank(4 + u % 4)[:, (D64 + 1) * i:(D64 + 1) * (i + 1)],
                                                      prob[:, u % 2, first[j] + P * (i - j):first[j] + P * (i - j) + P],
                                                      v[:, 4 * b + j, h, :], start=(j == 0), stop=(j == i))
                        mm.then_inc(values_done, 1)

                    scores(0)
                    for u in range(U):
                        if u + 1 < U:
                            scores(u + 1)
                        values(u)

                @block.scalar
                def _(act):
                    for u in range(U):
                        for j in range(4):
                            act.wait_ge(scores_ready, 4 * u + j + 1)
                            if j == 0 and u >= 2:
                                act.wait_ge(values_done, u - 1)
                            nc.scalar.activation(prob[:, u % 2, first[j]:first[j] + S - P * j], core.bank(j)[:, 0:S - P * j], ACT.Tanh,
                                                 scale=D64 ** -0.5 / CAP).then_inc(tanh_done, 1)
                        act.wait_ge(tanh_done, 4 * (u + 1))
                        nc.scalar.activation(prob[:, u % 2, :], prob[:, u % 2, :], ACT.Exp, scale=CAP).then_inc(exp_done, 1)

                @block.vector
                def _(dve):
                    def finish(u):
                        b, h = u // H16, u % H16
                        out = core.bank(4 + u % 4)[:, 0:4 * (D64 + 1)].rearrange("p (i d) -> p i d", i=4)
                        dve.wait_ge(values_done, u + 1)
                        if u >= 2:
                            dve.wait_ge(head_out, u - 1)
                        r = inv[:, u % 2, :]
                        nc.vector.reciprocal(r.unsqueeze(2), out[:, :, D64:D64 + 1]).then_inc(inverted, 1)
                        dve.wait_ge(inverted, 2 * u + 1)
                        nc.vector.tensor_tensor(r, r, gates[:, 4 * b:4 * b + 4, h], ALU.mult).then_inc(inverted, 1)
                        dve.wait_ge(inverted, 2 * u + 2)
                        nc.vector.tensor_tensor(o[:, 4 * b:4 * b + 4, h // 2, D64 * (h % 2):D64 * (h % 2) + D64], out[:, :, 0:D64],
                                                r.unsqueeze(2).broadcast_to([P, 4, D64]), ALU.mult).then_inc(head_out, 1)
                    for u in range(U):
                        dve.wait_ge(exp_done, u + 1)
                        for j in range(4):
                            d = prob[:, u % 2, first[j]:first[j] + P]
                            nc.vector.tensor_tensor(d, d, core.const["upper"], ALU.mult).then_inc(masked, 1)
                        if u >= 1:
                            finish(u - 1)
                    finish(U - 1)
        turn_heads(core, o)
        normalise(core, x, x, XBLOCKS, terms=[(Wo[:, c, :], o[:, :, c, :]) for c in range(WC)])


def rotary_queries(core, W, qc, q):
    nc = core.nc
    U, HU = 2 * TILES, H16 // 2
    with ExitStack() as mem:
        sb = lambda shape, name: core.buffer(mem, shape, name)
        rows, sined = sb([P, 3, HU, P], "rows"), sb([P, 2, HU, D64], "sined")
        block, projected, plain_copied, rotated, added, turned, copied = mem.enter_context(
            core.stage("projected", "nope_copied", "rotated", "added", "turned", "turned_copied"))
        made = lambda u: core.bank(2 * (u % 2), 2).rearrange("p (h d) -> p h d", h=HU)
        back = lambda u: core.bank(4 + 2 * (u % 2), 2)

        @block.tensor
        def _(pe):
            def turn(u):
                pe.wait_ge(added, u + 1)
                if u >= 2:
                    pe.wait_ge(copied, u - 1)
                for h in range(HU):
                    mm = nc.tensor.transpose(back(u)[:, P * h:P * h + P], rows[:, u % 3, h, :], core.const["ident"])
                mm.then_inc(turned, 1)

            for u in range(U):
                t, first = u // 2, INNER * (u % 2)
                if u >= 2:
                    pe.wait_ge(rotated, u - 1)
                for half in range(2):
                    mm = nc.tensor.matmul(core.bank(2 * (u % 2) + half), qc[:, P * t:P * t + P],
                                          W[:, first + BLK * half:first + BLK * half + BLK], start=True, stop=True)
                mm.then_inc(projected, 1)
                if u >= 1:
                    turn(u - 1)
            turn(U - 1)

        @block.scalar
        def _(act):
            def copy_back(u):
                act.wait_ge(turned, u + 1)
                nc.scalar.copy(q[:, u // 2, HU * (u % 2):HU * (u % 2) + HU, :].rearrange("p h q -> p (h q)"), back(u)).then_inc(copied, 1)

            for u in range(U):
                act.wait_ge(projected, u + 1)
                if u >= 3:
                    act.wait_ge(turned, u - 2)
                nc.scalar.copy(rows[:, u % 3, :, 0:D64], made(u)[:, :, 0:D64]).then_inc(plain_copied, 1)
                if u >= 2:
                    copy_back(u - 2)
            copy_back(U - 2)
            copy_back(U - 1)

        @block.vector
        def _(dve):
            for u in range(U):
                dve.wait_ge(plain_copied, u + 1)
                if u >= 2:
                    dve.wait_ge(added, u - 1)
                a = made(u)
                tab = lambda i, lo, hi: core.const["rotary"][:, u // 2 % 4, i, lo:hi].unsqueeze(1).broadcast_to([P, HU, hi - lo])
                nc.vector.tensor_tensor(rows[:, u % 3, :, D64:P], a[:, :, D64:P], tab(0, 0, 64), ALU.mult)
                nc.vector.tensor_tensor(sined[:, u % 2, :, 0:32], a[:, :, D64 + 32:P], tab(1, 0, 32), ALU.mult)
                nc.vector.tensor_tensor(sined[:, u % 2, :, 32:64], a[:, :, D64:D64 + 32], tab(1, 32, 64), ALU.mult).then_inc(rotated, 1)

        @block.gpsimd
        def _(pool):
            for u in range(U):
                pool.wait_ge(rotated, u + 1)
                rope = rows[:, u % 3, :, D64:P]
                nc.gpsimd.tensor_tensor(rope, rope, sined[:, u % 2], ALU.add).then_inc(added, 1)


def l3_xattn(core):
    nc, io = core.nc, core.io
    x = core.xT
    SCALE = float(np.float32(1.0) / np.sqrt(2 * D64).astype(np.float32))
    with ExitStack() as mem:
        sb = lambda shape, name="work": core.buffer(mem, shape, name)
        W = {n: sb(list(io["L3_xattn_" + n].shape), n) for n in ("w_kv_comp", "w_q_down", "w_q", "w_k_up", "w_k_rope", "w_v_up", "w_out")}
        seg = core.buffer(mem, [P, TILES], "segment", I32)
        core.fetch("l3x", core.consts(mem, "rot", "cos", "sin", "keyno", "rotary") + [(W[n], io["L3_xattn_" + n]) for n in W]
                   + [(seg, io["segment"])])
        core.need("l3x")
        q, k, kr = sb([P, TILES, H16, P], "queries"), sb([P, H16, CT], "keys"), sb([P, CT], "k_rope")
        v, kvc, qc, o = sb([KT, 4, INNER], "v"), sb([P, CT], "kv_comp"), sb([P, N], "q_down"), sb([P, TILES, WC, P], "o")
        mask, segf, near = sb([P, TILES, SK], "mask"), sb([P, TILES], "segf"), sb([P, TILES, SK], "near")
        products(core, by_block(kvc, W["w_kv_comp"], core.ctx, n=CT) + by_block(qc, W["w_q_down"], x))
        jobs = by_block(kr, W["w_k_rope"], kvc, n=CT)
        jobs += [plain(k[0:D64, h, :], [(W["w_k_up"][:, D64 * h:D64 * h + D64], kvc)]) for h in range(H16)]
        jobs += [plain(v[:, i, BLK * j:BLK * j + BLK], [(kvc[:, KT * i:KT * i + KT], W["w_v_up"][:, BLK * j:BLK * j + BLK])]) for i in range(4) for j in range(2)]
        products(core, jobs)
        rotate(core, [(kr[:, SK * b:SK * b + SK], core.const["cos"], core.const["sin"]) for b in range(B)])
        with core.stage("dve_step", "keys_spread") as (block, dve_step, keys_spread):
            @block.scalar
            def _(act):
                for h in range(H16):
                    nc.scalar.copy(k[D64:P, h, :], kr[D64:P]).then_inc(keys_spread, 1)

            @block.vector
            def _(dve):
                link = chained(dve, dve_step)
                link(nc.vector.tensor_copy(segf, seg))
                link(nc.vector.tensor_tensor(mask, core.const["keyno"].unsqueeze(1).broadcast_to([P, TILES, SK]),
                                             segf.unsqueeze(2).broadcast_to([P, TILES, SK]), ALU.subtract))
                link(nc.vector.tensor_scalar(near, mask, -2.0, None, ALU.is_ge))
                link(nc.vector.tensor_scalar(mask, mask, 0.0, None, ALU.is_le))
                link(nc.vector.tensor_tensor(mask, mask, near, ALU.mult))
                link(nc.vector.tensor_scalar(mask, mask, 1.0, BIG, ALU.subtract, ALU.mult))
        rotary_queries(core, W["w_q"], qc, q)
        units = [(t, h, [(0, q[:, t, h, :], k[:, h, SK * (t // 4):SK * (t // 4) + SK], True, True)],
                  [v[:, 2 * (t // 4) + i, D64 * h:D64 * h + D64] for i in range(2)]) for t in range(TILES) for h in range(H16)]
        attend(core, units, XKEYS, D64, lambda t: o[:, t].rearrange("p c q -> p (c q)"), SCALE, lambda u: [(0, SK, mask[:, u[0], :])], nk=SK, lag=2)
        turn_heads(core, o)
        normalise(core, x, x, XBLOCKS, terms=[(W["w_out"][:, c, :], o[:, :, c, :]) for c in range(WC)])


def turn_heads(core, a):
    transposes(core, [(a[:, t, c:c + 4, :], [a[:, t, c + i, :] for i in range(4)]) for t in range(TILES) for c in (0, 4)])


def l3_ffn_weights(core, mem):
    names = ("proj", "C", "Win1", "Wout1", "Win2", "Wout2", "bias")
    W = {n: core.buffer(mem, core.io["L3_ffn_" + n].shape, n) for n in names}
    core.fetch("l3f", core.consts(mem, "restart16", "rank", "invrank") + [(W[n], core.io["L3_ffn_" + n]) for n in names])
    return W


def l3_ffn(core):
    nc = core.nc
    x = core.xT
    E, R = 16, 64
    with ExitStack() as mem:
        sb = lambda shape, name="work": core.buffer(mem, shape, name)
        W = core.weights("l3f", mem, l3_ffn_weights)
        core.need("l3f")
        z, zs, rest, cum, cq, t1, t2 = (sb([P, TILES, E], n) for n in ("z", "sorted", "rest", "mean", "meansq", "work", "tau"))
        m, s1 = sb([P, TILES], "row"), sb([P, TILES], "row2")
        per = lambda a: a.unsqueeze(2).broadcast_to([P, TILES, E])
        flat = lambda a: a.rearrange("p t e -> p (t e)")
        products(core, [plain(z[:, t, :], [(x[:, P * t:P * t + P], W["proj"])]) for t in range(TILES)])
        with core.stage("dve_step", "var_ready", "std_done", "delta_ready", "root_done") as (block, dve_step, var_ready, std_done, delta_ready, root_done):
            @block.vector
            def _(dve):
                link = chained(dve, dve_step)
                link(nc.vector.reduce_sum(m, z, AX))
                link(nc.vector.tensor_scalar(m, m, 1.0 / E, None, ALU.mult))
                link(nc.vector.tensor_tensor(z, z, per(m), ALU.subtract))
                link(nc.vector.tensor_tensor(t1, z, z, ALU.mult))
                link(nc.vector.reduce_sum(m, t1, AX))
                nc.vector.tensor_scalar(m, m, 1.0 / E, None, ALU.mult).then_inc(var_ready, 1)
                dve.wait_ge(std_done, 1)
                link(nc.vector.reciprocal(m, m))
                link(nc.vector.tensor_tensor(z, z, per(m), ALU.mult))
                link(nc.vector.tensor_scalar(z, z, 0.5, None, ALU.mult))
                link(nc.vector.reduce_max(m, z, AX))
                link(nc.vector.tensor_tensor(z, z, per(m), ALU.subtract))
                for t in range(TILES):
                    link(nc.vector.max(zs[:, t, 0:8], z[:, t, :]))
                for t in range(TILES):
                    link(nc.vector.match_replace(rest[:, t, :], zs[:, t, 0:8], z[:, t, :], -BIG))
                for t in range(TILES):
                    link(nc.vector.max(zs[:, t, 8:16], rest[:, t, :]))
                link(nc.vector.tensor_tensor(t1, zs, zs, ALU.mult))
                link(nc.vector.tensor_tensor_scan(flat(cum), core.const["restart16"], flat(zs), 0.0, ALU.mult, ALU.add))
                link(nc.vector.tensor_tensor_scan(flat(cq), core.const["restart16"], flat(t1), 0.0, ALU.mult, ALU.add))
                link(nc.vector.tensor_tensor(flat(cum), flat(cum), core.const["invrank"], ALU.mult))
                link(nc.vector.tensor_tensor(flat(cq), flat(cq), core.const["invrank"], ALU.mult))
                link(nc.vector.tensor_tensor(t1, cum, cum, ALU.mult))
                link(nc.vector.tensor_tensor(t1, cq, t1, ALU.subtract))
                link(nc.vector.tensor_tensor(flat(t1), flat(t1), core.const["rank"], ALU.mult))
                link(nc.vector.tensor_scalar(t1, t1, -1.0, 1.0, ALU.mult, ALU.add))
                link(nc.vector.tensor_tensor(flat(t1), flat(t1), core.const["invrank"], ALU.mult))
                nc.vector.tensor_scalar(t1, t1, 0.0, None, ALU.max).then_inc(delta_ready, 1)
                dve.wait_ge(root_done, 1)
                link(nc.vector.tensor_tensor(t2, cum, t1, ALU.subtract))
                link(nc.vector.tensor_tensor(t1, t2, zs, ALU.is_le))
                link(nc.vector.reduce_sum(m, t1, AX))
                link(nc.vector.tensor_tensor(t1, core.const["rank"].rearrange("p (t e) -> p t e", e=E), per(m), ALU.is_equal))
                link(nc.vector.tensor_tensor(t1, t1, t2, ALU.mult))
                link(nc.vector.reduce_sum(m, t1, AX))
                link(nc.vector.tensor_tensor(z, z, per(m), ALU.subtract))
                link(nc.vector.tensor_scalar(z, z, 0.0, None, ALU.max))
                link(nc.vector.tensor_tensor(z, z, z, ALU.mult))

            @block.scalar
            def _(act):
                act.wait_ge(var_ready, 1)
                nc.scalar.activation(m, m, ACT.Sqrt, bias=core.const["cols"][:, 0:1]).then_inc(std_done, 1)
                act.wait_ge(delta_ready, 1)
                nc.scalar.activation(t1, t1, ACT.Sqrt).then_inc(root_done, 1)
        aT, g, z1, h, z2 = sb([E, N], "weights"), sb([R, 2, N], "gates"), sb([R, N], "z1"), sb([P, 4, N], "h"), sb([R, N], "z2")
        transposes(core, [(aT[:, P * t:P * t + 4 * P], [z[:, t + i, :] for i in range(4)]) for t in (0, 4)])
        products(core, by_block(g[:, 0, :], W["C"][:, 0, :], aT) + by_block(g[:, 1, :], W["C"][:, 1, :], aT)
                 + by_block(z1, W["Win1"], x, None, 1.0, W["bias"][:, 0:1]))

        def gated(a, i):
            with core.stage("gated") as (block, done):
                @block.vector
                def _(dve):
                    nc.vector.tensor_tensor(a, a, g[:, i, :], ALU.mult).then_inc(done, 1)
        gated(z1, 0)
        products(core, [j for c in range(4) for j in by_block(h[:, c, :], W["Wout1"][:, P * c:P * c + P], z1, ACT.Gelu)])
        products(core, [plain(z2[:, BLK * n:BLK * n + BLK], [(W["Win2"][:, c, :], h[:, c, BLK * n:BLK * n + BLK]) for c in range(4)], None, 1.0, W["bias"][:, 1:2])
                        for n in range(NB)])
        gated(z2, 1)
        normalise(core, x, x, XBLOCKS, terms=[(W["Wout2"], z2)])


def turn_tokens(core, dstT, src):
    transposes(core, [(dstT[:, P * t:P * t + 4 * P], [src[:, t + i, :] for i in range(4)]) for t in range(0, src.shape[1], 4)])


def network(nc, io):
    core = Core(nc, io)
    with ExitStack() as mem:
        sb = lambda shape, name="work": core.buffer(mem, shape, name)
        core.xT = sb([P, N])
        core.ctx = sb([P, CT])
        c = {n: sb(list(io["c_" + n].shape)) for n in ("ident", "mean", "cols")}
        for n, t in c.items():
            core.const[n] = t
        with nc.sbuf_tensor("x_tok", [P, TILES, P], F32) as x_tok, nc.sbuf_tensor("c_tok", [KT, 4, P], F32) as c_tok:
            load(core, [(c[n][:], io["c_" + n]) for n in c] + [
                (x_tok[:], io["x"].rearrange("b (t p) f -> p (b t) f", p=P)),
                (c_tok[:], io["ctx_1024"].rearrange("b (t p) f -> p (b t) f", p=KT))])
            turn_tokens(core, core.xT, x_tok)
            transposes(core, [(core.ctx[:], [c_tok[:, i, :] for i in range(4)])])

        def consts(m, *names):
            ts = {n: core.buffer(m, io["c_" + n].shape, n) for n in names}
            for n, t in ts.items():
                core.const[n] = t
            return [(t[:], io["c_" + n]) for n, t in ts.items()]
        core.consts = consts

        first, local, early, late, moe = (ExitStack() for _ in range(5))
        until = {l0_xattn: first, l1_xattn: early, l1_ffn: local, l2_ffn: moe, l3_attn: late}
        plan = {l0_attn: [("l0x", first, l0_xattn_weights)],
                l0_ffn: [("l1f", local, l1_ffn_weights), ("l1a", early, l1_attn_weights), ("L1_xattn_", early, narrow_cross_weights("L1_xattn_", True))],
                l2_xattn: [("l3f", mem, l3_ffn_weights), ("l3a", late, l3_attn_weights), ("l2f", moe, l2_ffn_weights)]}
        head64 = core.buffer(first, [P, P], "head64")
        core.const["head64"] = head64
        core.fetch("head64", [(head64, io["c_head64"])])
        core.need("head64")
        for layer in LAYERS:
            for tag, where, make in plan.get(layer, []):
                core.reserve(tag, where, make)
            layer(core)
            if layer in until:
                until[layer].close()

        with nc.sbuf_tensor("y_tok", [P, TILES, P], F32) as y:
            transposes(core, [(y[:, t:t + 4, :], [core.xT[:, P * (t + i):P * (t + i) + P] for i in range(4)]) for t in (0, 4)])
            with core.stage("stored") as (block, stored):
                @block.sync
                def _(sp):
                    sp.dma_start(io["out"].rearrange("b (t p) f -> p (b t) f", p=P), y[:]).then_inc(stored, 16)
                    sp.wait_ge(stored, 16)


LAYERS = [l0_attn, l0_xattn, l0_ffn, l1_attn, l1_xattn, l1_ffn, l2_attn, l2_xattn, l2_ffn, l3_attn, l3_xattn, l3_ffn]


def layouts(inputs):
    a = {n: np.asarray(v) for n, v in inputs.items()}
    i = {"x": a["x"], "ctx_1024": a["ctx_1024"]}
    L = lambda n: a["L0_attn_" + n]
    i["mix"] = np.stack([L("x_" + n)[0, 0] for n in "rwkvag"], 1)
    i["vec"] = np.stack([L(n)[0, 0] for n in ("w0", "a0", "v0", "k_k", "k_a")] + [L("r_k").reshape(P)], 1)
    i["down"] = np.concatenate([L("w1"), L("a1"), L("v1")], 1)
    i["up"] = np.stack([L("w2"), L("a2"), np.concatenate([L("v2"), np.zeros((32, P), np.float32)])], 1)
    for n in ("Wr", "Wk", "Wv", "Wo", "g1", "g2", "ln_w", "ln_b"):
        i["L0_attn_" + n] = L(n)
    i["mask"] = a["mask_BxS2_bk0"].astype(np.int32)
    X = lambda n: a["L0_xattn_" + n]
    for n in ("W_q", "W_kv", "W_out"):
        i["L0_xattn_" + n] = X(n)
    i["L0_xattn_vec"] = np.stack([X("ln_x_g"), X("ln_x_b"), X("ln_l_g"), X("ln_l_b"), np.concatenate([X("q_gamma")] * 2),
                                  np.concatenate([X("k_gamma")] * 2), X("b_out")], 1)
    F = lambda n: a["L0_ffn_" + n]
    i["L0_ffn_router"], i["L0_ffn_router_bias"] = F("router_w").T, F("router_bias")
    i["L0_ffn_gate"] = np.concatenate([F("gate_w"), F("sgate_w").reshape(4, P, P)], 0).transpose(2, 0, 1)
    i["L0_ffn_up"] = np.concatenate([F("up_w"), F("sup_w").reshape(4, P, P)], 0).transpose(2, 0, 1)
    i["L0_ffn_down"] = np.concatenate([F("down_w"), F("sdown_w").reshape(P, 4, P).transpose(1, 0, 2)], 0).transpose(2, 0, 1)
    for n in ("w_Q", "w_K", "w_V"):
        i["L1_attn_" + n] = a["L1_attn_" + n]
    for l in ("L1_xattn_", "L2_xattn_"):
        for n in ("Wq", "Wk", "Wv", "Wo", "bv"):
            i[l + n] = a[l + n]
        i[l + "vec"] = np.stack([a[l + n] for n in ("bq", "bk", "bo")], 1)
    F = lambda n: a["L1_ffn_" + n]
    chunks = lambda w: w.reshape(*w.shape[:-2], WC, P, P).swapaxes(-3, -2)
    pad = lambda w, n, axis: np.concatenate([w, np.zeros(w.shape[:axis] + (n - w.shape[axis],) + w.shape[axis + 1:], w.dtype)], axis)
    one_more = lambda w: np.concatenate([w, w[:1]])
    i["L1_ffn_Wqkv"], i["L1_ffn_Wo"], i["L1_ffn_W1"] = one_more(F("Wqkv")), chunks(F("Wo")), F("W1")
    i["L1_ffn_W2"] = pad(F("W2"), 3 * P, 1).reshape(DEPTH, 3, P, P).transpose(0, 2, 1, 3)
    b1 = pad(F("b1").reshape(DEPTH, 2, DI), 3 * P, 2).reshape(DEPTH, 6, P).transpose(0, 2, 1)
    i["L1_ffn_vec"] = np.concatenate([np.stack([F("ln_g"), F("ln_b"), F("b2")], 2), b1], 2)
    g = np.stack([F("q_scale"), F("k_scale")], 1)
    i["L1_ffn_gains"] = one_more(np.stack([g, np.roll(g, D64 // 2, 2)], 2))
    A = lambda n: a["L2_attn_" + n]
    i["L2_attn_W"], i["L2_attn_Wo"] = A("in_proj_weight").T, A("out_w").T
    bias = A("in_proj_bias").reshape(3, P)
    i["L2_attn_vec"], i["L2_attn_bv"] = np.stack([bias[0], bias[1], A("out_b")], 1), bias[2]
    i["L2_attn_rel"] = np.tile(A("rel_pe")[np.clip(np.arange(EXT) - (P - 1), 0, 2 * REL)].T, (PAIRS, 1))
    i["L2_ffn_W"] = a["L2_ffn_W_experts"].transpose(2, 0, 1)
    i["L2_ffn_router"], i["L2_ffn_b_router"], i["L2_ffn_b_experts"] = a["L2_ffn_W_router"].T, a["L2_ffn_b_router"], a["L2_ffn_b_experts"]
    i["L3_attn_w_qkv"], i["L3_attn_w_gates"], i["L3_attn_w_out"] = a["L3_attn_w_qkv"], a["L3_attn_w_gates"], chunks(a["L3_attn_w_out"])
    X3 = lambda n: a["L3_xattn_" + n]
    i["L3_xattn_w_kv_comp"], i["L3_xattn_w_q_down"] = pad(X3("w_kv_comp"), P, 1), pad(X3("w_q_down"), P, 1)
    by_head = np.stack([X3(n).reshape(-1, H16, D64) for n in ("w_q_up", "w_q_rope")], 2)
    i["L3_xattn_w_q"] = pad(by_head.reshape(-1, 2 * INNER), P, 0)
    i["L3_xattn_w_k_up"], i["L3_xattn_w_v_up"] = pad(X3("w_k_up"), P, 0), pad(X3("w_v_up"), P, 0)
    i["L3_xattn_w_k_rope"] = pad(np.concatenate([X3("w_k_rope")] * 2, 1), P, 0)
    i["L3_xattn_w_out"] = chunks(X3("w_out"))
    i["segment"] = a["itok_BxS_0_511"].reshape(TILES, P).T
    F3 = lambda n: a["L3_ffn_" + n]
    i["L3_ffn_proj"], i["L3_ffn_C"] = F3("proj"), np.stack([F3("C1"), F3("C2")], 1)
    i["L3_ffn_Win1"], i["L3_ffn_Wout1"], i["L3_ffn_Wout2"] = F3("Win1")[:P], F3("Wout1").T, F3("Wout2").T
    i["L3_ffn_Win2"] = F3("Win2")[:512].reshape(4, P, 64).transpose(1, 0, 2)
    i["L3_ffn_bias"] = np.stack([F3("Win1")[P], F3("Win2")[512]], 1)
    i.update({"c_" + n: v for n, v in shape_constants().items()})
    return {n: np.ascontiguousarray(v) for n, v in i.items()}


def build(nc, arrays):
    io = {n: nc.dram_tensor("in_" + n, v.shape, mybir.dt.from_np(v.dtype), kind="ExternalInput").ap()
          for n, v in arrays.items()}
    io["out"] = nc.dram_tensor("out", (B, S, P), F32, kind="ExternalOutput").ap()
    network(nc, io)


def kernel(**inputs):
    import concourse.bacc as bacc
    from concourse.bass_utils import run_bass_kernel_spmd

    arrays = layouts(inputs)
    nc = bacc.Bacc("TRN2", target_bir_lowering=False, num_devices=1)
    build(nc, arrays)
    result = run_bass_kernel_spmd(nc, [{"in_" + n: v for n, v in arrays.items()}], core_ids=[0])
    return result.results[0]["out"]
```
